# Optimizing a Trainium2 kernel written in Bass

```python
import numpy as np
import jax
import jax.numpy as jnp

def _softmax(x, axis=-1):
    return jax.nn.softmax(x, axis=axis)

def _gelu(x):
    return jax.nn.gelu(x, approximate=True)

def _silu(x):
    return jax.nn.silu(x)

def _sigmoid(x):
    return jax.nn.sigmoid(x)

def _layernorm(x, axis=-1, eps=1e-05):
    m = jnp.mean(x, axis=axis, keepdims=True)
    v = jnp.var(x, axis=axis, keepdims=True)
    return (x - m) / jnp.sqrt(v + eps)

def _scatter_add(tgt, idx, src, axis=0):
    return tgt.at[idx].add(src)

def _segment_sum(src, seg, n):
    return jax.ops.segment_sum(src, seg, n)
kernel_name = 'mk_hybrid_d4_jaxref_r8_26cd5c'

def setup_inputs(seed: int=0):
    np.random.seed(seed)
    _w = jnp.asarray

    def _L0_attn_a_setup():
        import jax, jax.numpy as jnp
        import numpy as np
        HIDDEN = 256
        HEADS = 16
        HEAD_DIM = HIDDEN // HEADS
        key = jax.random.key(seed)
        kx, kq, kk, kv, ko = jax.random.split(key, 5)
        s = 1.0 / np.sqrt(HIDDEN)
        return {'x': jax.random.normal(kx, (2, 256, HIDDEN), dtype=jnp.float32), 'Wq': jax.random.normal(kq, (HIDDEN, HIDDEN), dtype=jnp.float32) * s, 'Wk': jax.random.normal(kk, (HIDDEN, HIDDEN), dtype=jnp.float32) * s, 'Wv': jax.random.normal(kv, (HIDDEN, HIDDEN), dtype=jnp.float32) * s, 'Wo': jax.random.normal(ko, (HIDDEN, HIDDEN), dtype=jnp.float32) * s}
    _L0_attn_a_in = _L0_attn_a_setup()

    def _L0_attn_b_setup():
        import jax, jax.numpy as jnp
        import numpy as np
        DIMS = 256
        HEAD_DIM = 64
        NUM_HEADS = DIMS // HEAD_DIM
        GQA_HEADS = 2
        EPS = 1e-08
        key = jax.random.key(seed)
        ks = jax.random.split(key, 6)
        b, s = (2, 256)
        kv_dims = HEAD_DIM * GQA_HEADS
        x = jax.random.normal(ks[0], (b, s, DIMS), dtype=jnp.float32)
        Wq = jax.random.normal(ks[1], (DIMS, DIMS), dtype=jnp.float32) * 0.02
        Wk = jax.random.normal(ks[2], (kv_dims, DIMS), dtype=jnp.float32) * 0.02
        Wv = jax.random.normal(ks[3], (kv_dims, DIMS), dtype=jnp.float32) * 0.02
        Wo = jax.random.normal(ks[4], (DIMS, DIMS), dtype=jnp.float32) * 0.02
        norm_scale = jnp.ones((DIMS,), dtype=jnp.float32)
        split_scale = jnp.full((DIMS,), 0.1, dtype=jnp.float32)
        return {'x': x, 'norm_scale': norm_scale, 'split_scale': split_scale, 'Wq': Wq, 'Wk': Wk, 'Wv': Wv, 'Wo': Wo}
    _L0_attn_b_in = _L0_attn_b_setup()

    def _L0_ffn_setup():
        import jax, jax.numpy as jnp
        import numpy as np
        B_, S, D = (2, 256, 256)
        F_ = 1024
        R = 16
        H = 16
        HD = D // H
        MOD_SCALE = 0.1
        EPS = 1e-06

        def _rmsnorm(x, w):
            v = jnp.mean(x * x, axis=-1, keepdims=True)
            return x * jax.lax.rsqrt(v + EPS) * w

        def _attention(x, Wq, Wk, Wv, Wo):
            b, s, d = x.shape
            q = (x @ Wq.T).reshape(b, s, H, HD)
            k = (x @ Wk.T).reshape(b, s, H, HD)
            v = (x @ Wv.T).reshape(b, s, H, HD)
            scores = jnp.einsum('bqhd,bkhd->bhqk', q, k) / np.sqrt(HD).astype(np.float32)
            causal = jnp.tril(jnp.ones((s, s), bool))
            scores = jnp.where(causal, scores, jnp.finfo(scores.dtype).min)
            probs = jax.nn.softmax(scores, axis=-1)
            out = jnp.einsum('bhqk,bkhd->bqhd', probs, v).reshape(b, s, d)
            return out @ Wo.T
        key = jax.random.key(seed)
        ks = jax.random.split(key, 12)
        sd = 0.02
        return {'hidden_states': jax.random.normal(ks[0], (B_, S, D), jnp.float32), 'ln1_w': jnp.ones((D,), jnp.float32), 'ln2_w': jnp.ones((D,), jnp.float32), 'Wq': jax.random.normal(ks[1], (D, D), jnp.float32) * sd, 'Wk': jax.random.normal(ks[2], (D, D), jnp.float32) * sd, 'Wv': jax.random.normal(ks[3], (D, D), jnp.float32) * sd, 'Wo': jax.random.normal(ks[4], (D, D), jnp.float32) * sd, 'A': jax.random.normal(ks[5], (D, R), jnp.float32) * (0.01 / np.sqrt(D)), 'B': jax.random.normal(ks[6], (R, F_), jnp.float32) * (0.01 / np.sqrt(R)), 'W_in_base': jax.random.normal(ks[7], (F_, D), jnp.float32) * sd, 'W_up_base': jax.random.normal(ks[8], (F_, D), jnp.float32) * sd, 'W_down': jax.random.normal(ks[9], (D, F_), jnp.float32) * sd}
    _L0_ffn_in = _L0_ffn_setup()

    def _L1_attn_a_setup():
        import jax, jax.numpy as jnp
        import numpy as np
        from jax import lax
        B, L, H = (2, 512, 256)
        NH = 16
        DK = H // NH
        C = 64
        EPS = 1e-05
        N_LAYER = 24

        def _gla_chunk(q, k, v, gf):
            b, Ls, dk = q.shape
            dv = v.shape[-1]
            n = Ls // C
            qc = q.reshape(b, n, C, dk).transpose(1, 0, 2, 3)
            kc = k.reshape(b, n, C, dk).transpose(1, 0, 2, 3)
            vc = v.reshape(b, n, C, dv).transpose(1, 0, 2, 3)
            gc = gf.reshape(b, n, C, dk).transpose(1, 0, 2, 3)
            Bc = jnp.cumsum(gc, axis=2)
            tril = jnp.tril(jnp.ones((C, C), bool))

            def step(S, inp):
                qh, kh, vh, Bh = inp
                Blast = Bh[:, -1, :]
                D = Bh[:, :, None, :] - Bh[:, None, :, :]
                A = jnp.einsum('bid,bjd,bijd->bij', qh, kh, jnp.exp(D))
                A = jnp.where(tril, A, 0.0)
                o_intra = jnp.einsum('bij,bjv->biv', A, vh)
                o_inter = jnp.einsum('bid,bdv->biv', qh * jnp.exp(Bh), S)
                kd = kh * jnp.exp(Blast[:, None, :] - Bh)
                S_new = S * jnp.exp(Blast)[..., None] + jnp.einsum('bjd,bjv->bdv', kd, vh)
                return (S_new, o_intra + o_inter)
            S0 = jnp.zeros((b, dk, dv), q.dtype)
            _, o = lax.scan(step, S0, (qc, kc, vc, Bc))
            return o.transpose(1, 0, 2, 3).reshape(b, Ls, dv)
        key = jax.random.key(seed)
        ks = jax.random.split(key, 7)
        std = 0.02
        return {'hidden_states': jax.random.normal(ks[0], (B, L, H), jnp.float32), 'Wq': jax.random.normal(ks[1], (DK, H), jnp.float32) * std, 'Wk': jax.random.normal(ks[2], (DK, H), jnp.float32) * std, 'Wog': jax.random.normal(ks[3], (H, H), jnp.float32) * std, 'Wig': jax.random.normal(ks[4], (H, H), jnp.float32) * std, 'Wo': jax.random.normal(ks[5], (H, H), jnp.float32) * (std / np.sqrt(2 * N_LAYER)), 'g_norm_w': jnp.ones((H,), jnp.float32)}
    _L1_attn_a_in = _L1_attn_a_setup()

    def _L1_attn_b_setup():
        import jax, jax.numpy as jnp
        import numpy as np
        B, K, D = (4, 512, 256)
        key = jax.random.key(seed)
        k1, k2, k3 = jax.random.split(key, 3)
        x = jax.random.normal(k1, (B, K, D), dtype=jnp.float32)
        W = jax.random.normal(k2, (D, D), dtype=jnp.float32) / np.sqrt(D)
        b = jax.random.normal(k3, (D,), dtype=jnp.float32) * 0.02
        return {'x': x, 'W': W, 'b': b}
    _L1_attn_b_in = _L1_attn_b_setup()

    def _L1_ffn_setup():
        import jax, jax.numpy as jnp
        import numpy as np
        NUM_EXPERTS = 32
        TOP_K = 8
        THRESHOLD = 0.8
        HIDDEN = 256
        INTER = 96
        key = jax.random.key(seed)
        k1, k2, k3, k4 = jax.random.split(key, 4)
        hidden_states = jax.random.normal(k1, (2, 128, HIDDEN), jnp.float32)
        gate_weight = jax.random.normal(k2, (NUM_EXPERTS, HIDDEN), jnp.float32) * 0.02
        gate_up_proj = jax.random.normal(k3, (NUM_EXPERTS, 2 * INTER, HIDDEN), jnp.float32) * 0.02
        down_proj = jax.random.normal(k4, (NUM_EXPERTS, HIDDEN, INTER), jnp.float32) * 0.02
        return {'hidden_states': hidden_states, 'gate_weight': gate_weight, 'gate_up_proj': gate_up_proj, 'down_proj': down_proj}
    _L1_ffn_in = _L1_ffn_setup()

    def _L2_attn_a_setup():
        import jax, jax.numpy as jnp
        import numpy as np
        import math
        D_MODEL = 256
        N_HEADS = 16
        D_HEAD = 128
        BATCH = 2
        SEQ = 256
        key = jax.random.key(seed)
        ks = jax.random.split(key, 5)
        std = 0.02
        x = jax.random.normal(ks[0], (BATCH, SEQ, D_MODEL), dtype=jnp.float32)
        W_Q = std * jax.random.normal(ks[1], (N_HEADS, D_HEAD, D_MODEL), dtype=jnp.float32)
        W_K = std * jax.random.normal(ks[2], (N_HEADS, D_HEAD, D_MODEL), dtype=jnp.float32)
        W_V = std * jax.random.normal(ks[3], (N_HEADS, D_HEAD, D_MODEL), dtype=jnp.float32)
        W_O = std * jax.random.normal(ks[4], (N_HEADS, D_MODEL, D_HEAD), dtype=jnp.float32)
        return {'x': x, 'W_Q': W_Q, 'W_K': W_K, 'W_V': W_V, 'W_O': W_O}
    _L2_attn_a_in = _L2_attn_a_setup()

    def _L2_attn_b_setup():
        import jax, jax.numpy as jnp
        import numpy as np
        B, T, D_MODEL = (2, 256, 256)
        N_HEADS, D_HEAD = (16, 128)
        MAX_SEQ_LEN = 256
        LOGIT_SOFTCAP = 50.0
        EPS = 1e-06

        def precompute_rope(dim, max_seq_len, theta=10000.0):
            freqs = 1.0 / theta ** (np.arange(0, dim, 2, dtype=np.float32) / dim)
            t = np.arange(max_seq_len, dtype=np.float32)
            angles = np.outer(t, freqs)
            return (jnp.asarray(np.cos(angles)), jnp.asarray(np.sin(angles)))

        def rmsnorm(x, w):
            return x * jax.lax.rsqrt(jnp.mean(x * x, axis=-1, keepdims=True) + EPS) * w

        def apply_rope(x, cos, sin):
            n = x.shape[1]
            x1, x2 = (x[..., ::2], x[..., 1::2])
            c = cos[:n][None, :, None, :]
            s = sin[:n][None, :, None, :]
            out = jnp.stack([x1 * c - x2 * s, x1 * s + x2 * c], axis=-1)
            return out.reshape(x.shape)
        key = jax.random.key(seed)
        ks = jax.random.split(key, 6)
        x = jax.random.normal(ks[0], (B, T, D_MODEL), dtype=jnp.float32)
        wq = 0.02 * jax.random.normal(ks[1], (N_HEADS * D_HEAD, D_MODEL), dtype=jnp.float32)
        wk = 0.02 * jax.random.normal(ks[2], (N_HEADS * D_HEAD, D_MODEL), dtype=jnp.float32)
        wv = 0.02 * jax.random.normal(ks[3], (N_HEADS * D_HEAD, D_MODEL), dtype=jnp.float32)
        wo = 0.02 * jax.random.normal(ks[4], (D_MODEL, N_HEADS * D_HEAD), dtype=jnp.float32)
        q_norm_w = jnp.ones((D_HEAD,), dtype=jnp.float32)
        k_norm_w = jnp.ones((D_HEAD,), dtype=jnp.float32)
        rope_cos, rope_sin = precompute_rope(D_HEAD, MAX_SEQ_LEN)
        return {'x': x, 'wq': wq, 'wk': wk, 'wv': wv, 'wo': wo, 'q_norm_w': q_norm_w, 'k_norm_w': k_norm_w, 'rope_cos': rope_cos, 'rope_sin': rope_sin}
    _L2_attn_b_in = _L2_attn_b_setup()

    def _L2_ffn_setup():
        import jax, jax.numpy as jnp
        import numpy as np
        HIDDEN = 256
        INTER = 704
        B, S = (2, 256)

        def _ternary(key, shape):
            return jax.random.randint(key, shape, -1, 2).astype(jnp.float32)
        key = jax.random.key(seed)
        ks = jax.random.split(key, 7)
        x = jax.random.normal(ks[0], (B, S, HIDDEN), dtype=jnp.float32)
        gate_w = _ternary(ks[1], (INTER, HIDDEN))
        up_w = _ternary(ks[2], (INTER, HIDDEN))
        down_w = _ternary(ks[3], (HIDDEN, INTER))
        gate_s = jax.random.uniform(ks[4], (INTER,), minval=0.01, maxval=0.1, dtype=jnp.float32)
        up_s = jax.random.uniform(ks[5], (INTER,), minval=0.01, maxval=0.1, dtype=jnp.float32)
        down_s = jax.random.uniform(ks[6], (HIDDEN,), minval=0.01, maxval=0.1, dtype=jnp.float32)
        return {'x': x, 'gate_w': gate_w, 'up_w': up_w, 'down_w': down_w, 'gate_s': gate_s, 'up_s': up_s, 'down_s': down_s}
    _L2_ffn_in = _L2_ffn_setup()

    def _L3_attn_a_setup():
        import jax, jax.numpy as jnp
        import numpy as np
        D_MODEL = 256
        N_HEADS = 16
        HEAD_DIM = D_MODEL // N_HEADS
        B, T = (2, 256)
        key = jax.random.key(seed)
        ks = jax.random.split(key, 9)
        s = 0.02
        x = jax.random.normal(ks[0], (B, T, D_MODEL), dtype=jnp.float32)
        Wq = jax.random.normal(ks[1], (N_HEADS, D_MODEL, HEAD_DIM), dtype=jnp.float32) * s
        bq = jax.random.normal(ks[2], (N_HEADS, HEAD_DIM), dtype=jnp.float32) * s
        Wk = jax.random.normal(ks[3], (N_HEADS, D_MODEL, HEAD_DIM), dtype=jnp.float32) * s
        bk = jax.random.normal(ks[4], (N_HEADS, HEAD_DIM), dtype=jnp.float32) * s
        Wv = jax.random.normal(ks[5], (N_HEADS, D_MODEL, HEAD_DIM), dtype=jnp.float32) * s
        bv = jax.random.normal(ks[6], (N_HEADS, HEAD_DIM), dtype=jnp.float32) * s
        Wo = jax.random.normal(ks[7], (D_MODEL, D_MODEL), dtype=jnp.float32) * s
        bo = jax.random.normal(ks[8], (D_MODEL,), dtype=jnp.float32) * s
        return {'x': x, 'Wq': Wq, 'bq': bq, 'Wk': Wk, 'bk': bk, 'Wv': Wv, 'bv': bv, 'Wo': Wo, 'bo': bo}
    _L3_attn_a_in = _L3_attn_a_setup()

    def _L3_attn_b_setup():
        import jax, jax.numpy as jnp
        import numpy as np
        B_, L_, D_IN, N_, DT_RANK = (2, 256, 256, 16, 128)
        key = jax.random.key(seed)
        k0, k1, k2, k3 = jax.random.split(key, 4)
        x = jax.random.normal(k0, (B_, L_, D_IN), dtype=jnp.float32)
        W_xproj = jax.random.normal(k1, (DT_RANK + 2 * N_, D_IN), dtype=jnp.float32) * D_IN ** (-0.5)
        W_dt = jax.random.normal(k2, (D_IN, DT_RANK), dtype=jnp.float32) * DT_RANK ** (-0.5)
        b_dt = jax.random.normal(k3, (D_IN,), dtype=jnp.float32) * 0.01
        A = -jnp.broadcast_to(jnp.arange(1, N_ + 1, dtype=jnp.float32), (D_IN, N_)).copy()
        D = jnp.ones((D_IN,), dtype=jnp.float32)
        return {'x': x, 'W_xproj': W_xproj, 'W_dt': W_dt, 'b_dt': b_dt, 'A': A, 'D': D}
    _L3_attn_b_in = _L3_attn_b_setup()

    def _L3_ffn_setup():
        import jax, jax.numpy as jnp
        import numpy as np
        B, S, D, E, R, TOP_K = (4, 512, 256, 6, 16, 2)
        key = jax.random.key(seed)
        ks = jax.random.split(key, 9)
        scale = 0.02
        return {'x': jax.random.normal(ks[0], (B, S, D), dtype=jnp.float32), 'W_base': jax.random.normal(ks[1], (D, D), dtype=jnp.float32) * scale, 'b_base': jax.random.normal(ks[2], (D,), dtype=jnp.float32) * scale, 'A_s': jax.random.normal(ks[3], (D, R), dtype=jnp.float32) * scale, 'B_s': jax.random.normal(ks[4], (R, D), dtype=jnp.float32) * scale, 'A_r': jax.random.normal(ks[5], (E, D, R), dtype=jnp.float32) * scale, 'B_r': jax.random.normal(ks[6], (E, R, D), dtype=jnp.float32) * scale, 'W_router': jax.random.normal(ks[7], (D, E), dtype=jnp.float32) * scale, 'b_router': jax.random.normal(ks[8], (E,), dtype=jnp.float32) * scale}
    _L3_ffn_in = _L3_ffn_setup()
    _d = {'L0_attn_a_x': _L0_attn_a_in['x'], 'L0_attn_a_Wq': _L0_attn_a_in['Wq'], 'L0_attn_a_Wk': _L0_attn_a_in['Wk'], 'L0_attn_a_Wv': _L0_attn_a_in['Wv'], 'L0_attn_a_Wo': _L0_attn_a_in['Wo'], 'L0_attn_b_norm_scale': _L0_attn_b_in['norm_scale'], 'L0_attn_b_split_scale': _L0_attn_b_in['split_scale'], 'L0_attn_b_Wq': _L0_attn_b_in['Wq'], 'L0_attn_b_Wk': _L0_attn_b_in['Wk'], 'L0_attn_b_Wv': _L0_attn_b_in['Wv'], 'L0_attn_b_Wo': _L0_attn_b_in['Wo'], 'L0_ffn_ln1_w': _L0_ffn_in['ln1_w'], 'L0_ffn_ln2_w': _L0_ffn_in['ln2_w'], 'L0_ffn_Wq': _L0_ffn_in['Wq'], 'L0_ffn_Wk': _L0_ffn_in['Wk'], 'L0_ffn_Wv': _L0_ffn_in['Wv'], 'L0_ffn_Wo': _L0_ffn_in['Wo'], 'L0_ffn_A': _L0_ffn_in['A'], 'L0_ffn_B': _L0_ffn_in['B'], 'L0_ffn_W_in_base': _L0_ffn_in['W_in_base'], 'L0_ffn_W_up_base': _L0_ffn_in['W_up_base'], 'L0_ffn_W_down': _L0_ffn_in['W_down'], 'L1_attn_a_Wq': _L1_attn_a_in['Wq'], 'L1_attn_a_Wk': _L1_attn_a_in['Wk'], 'L1_attn_a_Wog': _L1_attn_a_in['Wog'], 'L1_attn_a_Wig': _L1_attn_a_in['Wig'], 'L1_attn_a_Wo': _L1_attn_a_in['Wo'], 'L1_attn_a_g_norm_w': _L1_attn_a_in['g_norm_w'], 'L1_attn_b_W': _L1_attn_b_in['W'], 'L1_attn_b_b': _L1_attn_b_in['b'], 'L1_ffn_gate_weight': _L1_ffn_in['gate_weight'], 'L1_ffn_gate_up_proj': _L1_ffn_in['gate_up_proj'], 'L1_ffn_down_proj': _L1_ffn_in['down_proj'], 'L2_attn_a_W_Q': _L2_attn_a_in['W_Q'], 'L2_attn_a_W_K': _L2_attn_a_in['W_K'], 'L2_attn_a_W_V': _L2_attn_a_in['W_V'], 'L2_attn_a_W_O': _L2_attn_a_in['W_O'], 'L2_attn_b_wq': _L2_attn_b_in['wq'], 'L2_attn_b_wk': _L2_attn_b_in['wk'], 'L2_attn_b_wv': _L2_attn_b_in['wv'], 'L2_attn_b_wo': _L2_attn_b_in['wo'], 'L2_attn_b_q_norm_w': _L2_attn_b_in['q_norm_w'], 'L2_attn_b_k_norm_w': _L2_attn_b_in['k_norm_w'], 'L2_attn_b_rope_cos': _L2_attn_b_in['rope_cos'], 'L2_attn_b_rope_sin': _L2_attn_b_in['rope_sin'], 'L2_ffn_gate_w': _L2_ffn_in['gate_w'], 'L2_ffn_up_w': _L2_ffn_in['up_w'], 'L2_ffn_down_w': _L2_ffn_in['down_w'], 'L2_ffn_gate_s': _L2_ffn_in['gate_s'], 'L2_ffn_up_s': _L2_ffn_in['up_s'], 'L2_ffn_down_s': _L2_ffn_in['down_s'], 'L3_attn_a_Wq': _L3_attn_a_in['Wq'], 'L3_attn_a_bq': _L3_attn_a_in['bq'], 'L3_attn_a_Wk': _L3_attn_a_in['Wk'], 'L3_attn_a_bk': _L3_attn_a_in['bk'], 'L3_attn_a_Wv': _L3_attn_a_in['Wv'], 'L3_attn_a_bv': _L3_attn_a_in['bv'], 'L3_attn_a_Wo': _L3_attn_a_in['Wo'], 'L3_attn_a_bo': _L3_attn_a_in['bo'], 'L3_attn_b_W_xproj': _L3_attn_b_in['W_xproj'], 'L3_attn_b_W_dt': _L3_attn_b_in['W_dt'], 'L3_attn_b_b_dt': _L3_attn_b_in['b_dt'], 'L3_attn_b_A': _L3_attn_b_in['A'], 'L3_attn_b_D': _L3_attn_b_in['D'], 'L3_ffn_W_base': _L3_ffn_in['W_base'], 'L3_ffn_b_base': _L3_ffn_in['b_base'], 'L3_ffn_A_s': _L3_ffn_in['A_s'], 'L3_ffn_B_s': _L3_ffn_in['B_s'], 'L3_ffn_A_r': _L3_ffn_in['A_r'], 'L3_ffn_B_r': _L3_ffn_in['B_r'], 'L3_ffn_W_router': _L3_ffn_in['W_router'], 'L3_ffn_b_router': _L3_ffn_in['b_router']}
    _x0 = _d['L0_attn_a_x']
    _d['L0_attn_a_x'] = jax.random.normal(jax.random.fold_in(jax.random.key(seed), 1), (1, 1024, 256), dtype=_x0.dtype)
    del _x0
    return _d

def reference(L0_attn_a_x, L0_attn_a_Wq, L0_attn_a_Wk, L0_attn_a_Wv, L0_attn_a_Wo, L0_attn_b_norm_scale, L0_attn_b_split_scale, L0_attn_b_Wq, L0_attn_b_Wk, L0_attn_b_Wv, L0_attn_b_Wo, L0_ffn_ln1_w, L0_ffn_ln2_w, L0_ffn_Wq, L0_ffn_Wk, L0_ffn_Wv, L0_ffn_Wo, L0_ffn_A, L0_ffn_B, L0_ffn_W_in_base, L0_ffn_W_up_base, L0_ffn_W_down, L1_attn_a_Wq, L1_attn_a_Wk, L1_attn_a_Wog, L1_attn_a_Wig, L1_attn_a_Wo, L1_attn_a_g_norm_w, L1_attn_b_W, L1_attn_b_b, L1_ffn_gate_weight, L1_ffn_gate_up_proj, L1_ffn_down_proj, L2_attn_a_W_Q, L2_attn_a_W_K, L2_attn_a_W_V, L2_attn_a_W_O, L2_attn_b_wq, L2_attn_b_wk, L2_attn_b_wv, L2_attn_b_wo, L2_attn_b_q_norm_w, L2_attn_b_k_norm_w, L2_attn_b_rope_cos, L2_attn_b_rope_sin, L2_ffn_gate_w, L2_ffn_up_w, L2_ffn_down_w, L2_ffn_gate_s, L2_ffn_up_s, L2_ffn_down_s, L3_attn_a_Wq, L3_attn_a_bq, L3_attn_a_Wk, L3_attn_a_bk, L3_attn_a_Wv, L3_attn_a_bv, L3_attn_a_Wo, L3_attn_a_bo, L3_attn_b_W_xproj, L3_attn_b_W_dt, L3_attn_b_b_dt, L3_attn_b_A, L3_attn_b_D, L3_ffn_W_base, L3_ffn_b_base, L3_ffn_A_s, L3_ffn_B_s, L3_ffn_A_r, L3_ffn_B_r, L3_ffn_W_router, L3_ffn_b_router):

    def _L0_attn_a_ref(x, Wq, Wk, Wv, Wo):
        import jax, jax.numpy as jnp
        import numpy as np
        HIDDEN = 256
        HEADS = 16
        HEAD_DIM = HIDDEN // HEADS
        b, s, _ = x.shape

        def split_heads(t):
            return t.reshape(b, s, HEADS, HEAD_DIM).transpose(0, 2, 1, 3)
        Q = split_heads(x @ Wq.T)
        K = split_heads(x @ Wk.T)
        V = split_heads(x @ Wv.T)
        scores = jnp.einsum('bhqd,bhkd->bhqk', Q, K) / jnp.sqrt(jnp.float32(HEAD_DIM))
        causal = jnp.tril(jnp.ones((s, s), dtype=bool))
        scores = jnp.where(causal, scores, jnp.float32(-jnp.inf))
        attn = jax.nn.softmax(scores, axis=-1)
        out = jnp.einsum('bhqk,bhkd->bhqd', attn, V)
        out = out.transpose(0, 2, 1, 3).reshape(b, s, HIDDEN)
        return out @ Wo.T

    def _L0_attn_b_ref(x, norm_scale, split_scale, Wq, Wk, Wv, Wo):
        import jax, jax.numpy as jnp
        import numpy as np
        DIMS = 256
        HEAD_DIM = 64
        NUM_HEADS = DIMS // HEAD_DIM
        GQA_HEADS = 2
        EPS = 1e-08
        b, s, d = x.shape
        H, G, dh = (NUM_HEADS, GQA_HEADS, HEAD_DIM)
        hpg = H // G
        nrm = jnp.linalg.norm(x, axis=-1, keepdims=True) * d ** (-0.5)
        h = norm_scale * x / (nrm + EPS) * split_scale
        q = (h @ Wq.T).reshape(b, s, H, dh)
        k = (h @ Wk.T).reshape(b, s, G, dh)
        v = (h @ Wv.T).reshape(b, s, G, dh)
        q = q.transpose(0, 2, 1, 3).reshape(b, G, hpg, s, dh)
        k = k.transpose(0, 2, 1, 3)
        v = v.transpose(0, 2, 1, 3)
        scores = jnp.einsum('bghsd,bgtd->bghst', q, k) / np.float32(np.sqrt(dh))
        attn = jax.nn.softmax(scores, axis=-1)
        out = jnp.einsum('bghst,bgtd->bghsd', attn, v)
        out = out.reshape(b, H, s, dh).transpose(0, 2, 1, 3).reshape(b, s, H * dh)
        return x + out @ Wo.T

    def _L0_ffn_ref(hidden_states, ln1_w, ln2_w, Wq, Wk, Wv, Wo, A, B, W_in_base, W_up_base, W_down):
        import jax, jax.numpy as jnp
        import numpy as np
        B_, S, D = (2, 256, 256)
        F_ = 1024
        R = 16
        H = 16
        HD = D // H
        MOD_SCALE = 0.1
        EPS = 1e-06

        def _rmsnorm(x, w):
            v = jnp.mean(x * x, axis=-1, keepdims=True)
            return x * jax.lax.rsqrt(v + EPS) * w

        def _attention(x, Wq, Wk, Wv, Wo):
            b, s, d = x.shape
            q = (x @ Wq.T).reshape(b, s, H, HD)
            k = (x @ Wk.T).reshape(b, s, H, HD)
            v = (x @ Wv.T).reshape(b, s, H, HD)
            scores = jnp.einsum('bqhd,bkhd->bhqk', q, k) / np.sqrt(HD).astype(np.float32)
            causal = jnp.tril(jnp.ones((s, s), bool))
            scores = jnp.where(causal, scores, jnp.finfo(scores.dtype).min)
            probs = jax.nn.softmax(scores, axis=-1)
            out = jnp.einsum('bhqk,bkhd->bqhd', probs, v).reshape(b, s, d)
            return out @ Wo.T
        residual = hidden_states
        x = _rmsnorm(hidden_states, ln1_w)
        attn = _attention(x, Wq, Wk, Wv, Wo)
        mod = MOD_SCALE * jnp.tanh(attn @ A)
        h = _rmsnorm(residual, ln2_w)
        gate_pre = h @ W_in_base.T + mod * (h @ A) @ B
        gate = jax.nn.silu(gate_pre)
        up = h @ W_up_base.T
        mlp_out = gate * up @ W_down.T
        return residual + mlp_out

    def _L1_attn_a_ref(hidden_states, Wq, Wk, Wog, Wig, Wo, g_norm_w):
        import jax, jax.numpy as jnp
        import numpy as np
        from jax import lax
        B, L, H = (2, 512, 256)
        NH = 16
        DK = H // NH
        C = 64
        EPS = 1e-05
        N_LAYER = 24

        def _gla_chunk(q, k, v, gf):
            b, Ls, dk = q.shape
            dv = v.shape[-1]
            n = Ls // C
            qc = q.reshape(b, n, C, dk).transpose(1, 0, 2, 3)
            kc = k.reshape(b, n, C, dk).transpose(1, 0, 2, 3)
            vc = v.reshape(b, n, C, dv).transpose(1, 0, 2, 3)
            gc = gf.reshape(b, n, C, dk).transpose(1, 0, 2, 3)
            Bc = jnp.cumsum(gc, axis=2)
            tril = jnp.tril(jnp.ones((C, C), bool))

            def step(S, inp):
                qh, kh, vh, Bh = inp
                Blast = Bh[:, -1, :]
                D = Bh[:, :, None, :] - Bh[:, None, :, :]
                A = jnp.einsum('bid,bjd,bijd->bij', qh, kh, jnp.exp(D))
                A = jnp.where(tril, A, 0.0)
                o_intra = jnp.einsum('bij,bjv->biv', A, vh)
                o_inter = jnp.einsum('bid,bdv->biv', qh * jnp.exp(Bh), S)
                kd = kh * jnp.exp(Blast[:, None, :] - Bh)
                S_new = S * jnp.exp(Blast)[..., None] + jnp.einsum('bjd,bjv->bdv', kd, vh)
                return (S_new, o_intra + o_inter)
            S0 = jnp.zeros((b, dk, dv), q.dtype)
            _, o = lax.scan(step, S0, (qc, kc, vc, Bc))
            return o.transpose(1, 0, 2, 3).reshape(b, Ls, dv)
        x = hidden_states
        q = jax.nn.softmax(x @ Wq.T, axis=-1)
        k = jax.nn.sigmoid(x @ Wk.T)
        v = x
        gf = jax.nn.log_sigmoid(-k)
        o = _gla_chunk(q, k, v, gf)
        go = o @ Wog.T + x @ Wig.T
        on = o * lax.rsqrt(jnp.mean(o * o, axis=-1, keepdims=True) + EPS) * g_norm_w
        o = on * (go * jax.nn.sigmoid(go))
        return o @ Wo.T

    def _L1_attn_b_ref(x, W, b):
        import jax, jax.numpy as jnp
        import numpy as np
        B, K, D = (4, 512, 256)
        lam = jax.nn.sigmoid(jnp.einsum('bkd,ed->bke', x, W) + b)

        def step(s, inp):
            lam_t, u_t = inp
            s = lam_t * s + (1.0 - lam_t) * u_t
            return (s, s)
        s0 = jnp.zeros((x.shape[0], x.shape[2]), dtype=x.dtype)
        _, ys = jax.lax.scan(step, s0, (jnp.moveaxis(lam, 1, 0), jnp.moveaxis(x, 1, 0)))
        return jnp.moveaxis(ys, 0, 1)

    def _L1_ffn_ref(hidden_states, gate_weight, gate_up_proj, down_proj):
        import jax, jax.numpy as jnp
        import numpy as np
        NUM_EXPERTS = 32
        TOP_K = 8
        THRESHOLD = 0.8
        HIDDEN = 256
        INTER = 96
        B, S, H = hidden_states.shape
        x = hidden_states.reshape(-1, H)
        logits = x @ gate_weight.T
        probs = jax.nn.softmax(logits.astype(jnp.float32), axis=-1).astype(logits.dtype)
        top_vals, top_idx = jax.lax.top_k(probs, TOP_K)
        renorm = top_vals / jnp.clip(jnp.sum(top_vals, axis=-1, keepdims=True), 1e-12)
        cum = jnp.cumsum(renorm, axis=-1)
        num_keep = jnp.minimum(jnp.sum((cum < THRESHOLD).astype(jnp.int32), axis=-1) + 1, TOP_K)
        active = jnp.arange(TOP_K)[None, :] < num_keep[:, None]
        rw = top_vals * active.astype(top_vals.dtype)
        rw = rw / jnp.clip(jnp.sum(rw, axis=-1, keepdims=True), 1e-12)
        combine = jnp.sum(jax.nn.one_hot(top_idx, NUM_EXPERTS, dtype=rw.dtype) * rw[..., None], axis=1)

        def body(acc, params):
            w_gu, w_d, ce = params
            gu = x @ w_gu.T
            g, u = jnp.split(gu, 2, axis=-1)
            h = jax.nn.silu(g) * u
            return (acc + h @ w_d.T * ce[:, None], None)
        out, _ = jax.lax.scan(body, jnp.zeros_like(x), (gate_up_proj, down_proj, combine.T))
        return out.reshape(B, S, H)

    def _L2_attn_a_ref(x, W_Q, W_K, W_V, W_O):
        import jax, jax.numpy as jnp
        import numpy as np
        import math
        D_MODEL = 256
        N_HEADS = 16
        D_HEAD = 128
        BATCH = 2
        SEQ = 256
        d_head = W_Q.shape[1]
        seq_len = x.shape[1]
        scale = 1.0 / math.sqrt(d_head)
        q = jnp.einsum('bsd,hed->bhse', x, W_Q)
        k = jnp.einsum('bsd,hed->bhse', x, W_K)
        v = jnp.einsum('bsd,hed->bhse', x, W_V)
        scores = jnp.einsum('bhse,bhme->bhsm', q, k) * scale
        causal = jnp.triu(jnp.ones((seq_len, seq_len), dtype=bool), k=1)
        scores = jnp.where(causal, jnp.float32(-1000000000.0), scores)
        pattern = jax.nn.softmax(scores, axis=-1)
        z = jnp.einsum('bhsm,bhme->bhse', pattern, v)
        out = jnp.einsum('bhse,hde->bsd', z, W_O)
        return out

    def _L2_attn_b_ref(x, wq, wk, wv, wo, q_norm_w, k_norm_w, rope_cos, rope_sin):
        import jax, jax.numpy as jnp
        import numpy as np
        B, T, D_MODEL = (2, 256, 256)
        N_HEADS, D_HEAD = (16, 128)
        MAX_SEQ_LEN = 256
        LOGIT_SOFTCAP = 50.0
        EPS = 1e-06

        def precompute_rope(dim, max_seq_len, theta=10000.0):
            freqs = 1.0 / theta ** (np.arange(0, dim, 2, dtype=np.float32) / dim)
            t = np.arange(max_seq_len, dtype=np.float32)
            angles = np.outer(t, freqs)
            return (jnp.asarray(np.cos(angles)), jnp.asarray(np.sin(angles)))

        def rmsnorm(x, w):
            return x * jax.lax.rsqrt(jnp.mean(x * x, axis=-1, keepdims=True) + EPS) * w

        def apply_rope(x, cos, sin):
            n = x.shape[1]
            x1, x2 = (x[..., ::2], x[..., 1::2])
            c = cos[:n][None, :, None, :]
            s = sin[:n][None, :, None, :]
            out = jnp.stack([x1 * c - x2 * s, x1 * s + x2 * c], axis=-1)
            return out.reshape(x.shape)
        Bx, Tx, _ = x.shape
        scale = D_HEAD ** (-0.5)
        q = (x @ wq.T).reshape(Bx, Tx, N_HEADS, D_HEAD).transpose(0, 2, 1, 3)
        k = (x @ wk.T).reshape(Bx, Tx, N_HEADS, D_HEAD).transpose(0, 2, 1, 3)
        v = (x @ wv.T).reshape(Bx, Tx, N_HEADS, D_HEAD).transpose(0, 2, 1, 3)
        q = rmsnorm(q, q_norm_w)
        k = rmsnorm(k, k_norm_w)
        q = apply_rope(q, rope_cos, rope_sin)
        k = apply_rope(k, rope_cos, rope_sin)
        scores = jnp.einsum('bhtd,bhsd->bhts', q, k) * scale
        scores = LOGIT_SOFTCAP * jnp.tanh(scores / LOGIT_SOFTCAP)
        mask = jnp.triu(jnp.ones((Tx, Tx), dtype=bool), k=1)
        scores = jnp.where(mask[None, None], -jnp.inf, scores)
        attn = jax.nn.softmax(scores, axis=-1)
        out = jnp.einsum('bhts,bhsd->bhtd', attn, v)
        out = out.transpose(0, 2, 1, 3).reshape(Bx, Tx, N_HEADS * D_HEAD)
        return out @ wo.T

    def _L2_ffn_ref(x, gate_w, up_w, down_w, gate_s, up_s, down_s):
        import jax, jax.numpy as jnp
        import numpy as np
        HIDDEN = 256
        INTER = 704
        B, S = (2, 256)

        def _ternary(key, shape):
            return jax.random.randint(key, shape, -1, 2).astype(jnp.float32)
        b, s, h = x.shape
        xf = x.reshape(b * s, h)
        g = jnp.einsum('th,ih->ti', xf, gate_w) * gate_s
        u = jnp.einsum('th,ih->ti', xf, up_w) * up_s
        hdn = jax.nn.silu(g) * u
        out = jnp.einsum('ti,hi->th', hdn, down_w) * down_s
        return out.reshape(b, s, -1)

    def _L3_attn_a_ref(x, Wq, bq, Wk, bk, Wv, bv, Wo, bo):
        import jax, jax.numpy as jnp
        import numpy as np
        D_MODEL = 256
        N_HEADS = 16
        HEAD_DIM = D_MODEL // N_HEADS
        B, T = (2, 256)
        Bn, Tn, C = x.shape
        H, _, D = Wq.shape
        scale = D ** (-0.5)
        q = jnp.einsum('btc,hcd->bhtd', x, Wq) + bq[None, :, None, :]
        k = jnp.einsum('btc,hcd->bhtd', x, Wk) + bk[None, :, None, :]
        v = jnp.einsum('btc,hcd->bhtd', x, Wv) + bv[None, :, None, :]
        scores = jnp.einsum('bhtd,bhsd->bhts', q, k) * scale
        neg = jnp.finfo(scores.dtype).min
        causal = jnp.triu(jnp.full((Tn, Tn), neg, dtype=scores.dtype), k=1)
        probs = jax.nn.softmax(scores + causal, axis=-1)
        y = jnp.einsum('bhts,bhsd->bhtd', probs, v)
        y = y.transpose(0, 2, 1, 3).reshape(Bn, Tn, H * D)
        return y @ Wo + bo

    def _L3_attn_b_ref(x, W_xproj, W_dt, b_dt, A, D):
        import jax, jax.numpy as jnp
        import numpy as np
        B_, L_, D_IN, N_, DT_RANK = (2, 256, 256, 16, 128)
        n = A.shape[1]
        dt_rank = W_dt.shape[1]
        bcd = jnp.einsum('bld,ed->ble', x, W_xproj)
        dt, Bm, Cm = jnp.split(bcd, [dt_rank, dt_rank + n], axis=-1)
        delta = jax.nn.softplus(jnp.einsum('blr,dr->bld', dt, W_dt) + b_dt)
        Ad = jnp.exp(delta[..., None] * A)
        Bx = delta[..., None] * Bm[:, :, None, :] * x[..., None]
        b, l, d_in = x.shape

        def step(h, inp):
            Ad_t, Bx_t, C_t = inp
            h = Ad_t * h + Bx_t
            y = jnp.einsum('bdn,bn->bd', h, C_t)
            return (h, y)
        h0 = jnp.zeros((b, d_in, n), dtype=x.dtype)
        _, ys = jax.lax.scan(step, h0, (jnp.moveaxis(Ad, 1, 0), jnp.moveaxis(Bx, 1, 0), jnp.moveaxis(Cm, 1, 0)))
        y = jnp.moveaxis(ys, 0, 1) + x * D
        return y

    def _L3_ffn_ref(x, W_base, b_base, A_s, B_s, A_r, B_r, W_router, b_router):
        import jax, jax.numpy as jnp
        import numpy as np
        B, S, D, E, R, TOP_K = (4, 512, 256, 6, 16, 2)
        base_out = jax.lax.stop_gradient(jnp.einsum('bsd,df->bsf', x, W_base) + b_base)
        shared_out = jnp.einsum('bsr,rf->bsf', jnp.einsum('bsd,dr->bsr', x, A_s), B_s)
        gates = jax.nn.softmax(jnp.einsum('bsd,de->bse', x, W_router) + b_router, axis=-1)
        topk_w, topk_i = jax.lax.top_k(gates, TOP_K)
        w_per_e = jnp.sum(topk_w[..., None] * jax.nn.one_hot(topk_i, E, dtype=x.dtype), axis=2)
        h = jnp.einsum('bsd,edr->bser', x, A_r)
        hw = h * w_per_e[..., None]
        routed_out = jnp.einsum('bser,erf->bsf', hw, B_r)
        return base_out + shared_out + routed_out
    x = L0_attn_a_x
    x = x + _L0_attn_a_ref(_layernorm(x, axis=-1), L0_attn_a_Wq, L0_attn_a_Wk, L0_attn_a_Wv, L0_attn_a_Wo)
    x = x + _L0_ffn_ref(_layernorm(x, axis=-1), L0_ffn_ln1_w, L0_ffn_ln2_w, L0_ffn_Wq, L0_ffn_Wk, L0_ffn_Wv, L0_ffn_Wo, L0_ffn_A, L0_ffn_B, L0_ffn_W_in_base, L0_ffn_W_up_base, L0_ffn_W_down)
    x = x + _L0_attn_b_ref(_layernorm(x, axis=-1), L0_attn_b_norm_scale, L0_attn_b_split_scale, L0_attn_b_Wq, L0_attn_b_Wk, L0_attn_b_Wv, L0_attn_b_Wo)
    x = x + _L0_ffn_ref(_layernorm(x, axis=-1), L0_ffn_ln1_w, L0_ffn_ln2_w, L0_ffn_Wq, L0_ffn_Wk, L0_ffn_Wv, L0_ffn_Wo, L0_ffn_A, L0_ffn_B, L0_ffn_W_in_base, L0_ffn_W_up_base, L0_ffn_W_down)
    x = x + _L1_attn_a_ref(_layernorm(x, axis=-1), L1_attn_a_Wq, L1_attn_a_Wk, L1_attn_a_Wog, L1_attn_a_Wig, L1_attn_a_Wo, L1_attn_a_g_norm_w)
    x = x + _L1_ffn_ref(_layernorm(x, axis=-1), L1_ffn_gate_weight, L1_ffn_gate_up_proj, L1_ffn_down_proj)
    x = x + _L1_attn_b_ref(_layernorm(x, axis=-1), L1_attn_b_W, L1_attn_b_b)
    x = x + _L1_ffn_ref(_layernorm(x, axis=-1), L1_ffn_gate_weight, L1_ffn_gate_up_proj, L1_ffn_down_proj)
    x = x + _L2_attn_a_ref(_layernorm(x, axis=-1), L2_attn_a_W_Q, L2_attn_a_W_K, L2_attn_a_W_V, L2_attn_a_W_O)
    x = x + _L2_ffn_ref(_layernorm(x, axis=-1), L2_ffn_gate_w, L2_ffn_up_w, L2_ffn_down_w, L2_ffn_gate_s, L2_ffn_up_s, L2_ffn_down_s)
    x = x + _L2_attn_b_ref(_layernorm(x, axis=-1), L2_attn_b_wq, L2_attn_b_wk, L2_attn_b_wv, L2_attn_b_wo, L2_attn_b_q_norm_w, L2_attn_b_k_norm_w, L2_attn_b_rope_cos, L2_attn_b_rope_sin)
    x = x + _L2_ffn_ref(_layernorm(x, axis=-1), L2_ffn_gate_w, L2_ffn_up_w, L2_ffn_down_w, L2_ffn_gate_s, L2_ffn_up_s, L2_ffn_down_s)
    x = x + _L3_attn_a_ref(_layernorm(x, axis=-1), L3_attn_a_Wq, L3_attn_a_bq, L3_attn_a_Wk, L3_attn_a_bk, L3_attn_a_Wv, L3_attn_a_bv, L3_attn_a_Wo, L3_attn_a_bo)
    x = x + _L3_ffn_ref(_layernorm(x, axis=-1), L3_ffn_W_base, L3_ffn_b_base, L3_ffn_A_s, L3_ffn_B_s, L3_ffn_A_r, L3_ffn_B_r, L3_ffn_W_router, L3_ffn_b_router)
    x = x + _L3_attn_b_ref(_layernorm(x, axis=-1), L3_attn_b_W_xproj, L3_attn_b_W_dt, L3_attn_b_b_dt, L3_attn_b_A, L3_attn_b_D)
    x = x + _L3_ffn_ref(_layernorm(x, axis=-1), L3_ffn_W_base, L3_ffn_b_base, L3_ffn_A_s, L3_ffn_B_s, L3_ffn_A_r, L3_ffn_B_r, L3_ffn_W_router, L3_ffn_b_router)
    return x

_drawn_inputs = setup_inputs


def setup_inputs(seed=0):
    import zlib

    import numpy as np

    out = dict(_drawn_inputs(seed))
    spreads = {'L0_attn_b_norm_scale': (1.0, 0.6),
     'L0_attn_b_split_scale': (0.10000000149011612, 0.6),
     'L0_ffn_ln1_w': (1.0, 0.6),
     'L0_ffn_ln2_w': (1.0, 0.6),
     'L1_attn_a_g_norm_w': (1.0, 0.6),
     'L2_attn_b_q_norm_w': (1.0, 0.6),
     'L2_attn_b_k_norm_w': (1.0, 0.6),
     'L3_attn_b_D': (1.0, 0.563)}
    factors = {'L0_attn_b_Wq': 8.0,
     'L0_attn_b_Wk': 8.0,
     'L0_attn_b_Wv': 8.0,
     'L0_attn_b_Wo': 8.0,
     'L0_ffn_Wq': 8.0,
     'L0_ffn_Wk': 8.0,
     'L0_ffn_Wv': 8.0,
     'L0_ffn_Wo': 8.0,
     'L0_ffn_A': 8.0,
     'L0_ffn_B': 8.0,
     'L1_attn_a_Wq': 8.0,
     'L1_attn_a_Wk': 8.0,
     'L1_attn_a_Wog': 8.0,
     'L1_attn_a_Wig': 8.0,
     'L1_attn_a_Wo': 8.0,
     'L1_attn_b_b': 8.0,
     'L1_ffn_gate_weight': 8.0,
     'L1_ffn_gate_up_proj': 8.0,
     'L1_ffn_down_proj': 8.0,
     'L2_attn_a_W_Q': 8.0,
     'L2_attn_a_W_K': 8.0,
     'L2_attn_a_W_V': 4.085,
     'L2_attn_a_W_O': 3.817,
     'L2_attn_b_wq': 5.211,
     'L2_attn_b_wk': 5.153,
     'L2_attn_b_wv': 3.365,
     'L2_attn_b_wo': 3.289,
     'L2_attn_b_rope_cos': 8.0,
     'L2_attn_b_rope_sin': 8.0,
     'L3_attn_a_Wq': 8.0,
     'L3_attn_a_bq': 8.0,
     'L3_attn_a_Wk': 8.0,
     'L3_attn_a_bk': 64.0,
     'L3_attn_a_Wv': 8.0,
     'L3_attn_a_bv': 8.0,
     'L3_attn_a_Wo': 8.0,
     'L3_attn_a_bo': 27.525,
     'L3_attn_b_b_dt': 34.264,
     'L3_ffn_b_base': 7.087,
     'L3_ffn_A_s': 5.851,
     'L3_ffn_B_s': 5.752,
     'L3_ffn_A_r': 8.0,
     'L3_ffn_B_r': 8.0,
     'L3_ffn_W_router': 8.0,
     'L3_ffn_b_router': 22.368}
    for name, (base, spread) in spreads.items():
        noise = np.random.default_rng([zlib.crc32(name.encode()), seed]).standard_normal(out[name].shape)
        drawn = base * np.exp(spread * noise) if base else spread * noise
        out[name] = jnp.asarray(drawn.astype(out[name].dtype))
    for name, factor in factors.items():
        out[name] = (out[name] * factor).astype(out[name].dtype)
    return out
```

```python
from contextlib import ExitStack

import concourse.bass as bass
import numpy as np
from concourse import mybir

ALU = mybir.AluOpType
ACT = mybir.ActivationFunctionType
AX = mybir.AxisListType.X
F32 = mybir.dt.float32
BF16 = mybir.dt.bfloat16
U32 = mybir.dt.uint32

P = 128
TOK = 1024
D = 256
NT = TOK // P
DC = D // P
HALF = 512
MASKED = -1.0e30


class Core:

    def __init__(self, nc, dram, whole):
        self.nc = nc
        self.dram = dram
        self.old = []
        self.count = 0

        def sb(name, shape, dt=F32):
            return whole.enter_context(nc.sbuf_tensor(name, shape, dt))

        self.x = sb("x", [P, NT, D])
        self.hT = sb("hT", [P, DC, TOK])
        self.ident = sb("ident", [P, P])
        self.ident_bf = sb("ident_bf", [P, P], BF16)
        self.causal = sb("causal", [P, P], BF16)
        self.causal_f = sb("causal_f", [P, P])
        self.ones = sb("ones", [P, P])


class Stage:

    def __init__(self, core, name):
        self.core, self.nc, self.name = core, core.nc, f"{name}{core.count}"
        core.count += 1
        self.stack = ExitStack()
        self.sems = []

    def sem(self, name):
        s = self.nc.alloc_semaphore(f"{self.name}_{name}")
        self.sems.append(s)
        return s

    def sb(self, name, shape, dt=F32):
        return self.stack.enter_context(self.nc.sbuf_tensor(f"{self.name}_{name}", shape, dt))

    def psum(self, name, shape, dt=F32):
        return self.stack.enter_context(self.nc.psum_tensor(f"{self.name}_ps_{name}", shape, dt))

    def clear_old(self, pool):
        numbers = sorted(s.num for s in self.core.old)
        while numbers:
            run = [numbers.pop(0)]
            while numbers and numbers[0] == run[-1] + 1:
                run.append(numbers.pop(0))
            pool.sem_clear(range(run[0], run[-1] + 1))

    def __enter__(self):
        self.block = self.nc.Block(no_gpsimd_drain=True)
        self.opened = self.block.__enter__()
        return self

    def __exit__(self, *error):
        out = self.block.__exit__(*error)
        self.stack.close()
        for s in self.core.old:
            self.nc.release_semaphore(s)
        self.core.old = self.sems
        return out


def linker(engine, sem):
    done = [0]

    def link(instruction):
        done[0] += 1
        instruction.then_inc(sem, 1)
        engine.wait_ge(sem, done[0])
    return link


def load_input(core):
    nc, x = core.nc, core.x
    with Stage(core, "load") as st:
        loaded, zeroed, ones_set = st.sem("loaded"), st.sem("zeroed"), st.sem("ones_set")
        block = st.opened

        @block.sync
        def _(sp):
            for c in range(2):
                half = slice(c * NT // 2, (c + 1) * NT // 2)
                sp.dma_start(x[:, half, :], core.dram["x"].rearrange("(t p) d -> p t d", p=P)[:, half, :]
                             ).then_inc(loaded, 16)
            sp.wait_ge(loaded, 32)

        @block.gpsimd
        def _(pool):
            nc.gpsimd.memset(core.ident[:], 0.0).then_inc(zeroed, 1)
            nc.gpsimd.memset(core.ident_bf[:], 0.0).then_inc(zeroed, 1)
            nc.gpsimd.memset(core.causal[:], 0.0).then_inc(zeroed, 1)
            nc.gpsimd.memset(core.causal_f[:], 0.0).then_inc(zeroed, 1)
            nc.gpsimd.memset(core.ones[:], 1.0).then_inc(ones_set, 1)
            pool.wait_ge(zeroed, 4)
            for t in (core.ident, core.ident_bf):
                nc.gpsimd.affine_select(out=t[:], in_=t[:], compare_op=ALU.not_equal, fill=1.0, base=0,
                                        pattern=[[-1, P]], channel_multiplier=1).then_inc(ones_set, 1)
            for t in (core.causal, core.causal_f):
                nc.gpsimd.affine_select(out=t[:], in_=t[:], compare_op=ALU.is_ge, fill=MASKED, base=0,
                                        pattern=[[-1, P]], channel_multiplier=1).then_inc(ones_set, 1)
            pool.wait_ge(ones_set, 5)


def store_output(core, out):
    with Stage(core, "store") as st:
        stored = st.sem("stored")
        block = st.opened

        @block.sync
        def _(sp):
            for c in range(2):
                half = slice(c * NT // 2, (c + 1) * NT // 2)
                sp.dma_start(out.rearrange("(t p) d -> p t d", p=P)[:, half, :], core.x[:, half, :]
                             ).then_inc(stored, 16)
            sp.wait_ge(stored, 32)


def normalise(core, outs, second=None, keep=False, rows=None):
    nc, x = core.nc, core.x
    with Stage(core, "norm") as st:
        block = st.opened
        stats, mv = st.sb("stats", [P, NT, 6]), st.sb("mv", [P, NT, 2])
        spread, inverse = st.sb("spread", [P, NT]), st.sb("inverse", [P, NT])
        h = rows if rows is not None else st.sb("h", [P, NT, D])
        squares, square_sum = st.sb("squares", [P, 2, D]), st.sb("square_sum", [P, NT])
        turned = [st.psum(f"turned{n}", [P, HALF]) for n in range(4)]
        step, variance, root = st.sem("step"), st.sem("variance"), st.sem("root")
        squared = st.sem("squared")
        tile_done, sums, turned_ready = st.sem("tile_done"), st.sem("sums"), st.sem("turned_ready")
        written_act, written_dve = st.sem("written_act"), st.sem("written_dve")
        columns = [(n, c, w) for n, (_, ws) in enumerate(outs) for c, w in enumerate(ws)]
        column_sb = {(n, c): st.sb(f"w{n}_{c}", [P, DC]) for n, c, _ in columns}
        columns_in = st.sem("columns_in")

        @block.sync
        def _(sp):
            for n, c, w in columns:
                sp.dma_start(column_sb[n, c][:], core.dram[w]).then_inc(columns_in, 16)

        @block.gpsimd
        def _(pool):
            st.clear_old(pool)
            if keep:
                for t in range(NT):
                    pool.wait_ge(tile_done, t + 1)
                    nc.gpsimd.tensor_tensor(x[:, t, :], x[:, t, :], h[:, t, :], ALU.add
                                            ).then_inc(sums, 1)

        @block.vector
        def _(dve):
            link = linker(dve, step)
            for t in range(NT):
                nc.vector.bn_stats(stats[:, t, :], x[:, t, :]).then_inc(variance, 1)
            for t in range(NT):
                dve.wait_ge(variance, t + 1)
                nc.vector.bn_aggr(mv[:, t, :], stats[:, t, :]).then_inc(variance, 1)
            dve.wait_ge(variance, 2 * NT)
            nc.vector.tensor_scalar(spread[:], mv[:, :, 1], 1e-5, None, ALU.add).then_inc(variance, 1)
            dve.wait_ge(root, 1)
            link(nc.vector.reciprocal(inverse[:], spread[:]))
            for t in range(NT):
                nc.vector.tensor_scalar(h[:, t, :], x[:, t, :], mv[:, t, 0:1], inverse[:, t:t + 1],
                                        ALU.subtract, ALU.mult).then_inc(tile_done, 1)
            if second:
                kind, eps = second
                dve.wait_ge(squared, NT)
                nc.vector.tensor_scalar(spread[:], square_sum[:], 1.0 / D, eps if kind == "rms" else 0.0,
                                        ALU.mult, ALU.add).then_inc(variance, 1)
                dve.wait_ge(root, 2)
                if kind == "norm":
                    link(nc.vector.tensor_scalar(spread[:], spread[:], eps, None, ALU.add))
                link(nc.vector.reciprocal(inverse[:], spread[:]))
                if keep:
                    dve.wait_ge(sums, NT)
                for t in range(NT):
                    nc.vector.tensor_scalar(h[:, t, :], h[:, t, :], inverse[:, t:t + 1], None,
                                            ALU.mult).then_inc(tile_done, 1)
            for n, (dst, ws) in enumerate(outs):
                if ws:
                    dve.wait_ge(columns_in, 16 * len(columns))
                for half in range(2):
                    for c in range(DC):
                        if half and len(ws) < 2:
                            continue
                        dve.wait_ge(turned_ready, 2 * half + c + 1)
                        src = turned[2 * half + c][:]
                        to = dst[:, c, half * HALF:(half + 1) * HALF]
                        if not ws:
                            nc.vector.tensor_copy(to, src).then_inc(written_dve, 1)
                        elif len(ws) == 1:
                            nc.vector.tensor_scalar(to, src, column_sb[n, 0][:, c:c + 1], None, ALU.mult
                                                    ).then_inc(written_dve, 1)
                        else:
                            nc.vector.tensor_scalar(to, src, column_sb[n, 0][:, c:c + 1],
                                                    column_sb[n, 1][:, c:c + 1], ALU.mult, ALU.mult
                                                    ).then_inc(written_dve, 1)

        @block.scalar
        def _(act):
            act.wait_ge(variance, 2 * NT + 1)
            nc.scalar.activation(spread[:], spread[:], ACT.Sqrt).then_inc(root, 1)
            if second:
                for t in range(NT):
                    act.wait_ge(tile_done, t + 1)
                    if t >= 2:
                        act.wait_ge(squared, t - 1)
                    nc.scalar.activation(squares[:, t % 2, :], h[:, t, :], ACT.Square,
                                         accum_out=square_sum[:, t:t + 1]).then_inc(squared, 1)
                act.wait_ge(variance, 2 * NT + 2)
                nc.scalar.activation(spread[:], spread[:], ACT.Sqrt).then_inc(root, 1)
            for n, (dst, ws) in enumerate(outs):
                if ws:
                    act.wait_ge(columns_in, 16 * len(columns))
                for half in range(2):
                    for c in range(DC):
                        if half == 0 or len(ws) >= 2:
                            continue
                        act.wait_ge(turned_ready, 2 * half + c + 1)
                        src = turned[2 * half + c][:]
                        to = dst[:, c, half * HALF:(half + 1) * HALF]
                        if ws:
                            nc.scalar.mul(to, src, column_sb[n, 0][:, c:c + 1]).then_inc(written_act, 1)
                        else:
                            nc.scalar.copy(to, src).then_inc(written_act, 1)

        @block.tensor
        def _(pe):
            for half in range(2):
                for c in range(DC):
                    for i in range(4):
                        t = 4 * half + i
                        pe.wait_ge(tile_done, (NT if second else 0) + t + 1)
                        last = nc.tensor.transpose(turned[2 * half + c][:, i * P:(i + 1) * P],
                                                   h[:, t, c * P:(c + 1) * P], core.ident[:])
                    last.then_inc(turned_ready, 1)


def attention(core, name, groups, heads, hd, shared_kv, causal, scale, bias=False, out_bias=None,
              into=None, softcap=None):
    nc, x, hT = core.nc, core.x, core.hT
    vw = hd if shared_kv else heads * hd
    gw = heads * hd
    stride = P // heads
    total = groups * gw
    NCH = total // P
    items = [(j, t) for j in range(heads) for t in range(NT)]
    NI = len(items)
    seconds = [sum(1 for _, t in items[:i] if not causal or t >= 4) for i in range(NI + 1)]
    NS = seconds[NI]
    LOADS = 2 if bias else 1
    FREE = 1

    with Stage(core, name) as st:
        block = st.opened
        w = st.sb("w", [P, DC, 2 * P + vw])
        wo = st.sb("wo", [P, NCH, D])
        qT, kT = st.sb("qT", [P, TOK]), st.sb("kT", [P, TOK])
        v = st.sb("v", [P, NT, vw])
        probs = [st.sb(f"probs{n}", [P, TOK]) for n in range(2)]
        probsT = [st.sb(f"probsT{n}", [P, TOK]) for n in range(2)]
        negmax, rowsum, rowinv = st.sb("negmax", [P, NI]), st.sb("rowsum", [P, NI]), st.sb("rowinv", [P, NI])
        rows = st.sb("rows", [P, NT, total])
        if bias:
            qk_bias = st.sb("qk_bias", [P, 2])
            v_bias = st.sb("v_bias", [P, total])
        if out_bias:
            o_bias = st.sb("o_bias", [P, D])
        if softcap:
            q_rows, k_rows = st.sb("q_rows", [P, NT, hd]), st.sb("k_rows", [P, NT, hd])
            squares = probs[0][:].rearrange("p (t c) -> p t c", t=NT)
            norms = st.sb("norms", [P, 2, NT])
            turns, pair = st.sb("turns", [P, 4, groups]), st.sb("pair", [P, 2, groups])
        ps_scores = [st.psum(f"scores{n}", [P, TOK]) for n in range(2)]
        ps_turn = [st.psum(f"turn{n}", [P, HALF]) for n in range(2)]
        ps_out = st.psum("out", [P, HALF])

        w_in, wo_in, projected = st.sem("w_in"), st.sem("wo_in"), st.sem("projected")
        v_kept, k_kept, q_kept = st.sem("v_kept"), st.sem("k_kept"), st.sem("q_kept")
        scored, maxed, exped = st.sem("scored"), st.sem("maxed"), st.sem("exped")
        turned, first_kept, second_kept = st.sem("turned"), st.sem("first_kept"), st.sem("second_kept")
        summed, inverted, scaled = st.sem("summed"), st.sem("inverted"), st.sem("scaled")
        rows_turned, rowsT_kept = st.sem("rows_turned"), st.sem("rowsT_kept")
        out_ready, out_added = st.sem("out_ready"), st.sem("out_added")
        raw_kept, means, rooted, normed = st.sem("raw_kept"), st.sem("means"), st.sem("rooted"), st.sem("normed")
        turned_qk, capped, pair_step = st.sem("turned_qk"), st.sem("capped"), st.sem("pair_step")
        norm_step = st.sem("norm_step")
        peaked, consts_in = st.sem("peaked"), st.sem("consts_in")

        def width(t):
            return (t + 1) * P if causal else TOK

        @block.sync
        def _(sp):
            sp.dma_start(w[:], core.dram[f"{name}_w"][0]).then_inc(w_in, 16)
            if bias:
                sp.dma_start(qk_bias[:], core.dram[f"{name}_qk_bias"][0]).then_inc(w_in, 16)
                sp.dma_start(v_bias[:], core.dram[f"{name}_v_bias"].broadcast_to([P, total])
                             ).then_inc(consts_in, 16)
            if softcap:
                sp.dma_start(turns[:], core.dram[f"{name}_turns"]).then_inc(consts_in, 16)
            sp.dma_start(wo[:], core.dram[f"{name}_wo"]).then_inc(wo_in, 16)
            if out_bias:
                sp.dma_start(o_bias[:], core.dram[out_bias].broadcast_to([P, D])).then_inc(wo_in, 16)
            with sp.Fori(1, groups) as g:
                sp.wait_ge(projected, 3 * g)
                if bias:
                    sp.wait_ge(q_kept, g)
                    sp.wait_ge(k_kept, g)
                sp.dma_start(w[:], core.dram[f"{name}_w"][bass.ds(g, 1)].rearrange("a p c n -> (a p) c n")
                             ).then_inc(w_in, 16)
                if bias:
                    sp.dma_start(qk_bias[:], core.dram[f"{name}_qk_bias"][bass.ds(g, 1)].rearrange(
                        "a p c -> (a p) c")).then_inc(w_in, 16)

        @block.gpsimd
        def _(pool):
            st.clear_old(pool)

        @block.tensor
        def _(pe):
            for s in (scored, turned, summed):
                pe.sem_inc(s, FREE)
            with pe.Fori(0, groups) as g:
                pe.wait_ge(w_in, g * (16 * LOADS) + 16 * LOADS)
                pe.wait_ge(exped, FREE + g * NI)
                for t in range(NT):
                    for c in range(DC):
                        last = nc.tensor.matmul(ps_scores[0][:, t * P:t * P + vw], hT[:, c, t * P:(t + 1) * P],
                                                w[:, c, 2 * P:], start=(c == 0), stop=(c == DC - 1))
                last.then_inc(projected, 1)
                if softcap:
                    for n in (1, 0):
                        if n == 0:
                            pe.wait_ge(v_kept, g + 1)
                        for t in range(NT):
                            for c in range(DC):
                                last = nc.tensor.matmul(ps_scores[n][:, t * P:(t + 1) * P],
                                                        hT[:, c, t * P:(t + 1) * P], w[:, c, n * P:(n + 1) * P],
                                                        start=(c == 0), stop=(c == DC - 1))
                        last.then_inc(projected, 1)
                    for n, rows_in in ((1, k_rows), (0, q_rows)):
                        pe.wait_ge(normed, 2 * g + 2 - n)
                        for t in range(NT):
                            last = nc.tensor.transpose(ps_scores[n][:, t * P:(t + 1) * P], rows_in[:, t, :],
                                                       core.ident[:])
                        last.then_inc(turned_qk, 1)
                else:
                    for half in range(2):
                        for c in range(DC):
                            last = nc.tensor.matmul(ps_scores[1][:, half * HALF:(half + 1) * HALF], w[:, c, P:2 * P],
                                                    hT[:, c, half * HALF:(half + 1) * HALF],
                                                    start=(c == 0), stop=(c == DC - 1))
                    last.then_inc(projected, 1)
                    pe.wait_ge(v_kept, g + 1)
                    for half in range(2):
                        for c in range(DC):
                            last = nc.tensor.matmul(ps_scores[0][:, half * HALF:(half + 1) * HALF], w[:, c, 0:P],
                                                    hT[:, c, half * HALF:(half + 1) * HALF],
                                                    start=(c == 0), stop=(c == DC - 1))
                    last.then_inc(projected, 1)
                pe.wait_ge(q_kept, g + 1)
                pe.wait_ge(k_kept, g + 1)
                for i in range(NI + 2):
                    if i < NI:
                        j, t = items[i]
                        rows_of = slice(j * stride, j * stride + hd)
                        if i >= 2:
                            pe.wait_ge(exped, FREE + g * NI + (i - 1))
                        for a in range(0, width(t), HALF):
                            b = min(a + HALF, width(t))
                            masks = causal and b == width(t) and not softcap
                            last = nc.tensor.matmul(ps_scores[i % 2][:, a:b], qT[rows_of, t * P:(t + 1) * P],
                                                    kT[rows_of, a:b], start=True, stop=not masks)
                        if causal and not softcap:
                            last = nc.tensor.matmul(ps_scores[i % 2][:, t * P:(t + 1) * P], core.ident_bf[:],
                                                    core.causal[:], start=False, stop=True)
                        last.then_inc(scored, 1)
                    if 1 <= i <= NI:
                        n = i - 1
                        j, t = items[n]
                        pe.wait_ge(exped, FREE + g * NI + (n + 1))
                        for c in range(width(t) // P):
                            if c == 0:
                                pe.wait_ge(first_kept, FREE + g * NI + n)
                            if c == 4:
                                pe.wait_ge(second_kept, FREE + g * NS + seconds[n])
                            last = nc.tensor.transpose(ps_turn[c // 4][:, c % 4 * P:(c % 4 + 1) * P],
                                                       probs[n % 2][:, c * P:(c + 1) * P], core.ident[:])
                            if c == 3 and width(t) > HALF:
                                last.then_inc(turned, 1)
                        last.then_inc(turned, 1)
                    if i >= 2:
                        n = i - 2
                        j, t = items[n]
                        pe.wait_ge(first_kept, FREE + g * NI + (n + 1))
                        if seconds[n + 1] > seconds[n]:
                            pe.wait_ge(second_kept, FREE + g * NS + seconds[n + 1])
                        pe.wait_ge(scaled, FREE + g * NI + n)
                        vs = slice(0, hd) if shared_kv else slice(j * hd, (j + 1) * hd)
                        blocks = width(t) // P
                        for c in range(blocks):
                            last = nc.tensor.matmul(ps_out[:, 0:hd],
                                                    probsT[n % 2][:, c * P:(c + 1) * P], v[:, c, vs],
                                                    start=(c == 0), stop=(c == blocks - 1))
                        last.then_inc(summed, 1)

            pe.wait_ge(scaled, FREE + groups * NI)
            pe.wait_ge(wo_in, 32 if out_bias else 16)
            per = min(NCH, 4)
            lots = [(t, a) for t in range(NT) for a in range(0, NCH, per)]
            for n in range(len(lots) + 1):
                if n < len(lots):
                    t, a = lots[n]
                    if n >= 2:
                        pe.wait_ge(rowsT_kept, n - 1)
                    for c in range(per):
                        last = nc.tensor.transpose(ps_turn[n % 2][:, c * P:(c + 1) * P],
                                                   rows[:, t, (a + c) * P:(a + c + 1) * P], core.ident[:])
                    last.then_inc(rows_turned, 1)
                if n >= 1:
                    t, a = lots[n - 1]
                    pe.wait_ge(rowsT_kept, n)
                    if a == 0 and t >= 2:
                        pe.wait_ge(out_added, t - 1)
                    for c in range(per):
                        last = nc.tensor.matmul(ps_scores[t % 2][:, 0:D],
                                                probsT[(n - 1) % 2][:, c * P:(c + 1) * P], wo[:, a + c, :],
                                                start=(a + c == 0), stop=(a + c == NCH - 1))
                    if a + per == NCH:
                        last.then_inc(out_ready, 1)

        @block.scalar
        def _(act):
            for s in (exped, first_kept):
                act.sem_inc(s, FREE)
            with act.Fori(0, groups) as g:
                act.wait_ge(projected, 3 * g + 1)
                act.wait_ge(summed, FREE + g * NI)
                vps = ps_scores[0][:].rearrange("p (t c) -> p t c", t=NT)[:, :, 0:vw]
                nc.scalar.copy(v[:], vps).then_inc(v_kept, 1)
                if softcap:
                    for n, to in ((1, k_rows), (0, q_rows)):
                        act.wait_ge(projected, 3 * g + 3 - n)
                        src = ps_scores[n][:].rearrange("p (t c) -> p t c", t=NT)
                        nc.scalar.copy(to[:], src).then_inc(raw_kept, 1)
                    act.wait_ge(means, g + 1)
                    nc.scalar.activation(norms[:], norms[:], ACT.Sqrt).then_inc(rooted, 1)
                    act.wait_ge(turned_qk, 2 * g + 2)
                    nc.scalar.copy(qT[:], ps_scores[0][:]).then_inc(q_kept, 1)
                else:
                    act.wait_ge(projected, 3 * g + 3)
                if softcap:
                    pass
                elif bias:
                    nc.scalar.activation(qT[:], ps_scores[0][:], ACT.Identity, bias=qk_bias[:, 0:1]
                                         ).then_inc(q_kept, 1)
                else:
                    nc.scalar.copy(qT[:], ps_scores[0][:]).then_inc(q_kept, 1)
                for i in range(NI + 1):
                    if i < NI:
                        j, t = items[i]
                        act.wait_ge(scored if softcap else maxed, g * NI + (i + 1) + (FREE if softcap else 0))
                        turns = (i - 2) + 1 + seconds[i - 1] if i >= 2 else 0
                        act.wait_ge(turned, FREE + g * (NI + NS) + turns)
                        if i >= 2:
                            act.wait_ge(inverted, g * NI + (i - 1))
                        if softcap:
                            nc.scalar.activation(probs[i % 2][:, 0:width(t)], ps_scores[i % 2][:, 0:width(t)],
                                                 ACT.Tanh, scale=scale / softcap).then_inc(capped, 1)
                            act.wait_ge(maxed, g * NI + (i + 1))
                            nc.scalar.activation(probs[i % 2][:, 0:width(t)], probs[i % 2][:, 0:width(t)],
                                                 ACT.Exp, scale=softcap, accum_out=rowsum[:, i:i + 1]
                                                 ).then_inc(exped, 1)
                        else:
                          nc.scalar.activation(probs[i % 2][:, 0:width(t)], ps_scores[i % 2][:, 0:width(t)],
                                             ACT.Exp, bias=negmax[:, i:i + 1], scale=scale,
                                             accum_out=rowsum[:, i:i + 1]).then_inc(exped, 1)
                    if i >= 1:
                        n = i - 1
                        j, t = items[n]
                        act.wait_ge(turned, FREE + g * (NI + NS) + (n + 1 + seconds[n]))
                        act.wait_ge(summed, FREE + g * NI + max(n - 1, 0))
                        b = min(width(t), HALF)
                        nc.scalar.copy(probsT[n % 2][:, 0:b], ps_turn[0][:, 0:b]).then_inc(first_kept, 1)

        @block.vector
        def _(dve):
            for s in (second_kept, scaled):
                dve.sem_inc(s, FREE)
            if bias or softcap:
                dve.wait_ge(consts_in, 16)
            if softcap:
                pairs = linker(dve, pair_step)
                for n in range(2):
                    pairs(nc.vector.tensor_tensor(pair[:, n], turns[:, n], turns[:, n], ALU.mult))
                pairs(nc.vector.tensor_tensor(pair[:, 0], pair[:, 0], pair[:, 1], ALU.add))
                for n in range(2):
                    pairs(nc.vector.tensor_tensor(pair[:, 0], pair[:, 0], turns[:, 2 + n], ALU.mult))
            with dve.Fori(0, groups) as g:
                if softcap:
                    for n, rows_in in ((1, k_rows), (0, q_rows)):
                        dve.wait_ge(raw_kept, 2 * g + 2 - n)
                        dve.wait_ge(turned, FREE + g * (NI + NS))
                        steps = 5 * g + (1 - n) * 2
                        nc.vector.tensor_tensor(squares, rows_in[:], rows_in[:], ALU.mult).then_inc(norm_step, 1)
                        dve.wait_ge(norm_step, steps + 1)
                        nc.vector.tensor_reduce(norms[:, n, :], squares, AX, ALU.add).then_inc(norm_step, 1)
                        dve.wait_ge(norm_step, steps + 2)
                    nc.vector.tensor_scalar(norms[:], norms[:], 1.0 / hd, 1e-6, ALU.mult, ALU.add
                                            ).then_inc(means, 1)
                    dve.wait_ge(rooted, g + 1)
                    nc.vector.reciprocal(norms[:], norms[:]).then_inc(norm_step, 1)
                    dve.wait_ge(norm_step, 5 * g + 5)
                    for n, rows_in in ((1, k_rows), (0, q_rows)):
                        nc.vector.tensor_tensor(rows_in[:], rows_in[:], norms[:, n, :].unsqueeze(2).broadcast_to(
                            [P, NT, hd]), ALU.mult).then_inc(normed, 1)
                    dve.wait_ge(turned_qk, 2 * g + 1)
                else:
                    dve.wait_ge(projected, 3 * g + 2)
                dve.wait_ge(scored, FREE + g * NI)
                if softcap:
                    nc.vector.tensor_scalar(kT[:], ps_scores[1][:], pair[:, 0, bass.ds(g, 1)], None, ALU.mult
                                            ).then_inc(k_kept, 1)
                elif bias:
                    nc.vector.tensor_scalar(kT[:], ps_scores[1][:], qk_bias[:, 1:2], None, ALU.add
                                            ).then_inc(k_kept, 1)
                else:
                    nc.vector.tensor_copy(kT[:], ps_scores[1][:]).then_inc(k_kept, 1)
                for i in range(NI + 2):
                    if i < NI:
                        j, t = items[i]
                        if softcap:
                            dve.wait_ge(capped, g * NI + (i + 1))
                            diagonal = probs[i % 2][:, t * P:(t + 1) * P]
                            nc.vector.tensor_tensor(diagonal, diagonal, core.causal_f[:], ALU.add
                                                    ).then_inc(maxed, 1)
                    if i < NI and not softcap:
                        dve.wait_ge(scored, FREE + g * NI + (i + 1))
                        dve.wait_ge(exped, FREE + g * NI + max(i - 1, 0))
                        nc.vector.tensor_reduce(negmax[:, i:i + 1], ps_scores[i % 2][:, 0:width(t)], AX,
                                                ALU.max, negate=True).then_inc(peaked, 1)
                        dve.wait_ge(peaked, g * NI + (i + 1))
                        nc.vector.tensor_scalar(negmax[:, i:i + 1], negmax[:, i:i + 1], scale, None,
                                                ALU.mult).then_inc(maxed, 1)
                    if 1 <= i <= NI:
                        n = i - 1
                        j, t = items[n]
                        if seconds[n + 1] > seconds[n]:
                            dve.wait_ge(turned, FREE + g * (NI + NS) + (n + 1 + seconds[n + 1]))
                            dve.wait_ge(summed, FREE + g * NI + max(n - 1, 0))
                            nc.vector.tensor_copy(probsT[n % 2][:, HALF:width(t)],
                                                  ps_turn[1][:, 0:width(t) - HALF]).then_inc(second_kept, 1)
                        dve.wait_ge(exped, FREE + g * NI + (n + 1))
                        nc.vector.reciprocal(rowinv[:, n:n + 1], rowsum[:, n:n + 1]).then_inc(inverted, 1)
                    if i >= 2:
                        n = i - 2
                        j, t = items[n]
                        dve.wait_ge(inverted, g * NI + (n + 1))
                        dve.wait_ge(summed, FREE + g * NI + (n + 1))
                        to = rows[:, t, bass.ds(g * gw + j * hd, hd)]
                        src = ps_out[:, 0:hd]
                        if bias:
                            nc.vector.scalar_tensor_tensor(
                                to, src, rowinv[:, n:n + 1], v_bias[:, bass.ds(g * gw + j * hd, hd)],
                                ALU.mult, ALU.add).then_inc(scaled, 1)
                        else:
                            nc.vector.tensor_scalar(to, src, rowinv[:, n:n + 1], None, ALU.mult
                                                    ).then_inc(scaled, 1)
            per = min(NCH, 4)
            lots = [(t, a) for t in range(NT) for a in range(0, NCH, per)]
            if out_bias:
                dve.wait_ge(wo_in, 32)
                for t in range(NT):
                    nc.vector.tensor_tensor(x[:, t, :], x[:, t, :], o_bias[:], ALU.add).then_inc(consts_in, 1)
                dve.wait_ge(consts_in, (16 if bias else 0) + NT)

            def add_out(t):
                src = ps_scores[t % 2][:, 0:D]
                if into is not None:
                    nc.vector.tensor_copy(into[:, t, :], src).then_inc(out_added, 1)
                else:
                    nc.vector.tensor_tensor(x[:, t, :], x[:, t, :], src, ALU.add).then_inc(out_added, 1)

            for n in range(len(lots)):
                t, a = lots[n]
                dve.wait_ge(rows_turned, n + 1)
                nc.vector.tensor_copy(probsT[n % 2][:, 0:per * P], ps_turn[n % 2][:, 0:per * P]
                                      ).then_inc(rowsT_kept, 1)
                if a + per == NCH and t >= 1:
                    dve.wait_ge(out_ready, t)
                    add_out(t - 1)
            dve.wait_ge(out_ready, NT)
            add_out(NT - 1)


def gated_feed_forward(core, name, tiles, body, source=None, scaled=False, low_rank=None, combine=None,
                       down_scale=None):
    nc, x = core.nc, core.x
    hT = source if source is not None else core.hT
    UNITS = 2 * body
    TURNS = tiles // body
    FREE = 4
    wide = 3 * D + (P if low_rank is not None else 0) + (2 if scaled else 0)
    low0 = 3 * D
    scale0 = low0 + (P if low_rank is not None else 0)

    with Stage(core, name) as st:
        block = st.opened
        w = [st.sb(f"w{n}", [P, wide]) for n in range(2)]
        gate = [st.sb(f"gate{n}", [P, HALF]) for n in range(2)]
        inner = [st.sb(f"inner{n}", [P, HALF]) for n in range(2)]
        zeros = st.sb("zeros", [P, HALF], BF16)
        if combine is not None:
            weight = [st.sb(f"weight{n}", [P, TOK]) for n in range(2)]
        if down_scale:
            down_by = st.sb("down_by", [P, D])
        ps_gate = [st.psum(f"gate{n}", [P, HALF]) for n in range(2)]
        ps_up = [st.psum(f"up{n}", [P, HALF]) for n in range(2)]
        ps_out = [st.psum(f"out{n}", [P, HALF]) for n in range(4)]

        w_in = [st.sem(f"w_in{n}") for n in range(2)]
        weight_in = [st.sem(f"weight_in{n}") for n in range(2)]
        zeroed, consts_in, opened = st.sem("zeroed"), st.sem("consts_in"), st.sem("opened")
        gated_up, silued, weighted = st.sem("gated_up"), st.sem("silued"), st.sem("weighted")
        multiplied, lowered, finished = st.sem("multiplied"), st.sem("lowered"), st.sem("finished")

        @block.sync
        def _(sp):
            if down_scale:
                sp.dma_start(down_by[:], core.dram[down_scale].broadcast_to([P, D])).then_inc(consts_in, 16)
            with sp.Fori(0, TURNS) as k:
                for b in range(body):
                    sp.wait_ge(lowered, k * UNITS + (2 * b + 2))
                    sp.dma_start(w[b % 2][:], core.dram[f"{name}_w"][bass.ds(k * body + b, 1)].rearrange(
                        "a p n -> (a p) n")).then_inc(w_in[b % 2], 16)
                    if combine is not None:
                        row, left, at = b * P, P, 0
                        while left:
                            e, n = row // 96, min(left, 96 - row % 96)
                            src = combine[bass.ds(k * (body * P // 96) + e, 1)].broadcast_to([n, TOK])
                            sp.dma_start(weight[b % 2][at:at + n, :], src).then_inc(weight_in[b % 2], 16)
                            row, left, at = row + n, left - n, at + n

        @block.gpsimd
        def _(pool):
            nc.gpsimd.memset(zeros[:], 0.0).then_inc(zeroed, 1)
            st.clear_old(pool)
            if combine is not None:
                with pool.Fori(0, TURNS) as k:
                    for u in range(UNITS):
                        b, half = u // 2, u % 2
                        pool.wait_ge(silued, k * UNITS + (u + 1))
                        pool.wait_ge(weight_in[b % 2], k * (32 * body // 2) + 32 * (b // 2 + 1))
                        nc.gpsimd.tensor_tensor(gate[u % 2][:], gate[u % 2][:],
                                                weight[b % 2][:, half * HALF:(half + 1) * HALF], ALU.mult
                                                ).then_inc(weighted, 1)

        @block.tensor
        def _(pe):
            pe.sem_inc(lowered, FREE)
            pe.wait_ge(zeroed, 1)
            for n in range(4):
                nc.tensor.matmul(ps_out[n][:], zeros[:, 0:P], zeros[:], start=True, stop=False)

            def gate_and_up(k, u):
                b, half = u // 2, u % 2
                tokens = slice(half * HALF, (half + 1) * HALF)
                pe.wait_ge(w_in[b % 2], k * (16 * body // 2) + 16 * (b // 2 + 1))
                pe.wait_ge(multiplied, k * UNITS + (u + FREE - 1))
                for c in range(DC):
                    nc.tensor.matmul(ps_gate[u % 2][:], w[b % 2][:, c * P:(c + 1) * P], hT[:, c, tokens],
                                     start=(c == 0), stop=(c == DC - 1 and low_rank is None))
                if low_rank is not None:
                    nc.tensor.matmul(ps_gate[u % 2][:], w[b % 2][0:16, low0:low0 + P], low_rank[:, tokens],
                                     start=False, stop=True)
                for c in range(DC):
                    last = nc.tensor.matmul(ps_up[u % 2][:], w[b % 2][:, D + c * P:D + (c + 1) * P],
                                            hT[:, c, tokens], start=(c == 0), stop=(c == DC - 1))
                last.then_inc(gated_up, 1)

            def down(k, u):
                b, half = u // 2, u % 2
                pe.wait_ge(multiplied, k * UNITS + (u + FREE + 1))
                for i in range(4):
                    t = 4 * half + i
                    last = nc.tensor.matmul(ps_out[t // 2][:, t % 2 * D:(t % 2 + 1) * D],
                                            inner[u % 2][:, i * P:(i + 1) * P], w[b % 2][:, 2 * D:3 * D],
                                            start=False, stop=False, skip_group_check=True)
                last.then_inc(lowered, 1)

            with pe.Fori(0, TURNS) as k:
                for u in range(UNITS):
                    gate_and_up(k, u)
                    if u:
                        down(k, u - 1)
                down(k, UNITS - 1)
            for n in range(4):
                last = nc.tensor.matmul(ps_out[n][:], zeros[:, 0:P], zeros[:], start=False, stop=True)
            last.then_inc(finished, 1)

        @block.scalar
        def _(act):
            with act.Fori(0, TURNS) as k:
                for u in range(UNITS):
                    b = u // 2
                    act.wait_ge(gated_up, k * UNITS + (u + 1))
                    act.wait_ge(multiplied, k * UNITS + (u + FREE - 1))
                    by = w[b % 2][:, scale0:scale0 + 1] if scaled else 1.0
                    nc.scalar.activation(gate[u % 2][:], ps_gate[u % 2][:], ACT.Silu, scale=by
                                         ).then_inc(silued, 1)

        @block.vector
        def _(dve):
            dve.sem_inc(multiplied, FREE)
            with dve.Fori(0, TURNS) as k:
                for u in range(UNITS):
                    b = u // 2
                    dve.wait_ge(weighted if combine is not None else silued, k * UNITS + (u + 1))
                    dve.wait_ge(lowered, k * UNITS + (u + FREE - 1))
                    if scaled:
                        nc.vector.scalar_tensor_tensor(inner[u % 2][:], ps_up[u % 2][:],
                                                       w[b % 2][:, scale0 + 1:scale0 + 2], gate[u % 2][:],
                                                       ALU.mult, ALU.mult).then_inc(multiplied, 1)
                    else:
                        nc.vector.tensor_tensor(inner[u % 2][:], ps_up[u % 2][:], gate[u % 2][:], ALU.mult
                                                ).then_inc(multiplied, 1)
            dve.wait_ge(finished, 1)
            if down_scale:
                dve.wait_ge(consts_in, 16)
            for t in range(NT):
                src = ps_out[t // 2][:, t % 2 * D:(t % 2 + 1) * D]
                if down_scale:
                    buffer = inner[t % 2][:, 0:D]
                    nc.vector.tensor_tensor(buffer, src, down_by[:], ALU.mult).then_inc(consts_in, 1)
                    dve.wait_ge(consts_in, 16 + t + 1)
                    src = buffer
                nc.vector.tensor_tensor(x[:, t, :], x[:, t, :], src, ALU.add)


def feed_forward_0(core):
    with ExitStack() as layer:
        count = core.count

        def sb(name, shape):
            return layer.enter_context(core.nc.sbuf_tensor(f"ff{count}_{name}", shape, F32))

        h2T = sb("h2T", [P, DC, TOK])
        attended = sb("attended", [P, NT, D])
        modT = sb("modT", [16, TOK])
        normalise(core, [(core.hT, ["L0f_ln1"]), (h2T, ["L0f_ln2"])], second=("rms", 1e-6), keep=True)
        attention(core, "L0f", groups=4, heads=4, hd=16, shared_kv=False, causal=True, scale=0.25,
                  into=attended)
        low_rank_factor(core, attended, h2T, modT)
        gated_feed_forward(core, "L0g", tiles=8, body=2, source=h2T, low_rank=modT)


def low_rank_factor(core, attended, h2T, modT):
    nc = core.nc
    with Stage(core, "factor") as st:
        block = st.opened
        a = st.sb("a", [P, DC, 16])
        attendedT = st.sb("attendedT", [P, DC, TOK])
        factor = st.sb("factor", [16, TOK])
        ps_turn = [st.psum(f"turn{n}", [P, HALF]) for n in range(4)]
        ps_factor = [st.psum(f"factor{n}", [16, HALF]) for n in range(2)]
        ps_low = [st.psum(f"low{n}", [16, HALF]) for n in range(2)]
        a_in, turned, kept = st.sem("a_in"), st.sem("turned"), st.sem("kept")
        factored, tanhed = st.sem("factored"), st.sem("tanhed")

        @block.sync
        def _(sp):
            sp.dma_start(a[:], core.dram["L0f_A"]).then_inc(a_in, 16)

        @block.gpsimd
        def _(pool):
            st.clear_old(pool)

        @block.tensor
        def _(pe):
            for half in range(2):
                for c in range(DC):
                    for i in range(4):
                        last = nc.tensor.transpose(ps_turn[2 * half + c][:, i * P:(i + 1) * P],
                                                   attended[:, 4 * half + i, c * P:(c + 1) * P], core.ident[:])
                    last.then_inc(turned, 1)
            pe.wait_ge(a_in, 16)
            for half in range(2):
                tokens = slice(half * HALF, (half + 1) * HALF)
                for c in range(DC):
                    nc.tensor.matmul(ps_low[half][:], a[:, c, :], h2T[:, c, tokens],
                                     start=(c == 0), stop=(c == DC - 1))
                for c in range(DC):
                    pe.wait_ge(kept, 2 * half + c + 1)
                    last = nc.tensor.matmul(ps_factor[half][:], a[:, c, :], attendedT[:, c, tokens],
                                            start=(c == 0), stop=(c == DC - 1))
                last.then_inc(factored, 1)

        @block.scalar
        def _(act):
            for half in range(2):
                act.wait_ge(factored, half + 1)
                nc.scalar.activation(factor[:, half * HALF:(half + 1) * HALF], ps_factor[half][:], ACT.Tanh
                                     ).then_inc(tanhed, 1)

        @block.vector
        def _(dve):
            for half in range(2):
                for c in range(DC):
                    dve.wait_ge(turned, 2 * half + c + 1)
                    nc.vector.tensor_copy(attendedT[:, c, half * HALF:(half + 1) * HALF],
                                          ps_turn[2 * half + c][:]).then_inc(kept, 1)
            for half in range(2):
                tokens = slice(half * HALF, (half + 1) * HALF)
                dve.wait_ge(tanhed, half + 1)
                nc.vector.scalar_tensor_tensor(modT[:, tokens], factor[:, tokens], 0.1, ps_low[half][:],
                                               ALU.mult, ALU.mult)


def ternary_feed_forward(core):
    normalise(core, [(core.hT, [])])
    gated_feed_forward(core, "L2f", tiles=6, body=2, scaled=True, down_scale="L2f_down_s")


EXPERTS, TOP = 32, 8


def experts(core):
    normalise(core, [(core.hT, [])])
    combine = core.nc.dram_tensor(f"combine{core.count}", (EXPERTS, TOK), F32).ap()
    route(core, combine)
    gated_feed_forward(core, "L1f", tiles=24, body=6, combine=combine)


def route(core, combine):
    nc, hT = core.nc, core.hT
    with Stage(core, "route") as st:
        block = st.opened
        wr = st.sb("wr", [P, DC, EXPERTS])
        number = st.sb("number", [P, EXPERTS])
        logits, p = st.sb("logits", [P, NT, EXPERTS]), st.sb("p", [P, NT, EXPERTS])
        peak, total, inverse = st.sb("peak", [P, NT]), st.sb("total", [P, NT]), st.sb("inverse", [P, NT])
        top, share = st.sb("top", [P, NT, TOP]), st.sb("share", [P, NT, TOP])
        index, index_f = st.sb("index", [P, NT, TOP], U32), st.sb("index_f", [P, NT, TOP])
        chosen = st.sb("chosen", [P, NT, EXPERTS, TOP])
        weights = st.sb("weights", [P, NT, EXPERTS])
        weightsT = st.sb("weightsT", [EXPERTS, TOK])
        ps_logits = st.psum("logits", [P, NT, EXPERTS])
        ps_turn = [st.psum(f"turn{n}", [EXPERTS, HALF]) for n in range(2)]
        step, in_, projected, exped = st.sem("step"), st.sem("in"), st.sem("projected"), st.sem("exped")
        shifted, ready, turned = st.sem("shifted"), st.sem("ready"), st.sem("turned")
        copied, stored = st.sem("copied"), st.sem("stored")
        found = st.sem("found")

        def over_top(a):
            return a[:].unsqueeze(2).broadcast_to([P, NT, TOP])

        def over_experts(a):
            return a[:].unsqueeze(2).broadcast_to([P, NT, EXPERTS])

        @block.sync
        def _(sp):
            sp.dma_start(wr[:], core.dram["L1f_router"]).then_inc(in_, 16)
            sp.dma_start(number[:], core.dram["expert_number"].broadcast_to([P, EXPERTS])).then_inc(in_, 16)
            sp.wait_ge(copied, 2)
            sp.dma_start(combine, weightsT[:]).then_inc(stored, 16)
            sp.wait_ge(stored, 16)

        @block.gpsimd
        def _(pool):
            st.clear_old(pool)

        @block.tensor
        def _(pe):
            pe.wait_ge(in_, 32)
            for t in range(NT):
                for c in range(DC):
                    last = nc.tensor.matmul(ps_logits[:, t, :], hT[:, c, t * P:(t + 1) * P], wr[:, c, :],
                                            start=(c == 0), stop=(c == DC - 1))
            last.then_inc(projected, 1)
            pe.wait_ge(ready, 1)
            for t in range(NT):
                last = nc.tensor.transpose(ps_turn[t // 4][:, t % 4 * P:(t % 4 + 1) * P], weights[:, t, :],
                                           core.ident[:])
                if t % 4 == 3:
                    last.then_inc(turned, 1)

        @block.scalar
        def _(act):
            act.wait_ge(shifted, 1)
            nc.scalar.activation(p[:], logits[:], ACT.Exp).then_inc(exped, 1)

        @block.vector
        def _(dve):
            link = linker(dve, step)
            dve.wait_ge(projected, 1)
            link(nc.vector.tensor_reduce(peak[:], ps_logits[:], AX, ALU.max))
            nc.vector.tensor_tensor(logits[:], ps_logits[:], over_experts(peak), ALU.subtract
                                    ).then_inc(shifted, 1)
            dve.wait_ge(exped, 1)
            link(nc.vector.tensor_reduce(total[:], p[:], AX, ALU.add))
            link(nc.vector.reciprocal(inverse[:], total[:]))
            link(nc.vector.tensor_tensor(p[:], p[:], over_experts(inverse), ALU.mult))
            for t in range(NT):
                nc.vector.max(top[:, t, :], p[:, t, :]).then_inc(found, 1)
            for t in range(NT):
                dve.wait_ge(found, t + 1)
                nc.vector.max_index(index[:, t, :], top[:, t, :], p[:, t, :]).then_inc(found, 1)
            dve.wait_ge(found, 2 * NT)
            link(nc.vector.tensor_copy(index_f[:], index[:]))
            link(nc.vector.tensor_reduce(total[:], top[:], AX, ALU.add))
            link(nc.vector.tensor_scalar(total[:], total[:], 1e-12, None, ALU.max))
            link(nc.vector.reciprocal(inverse[:], total[:]))
            link(nc.vector.tensor_tensor(share[:], top[:], over_top(inverse), ALU.mult))
            for k in range(1, TOP):
                link(nc.vector.tensor_tensor(share[:, :, k], share[:, :, k], share[:, :, k - 1], ALU.add))
            link(nc.vector.tensor_scalar(share[:], share[:], 0.8, None, ALU.is_lt))
            link(nc.vector.tensor_tensor(top[:, :, 1:], top[:, :, 1:], share[:, :, 0:TOP - 1], ALU.mult))
            link(nc.vector.tensor_reduce(total[:], top[:], AX, ALU.add))
            link(nc.vector.tensor_scalar(total[:], total[:], 1e-12, None, ALU.max))
            link(nc.vector.reciprocal(inverse[:], total[:]))
            link(nc.vector.tensor_tensor(top[:], top[:], over_top(inverse), ALU.mult))
            dve.wait_ge(in_, 32)
            for t in range(NT):
                nc.vector.tensor_tensor(chosen[:, t], index_f[:, t].unsqueeze(1).broadcast_to([P, EXPERTS, TOP]),
                                        number[:].unsqueeze(2).broadcast_to([P, EXPERTS, TOP]), ALU.is_equal
                                        ).then_inc(found, 1)
            for t in range(NT):
                dve.wait_ge(found, 2 * NT + t + 1)
                nc.vector.tensor_tensor(chosen[:, t], chosen[:, t],
                                        top[:, t].unsqueeze(1).broadcast_to([P, EXPERTS, TOP]), ALU.mult
                                        ).then_inc(found, 1)
            dve.wait_ge(found, 4 * NT)
            nc.vector.tensor_reduce(weights[:], chosen[:], AX, ALU.add).then_inc(ready, 1)
            for n in range(2):
                dve.wait_ge(turned, n + 1)
                nc.vector.tensor_copy(weightsT[:, n * HALF:(n + 1) * HALF], ps_turn[n][:]).then_inc(copied, 1)


def decay_scan(core):
    normalise(core, [(core.hT, [])])
    nc, x, hT = core.nc, core.x, core.hT
    with Stage(core, "decay") as st:
        block = st.opened
        w, bias = st.sb("w", [P, DC, D]), st.sb("bias", [P, DC])
        lam, fed, s = st.sb("lam", [P, DC, TOK]), st.sb("fed", [P, DC, TOK]), st.sb("s", [P, DC, TOK])
        ps_lam = [st.psum(f"lam{n}", [P, HALF]) for n in range(4)]
        ps_rows = [st.psum(f"rows{n}", [P, HALF]) for n in range(4)]
        w_in, projected, decays, feeds = st.sem("w_in"), st.sem("projected"), st.sem("decays"), st.sem("feeds")
        scanned, turned = st.sem("scanned"), st.sem("turned")

        @block.sync
        def _(sp):
            sp.dma_start(w[:], core.dram["L1b_w"]).then_inc(w_in, 16)
            sp.dma_start(bias[:], core.dram["L1b_b"]).then_inc(w_in, 16)

        @block.gpsimd
        def _(pool):
            st.clear_old(pool)

        @block.tensor
        def _(pe):
            pe.wait_ge(w_in, 32)
            for e in range(DC):
                for half in range(2):
                    for c in range(DC):
                        last = nc.tensor.matmul(ps_lam[2 * e + half][:], w[:, c, e * P:(e + 1) * P],
                                                hT[:, c, half * HALF:(half + 1) * HALF],
                                                start=(c == 0), stop=(c == DC - 1))
                    last.then_inc(projected, 1)
            pe.wait_ge(scanned, 2)
            for t in range(NT):
                for c in range(DC):
                    last = nc.tensor.transpose(ps_rows[t // 2][:, t % 2 * D + c * P:t % 2 * D + (c + 1) * P],
                                               s[:, c, t * P:(t + 1) * P], core.ident[:])
                if t % 2:
                    last.then_inc(turned, 1)

        @block.scalar
        def _(act):
            act.wait_ge(w_in, 32)
            for e in range(DC):
                for half in range(2):
                    act.wait_ge(projected, 2 * e + half + 1)
                    nc.scalar.activation(lam[:, e, half * HALF:(half + 1) * HALF], ps_lam[2 * e + half][:],
                                         ACT.Sigmoid, bias=bias[:, e:e + 1]).then_inc(decays, 1)

        @block.vector
        def _(dve):
            for e in range(DC):
                dve.wait_ge(decays, 2 * e + 2)
                nc.vector.scalar_tensor_tensor(fed[:, e, :], lam[:, e, :], 1.0, hT[:, e, :], ALU.subtract,
                                               ALU.mult).then_inc(feeds, 1)
                dve.wait_ge(feeds, e + 1)
                nc.vector.tensor_tensor_scan(s[:, e, :], lam[:, e, :], fed[:, e, :], 0.0, ALU.mult,
                                             ALU.subtract).then_inc(scanned, 1)
            for n in range(4):
                dve.wait_ge(turned, n + 1)
                two = x[:, 2 * n:2 * n + 2, :]
                nc.vector.tensor_tensor(two, two, ps_rows[n][:].rearrange("p (t d) -> p t d", t=2), ALU.add)


ROUTES, RANK = 6, 16


def low_rank_experts(core):
    normalise(core, [(core.hT, [])])
    nc, x, hT = core.nc, core.x, core.hT
    LOW = RANK * (1 + ROUTES)
    with Stage(core, "low") as st:
        block = st.opened
        w1, base = st.sb("w1", [P, DC, LOW + ROUTES]), st.sb("base", [P, DC, D])
        w2 = st.sb("w2", [LOW + 1, D])
        router_bias, number = st.sb("router_bias", [P, ROUTES]), st.sb("number", [P, ROUTES])
        p, shifted_logits = st.sb("p", [P, NT, 8]), st.sb("shifted_logits", [P, NT, ROUTES])
        peak, total, inverse = st.sb("peak", [P, NT]), st.sb("total", [P, NT]), st.sb("inverse", [P, NT])
        top, index, index_f = st.sb("top", [P, NT, 8]), st.sb("index", [P, NT, 8], U32), st.sb("index_f", [P, NT, 8])
        chosen, weights = st.sb("chosen", [P, NT, ROUTES, 2]), st.sb("weights", [P, NT, ROUTES])
        z, zT = st.sb("z", [P, NT, LOW + 1]), st.sb("zT", [LOW + 1, TOK])
        ps_z = st.psum("z", [P, NT, P])
        ps_turn = [st.psum(f"turn{n}", [LOW + 1, HALF]) for n in range(2)]
        ps_out = [st.psum(f"out{n}", [P, HALF]) for n in range(4)]
        in_, step, projected, shifted = st.sem("in"), st.sem("step"), st.sem("projected"), st.sem("shifted")
        exped, found, weighted = st.sem("exped"), st.sem("found"), st.sem("weighted")
        turned, kept, out_ready, filled = st.sem("turned"), st.sem("kept"), st.sem("out_ready"), st.sem("filled")
        kept_act = st.sem("kept_act")

        @block.sync
        def _(sp):
            for to, src in ((w1[:], "L3f_w1"), (base[:], "L3f_base"), (w2[:], "L3f_w2")):
                sp.dma_start(to, core.dram[src]).then_inc(in_, 16)
            sp.dma_start(router_bias[:], core.dram["L3f_router_bias"].broadcast_to([P, ROUTES])).then_inc(in_, 16)
            sp.dma_start(number[:], core.dram["expert_number"][:, 0:ROUTES].broadcast_to([P, ROUTES])
                         ).then_inc(in_, 16)

        @block.gpsimd
        def _(pool):
            nc.gpsimd.memset(p[:], -1.0).then_inc(filled, 1)
            nc.gpsimd.memset(z[:], 1.0).then_inc(filled, 1)
            st.clear_old(pool)

        @block.tensor
        def _(pe):
            pe.wait_ge(in_, 80)
            for t in range(NT):
                for c in range(DC):
                    last = nc.tensor.matmul(ps_z[:, t, 0:LOW + ROUTES], hT[:, c, t * P:(t + 1) * P], w1[:, c, :],
                                            start=(c == 0), stop=(c == DC - 1))
            last.then_inc(projected, 1)
            pe.wait_ge(weighted, 2)
            for t in range(NT):
                last = nc.tensor.transpose(ps_turn[t // 4][:, t % 4 * P:(t % 4 + 1) * P], z[:, t, :],
                                           core.ident[:])
                if t % 4 == 3:
                    last.then_inc(turned, 1)
            for t in range(NT):
                if t % 4 == 0:
                    pe.wait_ge(kept if t == 0 else kept_act, 1)
                to = ps_out[t // 2][:, t % 2 * D:(t % 2 + 1) * D]
                for c in range(DC):
                    nc.tensor.matmul(to, hT[:, c, t * P:(t + 1) * P], base[:, c, :], start=(c == 0), stop=False)
                last = nc.tensor.matmul(to, zT[:, t * P:(t + 1) * P], w2[:], start=False, stop=True)
                if t % 2:
                    last.then_inc(out_ready, 1)

        @block.scalar
        def _(act):
            act.wait_ge(shifted, 1)
            act.wait_ge(filled, 1)
            nc.scalar.activation(p[:, :, 0:ROUTES], shifted_logits[:], ACT.Exp).then_inc(exped, 1)
            act.wait_ge(turned, 2)
            nc.scalar.copy(zT[:, HALF:], ps_turn[1][:]).then_inc(kept_act, 1)

        @block.vector
        def _(dve):
            link = linker(dve, step)

            def over_routes(a):
                return a[:].unsqueeze(2).broadcast_to([P, NT, ROUTES])

            dve.wait_ge(in_, 80)
            dve.wait_ge(projected, 1)
            link(nc.vector.tensor_tensor(shifted_logits[:], ps_z[:, :, LOW:LOW + ROUTES],
                                         router_bias[:].unsqueeze(1).broadcast_to([P, NT, ROUTES]), ALU.add))
            link(nc.vector.tensor_reduce(peak[:], shifted_logits[:], AX, ALU.max))
            nc.vector.tensor_tensor(shifted_logits[:], shifted_logits[:], over_routes(peak), ALU.subtract
                                    ).then_inc(shifted, 1)
            dve.wait_ge(exped, 1)
            link(nc.vector.tensor_reduce(total[:], p[:, :, 0:ROUTES], AX, ALU.add))
            link(nc.vector.reciprocal(inverse[:], total[:]))
            link(nc.vector.tensor_tensor(p[:, :, 0:ROUTES], p[:, :, 0:ROUTES], over_routes(inverse), ALU.mult))
            for t in range(NT):
                nc.vector.max(top[:, t, :], p[:, t, :]).then_inc(found, 1)
            for t in range(NT):
                dve.wait_ge(found, t + 1)
                nc.vector.max_index(index[:, t, :], top[:, t, :], p[:, t, :]).then_inc(found, 1)
            dve.wait_ge(found, 2 * NT)
            link(nc.vector.tensor_copy(index_f[:], index[:]))
            for k in range(2):
                nc.vector.tensor_tensor(chosen[:, :, :, k],
                                        index_f[:, :, k].unsqueeze(2).broadcast_to([P, NT, ROUTES]),
                                        number[:].unsqueeze(1).broadcast_to([P, NT, ROUTES]), ALU.is_equal
                                        ).then_inc(found, 1)
            for k in range(2):
                dve.wait_ge(found, 2 * NT + k + 1)
                nc.vector.tensor_tensor(chosen[:, :, :, k], chosen[:, :, :, k],
                                        top[:, :, k].unsqueeze(2).broadcast_to([P, NT, ROUTES]), ALU.mult
                                        ).then_inc(found, 1)
            dve.wait_ge(found, 2 * NT + 4)
            link(nc.vector.tensor_tensor(weights[:], chosen[:, :, :, 0], chosen[:, :, :, 1], ALU.add))
            dve.wait_ge(filled, 2)
            nc.vector.tensor_copy(z[:, :, 0:RANK], ps_z[:, :, 0:RANK]).then_inc(weighted, 1)
            nc.vector.tensor_tensor(z[:, :, RANK:LOW].rearrange("p t (e r) -> p t e r", e=ROUTES),
                                    ps_z[:, :, RANK:LOW].rearrange("p t (e r) -> p t e r", e=ROUTES),
                                    weights[:].unsqueeze(3).broadcast_to([P, NT, ROUTES, RANK]), ALU.mult
                                    ).then_inc(weighted, 1)
            dve.wait_ge(turned, 1)
            nc.vector.tensor_copy(zT[:, 0:HALF], ps_turn[0][:]).then_inc(kept, 1)
            for n in range(4):
                dve.wait_ge(out_ready, n + 1)
                two = x[:, 2 * n:2 * n + 2, :]
                nc.vector.tensor_tensor(two, two, ps_out[n][:].rearrange("p (t d) -> p t d", t=2), ALU.add)


STATES = 16


def state_space(core):
    normalise(core, [(core.hT, [])])
    nc, x, hT = core.nc, core.x, core.hT
    with ExitStack() as layer:
        count = core.count

        def sb(name, shape):
            return layer.enter_context(nc.sbuf_tensor(f"ss{count}_{name}", shape, F32))

        delta, fed = sb("delta", [P, DC, TOK]), sb("fed", [P, DC, TOK])
        bc = nc.dram_tensor(f"bc{count}", (2 * STATES, TOK), F32).ap()
        steps_and_feeds(core, delta, fed, bc)
        scan_states(core, delta, fed, bc)


def steps_and_feeds(core, delta, fed, bc):
    nc, hT = core.nc, core.hT
    with Stage(core, "steps") as st:
        block = st.opened
        wx, wdt, bias = st.sb("wx", [P, DC, P + 2 * STATES]), st.sb("wdt", [P, D]), st.sb("bias", [P, DC])
        dtT, bcT = st.sb("dtT", [P, TOK]), st.sb("bcT", [2 * STATES, TOK])
        raw, size = st.sb("raw", [P, DC, TOK]), st.sb("size", [P, DC, TOK])
        small, one_more, log = st.sb("small", [P, DC, TOK]), st.sb("one_more", [P, DC, TOK]), st.sb("log", [P, DC, TOK])
        ps_dt = [st.psum(f"dt{n}", [P, HALF]) for n in range(2)]
        ps_bc = [st.psum(f"bc{n}", [2 * STATES, HALF]) for n in range(2)]
        ps_raw = [st.psum(f"raw{n}", [P, HALF]) for n in range(4)]
        in_, projected, kept, bc_kept = st.sem("in"), st.sem("projected"), st.sem("kept"), st.sem("bc_kept")
        raw_ready, biased, sized = st.sem("raw_ready"), st.sem("biased"), st.sem("sized")
        small_ready, added, logged = st.sem("small_ready"), st.sem("added"), st.sem("logged")
        step, stored = st.sem("step"), st.sem("stored")

        @block.sync
        def _(sp):
            for to, src in ((wx[:], "L3b_wx"), (wdt[:], "L3b_wdt"), (bias[:], "L3b_bdt")):
                sp.dma_start(to, core.dram[src]).then_inc(in_, 16)
            sp.wait_ge(bc_kept, 2)
            sp.dma_start(bc, bcT[:]).then_inc(stored, 16)
            sp.wait_ge(stored, 16)

        @block.gpsimd
        def _(pool):
            st.clear_old(pool)

        @block.tensor
        def _(pe):
            pe.wait_ge(in_, 48)
            for half in range(2):
                tokens = slice(half * HALF, (half + 1) * HALF)
                for c in range(DC):
                    nc.tensor.matmul(ps_dt[half][:], wx[:, c, 0:P], hT[:, c, tokens],
                                     start=(c == 0), stop=(c == DC - 1))
                for c in range(DC):
                    last = nc.tensor.matmul(ps_bc[half][:], wx[:, c, P:], hT[:, c, tokens],
                                            start=(c == 0), stop=(c == DC - 1))
                last.then_inc(projected, 1)
            for half in range(2):
                pe.wait_ge(kept, half + 1)
                for e in range(DC):
                    nc.tensor.matmul(ps_raw[2 * half + e][:], wdt[:, e * P:(e + 1) * P],
                                     dtT[:, half * HALF:(half + 1) * HALF], start=True, stop=True
                                     ).then_inc(raw_ready, 1)

        @block.scalar
        def _(act):
            for half in range(2):
                tokens = slice(half * HALF, (half + 1) * HALF)
                act.wait_ge(projected, half + 1)
                nc.scalar.copy(dtT[:, tokens], ps_dt[half][:]).then_inc(kept, 1)
                nc.scalar.copy(bcT[:, tokens], ps_bc[half][:]).then_inc(bc_kept, 1)
            act.wait_ge(sized, 1)
            nc.scalar.activation(small[:], size[:], ACT.Exp, scale=-1.0).then_inc(small_ready, 1)
            act.wait_ge(added, 1)
            nc.scalar.activation(log[:], one_more[:], ACT.Ln).then_inc(logged, 1)

        @block.vector
        def _(dve):
            link = linker(dve, step)
            dve.wait_ge(in_, 48)
            for half in range(2):
                for e in range(DC):
                    dve.wait_ge(raw_ready, 2 * half + e + 1)
                    nc.vector.tensor_scalar(raw[:, e, half * HALF:(half + 1) * HALF], ps_raw[2 * half + e][:],
                                            bias[:, e:e + 1], None, ALU.add).then_inc(biased, 1)
            dve.wait_ge(biased, 4)
            nc.vector.scalar_tensor_tensor(size[:], raw[:], -1.0, raw[:], ALU.mult, ALU.max).then_inc(sized, 1)
            dve.wait_ge(small_ready, 1)
            nc.vector.tensor_scalar(one_more[:], small[:], 1.0, None, ALU.add).then_inc(added, 1)
            dve.wait_ge(added, 1)
            link(nc.vector.scalar_tensor_tensor(size[:], one_more[:], 1.0, small[:], ALU.subtract, ALU.subtract))
            link(nc.vector.scalar_tensor_tensor(size[:], raw[:], 0.0, size[:], ALU.max, ALU.subtract))
            dve.wait_ge(logged, 1)
            link(nc.vector.tensor_tensor(delta[:], size[:], log[:], ALU.add))
            nc.vector.tensor_tensor(fed[:], delta[:], hT[:], ALU.mult)


def scan_states(core, delta, fed, bc):
    nc, x, hT = core.nc, core.x, core.hT
    PAIRS = STATES // 2
    FREE = 4
    with Stage(core, "scan") as st:
        block = st.opened
        a, skip = st.sb("a", [P, DC, STATES]), st.sb("skip", [P, DC])
        spread_b = [st.sb(f"spread_b{n}", [P, TOK]) for n in range(2)]
        spread_c = [st.sb(f"spread_c{n}", [P, TOK]) for n in range(2)]
        decay = [st.sb(f"decay{n}", [P, TOK]) for n in range(2)]
        feed = [st.sb(f"feed{n}", [P, TOK]) for n in range(2)]
        state = [st.sb(f"state{n}", [P, TOK]) for n in range(2)]
        seen = [st.sb(f"seen{n}", [P, TOK]) for n in range(2)]
        yT = st.sb("yT", [P, DC, TOK])
        ps_y = [st.psum(f"y{n}", [P, HALF]) for n in range(4)]
        ps_rows = [st.psum(f"rows{n}", [P, HALF]) for n in range(4)]
        zeros = st.sb("zeros", [P, HALF], BF16)
        a_in, b_in, c_in = st.sem("a_in"), [st.sem(f"b_in{n}") for n in range(2)], [st.sem(f"c_in{n}") for n in range(2)]
        decays, feeds, scans, seens = st.sem("decays"), st.sem("feeds"), st.sem("scans"), st.sem("seens")
        summed, zeroed, finished, y_ready, turned = (st.sem("summed"), st.sem("zeroed"), st.sem("finished"),
                                                     st.sem("y_ready"), st.sem("turned"))

        @block.sync
        def _(sp):
            sp.dma_start(a[:], core.dram["L3b_A"]).then_inc(a_in, 16)
            sp.dma_start(skip[:], core.dram["L3b_D"]).then_inc(a_in, 16)
            with sp.Fori(0, PAIRS) as k:
                for b in range(2):
                    sp.wait_ge(feeds, k * 4 + (2 * b + 2))
                    sp.dma_start(spread_b[b][:], bc[bass.ds(2 * k + b, 1)].broadcast_to([P, TOK])
                                 ).then_inc(b_in[b], 16)
                    sp.wait_ge(seens, k * 4 + (2 * b + 2))
                    sp.dma_start(spread_c[b][:], bc[bass.ds(2 * k + b + STATES, 1)].broadcast_to([P, TOK])
                                 ).then_inc(c_in[b], 16)

        @block.gpsimd
        def _(pool):
            pool.sem_inc(feeds, FREE)
            nc.gpsimd.memset(zeros[:], 0.0).then_inc(zeroed, 1)
            st.clear_old(pool)
            with pool.Fori(0, PAIRS) as k:
                for u in range(4):
                    b, c = u // 2, u % 2
                    pool.wait_ge(b_in[b], k * 16 + 16)
                    pool.wait_ge(scans, k * 4 + (u + FREE - 1))
                    nc.gpsimd.tensor_tensor(feed[c][:], fed[:, c, :], spread_b[b][:], ALU.mult
                                            ).then_inc(feeds, 1)

        @block.scalar
        def _(act):
            act.wait_ge(a_in, 32)
            with act.Fori(0, PAIRS) as k:
                for u in range(4):
                    b, c = u // 2, u % 2
                    act.wait_ge(scans, k * 4 + (u + FREE - 1))
                    nc.scalar.activation(decay[c][:], delta[:, c, :], ACT.Exp,
                                         scale=a[:, c, bass.ds(2 * k + b, 1)]).then_inc(decays, 1)

        @block.vector
        def _(dve):
            dve.sem_inc(scans, FREE)
            dve.sem_inc(seens, FREE)
            with dve.Fori(0, PAIRS) as k:
                for u in range(4):
                    b, c = u // 2, u % 2
                    dve.wait_ge(decays, k * 4 + (u + 1))
                    dve.wait_ge(feeds, k * 4 + (u + FREE + 1))
                    dve.wait_ge(seens, k * 4 + (u + FREE - 1))
                    nc.vector.tensor_tensor_scan(state[c][:], decay[c][:], feed[c][:], 0.0, ALU.mult, ALU.add
                                                 ).then_inc(scans, 1)
                    dve.wait_ge(scans, k * 4 + (u + FREE + 1))
                    dve.wait_ge(c_in[b], k * 16 + 16)
                    dve.wait_ge(summed, k * 4 + (u + FREE - 1))
                    nc.vector.tensor_tensor(seen[c][:], state[c][:], spread_c[b][:], ALU.mult
                                            ).then_inc(seens, 1)
            dve.wait_ge(finished, 1)
            dve.wait_ge(a_in, 32)
            for c in range(DC):
                for half in range(2):
                    tokens = slice(half * HALF, (half + 1) * HALF)
                    nc.vector.scalar_tensor_tensor(yT[:, c, tokens], hT[:, c, tokens], skip[:, c:c + 1],
                                                   ps_y[2 * c + half][:], ALU.mult, ALU.add
                                                   ).then_inc(y_ready, 1)
            for n in range(4):
                dve.wait_ge(turned, n + 1)
                two = x[:, 2 * n:2 * n + 2, :]
                nc.vector.tensor_tensor(two, two, ps_rows[n][:].rearrange("p (t d) -> p t d", t=2), ALU.add)

        @block.tensor
        def _(pe):
            pe.sem_inc(summed, FREE)
            pe.wait_ge(zeroed, 1)
            for n in range(4):
                nc.tensor.matmul(ps_y[n][:], zeros[:, 0:P], zeros[:], start=True, stop=False)
            with pe.Fori(0, PAIRS) as k:
                for u in range(4):
                    c = u % 2
                    pe.wait_ge(seens, k * 4 + (u + FREE + 1))
                    for half in range(2):
                        last = nc.tensor.matmul(ps_y[2 * c + half][:], core.ident[:],
                                                seen[c][:, half * HALF:(half + 1) * HALF],
                                                start=False, stop=False, skip_group_check=True)
                    last.then_inc(summed, 1)
            for n in range(4):
                last = nc.tensor.matmul(ps_y[n][:], zeros[:, 0:P], zeros[:], start=False, stop=True)
            last.then_inc(finished, 1)
            pe.wait_ge(y_ready, 4)
            for t in range(NT):
                for c in range(DC):
                    last = nc.tensor.transpose(ps_rows[t // 2][:, t % 2 * D + c * P:t % 2 * D + (c + 1) * P],
                                               yT[:, c, t * P:(t + 1) * P], core.ident[:])
                if t % 2:
                    last.then_inc(turned, 1)


CHUNK = 64
KEYS = 16


def linear_attention(core):
    nc = core.nc
    with ExitStack() as layer:
        def sb(name, shape):
            return layer.enter_context(nc.sbuf_tensor(f"la_{name}", shape, F32))

        h = sb("h", [P, NT, D])
        anchored_q, anchored_k = sb("anchored_q", [KEYS, TOK]), sb("anchored_k", [KEYS, TOK])
        decayed_q = sb("decayed_q", [KEYS, TOK])
        kept_k = sb("kept_k", [P, NT, KEYS])
        chunk_decay = sb("chunk_decay", [KEYS, 2 * NT])
        o = sb("o", [P, NT, D])
        normalise(core, [(core.hT, [])], rows=h)
        decayed_keys(core, anchored_q, anchored_k, decayed_q, kept_k, chunk_decay)
        chunks(core, h, anchored_q, anchored_k, decayed_q, kept_k, chunk_decay, o)
        gate_and_project(core, o)


def decayed_keys(core, anchored_q, anchored_k, decayed_q, kept_k, chunk_decay):
    nc, hT = core.nc, core.hT
    with Stage(core, "keys") as st:
        block = st.opened
        w = st.sb("w", [P, DC, 2 * KEYS])
        sums = st.sb("sums", [P, 3, P])
        ends = st.sb("ends", [P, 2])
        q, k = st.sb("q", [P, NT, KEYS]), st.sb("k", [P, NT, KEYS])
        peak, total = st.sb("peak", [P, NT]), st.sb("total", [P, NT])
        g = st.sb("g", [P, NT, KEYS])
        turn_in = [st.sb(f"turn_in{n}", [P, NT, KEYS]) for n in range(3)]
        exps = [st.sb(f"exps{n}", [P, NT, KEYS]) for n in range(4)]
        ps_qk = st.psum("qk", [P, NT, 2 * KEYS])
        ps_sum = [st.psum(f"sum{n}", [P, NT, KEYS]) for n in range(3)]
        ps_end = st.psum("end", [KEYS, 2 * NT])
        ps_turn = [st.psum(f"turn{n}", [KEYS, HALF]) for n in range(3)]
        in_, step, projected, shifted = st.sem("in"), st.sem("step"), st.sem("projected"), st.sem("shifted")
        exped, gates, summed, exps_ready = st.sem("exped"), st.sem("gates"), st.sem("summed"), st.sem("exps_ready")
        ready, turned, kept = st.sem("ready"), st.sem("turned"), st.sem("kept")
        act_step, e_ready = st.sem("act_step"), st.sem("e_ready")

        @block.sync
        def _(sp):
            sp.dma_start(w[:], core.dram["L1a_wqk"]).then_inc(in_, 16)
            sp.dma_start(sums[:], core.dram["chunk_sums"]).then_inc(in_, 16)
            sp.dma_start(ends[:], core.dram["chunk_ends"]).then_inc(in_, 16)

        @block.gpsimd
        def _(pool):
            st.clear_old(pool)

        @block.tensor
        def _(pe):
            pe.wait_ge(in_, 48)
            for t in range(NT):
                for c in range(DC):
                    last = nc.tensor.matmul(ps_qk[:, t, :], hT[:, c, t * P:(t + 1) * P], w[:, c, :],
                                            start=(c == 0), stop=(c == DC - 1))
            last.then_inc(projected, 1)
            pe.wait_ge(gates, 1)
            for n in range(3):
                nc.tensor.matmul(ps_sum[n][:], sums[:, n, :], g[:], start=True, stop=True)
            for t in range(NT):
                last = nc.tensor.matmul(ps_end[:, 2 * t:2 * t + 2], g[:, t, :], ends[:], start=True, stop=True)
            last.then_inc(summed, 1)
            for n in range(6):
                pe.wait_ge(ready, n // 2 + 1)
                if n >= 3:
                    pe.wait_ge(kept, n - 2)
                for i in range(4):
                    last = nc.tensor.transpose(ps_turn[n % 3][:, i * P:(i + 1) * P],
                                               turn_in[n // 2][:, n % 2 * 4 + i, :], core.ident[:])
                last.then_inc(turned, 1)

        @block.scalar
        def _(act):
            link = linker(act, act_step)
            act.wait_ge(projected, 1)
            link(nc.scalar.activation(k[:], ps_qk[:, :, KEYS:], ACT.Sigmoid))
            link(nc.scalar.activation(g[:], k[:], ACT.Exp))
            act.wait_ge(shifted, 1)
            nc.scalar.activation(q[:], q[:], ACT.Exp).then_inc(exped, 1)
            act.wait_ge(e_ready, 1)
            nc.scalar.activation(g[:], g[:], ACT.Ln).then_inc(gates, 1)
            act.wait_ge(summed, 1)
            nc.scalar.activation(exps[0][:], ps_sum[0][:], ACT.Exp, scale=-1.0).then_inc(exps_ready, 1)
            nc.scalar.activation(exps[1][:], ps_sum[0][:], ACT.Exp).then_inc(exps_ready, 1)
            nc.scalar.activation(exps[2][:], ps_sum[1][:], ACT.Exp, scale=-1.0).then_inc(exps_ready, 1)
            nc.scalar.activation(exps[3][:], ps_sum[2][:], ACT.Exp, scale=-1.0).then_inc(exps_ready, 1)
            nc.scalar.activation(chunk_decay[:], ps_end[:], ACT.Exp, scale=-1.0).then_inc(exps_ready, 1)

        @block.vector
        def _(dve):
            link = linker(dve, step)
            dve.wait_ge(act_step, 2)
            nc.vector.tensor_scalar(g[:], g[:], 1.0, None, ALU.add).then_inc(e_ready, 1)
            link(nc.vector.tensor_reduce(peak[:], ps_qk[:, :, 0:KEYS], AX, ALU.max))
            nc.vector.tensor_tensor(q[:], ps_qk[:, :, 0:KEYS], peak[:].unsqueeze(2).broadcast_to([P, NT, KEYS]),
                                    ALU.subtract).then_inc(shifted, 1)
            dve.wait_ge(exped, 1)
            link(nc.vector.tensor_reduce(total[:], q[:], AX, ALU.add))
            link(nc.vector.reciprocal(peak[:], total[:]))
            link(nc.vector.tensor_tensor(q[:], q[:], peak[:].unsqueeze(2).broadcast_to([P, NT, KEYS]), ALU.mult))
            for n, (a, out) in enumerate(((q, turn_in[0]), (k, turn_in[1]), (q, turn_in[2]), (k, kept_k))):
                dve.wait_ge(exps_ready, n + 1)
                nc.vector.tensor_tensor(out[:], a[:], exps[n][:], ALU.mult).then_inc(ready, 1)
            for n in range(6):
                to = (anchored_q, anchored_k, decayed_q)[n // 2]
                dve.wait_ge(turned, n + 1)
                nc.vector.tensor_copy(to[:, n % 2 * HALF:(n % 2 + 1) * HALF], ps_turn[n % 3][:]).then_inc(kept, 1)


def chunks(core, h, anchored_q, anchored_k, decayed_q, kept_k, chunk_decay, o):
    nc = core.nc
    NC = 2 * NT
    with Stage(core, "chunks") as st:
        block = st.opened
        mask = st.sb("mask", [P, CHUNK])
        scores = st.sb("scores", [P, NT, CHUNK])
        states = st.sb("states", [KEYS, NC, D])
        ps_scores = st.psum("scores", [P, NT, CHUNK])
        ps_state = [st.psum(f"state{n}", [KEYS, HALF]) for n in range(4)]
        ps_o = [st.psum(f"o{n}", [P, HALF]) for n in range(2)]
        in_, scored, masked, zeroed = st.sem("in"), st.sem("scored"), st.sem("masked"), st.sem("zeroed")
        added, state_ready, o_ready, o_kept = st.sem("added"), st.sem("state_ready"), st.sem("o_ready"), st.sem("o_kept")

        def place(c):
            return c // 2, slice(c % 2 * CHUNK, (c % 2 + 1) * CHUNK)

        def state_bank(c):
            return ps_state[c // 4 % 2 * 2 + c % 2][:, c // 2 % 2 * D:(c // 2 % 2 + 1) * D]

        @block.sync
        def _(sp):
            sp.dma_start(mask[:], core.dram["chunk_mask"]).then_inc(in_, 16)

        @block.gpsimd
        def _(pool):
            nc.gpsimd.memset(states[:, 0, :], 0.0).then_inc(zeroed, 1)
            st.clear_old(pool)

        @block.tensor
        def _(pe):
            for c in range(NC):
                t, at = place(c)
                tokens = slice(c * CHUNK, (c + 1) * CHUNK)
                last = nc.tensor.matmul(ps_scores[at, t, :], anchored_k[:, tokens], anchored_q[:, tokens],
                                        start=True, stop=True)
            last.then_inc(scored, 1)
            for c in range(NC):
                t, at = place(c)
                if c % 4 == 0 and c >= 8:
                    pe.wait_ge(state_ready, c - 4)
                nc.tensor.matmul(state_bank(c), kept_k[at, t, :], h[at, t, :], start=True, stop=True
                                 ).then_inc(added, 1)
            pe.wait_ge(masked, 1)
            pe.wait_ge(zeroed, 1)
            for c in range(NC):
                t, at = place(c)
                pe.wait_ge(state_ready, max(c, 1))
                if c % 4 == 0 and c >= 8:
                    pe.wait_ge(o_kept, c // 4 - 1)
                to = ps_o[t // 2 % 2][at, t % 2 * D:(t % 2 + 1) * D]
                nc.tensor.matmul(to, scores[at, t, :], h[at, t, :], start=True, stop=False)
                last = nc.tensor.matmul(to, decayed_q[:, c * CHUNK:(c + 1) * CHUNK], states[:, c, :],
                                        start=False, stop=True)
                if c % 4 == 3:
                    last.then_inc(o_ready, 1)

        @block.scalar
        def _(act):
            for n in range(4):
                act.wait_ge(o_ready, n + 1)
                nc.scalar.copy(o[:, 2 * n:2 * n + 2, :], ps_o[n % 2][:].rearrange("p (t d) -> p t d", t=2)
                               ).then_inc(o_kept, 1)

        @block.vector
        def _(dve):
            dve.wait_ge(scored, 1)
            dve.wait_ge(in_, 16)
            nc.vector.tensor_tensor(scores[:], ps_scores[:], mask[:].unsqueeze(1).broadcast_to([P, NT, CHUNK]),
                                    ALU.mult).then_inc(masked, 1)
            dve.wait_ge(zeroed, 1)
            for c in range(NC):
                if c == NC - 1:
                    break
                dve.wait_ge(added, c // 4 * 4 + 4)
                if c:
                    dve.wait_ge(state_ready, c)
                nc.vector.scalar_tensor_tensor(states[:, c + 1, :], states[:, c, :], chunk_decay[:, c:c + 1], state_bank(c),
                                               ALU.mult, ALU.add).then_inc(state_ready, 1)


def gate_and_project(core, o):
    nc, x, hT = core.nc, core.x, core.hT
    with Stage(core, "gate") as st:
        block = st.opened
        w = st.sb("w", [P, 3, DC, D])
        norm_w = st.sb("norm_w", [P, DC])
        oT, rT = st.sb("oT", [P, DC, TOK]), st.sb("rT", [P, DC, TOK])
        squares = st.sb("squares", [P, 2, D])
        square_sum, inverse = st.sb("square_sum", [P, NT]), st.sb("inverse", [P, NT])
        silu, r = st.sb("silu", [P, NT, D]), st.sb("r", [P, NT, D])
        ps_turn = [st.psum(f"turn{n}", [P, HALF]) for n in range(4)]
        ps_go = [st.psum(f"go{n}", [P, HALF]) for n in range(2)]
        ps_y = [st.psum(f"y{n}", [P, HALF]) for n in range(2)]
        in_, turned, kept, gone = st.sem("in"), st.sem("turned"), st.sem("kept"), st.sem("gone")
        squared, root, step, silued = st.sem("squared"), st.sem("root"), st.sem("step"), st.sem("silued")
        gated, r_turned, r_kept, y_ready = st.sem("gated"), st.sem("r_turned"), st.sem("r_kept"), st.sem("y_ready")
        y_added, mean_ready = st.sem("y_added"), st.sem("mean_ready")

        @block.sync
        def _(sp):
            sp.dma_start(w[:], core.dram["L1a_w"]).then_inc(in_, 16)
            sp.dma_start(norm_w[:], core.dram["L1a_norm"]).then_inc(in_, 16)

        @block.gpsimd
        def _(pool):
            st.clear_old(pool)

        @block.tensor
        def _(pe):
            for half in range(2):
                for c in range(DC):
                    for i in range(4):
                        last = nc.tensor.transpose(ps_turn[2 * half + c][:, i * P:(i + 1) * P],
                                                   o[:, 4 * half + i, c * P:(c + 1) * P], core.ident[:])
                    last.then_inc(turned, 1)
            pe.wait_ge(in_, 32)
            for t in range(NT):
                pe.wait_ge(kept, 2 if t < 4 else 4)
                if t % 2 == 0 and t >= 4:
                    pe.wait_ge(silued, t // 2 - 1)
                to = ps_go[t // 2 % 2][:, t % 2 * D:(t % 2 + 1) * D]
                for n, src in enumerate((oT, hT)):
                    for c in range(DC):
                        last = nc.tensor.matmul(to, src[:, c, t * P:(t + 1) * P], w[:, n, c, :],
                                                start=(n == 0 and c == 0), stop=(n == 1 and c == DC - 1))
                if t % 2:
                    last.then_inc(gone, 1)
            for half in range(2):
                for c in range(DC):
                    for i in range(4):
                        pe.wait_ge(gated, (4 * half + i) // 2 + 1)
                        last = nc.tensor.transpose(ps_turn[2 * half + c][:, i * P:(i + 1) * P],
                                                   r[:, 4 * half + i, c * P:(c + 1) * P], core.ident[:])
                    last.then_inc(r_turned, 1)
            for t in range(NT):
                pe.wait_ge(r_kept, 2 if t < 4 else 4)
                if t % 2 == 0 and t >= 4:
                    pe.wait_ge(y_added, t // 2 - 1)
                for c in range(DC):
                    last = nc.tensor.matmul(ps_y[t // 2 % 2][:, t % 2 * D:(t % 2 + 1) * D],
                                            rT[:, c, t * P:(t + 1) * P], w[:, 2, c, :],
                                            start=(c == 0), stop=(c == DC - 1))
                if t % 2:
                    last.then_inc(y_ready, 1)

        @block.scalar
        def _(act):
            for t in range(NT):
                if t >= 2:
                    act.wait_ge(squared, t - 1)
                nc.scalar.activation(squares[:, t % 2, :], o[:, t, :], ACT.Square,
                                     accum_out=square_sum[:, t:t + 1]).then_inc(squared, 1)
            act.wait_ge(mean_ready, 1)
            nc.scalar.activation(square_sum[:], square_sum[:], ACT.Sqrt).then_inc(root, 1)
            for n in range(4):
                act.wait_ge(gone, n + 1)
                nc.scalar.activation(silu[:, 2 * n:2 * n + 2, :], ps_go[n % 2][:].rearrange(
                    "p (t d) -> p t d", t=2), ACT.Silu).then_inc(silued, 1)

        @block.vector
        def _(dve):
            link = linker(dve, step)
            for n in range(4):
                dve.wait_ge(turned, n + 1)
                nc.vector.tensor_copy(oT[:, n % 2, n // 2 * HALF:(n // 2 + 1) * HALF], ps_turn[n][:]
                                      ).then_inc(kept, 1)
            dve.wait_ge(squared, NT)
            nc.vector.tensor_scalar(square_sum[:], square_sum[:], 1.0 / D, 1e-5, ALU.mult, ALU.add
                                    ).then_inc(mean_ready, 1)
            dve.wait_ge(root, 1)
            link(nc.vector.reciprocal(inverse[:], square_sum[:]))
            for t in range(NT):
                dve.wait_ge(silued, t // 2 + 1)
                last = nc.vector.scalar_tensor_tensor(r[:, t, :], o[:, t, :], inverse[:, t:t + 1], silu[:, t, :],
                                                      ALU.mult, ALU.mult)
                if t % 2:
                    last.then_inc(gated, 1)
            dve.wait_ge(in_, 32)
            for n in range(4):
                dve.wait_ge(r_turned, n + 1)
                c = n % 2
                nc.vector.tensor_scalar(rT[:, c, n // 2 * HALF:(n // 2 + 1) * HALF], ps_turn[n][:],
                                        norm_w[:, c:c + 1], None, ALU.mult).then_inc(r_kept, 1)
            for n in range(4):
                dve.wait_ge(y_ready, n + 1)
                two = x[:, 2 * n:2 * n + 2, :]
                nc.vector.tensor_tensor(two, two, ps_y[n % 2][:].rearrange("p (t d) -> p t d", t=2), ALU.add
                                        ).then_inc(y_added, 1)


def build(nc, dram, out, first, last):
    with ExitStack() as whole:
        core = Core(nc, dram, whole)
        load_input(core)
        layers = [
            attention_layer_0a, feed_forward_0, attention_layer_0b, feed_forward_0,
            linear_attention, experts, decay_scan, experts,
            attention_layer_2a, ternary_feed_forward, attention_layer_2b, ternary_feed_forward,
            attention_layer_3a, low_rank_experts, state_space, low_rank_experts,
        ]
        for layer in layers[first:last]:
            layer(core)
        store_output(core, out)


def attention_layer_0a(core):
    normalise(core, [(core.hT, [])])
    attention(core, "L0a", groups=4, heads=4, hd=16, shared_kv=False, causal=True, scale=0.25)


def attention_layer_0b(core):
    normalise(core, [(core.hT, ["L0b_norm", "L0b_split"])], second=("norm", 1e-8), keep=True)
    attention(core, "L0b", groups=2, heads=2, hd=64, shared_kv=True, causal=False, scale=0.125)


def attention_layer_2a(core):
    normalise(core, [(core.hT, [])])
    attention(core, "L2a", groups=16, heads=1, hd=128, shared_kv=False, causal=True, scale=128 ** -0.5)


def attention_layer_2b(core):
    normalise(core, [(core.hT, [])])
    attention(core, "L2b", groups=16, heads=1, hd=128, shared_kv=False, causal=True, scale=128 ** -0.5,
              softcap=50.0)


def attention_layer_3a(core):
    normalise(core, [(core.hT, [])])
    attention(core, "L3a", groups=4, heads=4, hd=16, shared_kv=False, causal=True, scale=0.25,
              bias=True, out_bias="L3a_bo")



def rows_in_chunks(w):
    k, n = w.shape
    return np.ascontiguousarray(w.reshape(k // P, P, n).transpose(1, 0, 2))


def column_pairs(v):
    return np.ascontiguousarray(v.reshape(-1, P).T)


def spread_heads(w, group, heads, hd):
    to = np.zeros((w.shape[0], P), w.dtype)
    for j in range(heads):
        h = group * heads + j
        to[:, j * (P // heads):j * (P // heads) + hd] = w[:, h * hd:(h + 1) * hd]
    return to


def attention_weights(wq, wk, wv, groups, heads, hd, shared_kv):
    out = []
    for g in range(groups):
        q = spread_heads(wq, g, heads, hd)
        if shared_kv:
            k = np.concatenate([wk[:, g * hd:(g + 1) * hd]] * heads, 1)
            v = wv[:, g * hd:(g + 1) * hd]
        else:
            k = spread_heads(wk, g, heads, hd)
            v = wv[:, g * heads * hd:(g + 1) * heads * hd]
        out.append(rows_in_chunks(np.concatenate([q, k, v], 1)))
    return np.stack(out)


def gated_weights(gate, up, down, *more):
    tiles = -(-gate.shape[0] // P)
    parts = []
    for w in (gate, up, down):
        whole = np.zeros((tiles * P, D), w.dtype)
        whole[0:w.shape[0]] = w
        parts.append(whole.reshape(tiles, P, D))
    turned = [w.reshape(tiles, P, DC, P).transpose(0, 3, 2, 1).reshape(tiles, P, D) for w in parts[0:2]]
    return np.concatenate([*turned, parts[2], *more], 2)


def lay_out(a):
    o = {"x": a["L0_attn_a_x"][0]}
    o["L0a_w"] = attention_weights(a["L0_attn_a_Wq"].T, a["L0_attn_a_Wk"].T, a["L0_attn_a_Wv"].T, 4, 4, 16, False)
    o["L0a_wo"] = rows_in_chunks(a["L0_attn_a_Wo"].T)
    o["L0b_w"] = attention_weights(a["L0_attn_b_Wq"].T, a["L0_attn_b_Wk"].T, a["L0_attn_b_Wv"].T, 2, 2, 64, True)
    o["L0b_wo"] = rows_in_chunks(a["L0_attn_b_Wo"].T)
    o["L0b_norm"] = column_pairs(a["L0_attn_b_norm_scale"])
    o["L0b_split"] = column_pairs(a["L0_attn_b_split_scale"])
    o["L2a_w"] = attention_weights(*(a["L2_attn_a_W_" + n].reshape(-1, D).T for n in "QKV"), 16, 1, 128, False)
    o["L2a_wo"] = rows_in_chunks(a["L2_attn_a_W_O"].transpose(0, 2, 1).reshape(-1, D))
    o["L2b_w"] = attention_weights(*(a["L2_attn_b_w" + n].T for n in "qkv"), 16, 1, 128, False)
    o["L2b_wo"] = rows_in_chunks(a["L2_attn_b_wo"].T)
    o["L2b_turns"] = np.stack([np.repeat(a["L2_attn_b_rope_cos"][0:16].T, 2, 0),
                               np.repeat(a["L2_attn_b_rope_sin"][0:16].T, 2, 0),
                               np.repeat(a["L2_attn_b_q_norm_w"][:, None], 16, 1),
                               np.repeat(a["L2_attn_b_k_norm_w"][:, None], 16, 1)], 1)
    o["L3a_w"] = attention_weights(*(a["L3_attn_a_W" + n].transpose(1, 0, 2).reshape(D, -1) for n in "qkv"),
                                   4, 4, 16, False)
    o["L3a_wo"] = rows_in_chunks(a["L3_attn_a_Wo"])
    qk = np.stack([spread_heads(a["L3_attn_a_b" + n].reshape(1, -1), g, 4, 16)[0]
                   for g in range(4) for n in "qk"])
    o["L3a_qk_bias"] = qk.reshape(4, 2, P).transpose(0, 2, 1)
    o["L3a_v_bias"] = a["L3_attn_a_bv"].reshape(1, -1)
    o["L3a_bo"] = a["L3_attn_a_bo"].reshape(1, -1)
    o["L0f_w"] = attention_weights(*(a["L0_ffn_W" + n].T for n in "qkv"), 4, 4, 16, False)
    o["L0f_wo"] = rows_in_chunks(a["L0_ffn_Wo"].T)
    o["L0f_ln1"], o["L0f_ln2"] = column_pairs(a["L0_ffn_ln1_w"]), column_pairs(a["L0_ffn_ln2_w"])
    o["L0f_A"] = rows_in_chunks(a["L0_ffn_A"])
    low = np.zeros((8, P, P), np.float32)
    low[:, 0:16] = a["L0_ffn_B"].reshape(16, 8, P).transpose(1, 0, 2)
    o["L0g_w"] = gated_weights(a["L0_ffn_W_in_base"], a["L0_ffn_W_up_base"], a["L0_ffn_W_down"].T, low)
    scales = np.zeros((6 * P, 2), np.float32)
    scales[0:704, 0], scales[0:704, 1] = a["L2_ffn_gate_s"], a["L2_ffn_up_s"]
    o["L2f_w"] = gated_weights(a["L2_ffn_gate_w"], a["L2_ffn_up_w"], a["L2_ffn_down_w"].T,
                               scales.reshape(6, P, 2))
    o["L2f_down_s"] = a["L2_ffn_down_s"].reshape(1, D)
    gu = a["L1_ffn_gate_up_proj"]
    o["L1f_w"] = gated_weights(gu[:, 0:96].reshape(-1, D), gu[:, 96:].reshape(-1, D),
                               a["L1_ffn_down_proj"].transpose(0, 2, 1).reshape(-1, D))
    o["L1f_router"] = rows_in_chunks(a["L1_ffn_gate_weight"].T)
    o["expert_number"] = np.arange(EXPERTS, dtype=np.float32).reshape(1, -1)
    o["L1b_w"], o["L1b_b"] = rows_in_chunks(a["L1_attn_b_W"].T), column_pairs(a["L1_attn_b_b"])
    routed = a["L3_ffn_A_r"].transpose(1, 0, 2).reshape(D, -1)
    o["L3f_w1"] = rows_in_chunks(np.concatenate([a["L3_ffn_A_s"], routed, a["L3_ffn_W_router"]], 1))
    o["L3f_base"] = rows_in_chunks(a["L3_ffn_W_base"])
    o["L3f_w2"] = np.concatenate([a["L3_ffn_B_s"], a["L3_ffn_B_r"].reshape(-1, D),
                                  a["L3_ffn_b_base"].reshape(1, D)])
    o["L3f_router_bias"] = a["L3_ffn_b_router"].reshape(1, -1)
    o["L3b_wx"], o["L3b_wdt"] = rows_in_chunks(a["L3_attn_b_W_xproj"].T), a["L3_attn_b_W_dt"].T
    o["L3b_bdt"], o["L3b_D"] = column_pairs(a["L3_attn_b_b_dt"]), column_pairs(a["L3_attn_b_D"])
    o["L3b_A"] = rows_in_chunks(a["L3_attn_b_A"])
    o["L1a_wqk"] = rows_in_chunks(np.concatenate([a["L1_attn_a_Wq"], a["L1_attn_a_Wk"]]).T)
    o["L1a_w"] = np.stack([rows_in_chunks(a["L1_attn_a_W" + n].T) for n in ("og", "ig", "o")], 1)
    o["L1a_norm"] = column_pairs(a["L1_attn_a_g_norm_w"])
    frm, to = np.arange(P)[:, None], np.arange(P)[None, :]
    chunk = frm // CHUNK == to // CHUNK
    here, middle = chunk & (frm <= to), chunk & (frm % CHUNK < CHUNK // 2)
    o["chunk_sums"] = np.stack([here.astype(np.float32) - middle, here, chunk & (frm > to)], 1).astype(np.float32)
    o["chunk_ends"] = (np.arange(P)[:, None] // CHUNK == np.arange(2)[None, :]).astype(np.float32)
    o["chunk_mask"] = (frm % CHUNK <= np.arange(CHUNK)[None, :]).astype(np.float32)
    return {n: np.ascontiguousarray(v) for n, v in o.items()}


FIRST, LAST = 0, 16


def kernel(**inputs):
    import concourse.bacc as bacc
    from concourse.bass_utils import run_bass_kernel_spmd

    nc = bacc.Bacc("TRN2", target_bir_lowering=False, num_devices=1)
    arrays = lay_out({n: np.asarray(v) for n, v in inputs.items()})
    dram = {n: nc.dram_tensor(f"in_{n}", v.shape, mybir.dt.from_np(v.dtype), kind="ExternalInput").ap()
            for n, v in arrays.items()}
    out = nc.dram_tensor("out", (TOK, D), F32, kind="ExternalOutput").ap()
    build(nc, dram, out, FIRST, LAST)
    r = run_bass_kernel_spmd(nc, [{f"in_{n}": v for n, v in arrays.items()}], core_ids=[0])
    return r.results[0]["out"].reshape(1, TOK, D)
```

```python
from contextlib import ExitStack

import concourse.bass as bass
import numpy as np
from concourse import mybir

ALU = mybir.AluOpType
ACT = mybir.ActivationFunctionType
AX = mybir.AxisListType.X
F32 = mybir.dt.float32
BF16 = mybir.dt.bfloat16
U32 = mybir.dt.uint32

P = 128
TOK = 1024
D = 256
NT = TOK // P
DC = D // P
HALF = 512
MASKED = -1.0e30


class Core:

    def __init__(self, nc, dram, whole):
        self.nc = nc
        self.dram = dram
        self.old = []
        self.count = 0

        def sb(name, shape, dt=F32):
            return whole.enter_context(nc.sbuf_tensor(name, shape, dt))

        self.x = sb("x", [P, NT, D])
        self.hT = sb("hT", [P, DC, TOK])
        self.ident = sb("ident", [P, P])
        self.ident_bf = sb("ident_bf", [P, P], BF16)
        self.causal = sb("causal", [P, P], BF16)
        self.causal_turned = sb("causal_turned", [P, P], BF16)
        self.causal_f = sb("causal_f", [P, P])
        self.ones = sb("ones", [P, P])


class Stage:

    def __init__(self, core, name):
        self.core, self.nc, self.name = core, core.nc, f"{name}{core.count}"
        core.count += 1
        self.stack = ExitStack()
        self.sems = []

    def sem(self, name):
        s = self.nc.alloc_semaphore(f"{self.name}_{name}")
        self.sems.append(s)
        return s

    def sb(self, name, shape, dt=F32):
        return self.stack.enter_context(self.nc.sbuf_tensor(f"{self.name}_{name}", shape, dt))

    def psum(self, name, shape, dt=F32):
        return self.stack.enter_context(self.nc.psum_tensor(f"{self.name}_ps_{name}", shape, dt))

    def clear_old(self, pool):
        numbers = sorted(s.num for s in self.core.old)
        while numbers:
            run = [numbers.pop(0)]
            while numbers and numbers[0] == run[-1] + 1:
                run.append(numbers.pop(0))
            pool.sem_clear(range(run[0], run[-1] + 1))

    def __enter__(self):
        self.block = self.nc.Block(no_gpsimd_drain=True)
        self.opened = self.block.__enter__()
        return self

    def __exit__(self, *error):
        out = self.block.__exit__(*error)
        self.stack.close()
        for s in self.core.old:
            self.nc.release_semaphore(s)
        self.core.old = self.sems
        return out


def linker(engine, sem):
    done = [0]

    def link(instruction):
        done[0] += 1
        instruction.then_inc(sem, 1)
        engine.wait_ge(sem, done[0])
    return link


def load_input(core):
    nc, x = core.nc, core.x
    with Stage(core, "load") as st:
        loaded, zeroed, ones_set = st.sem("loaded"), st.sem("zeroed"), st.sem("ones_set")
        block = st.opened

        @block.sync
        def _(sp):
            for c in range(2):
                half = slice(c * NT // 2, (c + 1) * NT // 2)
                sp.dma_start(x[:, half, :], core.dram["x"].rearrange("(t p) d -> p t d", p=P)[:, half, :]
                             ).then_inc(loaded, 16)
            sp.wait_ge(loaded, 32)

        @block.gpsimd
        def _(pool):
            nc.gpsimd.memset(core.ident[:], 0.0).then_inc(zeroed, 1)
            nc.gpsimd.memset(core.ident_bf[:], 0.0).then_inc(zeroed, 1)
            nc.gpsimd.memset(core.causal[:], 0.0).then_inc(zeroed, 1)
            nc.gpsimd.memset(core.causal_f[:], 0.0).then_inc(zeroed, 1)
            nc.gpsimd.memset(core.causal_turned[:], 0.0).then_inc(zeroed, 1)
            nc.gpsimd.memset(core.ones[:], 1.0).then_inc(ones_set, 1)
            pool.wait_ge(zeroed, 5)
            for t in (core.ident, core.ident_bf):
                nc.gpsimd.affine_select(out=t[:], in_=t[:], compare_op=ALU.not_equal, fill=1.0, base=0,
                                        pattern=[[-1, P]], channel_multiplier=1).then_inc(ones_set, 1)
            for t in (core.causal, core.causal_f):
                nc.gpsimd.affine_select(out=t[:], in_=t[:], compare_op=ALU.is_ge, fill=MASKED, base=0,
                                        pattern=[[-1, P]], channel_multiplier=1).then_inc(ones_set, 1)
            nc.gpsimd.affine_select(out=core.causal_turned[:], in_=core.causal_turned[:], compare_op=ALU.is_ge,
                                    fill=MASKED, base=0, pattern=[[1, P]], channel_multiplier=-1
                                    ).then_inc(ones_set, 1)
            pool.wait_ge(ones_set, 6)


def store_output(core, out):
    with Stage(core, "store") as st:
        stored = st.sem("stored")
        block = st.opened

        @block.sync
        def _(sp):
            for c in range(2):
                half = slice(c * NT // 2, (c + 1) * NT // 2)
                sp.dma_start(out.rearrange("(t p) d -> p t d", p=P)[:, half, :], core.x[:, half, :]
                             ).then_inc(stored, 16)
            sp.wait_ge(stored, 32)


def normalise(core, outs, second=None, keep=False, rows=None):
    nc, x = core.nc, core.x
    with Stage(core, "norm") as st:
        block = st.opened
        stats, mv = st.sb("stats", [P, NT, 6]), st.sb("mv", [P, NT, 2])
        spread, inverse = st.sb("spread", [P, NT]), st.sb("inverse", [P, NT])
        h = rows if rows is not None else st.sb("h", [P, NT, D])
        squares, square_sum = st.sb("squares", [P, 2, D]), st.sb("square_sum", [P, NT])
        turned = [st.psum(f"turned{n}", [P, HALF]) for n in range(4)]
        step, variance, root = st.sem("step"), st.sem("variance"), st.sem("root")
        squared = st.sem("squared")
        tile_done, sums, turned_ready = st.sem("tile_done"), st.sem("sums"), st.sem("turned_ready")
        written_act, written_dve = st.sem("written_act"), st.sem("written_dve")
        columns = [(n, c, w) for n, (_, ws) in enumerate(outs) for c, w in enumerate(ws)]
        column_sb = {(n, c): st.sb(f"w{n}_{c}", [P, DC]) for n, c, _ in columns}
        columns_in = st.sem("columns_in")

        @block.sync
        def _(sp):
            for n, c, w in columns:
                sp.dma_start(column_sb[n, c][:], core.dram[w]).then_inc(columns_in, 16)

        @block.gpsimd
        def _(pool):
            st.clear_old(pool)
            if keep:
                for t in range(NT):
                    pool.wait_ge(tile_done, t + 1)
                    nc.gpsimd.tensor_tensor(x[:, t, :], x[:, t, :], h[:, t, :], ALU.add
                                            ).then_inc(sums, 1)

        @block.vector
        def _(dve):
            link = linker(dve, step)
            for t in range(NT):
                nc.vector.bn_stats(stats[:, t, :], x[:, t, :]).then_inc(variance, 1)
            for t in range(NT):
                dve.wait_ge(variance, t + 1)
                nc.vector.bn_aggr(mv[:, t, :], stats[:, t, :]).then_inc(variance, 1)
            dve.wait_ge(variance, 2 * NT)
            nc.vector.tensor_scalar(spread[:], mv[:, :, 1], 1e-5, None, ALU.add).then_inc(variance, 1)
            dve.wait_ge(root, 1)
            link(nc.vector.reciprocal(inverse[:], spread[:]))
            for t in range(NT):
                nc.vector.tensor_scalar(h[:, t, :], x[:, t, :], mv[:, t, 0:1], inverse[:, t:t + 1],
                                        ALU.subtract, ALU.mult).then_inc(tile_done, 1)
            if second:
                kind, eps = second
                dve.wait_ge(squared, NT)
                nc.vector.tensor_scalar(spread[:], square_sum[:], 1.0 / D, eps if kind == "rms" else 0.0,
                                        ALU.mult, ALU.add).then_inc(variance, 1)
                dve.wait_ge(root, 2)
                if kind == "norm":
                    link(nc.vector.tensor_scalar(spread[:], spread[:], eps, None, ALU.add))
                link(nc.vector.reciprocal(inverse[:], spread[:]))
                if keep:
                    dve.wait_ge(sums, NT)
                for t in range(NT):
                    nc.vector.tensor_scalar(h[:, t, :], h[:, t, :], inverse[:, t:t + 1], None,
                                            ALU.mult).then_inc(tile_done, 1)
            for n, (dst, ws) in enumerate(outs):
                if ws:
                    dve.wait_ge(columns_in, 16 * len(columns))
                for half in range(2):
                    for c in range(DC):
                        if half and len(ws) < 2:
                            continue
                        dve.wait_ge(turned_ready, 2 * half + c + 1)
                        src = turned[2 * half + c][:]
                        to = dst[:, c, half * HALF:(half + 1) * HALF]
                        if not ws:
                            nc.vector.tensor_copy(to, src).then_inc(written_dve, 1)
                        elif len(ws) == 1:
                            nc.vector.tensor_scalar(to, src, column_sb[n, 0][:, c:c + 1], None, ALU.mult
                                                    ).then_inc(written_dve, 1)
                        else:
                            nc.vector.tensor_scalar(to, src, column_sb[n, 0][:, c:c + 1],
                                                    column_sb[n, 1][:, c:c + 1], ALU.mult, ALU.mult
                                                    ).then_inc(written_dve, 1)

        @block.scalar
        def _(act):
            act.wait_ge(variance, 2 * NT + 1)
            nc.scalar.activation(spread[:], spread[:], ACT.Sqrt).then_inc(root, 1)
            if second:
                for t in range(NT):
                    act.wait_ge(tile_done, t + 1)
                    if t >= 2:
                        act.wait_ge(squared, t - 1)
                    nc.scalar.activation(squares[:, t % 2, :], h[:, t, :], ACT.Square,
                                         accum_out=square_sum[:, t:t + 1]).then_inc(squared, 1)
                act.wait_ge(variance, 2 * NT + 2)
                nc.scalar.activation(spread[:], spread[:], ACT.Sqrt).then_inc(root, 1)
            for n, (dst, ws) in enumerate(outs):
                if ws:
                    act.wait_ge(columns_in, 16 * len(columns))
                for half in range(2):
                    for c in range(DC):
                        if half == 0 or len(ws) >= 2:
                            continue
                        act.wait_ge(turned_ready, 2 * half + c + 1)
                        src = turned[2 * half + c][:]
                        to = dst[:, c, half * HALF:(half + 1) * HALF]
                        if ws:
                            nc.scalar.mul(to, src, column_sb[n, 0][:, c:c + 1]).then_inc(written_act, 1)
                        else:
                            nc.scalar.copy(to, src).then_inc(written_act, 1)

        @block.tensor
        def _(pe):
            for half in range(2):
                for c in range(DC):
                    for i in range(4):
                        t = 4 * half + i
                        pe.wait_ge(tile_done, (NT if second else 0) + t + 1)
                        last = nc.tensor.transpose(turned[2 * half + c][:, i * P:(i + 1) * P],
                                                   h[:, t, c * P:(c + 1) * P], core.ident[:])
                    last.then_inc(turned_ready, 1)


def attention(core, name, groups, heads, hd, shared_kv, causal, scale, bias=False, out_bias=None,
              into=None, softcap=None):
    nc, x, hT = core.nc, core.x, core.hT
    vw = hd if shared_kv else heads * hd
    gw = heads * hd
    stride = P // heads
    total = groups * gw
    NCH = total // P
    items = [(j, t) for j in range(heads) for t in range(NT)]
    NI = len(items)
    seconds = [sum(1 for _, t in items[:i] if not causal or t >= 4) for i in range(NI + 1)]
    NS = seconds[NI]
    LOADS = 2 if bias else 1
    FREE = 1

    with Stage(core, name) as st:
        block = st.opened
        w = st.sb("w", [P, DC, 2 * P + vw])
        wo = st.sb("wo", [P, NCH, D])
        qT, kT = st.sb("qT", [P, TOK]), st.sb("kT", [P, TOK])
        v = st.sb("v", [P, NT, vw])
        probs = [st.sb(f"probs{n}", [P, TOK]) for n in range(2)]
        probsT = [st.sb(f"probsT{n}", [P, TOK]) for n in range(2)]
        negmax, rowsum, rowinv = st.sb("negmax", [P, NI]), st.sb("rowsum", [P, NI]), st.sb("rowinv", [P, NI])
        rows = st.sb("rows", [P, NT, total])
        if bias:
            qk_bias = st.sb("qk_bias", [P, 2])
            v_bias = st.sb("v_bias", [P, total])
        if out_bias:
            o_bias = st.sb("o_bias", [P, D])
        if softcap:
            q_rows, k_rows = st.sb("q_rows", [P, NT, hd]), st.sb("k_rows", [P, NT, hd])
            squares = probs[0][:].rearrange("p (t c) -> p t c", t=NT)
            norms = st.sb("norms", [P, 2, NT])
            turns, pair = st.sb("turns", [P, 4, groups]), st.sb("pair", [P, 2, groups])
        ps_scores = [st.psum(f"scores{n}", [P, TOK]) for n in range(2)]
        ps_turn = [st.psum(f"turn{n}", [P, HALF]) for n in range(2)]
        ps_out = st.psum("out", [P, HALF])

        w_in, wo_in, projected = st.sem("w_in"), st.sem("wo_in"), st.sem("projected")
        v_kept, k_kept, q_kept = st.sem("v_kept"), st.sem("k_kept"), st.sem("q_kept")
        scored, maxed, exped = st.sem("scored"), st.sem("maxed"), st.sem("exped")
        turned, first_kept, second_kept = st.sem("turned"), st.sem("first_kept"), st.sem("second_kept")
        summed, inverted, scaled = st.sem("summed"), st.sem("inverted"), st.sem("scaled")
        rows_turned, rowsT_kept = st.sem("rows_turned"), st.sem("rowsT_kept")
        out_ready, out_added = st.sem("out_ready"), st.sem("out_added")
        raw_kept, means, rooted, normed = st.sem("raw_kept"), st.sem("means"), st.sem("rooted"), st.sem("normed")
        turned_qk, capped, pair_step = st.sem("turned_qk"), st.sem("capped"), st.sem("pair_step")
        norm_step = st.sem("norm_step")
        peaked, consts_in = st.sem("peaked"), st.sem("consts_in")

        def width(t):
            return (t + 1) * P if causal else TOK

        @block.sync
        def _(sp):
            sp.dma_start(w[:], core.dram[f"{name}_w"][0]).then_inc(w_in, 16)
            if bias:
                sp.dma_start(qk_bias[:], core.dram[f"{name}_qk_bias"][0]).then_inc(w_in, 16)
                sp.dma_start(v_bias[:], core.dram[f"{name}_v_bias"].broadcast_to([P, total])
                             ).then_inc(consts_in, 16)
            if softcap:
                sp.dma_start(turns[:], core.dram[f"{name}_turns"]).then_inc(consts_in, 16)
            sp.dma_start(wo[:], core.dram[f"{name}_wo"]).then_inc(wo_in, 16)
            if out_bias:
                sp.dma_start(o_bias[:], core.dram[out_bias].broadcast_to([P, D])).then_inc(wo_in, 16)
            with sp.Fori(1, groups) as g:
                sp.wait_ge(projected, 3 * g)
                if bias:
                    sp.wait_ge(q_kept, g)
                    sp.wait_ge(k_kept, g)
                sp.dma_start(w[:], core.dram[f"{name}_w"][bass.ds(g, 1)].rearrange("a p c n -> (a p) c n")
                             ).then_inc(w_in, 16)
                if bias:
                    sp.dma_start(qk_bias[:], core.dram[f"{name}_qk_bias"][bass.ds(g, 1)].rearrange(
                        "a p c -> (a p) c")).then_inc(w_in, 16)

        @block.gpsimd
        def _(pool):
            st.clear_old(pool)

        @block.tensor
        def _(pe):
            for s in (scored, turned, summed):
                pe.sem_inc(s, FREE)
            with pe.Fori(0, groups) as g:
                pe.wait_ge(w_in, g * (16 * LOADS) + 16 * LOADS)
                pe.wait_ge(exped, FREE + g * NI)
                for t in range(NT):
                    for c in range(DC):
                        last = nc.tensor.matmul(ps_scores[0][:, t * P:t * P + vw], hT[:, c, t * P:(t + 1) * P],
                                                w[:, c, 2 * P:], start=(c == 0), stop=(c == DC - 1))
                last.then_inc(projected, 1)
                if softcap:
                    for n in (1, 0):
                        if n == 0:
                            pe.wait_ge(v_kept, g + 1)
                        for t in range(NT):
                            for c in range(DC):
                                last = nc.tensor.matmul(ps_scores[n][:, t * P:(t + 1) * P],
                                                        hT[:, c, t * P:(t + 1) * P], w[:, c, n * P:(n + 1) * P],
                                                        start=(c == 0), stop=(c == DC - 1))
                        last.then_inc(projected, 1)
                    for n, rows_in in ((1, k_rows), (0, q_rows)):
                        pe.wait_ge(normed, 2 * g + 2 - n)
                        for t in range(NT):
                            last = nc.tensor.transpose(ps_scores[n][:, t * P:(t + 1) * P], rows_in[:, t, :],
                                                       core.ident[:])
                        last.then_inc(turned_qk, 1)
                else:
                    for half in range(2):
                        for c in range(DC):
                            last = nc.tensor.matmul(ps_scores[1][:, half * HALF:(half + 1) * HALF], w[:, c, P:2 * P],
                                                    hT[:, c, half * HALF:(half + 1) * HALF],
                                                    start=(c == 0), stop=(c == DC - 1))
                    last.then_inc(projected, 1)
                    pe.wait_ge(v_kept, g + 1)
                    for half in range(2):
                        for c in range(DC):
                            last = nc.tensor.matmul(ps_scores[0][:, half * HALF:(half + 1) * HALF], w[:, c, 0:P],
                                                    hT[:, c, half * HALF:(half + 1) * HALF],
                                                    start=(c == 0), stop=(c == DC - 1))
                    last.then_inc(projected, 1)
                pe.wait_ge(q_kept, g + 1)
                pe.wait_ge(k_kept, g + 1)
                for i in range(NI + 2):
                    if i < NI:
                        j, t = items[i]
                        rows_of = slice(j * stride, j * stride + hd)
                        if i >= 2:
                            pe.wait_ge(exped, FREE + g * NI + (i - 1))
                        for a in range(0, width(t), HALF):
                            b = min(a + HALF, width(t))
                            masks = causal and b == width(t) and not softcap
                            last = nc.tensor.matmul(ps_scores[i % 2][:, a:b], qT[rows_of, t * P:(t + 1) * P],
                                                    kT[rows_of, a:b], start=True, stop=not masks)
                        if causal and not softcap:
                            last = nc.tensor.matmul(ps_scores[i % 2][:, t * P:(t + 1) * P], core.ident_bf[:],
                                                    core.causal[:], start=False, stop=True)
                        last.then_inc(scored, 1)
                    if 1 <= i <= NI:
                        n = i - 1
                        j, t = items[n]
                        pe.wait_ge(exped, FREE + g * NI + (n + 1))
                        for c in range(width(t) // P):
                            if c == 0:
                                pe.wait_ge(first_kept, FREE + g * NI + n)
                            if c == 4:
                                pe.wait_ge(second_kept, FREE + g * NS + seconds[n])
                            last = nc.tensor.transpose(ps_turn[c // 4][:, c % 4 * P:(c % 4 + 1) * P],
                                                       probs[n % 2][:, c * P:(c + 1) * P], core.ident[:])
                            if c == 3 and width(t) > HALF:
                                last.then_inc(turned, 1)
                        last.then_inc(turned, 1)
                    if i >= 2:
                        n = i - 2
                        j, t = items[n]
                        pe.wait_ge(first_kept, FREE + g * NI + (n + 1))
                        if seconds[n + 1] > seconds[n]:
                            pe.wait_ge(second_kept, FREE + g * NS + seconds[n + 1])
                        pe.wait_ge(scaled, FREE + g * NI + n)
                        vs = slice(0, hd) if shared_kv else slice(j * hd, (j + 1) * hd)
                        blocks = width(t) // P
                        for c in range(blocks):
                            last = nc.tensor.matmul(ps_out[:, 0:hd],
                                                    probsT[n % 2][:, c * P:(c + 1) * P], v[:, c, vs],
                                                    start=(c == 0), stop=(c == blocks - 1))
                        last.then_inc(summed, 1)

            pe.wait_ge(scaled, FREE + groups * NI)
            pe.wait_ge(wo_in, 32 if out_bias else 16)
            per = min(NCH, 4)
            lots = [(t, a) for t in range(NT) for a in range(0, NCH, per)]
            for n in range(len(lots) + 1):
                if n < len(lots):
                    t, a = lots[n]
                    if n >= 2:
                        pe.wait_ge(rowsT_kept, n - 1)
                    for c in range(per):
                        last = nc.tensor.transpose(ps_turn[n % 2][:, c * P:(c + 1) * P],
                                                   rows[:, t, (a + c) * P:(a + c + 1) * P], core.ident[:])
                    last.then_inc(rows_turned, 1)
                if n >= 1:
                    t, a = lots[n - 1]
                    pe.wait_ge(rowsT_kept, n)
                    if a == 0 and t >= 2:
                        pe.wait_ge(out_added, t - 1)
                    for c in range(per):
                        last = nc.tensor.matmul(ps_scores[t % 2][:, 0:D],
                                                probsT[(n - 1) % 2][:, c * P:(c + 1) * P], wo[:, a + c, :],
                                                start=(a + c == 0), stop=(a + c == NCH - 1))
                    if a + per == NCH:
                        last.then_inc(out_ready, 1)

        @block.scalar
        def _(act):
            for s in (exped, first_kept):
                act.sem_inc(s, FREE)
            with act.Fori(0, groups) as g:
                act.wait_ge(projected, 3 * g + 1)
                act.wait_ge(summed, FREE + g * NI)
                vps = ps_scores[0][:].rearrange("p (t c) -> p t c", t=NT)[:, :, 0:vw]
                nc.scalar.copy(v[:], vps).then_inc(v_kept, 1)
                if softcap:
                    for n, to in ((1, k_rows), (0, q_rows)):
                        act.wait_ge(projected, 3 * g + 3 - n)
                        src = ps_scores[n][:].rearrange("p (t c) -> p t c", t=NT)
                        nc.scalar.copy(to[:], src).then_inc(raw_kept, 1)
                    act.wait_ge(means, g + 1)
                    nc.scalar.activation(norms[:], norms[:], ACT.Sqrt).then_inc(rooted, 1)
                    act.wait_ge(turned_qk, 2 * g + 2)
                    nc.scalar.copy(qT[:], ps_scores[0][:]).then_inc(q_kept, 1)
                else:
                    act.wait_ge(projected, 3 * g + 3)
                if softcap:
                    pass
                elif bias:
                    nc.scalar.activation(qT[:], ps_scores[0][:], ACT.Identity, bias=qk_bias[:, 0:1]
                                         ).then_inc(q_kept, 1)
                else:
                    nc.scalar.copy(qT[:], ps_scores[0][:]).then_inc(q_kept, 1)
                for i in range(NI + 1):
                    if i < NI:
                        j, t = items[i]
                        act.wait_ge(scored if softcap else maxed, g * NI + (i + 1) + (FREE if softcap else 0))
                        turns = (i - 2) + 1 + seconds[i - 1] if i >= 2 else 0
                        act.wait_ge(turned, FREE + g * (NI + NS) + turns)
                        if i >= 2:
                            act.wait_ge(inverted, g * NI + (i - 1))
                        if softcap:
                            nc.scalar.activation(probs[i % 2][:, 0:width(t)], ps_scores[i % 2][:, 0:width(t)],
                                                 ACT.Tanh, scale=scale / softcap).then_inc(capped, 1)
                            act.wait_ge(maxed, g * NI + (i + 1))
                            nc.scalar.activation(probs[i % 2][:, 0:width(t)], probs[i % 2][:, 0:width(t)],
                                                 ACT.Exp, scale=softcap, accum_out=rowsum[:, i:i + 1]
                                                 ).then_inc(exped, 1)
                        else:
                          nc.scalar.activation(probs[i % 2][:, 0:width(t)], ps_scores[i % 2][:, 0:width(t)],
                                             ACT.Exp, bias=negmax[:, i:i + 1], scale=scale,
                                             accum_out=rowsum[:, i:i + 1]).then_inc(exped, 1)
                    if i >= 1:
                        n = i - 1
                        j, t = items[n]
                        act.wait_ge(turned, FREE + g * (NI + NS) + (n + 1 + seconds[n]))
                        act.wait_ge(summed, FREE + g * NI + max(n - 1, 0))
                        b = min(width(t), HALF)
                        nc.scalar.copy(probsT[n % 2][:, 0:b], ps_turn[0][:, 0:b]).then_inc(first_kept, 1)

        @block.vector
        def _(dve):
            for s in (second_kept, scaled):
                dve.sem_inc(s, FREE)
            if bias or softcap:
                dve.wait_ge(consts_in, 16)
            if softcap:
                pairs = linker(dve, pair_step)
                for n in range(2):
                    pairs(nc.vector.tensor_tensor(pair[:, n], turns[:, n], turns[:, n], ALU.mult))
                pairs(nc.vector.tensor_tensor(pair[:, 0], pair[:, 0], pair[:, 1], ALU.add))
                for n in range(2):
                    pairs(nc.vector.tensor_tensor(pair[:, 0], pair[:, 0], turns[:, 2 + n], ALU.mult))
            with dve.Fori(0, groups) as g:
                if softcap:
                    for n, rows_in in ((1, k_rows), (0, q_rows)):
                        dve.wait_ge(raw_kept, 2 * g + 2 - n)
                        dve.wait_ge(turned, FREE + g * (NI + NS))
                        steps = 5 * g + (1 - n) * 2
                        nc.vector.tensor_tensor(squares, rows_in[:], rows_in[:], ALU.mult).then_inc(norm_step, 1)
                        dve.wait_ge(norm_step, steps + 1)
                        nc.vector.tensor_reduce(norms[:, n, :], squares, AX, ALU.add).then_inc(norm_step, 1)
                        dve.wait_ge(norm_step, steps + 2)
                    nc.vector.tensor_scalar(norms[:], norms[:], 1.0 / hd, 1e-6, ALU.mult, ALU.add
                                            ).then_inc(means, 1)
                    dve.wait_ge(rooted, g + 1)
                    nc.vector.reciprocal(norms[:], norms[:]).then_inc(norm_step, 1)
                    dve.wait_ge(norm_step, 5 * g + 5)
                    for n, rows_in in ((1, k_rows), (0, q_rows)):
                        nc.vector.tensor_tensor(rows_in[:], rows_in[:], norms[:, n, :].unsqueeze(2).broadcast_to(
                            [P, NT, hd]), ALU.mult).then_inc(normed, 1)
                    dve.wait_ge(turned_qk, 2 * g + 1)
                else:
                    dve.wait_ge(projected, 3 * g + 2)
                dve.wait_ge(scored, FREE + g * NI)
                if softcap:
                    nc.vector.tensor_scalar(kT[:], ps_scores[1][:], pair[:, 0, bass.ds(g, 1)], None, ALU.mult
                                            ).then_inc(k_kept, 1)
                elif bias:
                    nc.vector.tensor_scalar(kT[:], ps_scores[1][:], qk_bias[:, 1:2], None, ALU.add
                                            ).then_inc(k_kept, 1)
                else:
                    nc.vector.tensor_copy(kT[:], ps_scores[1][:]).then_inc(k_kept, 1)
                for i in range(NI + 2):
                    if i < NI:
                        j, t = items[i]
                        if softcap:
                            dve.wait_ge(capped, g * NI + (i + 1))
                            diagonal = probs[i % 2][:, t * P:(t + 1) * P]
                            nc.vector.tensor_tensor(diagonal, diagonal, core.causal_f[:], ALU.add
                                                    ).then_inc(maxed, 1)
                    if i < NI and not softcap:
                        dve.wait_ge(scored, FREE + g * NI + (i + 1))
                        dve.wait_ge(exped, FREE + g * NI + max(i - 1, 0))
                        nc.vector.tensor_reduce(negmax[:, i:i + 1], ps_scores[i % 2][:, 0:width(t)], AX,
                                                ALU.max, negate=True).then_inc(peaked, 1)
                        dve.wait_ge(peaked, g * NI + (i + 1))
                        nc.vector.tensor_scalar(negmax[:, i:i + 1], negmax[:, i:i + 1], scale, None,
                                                ALU.mult).then_inc(maxed, 1)
                    if 1 <= i <= NI:
                        n = i - 1
                        j, t = items[n]
                        if seconds[n + 1] > seconds[n]:
                            dve.wait_ge(turned, FREE + g * (NI + NS) + (n + 1 + seconds[n + 1]))
                            dve.wait_ge(summed, FREE + g * NI + max(n - 1, 0))
                            nc.vector.tensor_copy(probsT[n % 2][:, HALF:width(t)],
                                                  ps_turn[1][:, 0:width(t) - HALF]).then_inc(second_kept, 1)
                        dve.wait_ge(exped, FREE + g * NI + (n + 1))
                        nc.vector.reciprocal(rowinv[:, n:n + 1], rowsum[:, n:n + 1]).then_inc(inverted, 1)
                    if i >= 2:
                        n = i - 2
                        j, t = items[n]
                        dve.wait_ge(inverted, g * NI + (n + 1))
                        dve.wait_ge(summed, FREE + g * NI + (n + 1))
                        to = rows[:, t, bass.ds(g * gw + j * hd, hd)]
                        src = ps_out[:, 0:hd]
                        if bias:
                            nc.vector.scalar_tensor_tensor(
                                to, src, rowinv[:, n:n + 1], v_bias[:, bass.ds(g * gw + j * hd, hd)],
                                ALU.mult, ALU.add).then_inc(scaled, 1)
                        else:
                            nc.vector.tensor_scalar(to, src, rowinv[:, n:n + 1], None, ALU.mult
                                                    ).then_inc(scaled, 1)
            per = min(NCH, 4)
            lots = [(t, a) for t in range(NT) for a in range(0, NCH, per)]
            if out_bias:
                dve.wait_ge(wo_in, 32)
                for t in range(NT):
                    nc.vector.tensor_tensor(x[:, t, :], x[:, t, :], o_bias[:], ALU.add).then_inc(consts_in, 1)
                dve.wait_ge(consts_in, (16 if bias else 0) + NT)

            def add_out(t):
                src = ps_scores[t % 2][:, 0:D]
                if into is not None:
                    nc.vector.tensor_copy(into[:, t, :], src).then_inc(out_added, 1)
                else:
                    nc.vector.tensor_tensor(x[:, t, :], x[:, t, :], src, ALU.add).then_inc(out_added, 1)

            for n in range(len(lots)):
                t, a = lots[n]
                dve.wait_ge(rows_turned, n + 1)
                nc.vector.tensor_copy(probsT[n % 2][:, 0:per * P], ps_turn[n % 2][:, 0:per * P]
                                      ).then_inc(rowsT_kept, 1)
                if a + per == NCH and t >= 1:
                    dve.wait_ge(out_ready, t)
                    add_out(t - 1)
            dve.wait_ge(out_ready, NT)
            add_out(NT - 1)


HEADS, HD = 16, 16
QUADS = HEADS // 4
TERMS = [(0, 0), (0, 1), (1, 0), (1, 1), (0, 2), (2, 0)]
SPLIT = HD * len(TERMS)
WITH_MAX = SPLIT + 3
UNITS = [(kt, half) for half in range(2) for kt in range(4 * half + 4)]
PIECES = [(j, t, c) for j in range(4) for t in range(NT) for c in range(1 + t // 4)]


def narrow_attention(core, name, bias=False, out_bias=None, into=None):
    nc = core.nc
    with ExitStack() as layer:
        count = core.count

        def sb(part, shape, dt=F32):
            return layer.enter_context(nc.sbuf_tensor(f"{name}{count}_{part}", shape, dt))

        oT = sb("oT", [P, QUADS, TOK])
        with ExitStack() as inner:
            def inner_sb(part, shape, dt=F32):
                return inner.enter_context(nc.sbuf_tensor(f"{name}{count}_{part}", shape, dt))

            qs, ks = inner_sb("qs", [WITH_MAX, HEADS, TOK], BF16), inner_sb("ks", [WITH_MAX, HEADS, TOK], BF16)
            v = inner_sb("v", [P, QUADS, NT, 4, 32])
            project_and_split(core, name, qs, ks, v, bias)
            weigh_values(core, name, qs, ks, v, oT)
        project_heads(core, name, oT, out_bias, into)


def project_and_split(core, name, qs, ks, v, bias):
    nc, hT = core.nc, core.hT
    with Stage(core, f"{name}p") as st:
        block = st.opened
        w = st.sb("w", [P, DC, 3 * D])
        biases = st.sb("biases", [P, 4])
        v_bias = st.sb("v_bias", [P, D])
        whole = [st.sb(f"whole{n}", [P, TOK]) for n in range(4)]
        rest = [st.sb(f"rest{n}", [P, TOK]) for n in range(2)]
        parts = [[st.sb(f"part{n}_{i}", [P, TOK], BF16) for i in range(3)] for n in range(4)]
        ps = [st.psum(f"qk{n}", [P, TOK]) for n in range(2)]
        ps_v = [st.psum(f"v{n}", [P, HALF]) for n in range(4)]
        w_in, projected, v_ready, filled = st.sem("w_in"), st.sem("projected"), st.sem("v_ready"), st.sem("filled")
        wholes, firsts, rests = st.sem("wholes"), st.sem("firsts"), st.sem("rests")
        seconds, thirds, stacked, ones_in = st.sem("seconds"), st.sem("thirds"), st.sem("stacked"), st.sem("ones_in")

        stored = [st.sem(f"stored{n}") for n in range(4)]
        parts_dram = nc.dram_tensor(f"{st.name}_parts", (4, 3, P, TOK), BF16).ap()

        @block.sync
        def _(sp):
            sp.dma_start(w[:], core.dram[f"{name}_wn"]).then_inc(w_in, 16)
            if bias:
                sp.dma_start(biases[:], core.dram[f"{name}_bn"]).then_inc(w_in, 16)
                sp.dma_start(v_bias[:], core.dram[f"{name}_v_bias"].broadcast_to([P, D])).then_inc(w_in, 16)
            for n in range(5):
                if n < 4:
                    sp.wait_ge(thirds, n + 1)
                    sp.wait_ge(firsts, n + 1)
                    for i in range(3):
                        sp.dma_start(parts_dram[n, i], parts[n][i][:]).then_inc(stored[n], 16)
                if n >= 1:
                    m = n - 1
                    to = qs if m % 2 == 0 else ks
                    sp.wait_ge(stored[m], 48)
                    for s, term in enumerate(TERMS):
                        src = parts_dram[m, term[m % 2]].rearrange("(h d) t -> d h t", h=8)
                        sp.dma_start(to[s * HD:(s + 1) * HD, m // 2 * 8:m // 2 * 8 + 8, :], src
                                     ).then_inc(stacked, 16)
            sp.wait_ge(stacked, 16 * 4 * len(TERMS))

        @block.gpsimd
        def _(pool):
            nc.gpsimd.memset(v[:], 0.0).then_inc(filled, 1)
            pool.wait_ge(filled, 1)
            nc.gpsimd.memset(v[:, :, :, :, HD:HD + 1], 1.0).then_inc(filled, 1)
            pool.wait_ge(filled, 2)
            nc.gpsimd.memset(ks[SPLIT:WITH_MAX, :, :], 1.0).then_inc(ones_in, 1)
            st.clear_old(pool)
            pool.wait_ge(ones_in, 1)

        @block.tensor
        def _(pe):
            pe.wait_ge(w_in, 48 if bias else 16)
            for n in range(4):
                if n >= 2:
                    pe.wait_ge(wholes, n - 1)
                col = (n % 2) * D + n // 2 * P
                for half in range(2):
                    for c in range(DC):
                        last = nc.tensor.matmul(ps[n % 2][:, half * HALF:(half + 1) * HALF], w[:, c, col:col + P],
                                                hT[:, c, half * HALF:(half + 1) * HALF],
                                                start=(c == 0), stop=(c == DC - 1))
                last.then_inc(projected, 1)
            for t in range(NT):
                for c in range(DC):
                    last = nc.tensor.matmul(ps_v[t // 2][:, t % 2 * D:(t % 2 + 1) * D],
                                            hT[:, c, t * P:(t + 1) * P], w[:, c, 2 * D:],
                                            start=(c == 0), stop=(c == DC - 1))
                if t % 2:
                    last.then_inc(v_ready, 1)

        @block.scalar
        def _(act):
            for n in range(4):
                act.wait_ge(projected, n + 1)
                if bias:
                    act.wait_ge(w_in, 48)
                    nc.scalar.activation(whole[n][:], ps[n % 2][:], ACT.Identity, bias=biases[:, n:n + 1]
                                         ).then_inc(wholes, 1)
                else:
                    nc.scalar.copy(whole[n][:], ps[n % 2][:]).then_inc(wholes, 1)
                act.wait_ge(wholes, n + 1)
                nc.scalar.copy(parts[n][0][:], whole[n][:]).then_inc(firsts, 1)
            for n in range(0 if bias else 4):
                act.wait_ge(v_ready, n + 1)
                act.wait_ge(filled, 2)
                for t in (2 * n, 2 * n + 1):
                    nc.scalar.copy(v[:, :, t, :, 0:HD],
                                   ps_v[n][:, t % 2 * D:(t % 2 + 1) * D].rearrange("p (q j d) -> p q j d", q=QUADS,
                                                                                   j=4))

        @block.vector
        def _(dve):
            if bias:
                dve.wait_ge(w_in, 48)
            for n in range(4):
                dve.wait_ge(firsts, n + 1)
                nc.vector.tensor_tensor(rest[n % 2][:], whole[n][:], parts[n][0][:], ALU.subtract
                                        ).then_inc(rests, 1)
                dve.wait_ge(rests, n + 1)
                nc.vector.tensor_copy(parts[n][1][:], rest[n % 2][:]).then_inc(seconds, 1)
                dve.wait_ge(seconds, n + 1)
                nc.vector.tensor_tensor(parts[n][2][:], rest[n % 2][:], parts[n][1][:], ALU.subtract
                                        ).then_inc(thirds, 1)
            for n in range(4 if bias else 0):
                dve.wait_ge(v_ready, n + 1)
                dve.wait_ge(filled, 2)
                for t in (2 * n, 2 * n + 1):
                    nc.vector.tensor_tensor(v[:, :, t, :, 0:HD],
                                            ps_v[n][:, t % 2 * D:(t % 2 + 1) * D].rearrange(
                                                "p (q j d) -> p q j d", q=QUADS, j=4),
                                            v_bias[:].rearrange("p (q j d) -> p q j d", q=QUADS, j=4), ALU.add)


def weigh_values(core, name, qs, ks, v, oT):
    nc = core.nc
    NP, NU = len(PIECES), len(UNITS)
    FREE = 2
    SLOTS = 2 * NU
    PER = 3
    PARTS_AT, SPREAD_AT, TURN_AT = 16, 13, 18
    with Stage(core, f"{name}w") as st:
        block = st.opened
        v_now = st.sb("v_now", [P, NT, 4, 32])
        piece_max = st.sb("piece_max", [P, 4, NT, 2])
        low = st.sb("low", [P, 4 * NT])
        left = st.sb("left", [P, 4 * NT])
        max_parts = st.sb("max_parts", [P, 3, 4 * NT], BF16)
        max_rows = st.sb("max_rows", [3 * 4 * NT, P], BF16)
        weights = [st.sb(f"weights{n}", [P, 2, HALF]) for n in range(4)]
        raw = [st.sb(f"raw{n}", [P, HALF]) for n in range(2)]
        inverse = [st.sb(f"inverse{n}", [P, HALF]) for n in range(2)]
        select = st.sb("select", [P, P])
        ps_max = [st.psum(f"max{n}", [P, HALF]) for n in range(2)]
        ps_scores = [st.psum(f"scores{n}", [P, 2, HALF]) for n in range(2)]
        ps_out = [st.psum(f"out{n}", [P, HALF]) for n in range(2)]

        scored, peaked, combined = st.sem("scored"), st.sem("peaked"), st.sem("combined")
        parted, part_step, max_turned = st.sem("parted"), st.sem("part_step"), st.sem("max_turned")
        max_kept, max_in, select_in = st.sem("max_kept"), st.sem("max_in"), st.sem("select_in")
        rescored, exped, added = st.sem("rescored"), st.sem("exped"), st.sem("added")
        out_copied, spread, inverted, normalised = (st.sem("out_copied"), st.sem("spread"), st.sem("inverted"),
                                                    st.sem("normalised"))
        v_in, filled = st.sem("v_in"), st.sem("filled")

        max_stored = st.sem("max_stored")
        max_dram = nc.dram_tensor(f"{st.name}_max", (3 * 4 * NT, P), BF16).ap()

        def first_query(unit):
            kt, half = UNITS[unit]
            return max(kt * P - half * HALF, 0)

        @block.sync
        def _(sp):
            sp.dma_start(select[:], core.dram["select_sum"]).then_inc(select_in, 16)

            def store_max(i):
                sp.wait_ge(max_kept, i + 1)
                sp.dma_start(max_dram, max_rows[:]).then_inc(max_stored, 16)
                sp.wait_ge(max_stored, 16 * i + 16)
                sp.dma_start(qs[SPLIT:WITH_MAX, 4 * i:4 * i + 4, :],
                             max_dram.rearrange("(i h t) q -> i h (t q)", i=3, h=4)).then_inc(max_in, 16)
                sp.wait_ge(max_in, 16 * i + 16)

            for i in range(QUADS):
                store_max(i)
            sp.wait_ge(max_in, 16 * QUADS)

        @block.gpsimd
        def _(pool):
            nc.gpsimd.memset(piece_max[:], 3.0e38).then_inc(filled, 1)
            st.clear_old(pool)
            pool.wait_ge(filled, 1)
            with pool.Fori(0, QUADS) as i:
                pool.wait_ge(added, i * NU + FREE)
                nc.gpsimd.tensor_copy(v_now[:], v[:, bass.ds(i, 1)].rearrange("p a t j d -> p (a t) j d")
                                      ).then_inc(v_in, 1)

        @block.tensor
        def _(pe):
            pe.sem_inc(added, FREE)

            def piece(i, n):
                j, t, c = PIECES[n]
                pe.wait_ge(peaked, i * NP + (n + 1))
                a, b = c * HALF, min((c + 1) * HALF, (t + 1) * P)
                masks = b == (t + 1) * P
                to = ps_max[n % 2]
                last = nc.tensor.matmul(to[:, 0:b - a],
                                        qs[0:SPLIT, bass.ds(4 * i + j, 1), t * P:(t + 1) * P].rearrange(
                                            "p a t -> p (a t)"),
                                        ks[0:SPLIT, bass.ds(4 * i + j, 1), a:b].rearrange("p a t -> p (a t)"),
                                        start=True, stop=not masks)
                if masks:
                    last = nc.tensor.matmul(to[:, b - a - P:b - a], core.ident_bf[:], core.causal[:],
                                            start=False, stop=True)
                last.then_inc(scored, 1)

            def turn_max(i):
                pe.wait_ge(parted, i + 1)
                nc.tensor.transpose(ps_max[0][:].bitcast(BF16)[0:3 * 4 * NT, 0:P],
                                    max_parts[:].rearrange("p i a -> p (i a)"), core.ident_bf[:]
                                    ).then_inc(max_turned, 1)

            def scores(i, s):
                kt, half = UNITS[s // 2]
                at = first_query(s // 2)
                if s == 0:
                    pe.wait_ge(max_in, i * 16 + 16)
                pe.wait_ge(exped, i * SLOTS + (s + 1))
                for e in range(2):
                    h = bass.ds(4 * i + s % 2 * 2 + e, 1)
                    to = ps_scores[s % 2]
                    masks = kt >= 4 * half
                    last = nc.tensor.matmul(to[:, e, at:],
                                            ks[:, h, kt * P:(kt + 1) * P].rearrange("p a t -> p (a t)"),
                                            qs[:, h, half * HALF + at:(half + 1) * HALF].rearrange(
                                                "p a t -> p (a t)"),
                                            start=True, stop=not masks)
                    if masks:
                        last = nc.tensor.matmul(to[:, e, at:at + P], core.ident_bf[:], core.causal_turned[:],
                                                start=False, stop=True)
                last.then_inc(rescored, 1)

            def add_values(i, n):
                kt, half = UNITS[n]
                at = first_query(n)
                pe.wait_ge(exped, i * SLOTS + (FREE + 2 * n + 2))
                if n == 0:
                    pe.wait_ge(v_in, i + 1)
                if kt == 0:
                    pe.wait_ge(inverted, i * 2 + (half + 1))
                for j in range(4):
                    last = nc.tensor.matmul(ps_out[half][32 * j:32 * j + 32, at:], v_now[:, kt, j, :],
                                            weights[(2 * n + j // 2) % 4][:, j % 2, at:],
                                            start=(kt == 0), stop=(kt == 4 * half + 3))
                last.then_inc(added, 1)

            def spread_sum(i, half):
                pe.wait_ge(out_copied, i * 2 + (half + 1))
                nc.tensor.matmul(ps_out[half][:], select[:], raw[half][:], start=True, stop=True
                                 ).then_inc(spread, 1)

            def quad(i, ahead):
                for s in range(SLOTS):
                    if ahead:
                        for n in range(PER * s, min(PER * s + PER, NP)):
                            if n == 0:
                                pe.wait_ge(max_kept, i + 1)
                            piece(i + 1, n)
                    if ahead and s == TURN_AT:
                        turn_max(i + 1)
                    scores(i, s)
                    if s % 2 and s > 1:
                        add_values(i, s // 2 - 1)
                    if s == SPREAD_AT:
                        spread_sum(i, 0)
                add_values(i, NU - 1)
                spread_sum(i, 1)

            pe.wait_ge(select_in, 16)
            for n in range(NP):
                piece(0, n)
            turn_max(0)
            with pe.Fori(0, QUADS - 1) as i:
                quad(i, True)
            quad(QUADS - 1, False)

        @block.scalar
        def _(act):
            act.sem_inc(exped, FREE)

            def weigh(i, s):
                n = s // 2
                at = first_query(n)
                act.wait_ge(rescored, i * SLOTS + (s + 1))
                act.wait_ge(added, i * NU + (n + 1))
                nc.scalar.activation(weights[s % 4][:, :, at:], ps_scores[s % 2][:, :, at:], ACT.Exp,
                                     scale=HD ** -0.5).then_inc(exped, 1)

            def copy_out(i, half):
                act.wait_ge(added, i * NU + (FREE + (NU if half else 4)))
                act.wait_ge(normalised, i * 2 + (half + 1))
                nc.scalar.copy(raw[half][:], ps_out[half][:]).then_inc(out_copied, 1)

            def quad(i):
                for s in range(SLOTS):
                    weigh(i, s)
                    if s == SPREAD_AT - 2:
                        copy_out(i, 0)
                copy_out(i, 1)

            with act.Fori(0, QUADS) as i:
                quad(i)

        @block.vector
        def _(dve):
            for s in (peaked, inverted, normalised):
                dve.sem_inc(s, FREE)

            def find_max(i, n):
                j, t, c = PIECES[n]
                dve.wait_ge(scored, i * NP + (n + 1))
                width = min((t + 1) * P - c * HALF, HALF)
                nc.vector.tensor_reduce(piece_max[:, j, t, c:c + 1], ps_max[n % 2][:, 0:width], AX, ALU.max,
                                        negate=True).then_inc(peaked, 1)

            def part_max(i):
                dve.wait_ge(peaked, i * NP + (NP + FREE))
                nc.vector.tensor_reduce(low[:], piece_max[:].rearrange("p j t c -> p (j t) c"), AX, ALU.min
                                        ).then_inc(part_step, 1)
                dve.wait_ge(part_step, 4 * i + 1)
                nc.vector.tensor_copy(max_parts[:, 0, :], low[:]).then_inc(part_step, 1)
                dve.wait_ge(part_step, 4 * i + 2)
                nc.vector.tensor_tensor(left[:], low[:], max_parts[:, 0, :], ALU.subtract).then_inc(part_step, 1)
                dve.wait_ge(part_step, 4 * i + 3)
                nc.vector.tensor_copy(max_parts[:, 1, :], left[:]).then_inc(part_step, 1)
                dve.wait_ge(part_step, 4 * i + 4)
                nc.vector.tensor_tensor(max_parts[:, 2, :], left[:], max_parts[:, 1, :], ALU.subtract
                                        ).then_inc(parted, 1)

            def keep_max(i, first):
                dve.wait_ge(max_turned, i + 1)
                if not first:
                    dve.wait_ge(max_stored, 16 * i)
                nc.vector.tensor_copy(max_rows[:], ps_max[0][:].bitcast(BF16)[0:3 * 4 * NT, 0:P]
                                      ).then_inc(max_kept, 1)

            def normalise_half(i, half):
                dve.wait_ge(spread, i * 2 + (half + 1))
                nc.vector.reciprocal(inverse[half][:], ps_out[half][:]).then_inc(inverted, 1)
                dve.wait_ge(inverted, i * 2 + (half + 1 + FREE))
                nc.vector.tensor_tensor(oT[:, bass.ds(i, 1), half * HALF:(half + 1) * HALF].rearrange(
                    "p a t -> p (a t)"), raw[half][:], inverse[half][:], ALU.mult).then_inc(normalised, 1)

            def quad(i, ahead):
                for s in range(SLOTS):
                    if ahead:
                        for n in range(PER * s, min(PER * s + PER, NP)):
                            find_max(i + 1, n)
                        if s == PARTS_AT:
                            part_max(i + 1)
                        if s == TURN_AT:
                            keep_max(i + 1, False)
                    if s == SPREAD_AT:
                        normalise_half(i, 0)
                normalise_half(i, 1)

            dve.wait_ge(filled, 1)
            for n in range(NP):
                find_max(0, n)
            part_max(0)
            keep_max(0, True)
            with dve.Fori(0, QUADS - 1) as i:
                quad(i, True)
            quad(QUADS - 1, False)


def project_heads(core, name, oT, out_bias, into):
    nc, x = core.nc, core.x
    with Stage(core, f"{name}o") as st:
        block = st.opened
        wo = st.sb("wo", [P, QUADS, D])
        o_bias = st.sb("o_bias", [P, D])
        ps = [st.psum(f"y{n}", [P, HALF]) for n in range(4)]
        wo_in, ready, biased = st.sem("wo_in"), st.sem("ready"), st.sem("biased")

        @block.sync
        def _(sp):
            sp.dma_start(wo[:], core.dram[f"{name}_won"]).then_inc(wo_in, 16)
            if out_bias:
                sp.dma_start(o_bias[:], core.dram[out_bias].broadcast_to([P, D])).then_inc(wo_in, 16)

        @block.gpsimd
        def _(pool):
            st.clear_old(pool)

        @block.tensor
        def _(pe):
            pe.wait_ge(wo_in, 32 if out_bias else 16)
            for t in range(NT):
                for q in range(QUADS):
                    last = nc.tensor.matmul(ps[t // 2][:, t % 2 * D:(t % 2 + 1) * D], oT[:, q, t * P:(t + 1) * P],
                                            wo[:, q, :], start=(q == 0), stop=(q == QUADS - 1))
                if t % 2:
                    last.then_inc(ready, 1)

        @block.vector
        def _(dve):
            if out_bias:
                dve.wait_ge(wo_in, 32)
                nc.vector.tensor_tensor(x[:], x[:], o_bias[:].unsqueeze(1).broadcast_to([P, NT, D]), ALU.add
                                        ).then_inc(biased, 1)
                dve.wait_ge(biased, 1)
            for n in range(4):
                dve.wait_ge(ready, n + 1)
                src = ps[n][:].rearrange("p (t d) -> p t d", t=2)
                if into is not None:
                    nc.vector.tensor_copy(into[:, 2 * n:2 * n + 2, :], src)
                else:
                    two = x[:, 2 * n:2 * n + 2, :]
                    nc.vector.tensor_tensor(two, two, src, ALU.add)


STEPS = ("s0 s1 q0 s2 q1 o0 s3 k0 o1 s4 k1 o2 s5 m0 o3 s6 v0 s7 v1 s8 b0 s9 b1 s10 o4 s11 o5 o6 o7").split()
MAKES = [s for s in STEPS if s[0] in "qkvmb"]


def capped_attention(core, name, heads, softcap):
    nc, x, hT = core.nc, core.x, core.hT
    scale = P ** -0.5 / softcap
    NU = len(UNITS)
    with ExitStack() as layer:
        rows = layer.enter_context(nc.sbuf_tensor(f"{name}_rows", [P, NT, heads * P], F32))
        wo = layer.enter_context(nc.sbuf_tensor(f"{name}_wo", [P, heads, D], F32))
        with Stage(core, name) as st:
            block = st.opened
            w = [st.sb(f"w{n}", [P, DC, 3 * P]) for n in range(2)]
            q, k = [st.sb(f"q{n}", [P, TOK]) for n in range(2)], [st.sb(f"k{n}", [P, TOK]) for n in range(2)]
            v = [st.sb(f"v{n}", [P, NT, P + 1]) for n in range(2)]
            squares = st.sb("squares", [P, 2, TOK])
            means = st.sb("means", [P, 2, NT])
            power = st.sb("power", [P, 2, NT])
            inverse = [st.sb(f"inverse{n}", [P, 2, NT]) for n in range(2)]
            tanhs = [st.sb(f"tanh{n}", [P, HALF]) for n in range(3)]
            weights = [st.sb(f"weights{u}", [P, HALF]) for u in range(NU)]
            sum_inverse = st.sb("sum_inverse", [P, NT])
            keep = st.sb("keep", [P, P])
            turns, pair = st.sb("turns", [P, 4, heads]), st.sb("pair", [P, 2, heads])
            ps_make = [st.psum(f"make{n}", [P, HALF]) for n in range(2)]
            ps_scores = [st.psum(f"scores{n}", [P, HALF]) for n in range(3)]
            ps_out = [st.psum(f"out{n}", [P, HALF]) for n in range(2)]
            ps_sums = st.psum("sums", [P, HALF])

            w_in = [st.sem("w_in_even"), st.sem("w_in_odd")]
            wo_in, turns_in = st.sem("wo_in"), st.sem("turns_in")
            made, kept, filled = st.sem("made"), st.sem("kept"), st.sem("filled")
            squares_summed, meaned, inverted = st.sem("squares_summed"), st.sem("meaned"), st.sem("inverted")
            scored, capped, exped, masked = st.sem("scored"), st.sem("capped"), st.sem("exped"), st.sem("masked")
            summed, sum_inverted, scaled = st.sem("summed"), st.sem("sum_inverted"), st.sem("scaled")
            pair_step, squared = st.sem("pair_step"), st.sem("squared")

            TWO, THREE, TILES = 2, 3, NT
            made_order = [s for s in MAKES if s[0] != "m"]
            NM = len(made_order)

            def span(unit):
                kt, half = UNITS[unit]
                return kt, half, max(kt * P - half * HALF, 0)

            @block.sync
            def _(sp):
                for h in range(heads):
                    if h >= 2:
                        sp.wait_ge(made, (h - 1) * NM - 2)
                    sp.dma_start(w[h % 2][:], core.dram[f"{name}_w"][h]).then_inc(w_in[h % 2], 16)
                    if h == 0:
                        sp.dma_start(turns[:], core.dram[f"{name}_turns"]).then_inc(turns_in, 16)
                sp.dma_start(wo[:], core.dram[f"{name}_wo"]).then_inc(wo_in, 16)
                sp.wait_ge(wo_in, 16)

            @block.gpsimd
            def _(pool):
                nc.gpsimd.memset(keep[:], 1.0).then_inc(filled, 1)
                nc.gpsimd.memset(power[:], -0.5).then_inc(filled, 1)
                for n in range(2):
                    nc.gpsimd.memset(v[n][:, :, P:P + 1], 1.0).then_inc(filled, 1)
                pool.wait_ge(filled, 4)
                nc.gpsimd.affine_select(out=keep[:], in_=keep[:], compare_op=ALU.is_ge, fill=0.0, base=0,
                                        pattern=[[1, P]], channel_multiplier=-1).then_inc(filled, 1)
                st.clear_old(pool)
                pool.wait_ge(filled, 5)

                def invert(h, e):
                    pool.wait_ge(meaned, h + 1)
                    nc.gpsimd.tensor_tensor(inverse[e][:], means[:], power[:], ALU.pow).then_inc(inverted, 1)

                def mask(h, t):
                    u = UNITS.index((t, t // 4))
                    pool.wait_ge(exped, h * NU + (u + 1 + THREE))
                    block_at = span(u)[2]
                    to = weights[u][:, block_at:block_at + P]
                    nc.gpsimd.tensor_tensor(to, to, keep[:], ALU.mult).then_inc(masked, 1)

                def square(h, e, step):
                    n, half = made_order.index(step), int(step[1])
                    part = slice(half * HALF, (half + 1) * HALF)
                    src = (q if step[0] == "q" else k)[e]
                    pool.wait_ge(kept, h * NM + (n + 1 + TWO))
                    nc.gpsimd.tensor_tensor(squares[:, "qk".index(step[0]), part], src[:, part], src[:, part],
                                            ALU.mult).then_inc(squared, 1)

                def head(h, e, more):
                    for step in STEPS:
                        if step[0] == "s":
                            kt, half = UNITS[int(step[1:])]
                            if kt >= 4 * half:
                                mask(h, kt)
                        elif more and step[0] in "qk":
                            square(h + 1, 1 - e, step)
                        elif more and step[0] == "m":
                            invert(h + 1, 1 - e)

                for step in MAKES[0:4]:
                    square(0, 0, step)
                invert(0, 0)
                with pool.Fori(0, heads // 2 - 1) as g:
                    head(2 * g, 0, True)
                    head(2 * g + 1, 1, True)
                head(heads - 2, 0, True)
                head(heads - 1, 1, False)

            @block.tensor
            def _(pe):
                pe.sem_inc(summed, TILES)

                def make(h, e, step):
                    kind, half = step[0], int(step[1])
                    if kind == "m":
                        pe.wait_ge(squared, h * 4 + 4)
                        for n in range(2):
                            for t in range(NT):
                                last = nc.tensor.matmul(ps_sums[:, n * NT + t:n * NT + t + 1],
                                                        squares[:, n, t * P:(t + 1) * P], core.ones[:, 0:1],
                                                        start=True, stop=True)
                        last.then_inc(squares_summed, 1)
                        return
                    n = made_order.index(step)
                    pe.wait_ge(kept, h * NM + (n - 2 + 1 + TWO))
                    to = ps_make[n % 2]
                    if step == "q0":
                        pe.wait_ge(w_in[e], h * 8 + (16 - 8 * e))
                    if kind == "b":
                        pe.wait_ge(inverted, h + 1)
                    for c in range(DC if kind in "qk" else 0):
                        at = "qk".index(kind) * P
                        last = nc.tensor.matmul(to[:], w[e][:, c, at:at + P], hT[:, c, half * HALF:(half + 1) * HALF],
                                                start=(c == 0), stop=(c == DC - 1))
                    for i in range(4 if kind in "vb" else 0):
                        t = 4 * half + i
                        part = to[:, i * P:(i + 1) * P]
                        if kind == "b":
                            last = nc.tensor.matmul(part, inverse[e][:, 0, t:t + 1].broadcast_to([P, P]),
                                                    core.ident[:], start=True, stop=True)
                        for c in range(DC if kind == "v" else 0):
                            last = nc.tensor.matmul(part, hT[:, c, t * P:(t + 1) * P], w[e][:, c, 2 * P:],
                                                    start=(c == 0), stop=(c == DC - 1))
                    last.then_inc(made, 1)

                def score(h, e, u):
                    kt, half, at = span(u)
                    if u == 0:
                        pe.wait_ge(kept, h * NM + (NM + TWO))
                    pe.wait_ge(capped, h * NU + (u - 3 + 1 + THREE))
                    nc.tensor.matmul(ps_scores[u % 3][:, at:], k[e][:, kt * P:(kt + 1) * P],
                                     q[e][:, half * HALF + at:(half + 1) * HALF], start=True, stop=True
                                     ).then_inc(scored, 1)

                def output(h, e, t):
                    pe.wait_ge(masked, h * NT + (t + 1))
                    pe.wait_ge(scaled, h * NT + (t - 2 + 1 + TWO))
                    at = t % 4 * P
                    for kt in range(t + 1):
                        last = nc.tensor.matmul(ps_out[t % 2][:, 0:P + 1],
                                                weights[UNITS.index((kt, t // 4))][:, at:at + P], v[e][:, kt, :],
                                                start=(kt == 0), stop=(kt == t))
                    last.then_inc(summed, 1)

                def head(h, e, more):
                    for step in STEPS:
                        if step[0] == "s":
                            score(h, e, int(step[1:]))
                        elif step[0] == "o":
                            output(h, e, int(step[1:]))
                        elif more:
                            make(h + 1, 1 - e, step)

                pe.wait_ge(filled, 5)
                for step in MAKES:
                    make(0, 0, step)
                with pe.Fori(0, heads // 2 - 1) as g:
                    head(2 * g, 0, True)
                    head(2 * g + 1, 1, True)
                head(heads - 2, 0, True)
                head(heads - 1, 1, False)

            @block.scalar
            def _(act):
                for s in (capped, exped):
                    act.sem_inc(s, THREE)

                def cap(h, e, u):
                    kt, half, at = span(u)
                    act.wait_ge(scored, h * NU + (u + 1))
                    act.wait_ge(exped, h * NU + (u - 3 + 1 + THREE))
                    nc.scalar.activation(tanhs[u % 3][:, at:], ps_scores[u % 3][:, at:], ACT.Tanh,
                                         scale=inverse[e][:, 1, kt:kt + 1]).then_inc(capped, 1)

                def weigh(h, u):
                    kt, half, at = span(u)
                    act.wait_ge(capped, h * NU + (u + 1 + THREE))
                    act.wait_ge(summed, h * NT + (TILES - 4 if u < 4 else TILES))
                    nc.scalar.activation(weights[u][:, at:], tanhs[u % 3][:, at:], ACT.Exp, scale=softcap
                                         ).then_inc(exped, 1)

                def head(h, e):
                    for u in range(NU + 1):
                        if u < NU:
                            cap(h, e, u)
                        if u >= 1:
                            weigh(h, u - 1)

                with act.Fori(0, heads // 2) as g:
                    head(2 * g, 0)
                    head(2 * g + 1, 1)

            @block.vector
            def _(dve):
                for s in (kept, scaled):
                    dve.sem_inc(s, TWO)
                dve.wait_ge(turns_in, 16)
                pairs = linker(dve, pair_step)
                for n in range(2):
                    pairs(nc.vector.tensor_tensor(pair[:, n], turns[:, n], turns[:, n], ALU.mult))
                pairs(nc.vector.tensor_tensor(pair[:, 0], pair[:, 0], pair[:, 1], ALU.add))
                for n in range(2):
                    pairs(nc.vector.tensor_tensor(pair[:, 0], pair[:, 0], turns[:, 2 + n], ALU.mult))

                def keep_made(h, e, step):
                    kind, half = step[0], int(step[1])
                    if kind == "m":
                        dve.wait_ge(squares_summed, h + 1)
                        for n, factor in ((0, 1.0), (1, scale ** -2)):
                            last = nc.vector.tensor_scalar(means[:, n, :], ps_sums[:, n * NT:(n + 1) * NT],
                                                           factor / P, 1e-6 * factor, ALU.mult, ALU.add)
                        last.then_inc(meaned, 1)
                        return
                    n = made_order.index(step)
                    src = ps_make[n % 2]
                    part = slice(half * HALF, (half + 1) * HALF)
                    dve.wait_ge(made, h * NM + (n + 1))
                    if kind == "q":
                        nc.vector.tensor_copy(q[e][:, part], src[:]).then_inc(kept, 1)
                    elif kind == "k":
                        nc.vector.tensor_copy(k[e][:, part], src[:]).then_inc(kept, 1)
                    elif kind == "v":
                        nc.vector.tensor_copy(v[e][:, 4 * half:4 * half + 4, 0:P],
                                              src[:].rearrange("p (t c) -> p t c", t=4)).then_inc(kept, 1)
                    else:
                        dve.wait_ge(kept, h * NM + (2 + TWO))
                        nc.vector.scalar_tensor_tensor(q[e][:, part], q[e][:, part], pair[:, 0, bass.ds(h, 1)], src[:],
                                                       ALU.mult, ALU.mult).then_inc(kept, 1)

                def scale_output(h, t):
                    dve.wait_ge(summed, h * NT + (t + 1 + TILES))
                    nc.vector.reciprocal(sum_inverse[:, t:t + 1], ps_out[t % 2][:, P:P + 1]).then_inc(sum_inverted, 1)
                    dve.wait_ge(sum_inverted, h * NT + (t + 1))
                    nc.vector.tensor_scalar(rows[:, t, bass.ds(h * P, P)], ps_out[t % 2][:, 0:P],
                                            sum_inverse[:, t:t + 1], None, ALU.mult).then_inc(scaled, 1)

                def head(h, e, more):
                    for step in STEPS:
                        if step[0] == "o":
                            scale_output(h, int(step[1:]))
                        elif step[0] != "s" and more:
                            keep_made(h + 1, 1 - e, step)

                for step in MAKES:
                    keep_made(0, 0, step)
                with dve.Fori(0, heads // 2 - 1) as g:
                    head(2 * g, 0, True)
                    head(2 * g + 1, 1, True)
                head(heads - 2, 0, True)
                head(heads - 1, 1, False)
        project_rows(core, name, rows, wo, heads)


def project_rows(core, name, rows, wo, chunks):
    nc, x = core.nc, core.x
    with Stage(core, f"{name}o") as st:
        block = st.opened
        turned = [st.sb(f"turned{n}", [P, HALF]) for n in range(3)]
        ps_turn = [st.psum(f"turn{n}", [P, HALF]) for n in range(3)]
        ps_y = [st.psum(f"y{n}", [P, HALF]) for n in range(2)]
        rows_turned, ready = st.sem("rows_turned"), st.sem("ready")
        kept = [st.sem("kept_dve"), st.sem("kept_act")]
        added = st.sem("added")
        lots = [(t, a) for t in range(NT) for a in range(0, chunks, 4)]
        NL = len(lots)

        def wait_kept(engine, n):
            engine.wait_ge(kept[n % 2], n // 2 + 1)

        @block.gpsimd
        def _(pool):
            st.clear_old(pool)

        @block.tensor
        def _(pe):
            for n in range(NL + 2):
                if n < NL:
                    t, a = lots[n]
                    if n >= 3:
                        wait_kept(pe, n - 3)
                    for c in range(4):
                        last = nc.tensor.transpose(ps_turn[n % 3][:, c * P:(c + 1) * P],
                                                   rows[:, t, (a + c) * P:(a + c + 1) * P], core.ident[:])
                    last.then_inc(rows_turned, 1)
                if n >= 2:
                    t, a = lots[n - 2]
                    wait_kept(pe, n - 2)
                    if a == 0 and t >= 2:
                        pe.wait_ge(added, t - 1)
                    for c in range(4):
                        last = nc.tensor.matmul(ps_y[t % 2][:, 0:D], turned[(n - 2) % 3][:, c * P:(c + 1) * P],
                                                wo[:, a + c, :], start=(a + c == 0), stop=(a + c == chunks - 1))
                    last.then_inc(ready, 1)

        def copy_lot(engine, copy, n):
            engine.wait_ge(rows_turned, n + 1)
            if n >= 3:
                engine.wait_ge(ready, n - 2)
            copy(turned[n % 3][:], ps_turn[n % 3][:]).then_inc(kept[n % 2], 1)

        @block.scalar
        def _(act):
            for n in range(1, NL, 2):
                copy_lot(act, nc.scalar.copy, n)

        @block.vector
        def _(dve):
            per = chunks // 4
            for n in range(0, NL, 2):
                copy_lot(dve, nc.vector.tensor_copy, n)
                t = n // per - 1
                if n % per == per - 2 and t >= 0:
                    dve.wait_ge(ready, (t + 1) * per)
                    nc.vector.tensor_tensor(x[:, t, :], x[:, t, :], ps_y[t % 2][:, 0:D], ALU.add).then_inc(added, 1)
            dve.wait_ge(ready, NL)
            nc.vector.tensor_tensor(x[:, NT - 1, :], x[:, NT - 1, :], ps_y[(NT - 1) % 2][:, 0:D], ALU.add)


def gated_feed_forward(core, name, tiles, body, source=None, scaled=False, low_rank=None, combine=None,
                       down_scale=None):
    nc, x = core.nc, core.x
    hT = source if source is not None else core.hT
    UNITS = 2 * body
    TURNS = tiles // body
    FREE = 4
    wide = 3 * D + (P if low_rank is not None else 0) + (2 if scaled else 0)
    low0 = 3 * D
    scale0 = low0 + (P if low_rank is not None else 0)

    with Stage(core, name) as st:
        block = st.opened
        w = [st.sb(f"w{n}", [P, wide]) for n in range(2)]
        gate = [st.sb(f"gate{n}", [P, HALF]) for n in range(2)]
        inner = [st.sb(f"inner{n}", [P, HALF]) for n in range(2)]
        zeros = st.sb("zeros", [P, HALF], BF16)
        if combine is not None:
            weight = [st.sb(f"weight{n}", [P, TOK]) for n in range(2)]
        if down_scale:
            down_by = st.sb("down_by", [P, D])
        ps_gate = [st.psum(f"gate{n}", [P, HALF]) for n in range(2)]
        ps_up = [st.psum(f"up{n}", [P, HALF]) for n in range(2)]
        ps_out = [st.psum(f"out{n}", [P, HALF]) for n in range(4)]

        w_in = [st.sem(f"w_in{n}") for n in range(2)]
        weight_in = [st.sem(f"weight_in{n}") for n in range(2)]
        zeroed, consts_in, opened = st.sem("zeroed"), st.sem("consts_in"), st.sem("opened")
        gated_up, silued, weighted = st.sem("gated_up"), st.sem("silued"), st.sem("weighted")
        multiplied, lowered, finished = st.sem("multiplied"), st.sem("lowered"), st.sem("finished")

        @block.sync
        def _(sp):
            if down_scale:
                sp.dma_start(down_by[:], core.dram[down_scale].broadcast_to([P, D])).then_inc(consts_in, 16)
            with sp.Fori(0, TURNS) as k:
                for b in range(body):
                    sp.wait_ge(lowered, k * UNITS + (2 * b + 2))
                    sp.dma_start(w[b % 2][:], core.dram[f"{name}_w"][bass.ds(k * body + b, 1)].rearrange(
                        "a p n -> (a p) n")).then_inc(w_in[b % 2], 16)
                    if combine is not None:
                        row, left, at = b * P, P, 0
                        while left:
                            e, n = row // 96, min(left, 96 - row % 96)
                            src = combine[bass.ds(k * (body * P // 96) + e, 1)].broadcast_to([n, TOK])
                            sp.dma_start(weight[b % 2][at:at + n, :], src).then_inc(weight_in[b % 2], 16)
                            row, left, at = row + n, left - n, at + n

        @block.gpsimd
        def _(pool):
            nc.gpsimd.memset(zeros[:], 0.0).then_inc(zeroed, 1)
            st.clear_old(pool)
            if combine is not None:
                with pool.Fori(0, TURNS) as k:
                    for u in range(UNITS):
                        b, half = u // 2, u % 2
                        pool.wait_ge(silued, k * UNITS + (u + 1))
                        pool.wait_ge(weight_in[b % 2], k * (32 * body // 2) + 32 * (b // 2 + 1))
                        nc.gpsimd.tensor_tensor(gate[u % 2][:], gate[u % 2][:],
                                                weight[b % 2][:, half * HALF:(half + 1) * HALF], ALU.mult
                                                ).then_inc(weighted, 1)

        @block.tensor
        def _(pe):
            pe.sem_inc(lowered, FREE)
            pe.wait_ge(zeroed, 1)
            for n in range(4):
                nc.tensor.matmul(ps_out[n][:], zeros[:, 0:P], zeros[:], start=True, stop=False)

            def gate_and_up(k, u):
                b, half = u // 2, u % 2
                tokens = slice(half * HALF, (half + 1) * HALF)
                pe.wait_ge(w_in[b % 2], k * (16 * body // 2) + 16 * (b // 2 + 1))
                pe.wait_ge(multiplied, k * UNITS + (u + FREE - 1))
                for c in range(DC):
                    nc.tensor.matmul(ps_gate[u % 2][:], w[b % 2][:, c * P:(c + 1) * P], hT[:, c, tokens],
                                     start=(c == 0), stop=(c == DC - 1 and low_rank is None))
                if low_rank is not None:
                    nc.tensor.matmul(ps_gate[u % 2][:], w[b % 2][0:16, low0:low0 + P], low_rank[:, tokens],
                                     start=False, stop=True)
                for c in range(DC):
                    last = nc.tensor.matmul(ps_up[u % 2][:], w[b % 2][:, D + c * P:D + (c + 1) * P],
                                            hT[:, c, tokens], start=(c == 0), stop=(c == DC - 1))
                last.then_inc(gated_up, 1)

            def down(k, u):
                b, half = u // 2, u % 2
                pe.wait_ge(multiplied, k * UNITS + (u + FREE + 1))
                for i in range(4):
                    t = 4 * half + i
                    last = nc.tensor.matmul(ps_out[t // 2][:, t % 2 * D:(t % 2 + 1) * D],
                                            inner[u % 2][:, i * P:(i + 1) * P], w[b % 2][:, 2 * D:3 * D],
                                            start=False, stop=False, skip_group_check=True)
                last.then_inc(lowered, 1)

            with pe.Fori(0, TURNS) as k:
                for u in range(UNITS):
                    gate_and_up(k, u)
                    if u:
                        down(k, u - 1)
                down(k, UNITS - 1)
            for n in range(4):
                last = nc.tensor.matmul(ps_out[n][:], zeros[:, 0:P], zeros[:], start=False, stop=True)
            last.then_inc(finished, 1)

        @block.scalar
        def _(act):
            with act.Fori(0, TURNS) as k:
                for u in range(UNITS):
                    b = u // 2
                    act.wait_ge(gated_up, k * UNITS + (u + 1))
                    act.wait_ge(multiplied, k * UNITS + (u + FREE - 1))
                    by = w[b % 2][:, scale0:scale0 + 1] if scaled else 1.0
                    nc.scalar.activation(gate[u % 2][:], ps_gate[u % 2][:], ACT.Silu, scale=by
                                         ).then_inc(silued, 1)

        @block.vector
        def _(dve):
            dve.sem_inc(multiplied, FREE)
            with dve.Fori(0, TURNS) as k:
                for u in range(UNITS):
                    b = u // 2
                    dve.wait_ge(weighted if combine is not None else silued, k * UNITS + (u + 1))
                    dve.wait_ge(lowered, k * UNITS + (u + FREE - 1))
                    if scaled:
                        nc.vector.scalar_tensor_tensor(inner[u % 2][:], ps_up[u % 2][:],
                                                       w[b % 2][:, scale0 + 1:scale0 + 2], gate[u % 2][:],
                                                       ALU.mult, ALU.mult).then_inc(multiplied, 1)
                    else:
                        nc.vector.tensor_tensor(inner[u % 2][:], ps_up[u % 2][:], gate[u % 2][:], ALU.mult
                                                ).then_inc(multiplied, 1)
            dve.wait_ge(finished, 1)
            if down_scale:
                dve.wait_ge(consts_in, 16)
            for t in range(NT):
                src = ps_out[t // 2][:, t % 2 * D:(t % 2 + 1) * D]
                if down_scale:
                    buffer = inner[t % 2][:, 0:D]
                    nc.vector.tensor_tensor(buffer, src, down_by[:], ALU.mult).then_inc(consts_in, 1)
                    dve.wait_ge(consts_in, 16 + t + 1)
                    src = buffer
                nc.vector.tensor_tensor(x[:, t, :], x[:, t, :], src, ALU.add)


def feed_forward_0(core):
    with ExitStack() as layer:
        count = core.count

        def sb(name, shape):
            return layer.enter_context(core.nc.sbuf_tensor(f"ff{count}_{name}", shape, F32))

        h2T = sb("h2T", [P, DC, TOK])
        attended = sb("attended", [P, NT, D])
        modT = sb("modT", [16, TOK])
        normalise(core, [(core.hT, ["L0f_ln1"]), (h2T, ["L0f_ln2"])], second=("rms", 1e-6), keep=True)
        narrow_attention(core, "L0f", into=attended)
        low_rank_factor(core, attended, h2T, modT)
        gated_feed_forward(core, "L0g", tiles=8, body=2, source=h2T, low_rank=modT)


def low_rank_factor(core, attended, h2T, modT):
    nc = core.nc
    with Stage(core, "factor") as st:
        block = st.opened
        a = st.sb("a", [P, DC, 16])
        attendedT = st.sb("attendedT", [P, DC, TOK])
        factor = st.sb("factor", [16, TOK])
        ps_turn = [st.psum(f"turn{n}", [P, HALF]) for n in range(4)]
        ps_factor = [st.psum(f"factor{n}", [16, HALF]) for n in range(2)]
        ps_low = [st.psum(f"low{n}", [16, HALF]) for n in range(2)]
        a_in, turned, kept = st.sem("a_in"), st.sem("turned"), st.sem("kept")
        factored, tanhed = st.sem("factored"), st.sem("tanhed")

        @block.sync
        def _(sp):
            sp.dma_start(a[:], core.dram["L0f_A"]).then_inc(a_in, 16)

        @block.gpsimd
        def _(pool):
            st.clear_old(pool)

        @block.tensor
        def _(pe):
            for half in range(2):
                for c in range(DC):
                    for i in range(4):
                        last = nc.tensor.transpose(ps_turn[2 * half + c][:, i * P:(i + 1) * P],
                                                   attended[:, 4 * half + i, c * P:(c + 1) * P], core.ident[:])
                    last.then_inc(turned, 1)
            pe.wait_ge(a_in, 16)
            for half in range(2):
                tokens = slice(half * HALF, (half + 1) * HALF)
                for c in range(DC):
                    nc.tensor.matmul(ps_low[half][:], a[:, c, :], h2T[:, c, tokens],
                                     start=(c == 0), stop=(c == DC - 1))
                for c in range(DC):
                    pe.wait_ge(kept, 2 * half + c + 1)
                    last = nc.tensor.matmul(ps_factor[half][:], a[:, c, :], attendedT[:, c, tokens],
                                            start=(c == 0), stop=(c == DC - 1))
                last.then_inc(factored, 1)

        @block.scalar
        def _(act):
            for half in range(2):
                act.wait_ge(factored, half + 1)
                nc.scalar.activation(factor[:, half * HALF:(half + 1) * HALF], ps_factor[half][:], ACT.Tanh
                                     ).then_inc(tanhed, 1)

        @block.vector
        def _(dve):
            for half in range(2):
                for c in range(DC):
                    dve.wait_ge(turned, 2 * half + c + 1)
                    nc.vector.tensor_copy(attendedT[:, c, half * HALF:(half + 1) * HALF],
                                          ps_turn[2 * half + c][:]).then_inc(kept, 1)
            for half in range(2):
                tokens = slice(half * HALF, (half + 1) * HALF)
                dve.wait_ge(tanhed, half + 1)
                nc.vector.scalar_tensor_tensor(modT[:, tokens], factor[:, tokens], 0.1, ps_low[half][:],
                                               ALU.mult, ALU.mult)


def ternary_feed_forward(core):
    normalise(core, [(core.hT, [])])
    gated_feed_forward(core, "L2f", tiles=6, body=2, scaled=True, down_scale="L2f_down_s")


EXPERTS, TOP = 32, 8


def experts(core):
    normalise(core, [(core.hT, [])])
    combine = core.nc.dram_tensor(f"combine{core.count}", (EXPERTS, TOK), F32).ap()
    route(core, combine)
    gated_feed_forward(core, "L1f", tiles=24, body=6, combine=combine)


def route(core, combine):
    nc, hT = core.nc, core.hT
    with Stage(core, "route") as st:
        block = st.opened
        wr = st.sb("wr", [P, DC, EXPERTS])
        number = st.sb("number", [P, EXPERTS])
        logits, p = st.sb("logits", [P, NT, EXPERTS]), st.sb("p", [P, NT, EXPERTS])
        peak, total, inverse = st.sb("peak", [P, NT]), st.sb("total", [P, NT]), st.sb("inverse", [P, NT])
        top, share = st.sb("top", [P, NT, TOP]), st.sb("share", [P, NT, TOP])
        index, index_f = st.sb("index", [P, NT, TOP], U32), st.sb("index_f", [P, NT, TOP])
        chosen = st.sb("chosen", [P, NT, EXPERTS, TOP])
        weights = st.sb("weights", [P, NT, EXPERTS])
        weightsT = st.sb("weightsT", [EXPERTS, TOK])
        ps_logits = st.psum("logits", [P, NT, EXPERTS])
        ps_turn = [st.psum(f"turn{n}", [EXPERTS, HALF]) for n in range(2)]
        step, in_, projected, exped = st.sem("step"), st.sem("in"), st.sem("projected"), st.sem("exped")
        shifted, ready, turned = st.sem("shifted"), st.sem("ready"), st.sem("turned")
        copied, stored = st.sem("copied"), st.sem("stored")
        found = st.sem("found")

        def over_top(a):
            return a[:].unsqueeze(2).broadcast_to([P, NT, TOP])

        def over_experts(a):
            return a[:].unsqueeze(2).broadcast_to([P, NT, EXPERTS])

        @block.sync
        def _(sp):
            sp.dma_start(wr[:], core.dram["L1f_router"]).then_inc(in_, 16)
            sp.dma_start(number[:], core.dram["expert_number"].broadcast_to([P, EXPERTS])).then_inc(in_, 16)
            sp.wait_ge(copied, 2)
            sp.dma_start(combine, weightsT[:]).then_inc(stored, 16)
            sp.wait_ge(stored, 16)

        @block.gpsimd
        def _(pool):
            st.clear_old(pool)

        @block.tensor
        def _(pe):
            pe.wait_ge(in_, 32)
            for t in range(NT):
                for c in range(DC):
                    last = nc.tensor.matmul(ps_logits[:, t, :], hT[:, c, t * P:(t + 1) * P], wr[:, c, :],
                                            start=(c == 0), stop=(c == DC - 1))
            last.then_inc(projected, 1)
            pe.wait_ge(ready, 1)
            for t in range(NT):
                last = nc.tensor.transpose(ps_turn[t // 4][:, t % 4 * P:(t % 4 + 1) * P], weights[:, t, :],
                                           core.ident[:])
                if t % 4 == 3:
                    last.then_inc(turned, 1)

        @block.scalar
        def _(act):
            act.wait_ge(shifted, 1)
            nc.scalar.activation(p[:], logits[:], ACT.Exp).then_inc(exped, 1)

        @block.vector
        def _(dve):
            link = linker(dve, step)
            dve.wait_ge(projected, 1)
            link(nc.vector.tensor_reduce(peak[:], ps_logits[:], AX, ALU.max))
            nc.vector.tensor_tensor(logits[:], ps_logits[:], over_experts(peak), ALU.subtract
                                    ).then_inc(shifted, 1)
            dve.wait_ge(exped, 1)
            link(nc.vector.tensor_reduce(total[:], p[:], AX, ALU.add))
            link(nc.vector.reciprocal(inverse[:], total[:]))
            link(nc.vector.tensor_tensor(p[:], p[:], over_experts(inverse), ALU.mult))
            for t in range(NT):
                nc.vector.max(top[:, t, :], p[:, t, :]).then_inc(found, 1)
            for t in range(NT):
                dve.wait_ge(found, t + 1)
                nc.vector.max_index(index[:, t, :], top[:, t, :], p[:, t, :]).then_inc(found, 1)
            dve.wait_ge(found, 2 * NT)
            link(nc.vector.tensor_copy(index_f[:], index[:]))
            link(nc.vector.tensor_reduce(total[:], top[:], AX, ALU.add))
            link(nc.vector.tensor_scalar(total[:], total[:], 1e-12, None, ALU.max))
            link(nc.vector.reciprocal(inverse[:], total[:]))
            link(nc.vector.tensor_tensor(share[:], top[:], over_top(inverse), ALU.mult))
            for k in range(1, TOP):
                link(nc.vector.tensor_tensor(share[:, :, k], share[:, :, k], share[:, :, k - 1], ALU.add))
            link(nc.vector.tensor_scalar(share[:], share[:], 0.8, None, ALU.is_lt))
            link(nc.vector.tensor_tensor(top[:, :, 1:], top[:, :, 1:], share[:, :, 0:TOP - 1], ALU.mult))
            link(nc.vector.tensor_reduce(total[:], top[:], AX, ALU.add))
            link(nc.vector.tensor_scalar(total[:], total[:], 1e-12, None, ALU.max))
            link(nc.vector.reciprocal(inverse[:], total[:]))
            link(nc.vector.tensor_tensor(top[:], top[:], over_top(inverse), ALU.mult))
            dve.wait_ge(in_, 32)
            for t in range(NT):
                nc.vector.tensor_tensor(chosen[:, t], index_f[:, t].unsqueeze(1).broadcast_to([P, EXPERTS, TOP]),
                                        number[:].unsqueeze(2).broadcast_to([P, EXPERTS, TOP]), ALU.is_equal
                                        ).then_inc(found, 1)
            for t in range(NT):
                dve.wait_ge(found, 2 * NT + t + 1)
                nc.vector.tensor_tensor(chosen[:, t], chosen[:, t],
                                        top[:, t].unsqueeze(1).broadcast_to([P, EXPERTS, TOP]), ALU.mult
                                        ).then_inc(found, 1)
            dve.wait_ge(found, 4 * NT)
            nc.vector.tensor_reduce(weights[:], chosen[:], AX, ALU.add).then_inc(ready, 1)
            for n in range(2):
                dve.wait_ge(turned, n + 1)
                nc.vector.tensor_copy(weightsT[:, n * HALF:(n + 1) * HALF], ps_turn[n][:]).then_inc(copied, 1)


def decay_scan(core):
    normalise(core, [(core.hT, [])])
    nc, x, hT = core.nc, core.x, core.hT
    with Stage(core, "decay") as st:
        block = st.opened
        w, bias = st.sb("w", [P, DC, D]), st.sb("bias", [P, DC])
        lam, fed, s = st.sb("lam", [P, DC, TOK]), st.sb("fed", [P, DC, TOK]), st.sb("s", [P, DC, TOK])
        ps_lam = [st.psum(f"lam{n}", [P, HALF]) for n in range(4)]
        ps_rows = [st.psum(f"rows{n}", [P, HALF]) for n in range(4)]
        w_in, projected, decays, feeds = st.sem("w_in"), st.sem("projected"), st.sem("decays"), st.sem("feeds")
        scanned, turned = st.sem("scanned"), st.sem("turned")

        @block.sync
        def _(sp):
            sp.dma_start(w[:], core.dram["L1b_w"]).then_inc(w_in, 16)
            sp.dma_start(bias[:], core.dram["L1b_b"]).then_inc(w_in, 16)

        @block.gpsimd
        def _(pool):
            st.clear_old(pool)

        @block.tensor
        def _(pe):
            pe.wait_ge(w_in, 32)
            for e in range(DC):
                for half in range(2):
                    for c in range(DC):
                        last = nc.tensor.matmul(ps_lam[2 * e + half][:], w[:, c, e * P:(e + 1) * P],
                                                hT[:, c, half * HALF:(half + 1) * HALF],
                                                start=(c == 0), stop=(c == DC - 1))
                    last.then_inc(projected, 1)
            pe.wait_ge(scanned, 2)
            for t in range(NT):
                for c in range(DC):
                    last = nc.tensor.transpose(ps_rows[t // 2][:, t % 2 * D + c * P:t % 2 * D + (c + 1) * P],
                                               s[:, c, t * P:(t + 1) * P], core.ident[:])
                if t % 2:
                    last.then_inc(turned, 1)

        @block.scalar
        def _(act):
            act.wait_ge(w_in, 32)
            for e in range(DC):
                for half in range(2):
                    act.wait_ge(projected, 2 * e + half + 1)
                    nc.scalar.activation(lam[:, e, half * HALF:(half + 1) * HALF], ps_lam[2 * e + half][:],
                                         ACT.Sigmoid, bias=bias[:, e:e + 1]).then_inc(decays, 1)

        @block.vector
        def _(dve):
            for e in range(DC):
                dve.wait_ge(decays, 2 * e + 2)
                nc.vector.scalar_tensor_tensor(fed[:, e, :], lam[:, e, :], 1.0, hT[:, e, :], ALU.subtract,
                                               ALU.mult).then_inc(feeds, 1)
                dve.wait_ge(feeds, e + 1)
                nc.vector.tensor_tensor_scan(s[:, e, :], lam[:, e, :], fed[:, e, :], 0.0, ALU.mult,
                                             ALU.subtract).then_inc(scanned, 1)
            for n in range(4):
                dve.wait_ge(turned, n + 1)
                two = x[:, 2 * n:2 * n + 2, :]
                nc.vector.tensor_tensor(two, two, ps_rows[n][:].rearrange("p (t d) -> p t d", t=2), ALU.add)


ROUTES, RANK = 6, 16


def low_rank_experts(core):
    normalise(core, [(core.hT, [])])
    nc, x, hT = core.nc, core.x, core.hT
    LOW = RANK * (1 + ROUTES)
    with Stage(core, "low") as st:
        block = st.opened
        w1, base = st.sb("w1", [P, DC, LOW + ROUTES]), st.sb("base", [P, DC, D])
        w2 = st.sb("w2", [LOW + 1, D])
        router_bias, number = st.sb("router_bias", [P, ROUTES]), st.sb("number", [P, ROUTES])
        p, shifted_logits = st.sb("p", [P, NT, 8]), st.sb("shifted_logits", [P, NT, ROUTES])
        peak, total, inverse = st.sb("peak", [P, NT]), st.sb("total", [P, NT]), st.sb("inverse", [P, NT])
        top, index, index_f = st.sb("top", [P, NT, 8]), st.sb("index", [P, NT, 8], U32), st.sb("index_f", [P, NT, 8])
        chosen, weights = st.sb("chosen", [P, NT, ROUTES, 2]), st.sb("weights", [P, NT, ROUTES])
        z, zT = st.sb("z", [P, NT, LOW + 1]), st.sb("zT", [LOW + 1, TOK])
        ps_z = st.psum("z", [P, NT, P])
        ps_turn = [st.psum(f"turn{n}", [LOW + 1, HALF]) for n in range(2)]
        ps_out = [st.psum(f"out{n}", [P, HALF]) for n in range(4)]
        in_, step, projected, shifted = st.sem("in"), st.sem("step"), st.sem("projected"), st.sem("shifted")
        exped, found, weighted = st.sem("exped"), st.sem("found"), st.sem("weighted")
        turned, kept, out_ready, filled = st.sem("turned"), st.sem("kept"), st.sem("out_ready"), st.sem("filled")
        kept_act = st.sem("kept_act")

        @block.sync
        def _(sp):
            for to, src in ((w1[:], "L3f_w1"), (base[:], "L3f_base"), (w2[:], "L3f_w2")):
                sp.dma_start(to, core.dram[src]).then_inc(in_, 16)
            sp.dma_start(router_bias[:], core.dram["L3f_router_bias"].broadcast_to([P, ROUTES])).then_inc(in_, 16)
            sp.dma_start(number[:], core.dram["expert_number"][:, 0:ROUTES].broadcast_to([P, ROUTES])
                         ).then_inc(in_, 16)

        @block.gpsimd
        def _(pool):
            nc.gpsimd.memset(p[:], -1.0).then_inc(filled, 1)
            nc.gpsimd.memset(z[:], 1.0).then_inc(filled, 1)
            st.clear_old(pool)

        @block.tensor
        def _(pe):
            pe.wait_ge(in_, 80)
            for t in range(NT):
                for c in range(DC):
                    last = nc.tensor.matmul(ps_z[:, t, 0:LOW + ROUTES], hT[:, c, t * P:(t + 1) * P], w1[:, c, :],
                                            start=(c == 0), stop=(c == DC - 1))
            last.then_inc(projected, 1)
            pe.wait_ge(weighted, 2)
            for t in range(NT):
                last = nc.tensor.transpose(ps_turn[t // 4][:, t % 4 * P:(t % 4 + 1) * P], z[:, t, :],
                                           core.ident[:])
                if t % 4 == 3:
                    last.then_inc(turned, 1)
            for t in range(NT):
                if t % 4 == 0:
                    pe.wait_ge(kept if t == 0 else kept_act, 1)
                to = ps_out[t // 2][:, t % 2 * D:(t % 2 + 1) * D]
                for c in range(DC):
                    nc.tensor.matmul(to, hT[:, c, t * P:(t + 1) * P], base[:, c, :], start=(c == 0), stop=False)
                last = nc.tensor.matmul(to, zT[:, t * P:(t + 1) * P], w2[:], start=False, stop=True)
                if t % 2:
                    last.then_inc(out_ready, 1)

        @block.scalar
        def _(act):
            act.wait_ge(shifted, 1)
            act.wait_ge(filled, 1)
            nc.scalar.activation(p[:, :, 0:ROUTES], shifted_logits[:], ACT.Exp).then_inc(exped, 1)
            act.wait_ge(turned, 2)
            nc.scalar.copy(zT[:, HALF:], ps_turn[1][:]).then_inc(kept_act, 1)

        @block.vector
        def _(dve):
            link = linker(dve, step)

            def over_routes(a):
                return a[:].unsqueeze(2).broadcast_to([P, NT, ROUTES])

            dve.wait_ge(in_, 80)
            dve.wait_ge(projected, 1)
            link(nc.vector.tensor_tensor(shifted_logits[:], ps_z[:, :, LOW:LOW + ROUTES],
                                         router_bias[:].unsqueeze(1).broadcast_to([P, NT, ROUTES]), ALU.add))
            link(nc.vector.tensor_reduce(peak[:], shifted_logits[:], AX, ALU.max))
            nc.vector.tensor_tensor(shifted_logits[:], shifted_logits[:], over_routes(peak), ALU.subtract
                                    ).then_inc(shifted, 1)
            dve.wait_ge(exped, 1)
            link(nc.vector.tensor_reduce(total[:], p[:, :, 0:ROUTES], AX, ALU.add))
            link(nc.vector.reciprocal(inverse[:], total[:]))
            link(nc.vector.tensor_tensor(p[:, :, 0:ROUTES], p[:, :, 0:ROUTES], over_routes(inverse), ALU.mult))
            for t in range(NT):
                nc.vector.max(top[:, t, :], p[:, t, :]).then_inc(found, 1)
            for t in range(NT):
                dve.wait_ge(found, t + 1)
                nc.vector.max_index(index[:, t, :], top[:, t, :], p[:, t, :]).then_inc(found, 1)
            dve.wait_ge(found, 2 * NT)
            link(nc.vector.tensor_copy(index_f[:], index[:]))
            for k in range(2):
                nc.vector.tensor_tensor(chosen[:, :, :, k],
                                        index_f[:, :, k].unsqueeze(2).broadcast_to([P, NT, ROUTES]),
                                        number[:].unsqueeze(1).broadcast_to([P, NT, ROUTES]), ALU.is_equal
                                        ).then_inc(found, 1)
            for k in range(2):
                dve.wait_ge(found, 2 * NT + k + 1)
                nc.vector.tensor_tensor(chosen[:, :, :, k], chosen[:, :, :, k],
                                        top[:, :, k].unsqueeze(2).broadcast_to([P, NT, ROUTES]), ALU.mult
                                        ).then_inc(found, 1)
            dve.wait_ge(found, 2 * NT + 4)
            link(nc.vector.tensor_tensor(weights[:], chosen[:, :, :, 0], chosen[:, :, :, 1], ALU.add))
            dve.wait_ge(filled, 2)
            nc.vector.tensor_copy(z[:, :, 0:RANK], ps_z[:, :, 0:RANK]).then_inc(weighted, 1)
            nc.vector.tensor_tensor(z[:, :, RANK:LOW].rearrange("p t (e r) -> p t e r", e=ROUTES),
                                    ps_z[:, :, RANK:LOW].rearrange("p t (e r) -> p t e r", e=ROUTES),
                                    weights[:].unsqueeze(3).broadcast_to([P, NT, ROUTES, RANK]), ALU.mult
                                    ).then_inc(weighted, 1)
            dve.wait_ge(turned, 1)
            nc.vector.tensor_copy(zT[:, 0:HALF], ps_turn[0][:]).then_inc(kept, 1)
            for n in range(4):
                dve.wait_ge(out_ready, n + 1)
                two = x[:, 2 * n:2 * n + 2, :]
                nc.vector.tensor_tensor(two, two, ps_out[n][:].rearrange("p (t d) -> p t d", t=2), ALU.add)


STATES = 16


def state_space(core):
    normalise(core, [(core.hT, [])])
    nc, x, hT = core.nc, core.x, core.hT
    with ExitStack() as layer:
        count = core.count

        def sb(name, shape):
            return layer.enter_context(nc.sbuf_tensor(f"ss{count}_{name}", shape, F32))

        delta, fed = sb("delta", [P, DC, TOK]), sb("fed", [P, DC, TOK])
        bc = nc.dram_tensor(f"bc{count}", (2 * STATES, TOK), F32).ap()
        steps_and_feeds(core, delta, fed, bc)
        scan_states(core, delta, fed, bc)


def steps_and_feeds(core, delta, fed, bc):
    nc, hT = core.nc, core.hT
    with Stage(core, "steps") as st:
        block = st.opened
        wx, wdt, bias = st.sb("wx", [P, DC, P + 2 * STATES]), st.sb("wdt", [P, D]), st.sb("bias", [P, DC])
        dtT, bcT = st.sb("dtT", [P, TOK]), st.sb("bcT", [2 * STATES, TOK])
        raw, size = st.sb("raw", [P, DC, TOK]), st.sb("size", [P, DC, TOK])
        small, one_more, log = st.sb("small", [P, DC, TOK]), st.sb("one_more", [P, DC, TOK]), st.sb("log", [P, DC, TOK])
        ps_dt = [st.psum(f"dt{n}", [P, HALF]) for n in range(2)]
        ps_bc = [st.psum(f"bc{n}", [2 * STATES, HALF]) for n in range(2)]
        ps_raw = [st.psum(f"raw{n}", [P, HALF]) for n in range(4)]
        in_, projected, kept, bc_kept = st.sem("in"), st.sem("projected"), st.sem("kept"), st.sem("bc_kept")
        raw_ready, biased, sized = st.sem("raw_ready"), st.sem("biased"), st.sem("sized")
        small_ready, added, logged = st.sem("small_ready"), st.sem("added"), st.sem("logged")
        step, stored = st.sem("step"), st.sem("stored")

        @block.sync
        def _(sp):
            for to, src in ((wx[:], "L3b_wx"), (wdt[:], "L3b_wdt"), (bias[:], "L3b_bdt")):
                sp.dma_start(to, core.dram[src]).then_inc(in_, 16)
            sp.wait_ge(bc_kept, 2)
            sp.dma_start(bc, bcT[:]).then_inc(stored, 16)
            sp.wait_ge(stored, 16)

        @block.gpsimd
        def _(pool):
            st.clear_old(pool)

        @block.tensor
        def _(pe):
            pe.wait_ge(in_, 48)
            for half in range(2):
                tokens = slice(half * HALF, (half + 1) * HALF)
                for c in range(DC):
                    nc.tensor.matmul(ps_dt[half][:], wx[:, c, 0:P], hT[:, c, tokens],
                                     start=(c == 0), stop=(c == DC - 1))
                for c in range(DC):
                    last = nc.tensor.matmul(ps_bc[half][:], wx[:, c, P:], hT[:, c, tokens],
                                            start=(c == 0), stop=(c == DC - 1))
                last.then_inc(projected, 1)
            for half in range(2):
                pe.wait_ge(kept, half + 1)
                for e in range(DC):
                    nc.tensor.matmul(ps_raw[2 * half + e][:], wdt[:, e * P:(e + 1) * P],
                                     dtT[:, half * HALF:(half + 1) * HALF], start=True, stop=True
                                     ).then_inc(raw_ready, 1)

        @block.scalar
        def _(act):
            for half in range(2):
                tokens = slice(half * HALF, (half + 1) * HALF)
                act.wait_ge(projected, half + 1)
                nc.scalar.copy(dtT[:, tokens], ps_dt[half][:]).then_inc(kept, 1)
                nc.scalar.copy(bcT[:, tokens], ps_bc[half][:]).then_inc(bc_kept, 1)
            act.wait_ge(sized, 1)
            nc.scalar.activation(small[:], size[:], ACT.Exp, scale=-1.0).then_inc(small_ready, 1)
            act.wait_ge(added, 1)
            nc.scalar.activation(log[:], one_more[:], ACT.Ln).then_inc(logged, 1)

        @block.vector
        def _(dve):
            link = linker(dve, step)
            dve.wait_ge(in_, 48)
            for half in range(2):
                for e in range(DC):
                    dve.wait_ge(raw_ready, 2 * half + e + 1)
                    nc.vector.tensor_scalar(raw[:, e, half * HALF:(half + 1) * HALF], ps_raw[2 * half + e][:],
                                            bias[:, e:e + 1], None, ALU.add).then_inc(biased, 1)
            dve.wait_ge(biased, 4)
            nc.vector.scalar_tensor_tensor(size[:], raw[:], -1.0, raw[:], ALU.mult, ALU.max).then_inc(sized, 1)
            dve.wait_ge(small_ready, 1)
            nc.vector.tensor_scalar(one_more[:], small[:], 1.0, None, ALU.add).then_inc(added, 1)
            dve.wait_ge(added, 1)
            link(nc.vector.scalar_tensor_tensor(size[:], one_more[:], 1.0, small[:], ALU.subtract, ALU.subtract))
            link(nc.vector.scalar_tensor_tensor(size[:], raw[:], 0.0, size[:], ALU.max, ALU.subtract))
            dve.wait_ge(logged, 1)
            link(nc.vector.tensor_tensor(delta[:], size[:], log[:], ALU.add))
            nc.vector.tensor_tensor(fed[:], delta[:], hT[:], ALU.mult)


def scan_states(core, delta, fed, bc):
    nc, x, hT = core.nc, core.x, core.hT
    PAIRS = STATES // 2
    FREE = 4
    with Stage(core, "scan") as st:
        block = st.opened
        a, skip = st.sb("a", [P, DC, STATES]), st.sb("skip", [P, DC])
        spread_b = [st.sb(f"spread_b{n}", [P, TOK]) for n in range(2)]
        spread_c = [st.sb(f"spread_c{n}", [P, TOK]) for n in range(2)]
        decay = [st.sb(f"decay{n}", [P, TOK]) for n in range(2)]
        feed = [st.sb(f"feed{n}", [P, TOK]) for n in range(2)]
        state = [st.sb(f"state{n}", [P, TOK]) for n in range(2)]
        seen = [st.sb(f"seen{n}", [P, TOK]) for n in range(2)]
        yT = st.sb("yT", [P, DC, TOK])
        ps_y = [st.psum(f"y{n}", [P, HALF]) for n in range(4)]
        ps_rows = [st.psum(f"rows{n}", [P, HALF]) for n in range(4)]
        zeros = st.sb("zeros", [P, HALF], BF16)
        a_in, b_in, c_in = st.sem("a_in"), [st.sem(f"b_in{n}") for n in range(2)], [st.sem(f"c_in{n}") for n in range(2)]
        decays, feeds, scans, seens = st.sem("decays"), st.sem("feeds"), st.sem("scans"), st.sem("seens")
        summed, zeroed, finished, y_ready, turned = (st.sem("summed"), st.sem("zeroed"), st.sem("finished"),
                                                     st.sem("y_ready"), st.sem("turned"))

        @block.sync
        def _(sp):
            sp.dma_start(a[:], core.dram["L3b_A"]).then_inc(a_in, 16)
            sp.dma_start(skip[:], core.dram["L3b_D"]).then_inc(a_in, 16)
            with sp.Fori(0, PAIRS) as k:
                for b in range(2):
                    sp.wait_ge(feeds, k * 4 + (2 * b + 2))
                    sp.dma_start(spread_b[b][:], bc[bass.ds(2 * k + b, 1)].broadcast_to([P, TOK])
                                 ).then_inc(b_in[b], 16)
                    sp.wait_ge(seens, k * 4 + (2 * b + 2))
                    sp.dma_start(spread_c[b][:], bc[bass.ds(2 * k + b + STATES, 1)].broadcast_to([P, TOK])
                                 ).then_inc(c_in[b], 16)

        @block.gpsimd
        def _(pool):
            pool.sem_inc(feeds, FREE)
            nc.gpsimd.memset(zeros[:], 0.0).then_inc(zeroed, 1)
            st.clear_old(pool)
            with pool.Fori(0, PAIRS) as k:
                for u in range(4):
                    b, c = u // 2, u % 2
                    pool.wait_ge(b_in[b], k * 16 + 16)
                    pool.wait_ge(scans, k * 4 + (u + FREE - 1))
                    nc.gpsimd.tensor_tensor(feed[c][:], fed[:, c, :], spread_b[b][:], ALU.mult
                                            ).then_inc(feeds, 1)

        @block.scalar
        def _(act):
            act.wait_ge(a_in, 32)
            with act.Fori(0, PAIRS) as k:
                for u in range(4):
                    b, c = u // 2, u % 2
                    act.wait_ge(scans, k * 4 + (u + FREE - 1))
                    nc.scalar.activation(decay[c][:], delta[:, c, :], ACT.Exp,
                                         scale=a[:, c, bass.ds(2 * k + b, 1)]).then_inc(decays, 1)

        @block.vector
        def _(dve):
            dve.sem_inc(scans, FREE)
            dve.sem_inc(seens, FREE)
            with dve.Fori(0, PAIRS) as k:
                for u in range(4):
                    b, c = u // 2, u % 2
                    dve.wait_ge(decays, k * 4 + (u + 1))
                    dve.wait_ge(feeds, k * 4 + (u + FREE + 1))
                    dve.wait_ge(seens, k * 4 + (u + FREE - 1))
                    nc.vector.tensor_tensor_scan(state[c][:], decay[c][:], feed[c][:], 0.0, ALU.mult, ALU.add
                                                 ).then_inc(scans, 1)
                    dve.wait_ge(scans, k * 4 + (u + FREE + 1))
                    dve.wait_ge(c_in[b], k * 16 + 16)
                    dve.wait_ge(summed, k * 4 + (u + FREE - 1))
                    nc.vector.tensor_tensor(seen[c][:], state[c][:], spread_c[b][:], ALU.mult
                                            ).then_inc(seens, 1)
            dve.wait_ge(finished, 1)
            dve.wait_ge(a_in, 32)
            for c in range(DC):
                for half in range(2):
                    tokens = slice(half * HALF, (half + 1) * HALF)
                    nc.vector.scalar_tensor_tensor(yT[:, c, tokens], hT[:, c, tokens], skip[:, c:c + 1],
                                                   ps_y[2 * c + half][:], ALU.mult, ALU.add
                                                   ).then_inc(y_ready, 1)
            for n in range(4):
                dve.wait_ge(turned, n + 1)
                two = x[:, 2 * n:2 * n + 2, :]
                nc.vector.tensor_tensor(two, two, ps_rows[n][:].rearrange("p (t d) -> p t d", t=2), ALU.add)

        @block.tensor
        def _(pe):
            pe.sem_inc(summed, FREE)
            pe.wait_ge(zeroed, 1)
            for n in range(4):
                nc.tensor.matmul(ps_y[n][:], zeros[:, 0:P], zeros[:], start=True, stop=False)
            with pe.Fori(0, PAIRS) as k:
                for u in range(4):
                    c = u % 2
                    pe.wait_ge(seens, k * 4 + (u + FREE + 1))
                    for half in range(2):
                        last = nc.tensor.matmul(ps_y[2 * c + half][:], core.ident[:],
                                                seen[c][:, half * HALF:(half + 1) * HALF],
                                                start=False, stop=False, skip_group_check=True)
                    last.then_inc(summed, 1)
            for n in range(4):
                last = nc.tensor.matmul(ps_y[n][:], zeros[:, 0:P], zeros[:], start=False, stop=True)
            last.then_inc(finished, 1)
            pe.wait_ge(y_ready, 4)
            for t in range(NT):
                for c in range(DC):
                    last = nc.tensor.transpose(ps_rows[t // 2][:, t % 2 * D + c * P:t % 2 * D + (c + 1) * P],
                                               yT[:, c, t * P:(t + 1) * P], core.ident[:])
                if t % 2:
                    last.then_inc(turned, 1)


CHUNK = 64
KEYS = 16


def linear_attention(core):
    nc = core.nc
    with ExitStack() as layer:
        def sb(name, shape):
            return layer.enter_context(nc.sbuf_tensor(f"la_{name}", shape, F32))

        h = sb("h", [P, NT, D])
        anchored_q, anchored_k = sb("anchored_q", [KEYS, TOK]), sb("anchored_k", [KEYS, TOK])
        decayed_q = sb("decayed_q", [KEYS, TOK])
        kept_k = sb("kept_k", [P, NT, KEYS])
        chunk_decay = sb("chunk_decay", [KEYS, 2 * NT])
        o = sb("o", [P, NT, D])
        normalise(core, [(core.hT, [])], rows=h)
        decayed_keys(core, anchored_q, anchored_k, decayed_q, kept_k, chunk_decay)
        chunks(core, h, anchored_q, anchored_k, decayed_q, kept_k, chunk_decay, o)
        gate_and_project(core, o)


def decayed_keys(core, anchored_q, anchored_k, decayed_q, kept_k, chunk_decay):
    nc, hT = core.nc, core.hT
    with Stage(core, "keys") as st:
        block = st.opened
        w = st.sb("w", [P, DC, 2 * KEYS])
        sums = st.sb("sums", [P, 3, P])
        ends = st.sb("ends", [P, 2])
        q, k = st.sb("q", [P, NT, KEYS]), st.sb("k", [P, NT, KEYS])
        peak, total = st.sb("peak", [P, NT]), st.sb("total", [P, NT])
        g = st.sb("g", [P, NT, KEYS])
        turn_in = [st.sb(f"turn_in{n}", [P, NT, KEYS]) for n in range(3)]
        exps = [st.sb(f"exps{n}", [P, NT, KEYS]) for n in range(4)]
        ps_qk = st.psum("qk", [P, NT, 2 * KEYS])
        ps_sum = [st.psum(f"sum{n}", [P, NT, KEYS]) for n in range(3)]
        ps_end = st.psum("end", [KEYS, 2 * NT])
        ps_turn = [st.psum(f"turn{n}", [KEYS, HALF]) for n in range(3)]
        in_, step, projected, shifted = st.sem("in"), st.sem("step"), st.sem("projected"), st.sem("shifted")
        exped, gates, summed, exps_ready = st.sem("exped"), st.sem("gates"), st.sem("summed"), st.sem("exps_ready")
        ready, turned, kept = st.sem("ready"), st.sem("turned"), st.sem("kept")
        act_step, e_ready = st.sem("act_step"), st.sem("e_ready")

        @block.sync
        def _(sp):
            sp.dma_start(w[:], core.dram["L1a_wqk"]).then_inc(in_, 16)
            sp.dma_start(sums[:], core.dram["chunk_sums"]).then_inc(in_, 16)
            sp.dma_start(ends[:], core.dram["chunk_ends"]).then_inc(in_, 16)

        @block.gpsimd
        def _(pool):
            st.clear_old(pool)

        @block.tensor
        def _(pe):
            pe.wait_ge(in_, 48)
            for t in range(NT):
                for c in range(DC):
                    last = nc.tensor.matmul(ps_qk[:, t, :], hT[:, c, t * P:(t + 1) * P], w[:, c, :],
                                            start=(c == 0), stop=(c == DC - 1))
            last.then_inc(projected, 1)
            pe.wait_ge(gates, 1)
            for n in range(3):
                nc.tensor.matmul(ps_sum[n][:], sums[:, n, :], g[:], start=True, stop=True)
            for t in range(NT):
                last = nc.tensor.matmul(ps_end[:, 2 * t:2 * t + 2], g[:, t, :], ends[:], start=True, stop=True)
            last.then_inc(summed, 1)
            for n in range(6):
                pe.wait_ge(ready, n // 2 + 1)
                if n >= 3:
                    pe.wait_ge(kept, n - 2)
                for i in range(4):
                    last = nc.tensor.transpose(ps_turn[n % 3][:, i * P:(i + 1) * P],
                                               turn_in[n // 2][:, n % 2 * 4 + i, :], core.ident[:])
                last.then_inc(turned, 1)

        @block.scalar
        def _(act):
            link = linker(act, act_step)
            act.wait_ge(projected, 1)
            link(nc.scalar.activation(k[:], ps_qk[:, :, KEYS:], ACT.Sigmoid))
            link(nc.scalar.activation(g[:], k[:], ACT.Exp))
            act.wait_ge(shifted, 1)
            nc.scalar.activation(q[:], q[:], ACT.Exp).then_inc(exped, 1)
            act.wait_ge(e_ready, 1)
            nc.scalar.activation(g[:], g[:], ACT.Ln).then_inc(gates, 1)
            act.wait_ge(summed, 1)
            nc.scalar.activation(exps[0][:], ps_sum[0][:], ACT.Exp, scale=-1.0).then_inc(exps_ready, 1)
            nc.scalar.activation(exps[1][:], ps_sum[0][:], ACT.Exp).then_inc(exps_ready, 1)
            nc.scalar.activation(exps[2][:], ps_sum[1][:], ACT.Exp, scale=-1.0).then_inc(exps_ready, 1)
            nc.scalar.activation(exps[3][:], ps_sum[2][:], ACT.Exp, scale=-1.0).then_inc(exps_ready, 1)
            nc.scalar.activation(chunk_decay[:], ps_end[:], ACT.Exp, scale=-1.0).then_inc(exps_ready, 1)

        @block.vector
        def _(dve):
            link = linker(dve, step)
            dve.wait_ge(act_step, 2)
            nc.vector.tensor_scalar(g[:], g[:], 1.0, None, ALU.add).then_inc(e_ready, 1)
            link(nc.vector.tensor_reduce(peak[:], ps_qk[:, :, 0:KEYS], AX, ALU.max))
            nc.vector.tensor_tensor(q[:], ps_qk[:, :, 0:KEYS], peak[:].unsqueeze(2).broadcast_to([P, NT, KEYS]),
                                    ALU.subtract).then_inc(shifted, 1)
            dve.wait_ge(exped, 1)
            link(nc.vector.tensor_reduce(total[:], q[:], AX, ALU.add))
            link(nc.vector.reciprocal(peak[:], total[:]))
            link(nc.vector.tensor_tensor(q[:], q[:], peak[:].unsqueeze(2).broadcast_to([P, NT, KEYS]), ALU.mult))
            for n, (a, out) in enumerate(((q, turn_in[0]), (k, turn_in[1]), (q, turn_in[2]), (k, kept_k))):
                dve.wait_ge(exps_ready, n + 1)
                nc.vector.tensor_tensor(out[:], a[:], exps[n][:], ALU.mult).then_inc(ready, 1)
            for n in range(6):
                to = (anchored_q, anchored_k, decayed_q)[n // 2]
                dve.wait_ge(turned, n + 1)
                nc.vector.tensor_copy(to[:, n % 2 * HALF:(n % 2 + 1) * HALF], ps_turn[n % 3][:]).then_inc(kept, 1)


def chunks(core, h, anchored_q, anchored_k, decayed_q, kept_k, chunk_decay, o):
    nc = core.nc
    NC = 2 * NT
    with Stage(core, "chunks") as st:
        block = st.opened
        mask = st.sb("mask", [P, CHUNK])
        scores = st.sb("scores", [P, NT, CHUNK])
        states = st.sb("states", [KEYS, NC, D])
        ps_scores = st.psum("scores", [P, NT, CHUNK])
        ps_state = [st.psum(f"state{n}", [KEYS, HALF]) for n in range(4)]
        ps_o = [st.psum(f"o{n}", [P, HALF]) for n in range(2)]
        in_, scored, masked, zeroed = st.sem("in"), st.sem("scored"), st.sem("masked"), st.sem("zeroed")
        added, state_ready, o_ready, o_kept = st.sem("added"), st.sem("state_ready"), st.sem("o_ready"), st.sem("o_kept")

        def place(c):
            return c // 2, slice(c % 2 * CHUNK, (c % 2 + 1) * CHUNK)

        def state_bank(c):
            return ps_state[c // 4 % 2 * 2 + c % 2][:, c // 2 % 2 * D:(c // 2 % 2 + 1) * D]

        @block.sync
        def _(sp):
            sp.dma_start(mask[:], core.dram["chunk_mask"]).then_inc(in_, 16)

        @block.gpsimd
        def _(pool):
            nc.gpsimd.memset(states[:, 0, :], 0.0).then_inc(zeroed, 1)
            st.clear_old(pool)

        @block.tensor
        def _(pe):
            for c in range(NC):
                t, at = place(c)
                tokens = slice(c * CHUNK, (c + 1) * CHUNK)
                last = nc.tensor.matmul(ps_scores[at, t, :], anchored_k[:, tokens], anchored_q[:, tokens],
                                        start=True, stop=True)
            last.then_inc(scored, 1)
            for c in range(NC):
                t, at = place(c)
                if c % 4 == 0 and c >= 8:
                    pe.wait_ge(state_ready, c - 4)
                nc.tensor.matmul(state_bank(c), kept_k[at, t, :], h[at, t, :], start=True, stop=True
                                 ).then_inc(added, 1)
            pe.wait_ge(masked, 1)
            pe.wait_ge(zeroed, 1)
            for c in range(NC):
                t, at = place(c)
                pe.wait_ge(state_ready, max(c, 1))
                if c % 4 == 0 and c >= 8:
                    pe.wait_ge(o_kept, c // 4 - 1)
                to = ps_o[t // 2 % 2][at, t % 2 * D:(t % 2 + 1) * D]
                nc.tensor.matmul(to, scores[at, t, :], h[at, t, :], start=True, stop=False)
                last = nc.tensor.matmul(to, decayed_q[:, c * CHUNK:(c + 1) * CHUNK], states[:, c, :],
                                        start=False, stop=True)
                if c % 4 == 3:
                    last.then_inc(o_ready, 1)

        @block.scalar
        def _(act):
            for n in range(4):
                act.wait_ge(o_ready, n + 1)
                nc.scalar.copy(o[:, 2 * n:2 * n + 2, :], ps_o[n % 2][:].rearrange("p (t d) -> p t d", t=2)
                               ).then_inc(o_kept, 1)

        @block.vector
        def _(dve):
            dve.wait_ge(scored, 1)
            dve.wait_ge(in_, 16)
            nc.vector.tensor_tensor(scores[:], ps_scores[:], mask[:].unsqueeze(1).broadcast_to([P, NT, CHUNK]),
                                    ALU.mult).then_inc(masked, 1)
            dve.wait_ge(zeroed, 1)
            for c in range(NC):
                if c == NC - 1:
                    break
                dve.wait_ge(added, c // 4 * 4 + 4)
                if c:
                    dve.wait_ge(state_ready, c)
                nc.vector.scalar_tensor_tensor(states[:, c + 1, :], states[:, c, :], chunk_decay[:, c:c + 1], state_bank(c),
                                               ALU.mult, ALU.add).then_inc(state_ready, 1)


def gate_and_project(core, o):
    nc, x, hT = core.nc, core.x, core.hT
    with Stage(core, "gate") as st:
        block = st.opened
        w = st.sb("w", [P, 3, DC, D])
        norm_w = st.sb("norm_w", [P, DC])
        oT, rT = st.sb("oT", [P, DC, TOK]), st.sb("rT", [P, DC, TOK])
        squares = st.sb("squares", [P, 2, D])
        square_sum, inverse = st.sb("square_sum", [P, NT]), st.sb("inverse", [P, NT])
        silu, r = st.sb("silu", [P, NT, D]), st.sb("r", [P, NT, D])
        ps_turn = [st.psum(f"turn{n}", [P, HALF]) for n in range(4)]
        ps_go = [st.psum(f"go{n}", [P, HALF]) for n in range(2)]
        ps_y = [st.psum(f"y{n}", [P, HALF]) for n in range(2)]
        in_, turned, kept, gone = st.sem("in"), st.sem("turned"), st.sem("kept"), st.sem("gone")
        squared, root, step, silued = st.sem("squared"), st.sem("root"), st.sem("step"), st.sem("silued")
        gated, r_turned, r_kept, y_ready = st.sem("gated"), st.sem("r_turned"), st.sem("r_kept"), st.sem("y_ready")
        y_added, mean_ready = st.sem("y_added"), st.sem("mean_ready")

        @block.sync
        def _(sp):
            sp.dma_start(w[:], core.dram["L1a_w"]).then_inc(in_, 16)
            sp.dma_start(norm_w[:], core.dram["L1a_norm"]).then_inc(in_, 16)

        @block.gpsimd
        def _(pool):
            st.clear_old(pool)

        @block.tensor
        def _(pe):
            for half in range(2):
                for c in range(DC):
                    for i in range(4):
                        last = nc.tensor.transpose(ps_turn[2 * half + c][:, i * P:(i + 1) * P],
                                                   o[:, 4 * half + i, c * P:(c + 1) * P], core.ident[:])
                    last.then_inc(turned, 1)
            pe.wait_ge(in_, 32)
            for t in range(NT):
                pe.wait_ge(kept, 2 if t < 4 else 4)
                if t % 2 == 0 and t >= 4:
                    pe.wait_ge(silued, t // 2 - 1)
                to = ps_go[t // 2 % 2][:, t % 2 * D:(t % 2 + 1) * D]
                for n, src in enumerate((oT, hT)):
                    for c in range(DC):
                        last = nc.tensor.matmul(to, src[:, c, t * P:(t + 1) * P], w[:, n, c, :],
                                                start=(n == 0 and c == 0), stop=(n == 1 and c == DC - 1))
                if t % 2:
                    last.then_inc(gone, 1)
            for half in range(2):
                for c in range(DC):
                    for i in range(4):
                        pe.wait_ge(gated, (4 * half + i) // 2 + 1)
                        last = nc.tensor.transpose(ps_turn[2 * half + c][:, i * P:(i + 1) * P],
                                                   r[:, 4 * half + i, c * P:(c + 1) * P], core.ident[:])
                    last.then_inc(r_turned, 1)
            for t in range(NT):
                pe.wait_ge(r_kept, 2 if t < 4 else 4)
                if t % 2 == 0 and t >= 4:
                    pe.wait_ge(y_added, t // 2 - 1)
                for c in range(DC):
                    last = nc.tensor.matmul(ps_y[t // 2 % 2][:, t % 2 * D:(t % 2 + 1) * D],
                                            rT[:, c, t * P:(t + 1) * P], w[:, 2, c, :],
                                            start=(c == 0), stop=(c == DC - 1))
                if t % 2:
                    last.then_inc(y_ready, 1)

        @block.scalar
        def _(act):
            for t in range(NT):
                if t >= 2:
                    act.wait_ge(squared, t - 1)
                nc.scalar.activation(squares[:, t % 2, :], o[:, t, :], ACT.Square,
                                     accum_out=square_sum[:, t:t + 1]).then_inc(squared, 1)
            act.wait_ge(mean_ready, 1)
            nc.scalar.activation(square_sum[:], square_sum[:], ACT.Sqrt).then_inc(root, 1)
            for n in range(4):
                act.wait_ge(gone, n + 1)
                nc.scalar.activation(silu[:, 2 * n:2 * n + 2, :], ps_go[n % 2][:].rearrange(
                    "p (t d) -> p t d", t=2), ACT.Silu).then_inc(silued, 1)

        @block.vector
        def _(dve):
            link = linker(dve, step)
            for n in range(4):
                dve.wait_ge(turned, n + 1)
                nc.vector.tensor_copy(oT[:, n % 2, n // 2 * HALF:(n // 2 + 1) * HALF], ps_turn[n][:]
                                      ).then_inc(kept, 1)
            dve.wait_ge(squared, NT)
            nc.vector.tensor_scalar(square_sum[:], square_sum[:], 1.0 / D, 1e-5, ALU.mult, ALU.add
                                    ).then_inc(mean_ready, 1)
            dve.wait_ge(root, 1)
            link(nc.vector.reciprocal(inverse[:], square_sum[:]))
            for t in range(NT):
                dve.wait_ge(silued, t // 2 + 1)
                last = nc.vector.scalar_tensor_tensor(r[:, t, :], o[:, t, :], inverse[:, t:t + 1], silu[:, t, :],
                                                      ALU.mult, ALU.mult)
                if t % 2:
                    last.then_inc(gated, 1)
            dve.wait_ge(in_, 32)
            for n in range(4):
                dve.wait_ge(r_turned, n + 1)
                c = n % 2
                nc.vector.tensor_scalar(rT[:, c, n // 2 * HALF:(n // 2 + 1) * HALF], ps_turn[n][:],
                                        norm_w[:, c:c + 1], None, ALU.mult).then_inc(r_kept, 1)
            for n in range(4):
                dve.wait_ge(y_ready, n + 1)
                two = x[:, 2 * n:2 * n + 2, :]
                nc.vector.tensor_tensor(two, two, ps_y[n % 2][:].rearrange("p (t d) -> p t d", t=2), ALU.add
                                        ).then_inc(y_added, 1)


def build(nc, dram, out, first, last):
    with ExitStack() as whole:
        core = Core(nc, dram, whole)
        load_input(core)
        layers = [
            attention_layer_0a, feed_forward_0, attention_layer_0b, feed_forward_0,
            linear_attention, experts, decay_scan, experts,
            attention_layer_2a, ternary_feed_forward, attention_layer_2b, ternary_feed_forward,
            attention_layer_3a, low_rank_experts, state_space, low_rank_experts,
        ]
        for layer in layers[first:last]:
            layer(core)
        store_output(core, out)


def attention_layer_0a(core):
    normalise(core, [(core.hT, [])])
    narrow_attention(core, "L0a")


def attention_layer_0b(core):
    normalise(core, [(core.hT, ["L0b_norm", "L0b_split"])], second=("norm", 1e-8), keep=True)
    attention(core, "L0b", groups=2, heads=2, hd=64, shared_kv=True, causal=False, scale=0.125)


def attention_layer_2a(core):
    normalise(core, [(core.hT, [])])
    attention(core, "L2a", groups=16, heads=1, hd=128, shared_kv=False, causal=True, scale=128 ** -0.5)


def attention_layer_2b(core):
    normalise(core, [(core.hT, [])])
    capped_attention(core, "L2b", 16, 50.0)


def attention_layer_3a(core):
    normalise(core, [(core.hT, [])])
    narrow_attention(core, "L3a", bias=True, out_bias="L3a_bo")



def rows_in_chunks(w):
    k, n = w.shape
    return np.ascontiguousarray(w.reshape(k // P, P, n).transpose(1, 0, 2))


def column_pairs(v):
    return np.ascontiguousarray(v.reshape(-1, P).T)


def spread_heads(w, group, heads, hd):
    to = np.zeros((w.shape[0], P), w.dtype)
    for j in range(heads):
        h = group * heads + j
        to[:, j * (P // heads):j * (P // heads) + hd] = w[:, h * hd:(h + 1) * hd]
    return to


def attention_weights(wq, wk, wv, groups, heads, hd, shared_kv):
    out = []
    for g in range(groups):
        q = spread_heads(wq, g, heads, hd)
        if shared_kv:
            k = np.concatenate([wk[:, g * hd:(g + 1) * hd]] * heads, 1)
            v = wv[:, g * hd:(g + 1) * hd]
        else:
            k = spread_heads(wk, g, heads, hd)
            v = wv[:, g * heads * hd:(g + 1) * heads * hd]
        out.append(rows_in_chunks(np.concatenate([q, k, v], 1)))
    return np.stack(out)


def spread_rows(w):
    to = np.zeros((P, QUADS, D), w.dtype)
    for h in range(HEADS):
        to[32 * (h % 4):32 * (h % 4) + HD, h // 4] = w[h * HD:(h + 1) * HD]
    return to


def gated_weights(gate, up, down, *more):
    tiles = -(-gate.shape[0] // P)
    parts = []
    for w in (gate, up, down):
        whole = np.zeros((tiles * P, D), w.dtype)
        whole[0:w.shape[0]] = w
        parts.append(whole.reshape(tiles, P, D))
    turned = [w.reshape(tiles, P, DC, P).transpose(0, 3, 2, 1).reshape(tiles, P, D) for w in parts[0:2]]
    return np.concatenate([*turned, parts[2], *more], 2)


def lay_out(a):
    o = {"x": a["L0_attn_a_x"][0]}
    o["L0a_wn"] = rows_in_chunks(np.concatenate([a["L0_attn_a_W" + n].T for n in "qkv"], 1))
    o["L0a_won"] = spread_rows(a["L0_attn_a_Wo"].T)
    o["select_sum"] = ((np.arange(P)[:, None] % 32 == HD) & (np.arange(P)[:, None] // 32 == np.arange(P)[None] // 32)
                       ).astype(np.float32)
    o["L0b_w"] = attention_weights(a["L0_attn_b_Wq"].T, a["L0_attn_b_Wk"].T, a["L0_attn_b_Wv"].T, 2, 2, 64, True)
    o["L0b_wo"] = rows_in_chunks(a["L0_attn_b_Wo"].T)
    o["L0b_norm"] = column_pairs(a["L0_attn_b_norm_scale"])
    o["L0b_split"] = column_pairs(a["L0_attn_b_split_scale"])
    o["L2a_w"] = attention_weights(*(a["L2_attn_a_W_" + n].reshape(-1, D).T for n in "QKV"), 16, 1, 128, False)
    o["L2a_wo"] = rows_in_chunks(a["L2_attn_a_W_O"].transpose(0, 2, 1).reshape(-1, D))
    o["L2b_w"] = attention_weights(*(a["L2_attn_b_w" + n].T for n in "qkv"), 16, 1, 128, False)
    o["L2b_wo"] = rows_in_chunks(a["L2_attn_b_wo"].T)
    o["L2b_turns"] = np.stack([np.repeat(a["L2_attn_b_rope_cos"][0:16].T, 2, 0),
                               np.repeat(a["L2_attn_b_rope_sin"][0:16].T, 2, 0),
                               np.repeat(a["L2_attn_b_q_norm_w"][:, None], 16, 1),
                               np.repeat(a["L2_attn_b_k_norm_w"][:, None], 16, 1)], 1)
    o["L3a_wn"] = rows_in_chunks(np.concatenate(
        [a["L3_attn_a_W" + n].transpose(1, 0, 2).reshape(D, -1) for n in "qkv"], 1))
    o["L3a_won"] = spread_rows(a["L3_attn_a_Wo"])
    o["L3a_bn"] = np.stack([a["L3_attn_a_b" + n].reshape(2, P)[g] for g in range(2) for n in "qk"], 1)
    o["L3a_v_bias"] = a["L3_attn_a_bv"].reshape(1, -1)
    o["L3a_bo"] = a["L3_attn_a_bo"].reshape(1, -1)
    o["L0f_wn"] = rows_in_chunks(np.concatenate([a["L0_ffn_W" + n].T for n in "qkv"], 1))
    o["L0f_won"] = spread_rows(a["L0_ffn_Wo"].T)
    o["L0f_ln1"], o["L0f_ln2"] = column_pairs(a["L0_ffn_ln1_w"]), column_pairs(a["L0_ffn_ln2_w"])
    o["L0f_A"] = rows_in_chunks(a["L0_ffn_A"])
    low = np.zeros((8, P, P), np.float32)
    low[:, 0:16] = a["L0_ffn_B"].reshape(16, 8, P).transpose(1, 0, 2)
    o["L0g_w"] = gated_weights(a["L0_ffn_W_in_base"], a["L0_ffn_W_up_base"], a["L0_ffn_W_down"].T, low)
    scales = np.zeros((6 * P, 2), np.float32)
    scales[0:704, 0], scales[0:704, 1] = a["L2_ffn_gate_s"], a["L2_ffn_up_s"]
    o["L2f_w"] = gated_weights(a["L2_ffn_gate_w"], a["L2_ffn_up_w"], a["L2_ffn_down_w"].T,
                               scales.reshape(6, P, 2))
    o["L2f_down_s"] = a["L2_ffn_down_s"].reshape(1, D)
    gu = a["L1_ffn_gate_up_proj"]
    o["L1f_w"] = gated_weights(gu[:, 0:96].reshape(-1, D), gu[:, 96:].reshape(-1, D),
                               a["L1_ffn_down_proj"].transpose(0, 2, 1).reshape(-1, D))
    o["L1f_router"] = rows_in_chunks(a["L1_ffn_gate_weight"].T)
    o["expert_number"] = np.arange(EXPERTS, dtype=np.float32).reshape(1, -1)
    o["L1b_w"], o["L1b_b"] = rows_in_chunks(a["L1_attn_b_W"].T), column_pairs(a["L1_attn_b_b"])
    routed = a["L3_ffn_A_r"].transpose(1, 0, 2).reshape(D, -1)
    o["L3f_w1"] = rows_in_chunks(np.concatenate([a["L3_ffn_A_s"], routed, a["L3_ffn_W_router"]], 1))
    o["L3f_base"] = rows_in_chunks(a["L3_ffn_W_base"])
    o["L3f_w2"] = np.concatenate([a["L3_ffn_B_s"], a["L3_ffn_B_r"].reshape(-1, D),
                                  a["L3_ffn_b_base"].reshape(1, D)])
    o["L3f_router_bias"] = a["L3_ffn_b_router"].reshape(1, -1)
    o["L3b_wx"], o["L3b_wdt"] = rows_in_chunks(a["L3_attn_b_W_xproj"].T), a["L3_attn_b_W_dt"].T
    o["L3b_bdt"], o["L3b_D"] = column_pairs(a["L3_attn_b_b_dt"]), column_pairs(a["L3_attn_b_D"])
    o["L3b_A"] = rows_in_chunks(a["L3_attn_b_A"])
    o["L1a_wqk"] = rows_in_chunks(np.concatenate([a["L1_attn_a_Wq"], a["L1_attn_a_Wk"]]).T)
    o["L1a_w"] = np.stack([rows_in_chunks(a["L1_attn_a_W" + n].T) for n in ("og", "ig", "o")], 1)
    o["L1a_norm"] = column_pairs(a["L1_attn_a_g_norm_w"])
    frm, to = np.arange(P)[:, None], np.arange(P)[None, :]
    chunk = frm // CHUNK == to // CHUNK
    here, middle = chunk & (frm <= to), chunk & (frm % CHUNK < CHUNK // 2)
    o["chunk_sums"] = np.stack([here.astype(np.float32) - middle, here, chunk & (frm > to)], 1).astype(np.float32)
    o["chunk_ends"] = (np.arange(P)[:, None] // CHUNK == np.arange(2)[None, :]).astype(np.float32)
    o["chunk_mask"] = (frm % CHUNK <= np.arange(CHUNK)[None, :]).astype(np.float32)
    return {n: np.ascontiguousarray(v) for n, v in o.items()}


FIRST, LAST = 0, 16


def kernel(**inputs):
    import concourse.bacc as bacc
    from concourse.bass_utils import run_bass_kernel_spmd

    nc = bacc.Bacc("TRN2", target_bir_lowering=False, num_devices=1)
    arrays = lay_out({n: np.asarray(v) for n, v in inputs.items()})
    dram = {n: nc.dram_tensor(f"in_{n}", v.shape, mybir.dt.from_np(v.dtype), kind="ExternalInput").ap()
            for n, v in arrays.items()}
    out = nc.dram_tensor("out", (TOK, D), F32, kind="ExternalOutput").ap()
    build(nc, dram, out, FIRST, LAST)
    r = run_bass_kernel_spmd(nc, [{f"in_{n}": v for n, v in arrays.items()}], core_ids=[0])
    return r.results[0]["out"].reshape(1, TOK, D)
```

```python
from contextlib import ExitStack

import concourse.bass as bass
import numpy as np
from concourse import mybir

ALU = mybir.AluOpType
ACT = mybir.ActivationFunctionType
AX = mybir.AxisListType.X
F32 = mybir.dt.float32
BF16 = mybir.dt.bfloat16
U32 = mybir.dt.uint32

P = 128
TOK = 1024
D = 256
NT = TOK // P
DC = D // P
HALF = 512
MASKED = -1.0e30


class Core:

    def __init__(self, nc, dram, whole):
        self.nc = nc
        self.dram = dram
        self.old = []
        self.count = 0

        def sb(name, shape, dt=F32):
            return whole.enter_context(nc.sbuf_tensor(name, shape, dt))

        self.x = sb("x", [P, NT, D])
        self.hT = sb("hT", [P, DC, TOK])
        self.ident = sb("ident", [P, P])
        self.ident_bf = sb("ident_bf", [P, P], BF16)
        self.causal = sb("causal", [P, P], BF16)
        self.causal_turned = sb("causal_turned", [P, P], BF16)
        self.ones = sb("ones", [P, P])


class Stage:

    def __init__(self, core, name):
        self.core, self.nc, self.name = core, core.nc, f"{name}{core.count}"
        core.count += 1
        self.stack = ExitStack()
        self.sems = []

    def sem(self, name):
        s = self.nc.alloc_semaphore(f"{self.name}_{name}")
        self.sems.append(s)
        return s

    def sb(self, name, shape, dt=F32):
        return self.stack.enter_context(self.nc.sbuf_tensor(f"{self.name}_{name}", shape, dt))

    def psum(self, name, shape, dt=F32):
        return self.stack.enter_context(self.nc.psum_tensor(f"{self.name}_ps_{name}", shape, dt))

    def clear_old(self, pool):
        numbers = sorted(s.num for s in self.core.old)
        while numbers:
            run = [numbers.pop(0)]
            while numbers and numbers[0] == run[-1] + 1:
                run.append(numbers.pop(0))
            pool.sem_clear(range(run[0], run[-1] + 1))

    def __enter__(self):
        self.block = self.nc.Block(no_gpsimd_drain=True)
        self.opened = self.block.__enter__()
        return self

    def __exit__(self, *error):
        out = self.block.__exit__(*error)
        self.stack.close()
        for s in self.core.old:
            self.nc.release_semaphore(s)
        self.core.old = self.sems
        return out


def linker(engine, sem):
    done = [0]

    def link(instruction):
        done[0] += 1
        instruction.then_inc(sem, 1)
        engine.wait_ge(sem, done[0])
    return link


def load_input(core):
    nc, x = core.nc, core.x
    with Stage(core, "load") as st:
        loaded, zeroed, ones_set = st.sem("loaded"), st.sem("zeroed"), st.sem("ones_set")
        block = st.opened

        @block.sync
        def _(sp):
            for c in range(2):
                half = slice(c * NT // 2, (c + 1) * NT // 2)
                sp.dma_start(x[:, half, :], core.dram["x"].rearrange("(t p) d -> p t d", p=P)[:, half, :]
                             ).then_inc(loaded, 16)
            sp.wait_ge(loaded, 32)

        @block.gpsimd
        def _(pool):
            nc.gpsimd.memset(core.ident[:], 0.0).then_inc(zeroed, 1)
            nc.gpsimd.memset(core.ident_bf[:], 0.0).then_inc(zeroed, 1)
            nc.gpsimd.memset(core.causal[:], 0.0).then_inc(zeroed, 1)
            nc.gpsimd.memset(core.causal_turned[:], 0.0).then_inc(zeroed, 1)
            nc.gpsimd.memset(core.ones[:], 1.0).then_inc(ones_set, 1)
            pool.wait_ge(zeroed, 4)
            for t in (core.ident, core.ident_bf):
                nc.gpsimd.affine_select(out=t[:], in_=t[:], compare_op=ALU.not_equal, fill=1.0, base=0,
                                        pattern=[[-1, P]], channel_multiplier=1).then_inc(ones_set, 1)
            nc.gpsimd.affine_select(out=core.causal[:], in_=core.causal[:], compare_op=ALU.is_ge, fill=MASKED,
                                    base=0, pattern=[[-1, P]], channel_multiplier=1).then_inc(ones_set, 1)
            nc.gpsimd.affine_select(out=core.causal_turned[:], in_=core.causal_turned[:], compare_op=ALU.is_ge,
                                    fill=MASKED, base=0, pattern=[[1, P]], channel_multiplier=-1
                                    ).then_inc(ones_set, 1)
            pool.wait_ge(ones_set, 5)


def store_output(core, out):
    with Stage(core, "store") as st:
        stored = st.sem("stored")
        block = st.opened

        @block.sync
        def _(sp):
            for c in range(2):
                half = slice(c * NT // 2, (c + 1) * NT // 2)
                sp.dma_start(out.rearrange("(t p) d -> p t d", p=P)[:, half, :], core.x[:, half, :]
                             ).then_inc(stored, 16)
            sp.wait_ge(stored, 32)


def early(core, stack, name, loads):
    tiles = [stack.enter_context(core.nc.sbuf_tensor(f"{name}{core.count}_early{n}", shape, F32))
             for n, (shape, _) in enumerate(loads)]
    return tiles, [(to, source) for to, (_, source) in zip(tiles, loads)]


def normalise(core, outs, second=None, keep=False, rows=None, loads=()):
    nc, x = core.nc, core.x
    with Stage(core, "norm") as st:
        block = st.opened
        stats, mv = st.sb("stats", [P, NT, 6]), st.sb("mv", [P, NT, 2])
        spread, inverse = st.sb("spread", [P, NT]), st.sb("inverse", [P, NT])
        h = rows if rows is not None else st.sb("h", [P, NT, D])
        squares, square_sum = st.sb("squares", [P, 2, D]), st.sb("square_sum", [P, NT])
        turned = [st.psum(f"turned{n}", [P, HALF]) for n in range(4)]
        step, variance, root = st.sem("step"), st.sem("variance"), st.sem("root")
        squared = st.sem("squared")
        tile_done, sums, turned_ready = st.sem("tile_done"), st.sem("sums"), st.sem("turned_ready")
        written_act, written_dve = st.sem("written_act"), st.sem("written_dve")
        columns = [(n, c, w) for n, (_, ws) in enumerate(outs) for c, w in enumerate(ws)]
        column_sb = {(n, c): st.sb(f"w{n}_{c}", [P, DC]) for n, c, _ in columns}
        columns_in, loaded = st.sem("columns_in"), st.sem("loaded")

        @block.sync
        def _(sp):
            for n, c, w in columns:
                sp.dma_start(column_sb[n, c][:], core.dram[w]).then_inc(columns_in, 16)
            for to, source in loads:
                sp.dma_start(to[:], source).then_inc(loaded, 16)
            if loads:
                sp.wait_ge(loaded, 16 * len(loads))

        @block.gpsimd
        def _(pool):
            st.clear_old(pool)
            if keep:
                for t in range(NT):
                    pool.wait_ge(tile_done, t + 1)
                    nc.gpsimd.tensor_tensor(x[:, t, :], x[:, t, :], h[:, t, :], ALU.add
                                            ).then_inc(sums, 1)

        @block.vector
        def _(dve):
            link = linker(dve, step)
            for t in range(NT):
                nc.vector.bn_stats(stats[:, t, :], x[:, t, :]).then_inc(variance, 1)
            for t in range(NT):
                dve.wait_ge(variance, t + 1)
                nc.vector.bn_aggr(mv[:, t, :], stats[:, t, :]).then_inc(variance, 1)
            dve.wait_ge(variance, 2 * NT)
            nc.vector.tensor_scalar(spread[:], mv[:, :, 1], 1e-5, None, ALU.add).then_inc(variance, 1)
            dve.wait_ge(root, 1)
            link(nc.vector.reciprocal(inverse[:], spread[:]))
            for t in range(NT):
                nc.vector.tensor_scalar(h[:, t, :], x[:, t, :], mv[:, t, 0:1], inverse[:, t:t + 1],
                                        ALU.subtract, ALU.mult).then_inc(tile_done, 1)
            if second:
                kind, eps = second
                dve.wait_ge(squared, NT)
                nc.vector.tensor_scalar(spread[:], square_sum[:], 1.0 / D, eps if kind == "rms" else 0.0,
                                        ALU.mult, ALU.add).then_inc(variance, 1)
                dve.wait_ge(root, 2)
                if kind == "norm":
                    link(nc.vector.tensor_scalar(spread[:], spread[:], eps, None, ALU.add))
                link(nc.vector.reciprocal(inverse[:], spread[:]))
                if keep:
                    dve.wait_ge(sums, NT)
                for t in range(NT):
                    nc.vector.tensor_scalar(h[:, t, :], h[:, t, :], inverse[:, t:t + 1], None,
                                            ALU.mult).then_inc(tile_done, 1)
            for n, (dst, ws) in enumerate(outs):
                if ws:
                    dve.wait_ge(columns_in, 16 * len(columns))
                for half in range(2):
                    for c in range(DC):
                        if half and len(ws) < 2:
                            continue
                        dve.wait_ge(turned_ready, 2 * half + c + 1)
                        src = turned[2 * half + c][:]
                        to = dst[:, c, half * HALF:(half + 1) * HALF]
                        if not ws:
                            nc.vector.tensor_copy(to, src).then_inc(written_dve, 1)
                        elif len(ws) == 1:
                            nc.vector.tensor_scalar(to, src, column_sb[n, 0][:, c:c + 1], None, ALU.mult
                                                    ).then_inc(written_dve, 1)
                        else:
                            nc.vector.tensor_scalar(to, src, column_sb[n, 0][:, c:c + 1],
                                                    column_sb[n, 1][:, c:c + 1], ALU.mult, ALU.mult
                                                    ).then_inc(written_dve, 1)

        @block.scalar
        def _(act):
            act.wait_ge(variance, 2 * NT + 1)
            nc.scalar.activation(spread[:], spread[:], ACT.Sqrt).then_inc(root, 1)
            if second:
                for t in range(NT):
                    act.wait_ge(tile_done, t + 1)
                    if t >= 2:
                        act.wait_ge(squared, t - 1)
                    nc.scalar.activation(squares[:, t % 2, :], h[:, t, :], ACT.Square,
                                         accum_out=square_sum[:, t:t + 1]).then_inc(squared, 1)
                act.wait_ge(variance, 2 * NT + 2)
                nc.scalar.activation(spread[:], spread[:], ACT.Sqrt).then_inc(root, 1)
            for n, (dst, ws) in enumerate(outs):
                if ws:
                    act.wait_ge(columns_in, 16 * len(columns))
                for half in range(2):
                    for c in range(DC):
                        if half == 0 or len(ws) >= 2:
                            continue
                        act.wait_ge(turned_ready, 2 * half + c + 1)
                        src = turned[2 * half + c][:]
                        to = dst[:, c, half * HALF:(half + 1) * HALF]
                        if ws:
                            nc.scalar.mul(to, src, column_sb[n, 0][:, c:c + 1]).then_inc(written_act, 1)
                        else:
                            nc.scalar.copy(to, src).then_inc(written_act, 1)

        @block.tensor
        def _(pe):
            for half in range(2):
                for c in range(DC):
                    for i in range(4):
                        t = 4 * half + i
                        pe.wait_ge(tile_done, (NT if second else 0) + t + 1)
                        last = nc.tensor.transpose(turned[2 * half + c][:, i * P:(i + 1) * P],
                                                   h[:, t, c * P:(c + 1) * P], core.ident[:])
                    last.then_inc(turned_ready, 1)


def attention(core, name, groups, heads, hd, scale):
    nc, x, hT = core.nc, core.x, core.hT
    gw = heads * hd
    stride = P // heads
    total = groups * gw
    NCH = total // P
    items = [(j, t) for j in range(heads) for t in range(NT)]
    NI = len(items)
    FREE = 1

    with Stage(core, name) as st:
        block = st.opened
        w = st.sb("w", [P, DC, 2 * P + hd])
        wo = st.sb("wo", [P, NCH, D])
        qT, kT = st.sb("qT", [P, TOK]), st.sb("kT", [P, TOK])
        v = st.sb("v", [P, NT, hd])
        probs = [st.sb(f"probs{n}", [P, TOK]) for n in range(2)]
        probsT = [st.sb(f"probsT{n}", [P, TOK]) for n in range(2)]
        negmax, rowsum, rowinv = st.sb("negmax", [P, NI]), st.sb("rowsum", [P, NI]), st.sb("rowinv", [P, NI])
        rows = st.sb("rows", [P, NT, total])
        ps_scores = [st.psum(f"scores{n}", [P, TOK]) for n in range(2)]
        ps_turn = [st.psum(f"turn{n}", [P, HALF]) for n in range(2)]
        ps_out = st.psum("out", [P, HALF])

        w_in, wo_in, projected = st.sem("w_in"), st.sem("wo_in"), st.sem("projected")
        v_kept, k_kept, q_kept = st.sem("v_kept"), st.sem("k_kept"), st.sem("q_kept")
        scored, maxed, exped = st.sem("scored"), st.sem("maxed"), st.sem("exped")
        turned, first_kept, second_kept = st.sem("turned"), st.sem("first_kept"), st.sem("second_kept")
        summed, inverted, scaled = st.sem("summed"), st.sem("inverted"), st.sem("scaled")
        rows_turned, rowsT_kept = st.sem("rows_turned"), st.sem("rowsT_kept")
        out_ready, out_added = st.sem("out_ready"), st.sem("out_added")
        peaked = st.sem("peaked")

        @block.sync
        def _(sp):
            sp.dma_start(w[:], core.dram[f"{name}_w"][0]).then_inc(w_in, 16)
            sp.dma_start(wo[:], core.dram[f"{name}_wo"]).then_inc(wo_in, 16)
            with sp.Fori(1, groups) as g:
                sp.wait_ge(projected, 3 * g)
                sp.dma_start(w[:], core.dram[f"{name}_w"][bass.ds(g, 1)].rearrange("a p c n -> (a p) c n")
                             ).then_inc(w_in, 16)

        @block.gpsimd
        def _(pool):
            st.clear_old(pool)

        @block.tensor
        def _(pe):
            for s in (scored, turned, summed):
                pe.sem_inc(s, FREE)
            with pe.Fori(0, groups) as g:
                pe.wait_ge(w_in, g * 16 + 16)
                pe.wait_ge(exped, FREE + g * NI)
                for t in range(NT):
                    for c in range(DC):
                        last = nc.tensor.matmul(ps_scores[0][:, t * P:t * P + hd], hT[:, c, t * P:(t + 1) * P],
                                                w[:, c, 2 * P:], start=(c == 0), stop=(c == DC - 1))
                last.then_inc(projected, 1)
                for half in range(2):
                    for c in range(DC):
                        last = nc.tensor.matmul(ps_scores[1][:, half * HALF:(half + 1) * HALF], w[:, c, P:2 * P],
                                                hT[:, c, half * HALF:(half + 1) * HALF],
                                                start=(c == 0), stop=(c == DC - 1))
                last.then_inc(projected, 1)
                pe.wait_ge(v_kept, g + 1)
                for half in range(2):
                    for c in range(DC):
                        last = nc.tensor.matmul(ps_scores[0][:, half * HALF:(half + 1) * HALF], w[:, c, 0:P],
                                                hT[:, c, half * HALF:(half + 1) * HALF],
                                                start=(c == 0), stop=(c == DC - 1))
                last.then_inc(projected, 1)
                pe.wait_ge(q_kept, g + 1)
                pe.wait_ge(k_kept, g + 1)
                for i in range(NI + 2):
                    if i < NI:
                        j, t = items[i]
                        rows_of = slice(j * stride, j * stride + hd)
                        if i >= 2:
                            pe.wait_ge(exped, FREE + g * NI + (i - 1))
                        for a in range(0, TOK, HALF):
                            b = a + HALF
                            last = nc.tensor.matmul(ps_scores[i % 2][:, a:b], qT[rows_of, t * P:(t + 1) * P],
                                                    kT[rows_of, a:b], start=True, stop=True)
                        last.then_inc(scored, 1)
                    if 1 <= i <= NI:
                        n = i - 1
                        j, t = items[n]
                        pe.wait_ge(exped, FREE + g * NI + (n + 1))
                        for c in range(TOK // P):
                            if c == 0:
                                pe.wait_ge(first_kept, FREE + g * NI + n)
                            if c == 4:
                                pe.wait_ge(second_kept, FREE + g * NI + n)
                            last = nc.tensor.transpose(ps_turn[c // 4][:, c % 4 * P:(c % 4 + 1) * P],
                                                       probs[n % 2][:, c * P:(c + 1) * P], core.ident[:])
                            if c == 3:
                                last.then_inc(turned, 1)
                        last.then_inc(turned, 1)
                    if i >= 2:
                        n = i - 2
                        j, t = items[n]
                        pe.wait_ge(first_kept, FREE + g * NI + (n + 1))
                        pe.wait_ge(second_kept, FREE + g * NI + (n + 1))
                        pe.wait_ge(scaled, FREE + g * NI + n)
                        blocks = TOK // P
                        for c in range(blocks):
                            last = nc.tensor.matmul(ps_out[:, 0:hd],
                                                    probsT[n % 2][:, c * P:(c + 1) * P], v[:, c, :],
                                                    start=(c == 0), stop=(c == blocks - 1))
                        last.then_inc(summed, 1)

            pe.wait_ge(scaled, FREE + groups * NI)
            pe.wait_ge(wo_in, 16)
            per = min(NCH, 4)
            lots = [(t, a) for t in range(NT) for a in range(0, NCH, per)]
            for n in range(len(lots) + 1):
                if n < len(lots):
                    t, a = lots[n]
                    if n >= 2:
                        pe.wait_ge(rowsT_kept, n - 1)
                    for c in range(per):
                        last = nc.tensor.transpose(ps_turn[n % 2][:, c * P:(c + 1) * P],
                                                   rows[:, t, (a + c) * P:(a + c + 1) * P], core.ident[:])
                    last.then_inc(rows_turned, 1)
                if n >= 1:
                    t, a = lots[n - 1]
                    pe.wait_ge(rowsT_kept, n)
                    if a == 0 and t >= 2:
                        pe.wait_ge(out_added, t - 1)
                    for c in range(per):
                        last = nc.tensor.matmul(ps_scores[t % 2][:, 0:D],
                                                probsT[(n - 1) % 2][:, c * P:(c + 1) * P], wo[:, a + c, :],
                                                start=(a + c == 0), stop=(a + c == NCH - 1))
                    if a + per == NCH:
                        last.then_inc(out_ready, 1)

        @block.scalar
        def _(act):
            for s in (exped, first_kept):
                act.sem_inc(s, FREE)
            with act.Fori(0, groups) as g:
                act.wait_ge(projected, 3 * g + 1)
                act.wait_ge(summed, FREE + g * NI)
                vps = ps_scores[0][:].rearrange("p (t c) -> p t c", t=NT)[:, :, 0:hd]
                nc.scalar.copy(v[:], vps).then_inc(v_kept, 1)
                act.wait_ge(projected, 3 * g + 3)
                nc.scalar.copy(qT[:], ps_scores[0][:]).then_inc(q_kept, 1)
                for i in range(NI + 1):
                    if i < NI:
                        j, t = items[i]
                        act.wait_ge(maxed, g * NI + (i + 1))
                        turns = 2 * (i - 1) if i >= 2 else 0
                        act.wait_ge(turned, FREE + g * (2 * NI) + turns)
                        if i >= 2:
                            act.wait_ge(inverted, g * NI + (i - 1))
                        nc.scalar.activation(probs[i % 2][:], ps_scores[i % 2][:], ACT.Exp,
                                             bias=negmax[:, i:i + 1], scale=scale,
                                             accum_out=rowsum[:, i:i + 1]).then_inc(exped, 1)
                    if i >= 1:
                        n = i - 1
                        j, t = items[n]
                        act.wait_ge(turned, FREE + g * (2 * NI) + (2 * n + 1))
                        act.wait_ge(summed, FREE + g * NI + max(n - 1, 0))
                        nc.scalar.copy(probsT[n % 2][:, 0:HALF], ps_turn[0][:]).then_inc(first_kept, 1)

        @block.vector
        def _(dve):
            for s in (second_kept, scaled):
                dve.sem_inc(s, FREE)
            with dve.Fori(0, groups) as g:
                dve.wait_ge(projected, 3 * g + 2)
                dve.wait_ge(scored, FREE + g * NI)
                nc.vector.tensor_copy(kT[:], ps_scores[1][:]).then_inc(k_kept, 1)
                for i in range(NI + 2):
                    if i < NI:
                        j, t = items[i]
                    if i < NI:
                        dve.wait_ge(scored, FREE + g * NI + (i + 1))
                        dve.wait_ge(exped, FREE + g * NI + max(i - 1, 0))
                        nc.vector.tensor_reduce(negmax[:, i:i + 1], ps_scores[i % 2][:], AX,
                                                ALU.max, negate=True).then_inc(peaked, 1)
                        dve.wait_ge(peaked, g * NI + (i + 1))
                        nc.vector.tensor_scalar(negmax[:, i:i + 1], negmax[:, i:i + 1], scale, None,
                                                ALU.mult).then_inc(maxed, 1)
                    if 1 <= i <= NI:
                        n = i - 1
                        j, t = items[n]
                        dve.wait_ge(turned, FREE + g * (2 * NI) + (2 * n + 2))
                        dve.wait_ge(summed, FREE + g * NI + max(n - 1, 0))
                        nc.vector.tensor_copy(probsT[n % 2][:, HALF:], ps_turn[1][:]).then_inc(second_kept, 1)
                        dve.wait_ge(exped, FREE + g * NI + (n + 1))
                        nc.vector.reciprocal(rowinv[:, n:n + 1], rowsum[:, n:n + 1]).then_inc(inverted, 1)
                    if i >= 2:
                        n = i - 2
                        j, t = items[n]
                        dve.wait_ge(inverted, g * NI + (n + 1))
                        dve.wait_ge(summed, FREE + g * NI + (n + 1))
                        to = rows[:, t, bass.ds(g * gw + j * hd, hd)]
                        src = ps_out[:, 0:hd]
                        nc.vector.tensor_scalar(to, src, rowinv[:, n:n + 1], None, ALU.mult
                                                ).then_inc(scaled, 1)
            per = min(NCH, 4)
            lots = [(t, a) for t in range(NT) for a in range(0, NCH, per)]

            def add_out(t):
                src = ps_scores[t % 2][:, 0:D]
                nc.vector.tensor_tensor(x[:, t, :], x[:, t, :], src, ALU.add).then_inc(out_added, 1)

            for n in range(len(lots)):
                t, a = lots[n]
                dve.wait_ge(rows_turned, n + 1)
                nc.vector.tensor_copy(probsT[n % 2][:, 0:per * P], ps_turn[n % 2][:, 0:per * P]
                                      ).then_inc(rowsT_kept, 1)
                if a + per == NCH and t >= 1:
                    dve.wait_ge(out_ready, t)
                    add_out(t - 1)
            dve.wait_ge(out_ready, NT)
            add_out(NT - 1)


HEADS, HD = 16, 16
QUADS = HEADS // 4
TERMS = [(0, 0), (0, 1), (1, 0), (1, 1), (0, 2), (2, 0)]
SPLIT = HD * len(TERMS)
WITH_MAX = SPLIT + 3
UNITS = [(kt, half) for half in range(2) for kt in range(4 * half + 4)]
STACKED = 16 * 2 * len(TERMS)
PIECES = [(j, t, c) for j in range(4) for t in range(NT) for c in range(1 + t // 4)]


def narrow_loads(core, stack, name, bias=False):
    loads = [([P, DC, 3 * D], core.dram[f"{name}_wn"])]
    if bias:
        loads += [([P, 4], core.dram[f"{name}_bn"]), ([P, D], core.dram[f"{name}_v_bias"].broadcast_to([P, D]))]
    return early(core, stack, name, loads)


def narrow_attention(core, name, loaded, bias=False, out_bias=None, into=None):
    nc = core.nc
    with ExitStack() as layer:
        count = core.count

        def sb(part, shape, dt=F32):
            return layer.enter_context(nc.sbuf_tensor(f"{name}{count}_{part}", shape, dt))

        oT = sb("oT", [P, QUADS, TOK])
        with ExitStack() as inner:
            def inner_sb(part, shape, dt=F32):
                return inner.enter_context(nc.sbuf_tensor(f"{name}{count}_{part}", shape, dt))

            qs, ks = inner_sb("qs", [WITH_MAX, HEADS, TOK], BF16), inner_sb("ks", [WITH_MAX, HEADS, TOK], BF16)
            v = inner_sb("v", [P, QUADS, NT, 4, 32])
            parts_dram = nc.dram_tensor(f"{name}{count}_parts", (4, 3, P, TOK), BF16).ap()
            project_and_split(core, name, loaded, parts_dram, qs, ks, v, bias)
            weigh_values(core, name, parts_dram, qs, ks, v, oT)
        project_heads(core, name, oT, out_bias, into)


def stack_parts(sp, qs, ks, parts_dram, i, signal):
    for to, n in ((qs, i // 2 * 2), (ks, i // 2 * 2 + 1)):
        rows = slice(i % 2 * 4 * HD, (i % 2 * 4 + 4) * HD)
        for s, term in enumerate(TERMS):
            sp.dma_start(to[s * HD:(s + 1) * HD, 4 * i:4 * i + 4, :],
                         parts_dram[n, term[n % 2], rows].rearrange("(h d) t -> d h t", h=4)
                         ).then_inc(signal, 16)


def project_and_split(core, name, loaded, parts_dram, qs, ks, v, bias):
    nc, hT = core.nc, core.hT
    with Stage(core, f"{name}p") as st:
        block = st.opened
        w, biases, v_bias = loaded if bias else (*loaded, None, None)
        whole = [st.sb(f"whole{n}", [P, TOK]) for n in range(4)]
        rest = [st.sb(f"rest{n}", [P, TOK]) for n in range(2)]
        parts = [[st.sb(f"part{n}_{i}", [P, TOK], BF16) for i in range(3)] for n in range(4)]
        ps = [st.psum(f"qk{n}", [P, TOK]) for n in range(2)]
        ps_v = [st.psum(f"v{n}", [P, HALF]) for n in range(4)]
        stored_act = st.sem("stored_act")
        projected, v_ready, filled, stacked = (st.sem("projected"), st.sem("v_ready"), st.sem("filled"),
                                               st.sem("stacked"))
        wholes, firsts, rests = st.sem("wholes"), st.sem("firsts"), st.sem("rests")
        seconds, thirds, stored, ones_in = st.sem("seconds"), st.sem("thirds"), st.sem("stored"), st.sem("ones_in")

        def store_parts(engine, n, signal):
            for i, ready in enumerate((firsts, seconds, thirds)):
                engine.wait_ge(ready, n + 1)
                engine.dma_start(parts_dram[n, i], parts[n][i][:]).then_inc(signal, 16)

        @block.sync
        def _(sp):
            for n in range(2):
                store_parts(sp, n, stored)
            sp.wait_ge(stored, 16 * 6)
            stack_parts(sp, qs, ks, parts_dram, 0, stacked)
            sp.wait_ge(stacked, STACKED)

        @block.gpsimd
        def _(pool):
            nc.gpsimd.memset(v[:], 0.0).then_inc(filled, 1)
            pool.wait_ge(filled, 1)
            nc.gpsimd.memset(v[:, :, :, :, HD:HD + 1], 1.0).then_inc(filled, 1)
            pool.wait_ge(filled, 2)
            nc.gpsimd.memset(ks[SPLIT:WITH_MAX, :, :], 1.0).then_inc(ones_in, 1)
            st.clear_old(pool)
            pool.wait_ge(ones_in, 1)

        @block.tensor
        def _(pe):
            for n in range(4):
                if n >= 2:
                    pe.wait_ge(wholes, n - 1)
                col = (n % 2) * D + n // 2 * P
                for half in range(2):
                    for c in range(DC):
                        last = nc.tensor.matmul(ps[n % 2][:, half * HALF:(half + 1) * HALF], w[:, c, col:col + P],
                                                hT[:, c, half * HALF:(half + 1) * HALF],
                                                start=(c == 0), stop=(c == DC - 1))
                last.then_inc(projected, 1)
            for t in range(NT):
                for c in range(DC):
                    last = nc.tensor.matmul(ps_v[t // 2][:, t % 2 * D:(t % 2 + 1) * D],
                                            hT[:, c, t * P:(t + 1) * P], w[:, c, 2 * D:],
                                            start=(c == 0), stop=(c == DC - 1))
                if t % 2:
                    last.then_inc(v_ready, 1)

        @block.scalar
        def _(act):
            for n in range(4):
                act.wait_ge(projected, n + 1)
                if bias:
                    nc.scalar.activation(whole[n][:], ps[n % 2][:], ACT.Identity, bias=biases[:, n:n + 1]
                                         ).then_inc(wholes, 1)
                else:
                    nc.scalar.copy(whole[n][:], ps[n % 2][:]).then_inc(wholes, 1)
                act.wait_ge(wholes, n + 1)
                nc.scalar.copy(parts[n][0][:], whole[n][:]).then_inc(firsts, 1)
            for n in range(0 if bias else 4):
                act.wait_ge(v_ready, n + 1)
                act.wait_ge(filled, 2)
                for t in (2 * n, 2 * n + 1):
                    nc.scalar.copy(v[:, :, t, :, 0:HD],
                                   ps_v[n][:, t % 2 * D:(t % 2 + 1) * D].rearrange("p (q j d) -> p q j d", q=QUADS,
                                                                                   j=4))
            for n in range(2, 4):
                store_parts(act, n, stored_act)
            act.wait_ge(stored_act, 16 * 6)

        @block.vector
        def _(dve):
            for n in range(4):
                dve.wait_ge(firsts, n + 1)
                nc.vector.tensor_tensor(rest[n % 2][:], whole[n][:], parts[n][0][:], ALU.subtract
                                        ).then_inc(rests, 1)
                dve.wait_ge(rests, n + 1)
                nc.vector.tensor_copy(parts[n][1][:], rest[n % 2][:]).then_inc(seconds, 1)
                dve.wait_ge(seconds, n + 1)
                nc.vector.tensor_tensor(parts[n][2][:], rest[n % 2][:], parts[n][1][:], ALU.subtract
                                        ).then_inc(thirds, 1)
            for n in range(4 if bias else 0):
                dve.wait_ge(v_ready, n + 1)
                dve.wait_ge(filled, 2)
                for t in (2 * n, 2 * n + 1):
                    nc.vector.tensor_tensor(v[:, :, t, :, 0:HD],
                                            ps_v[n][:, t % 2 * D:(t % 2 + 1) * D].rearrange(
                                                "p (q j d) -> p q j d", q=QUADS, j=4),
                                            v_bias[:].rearrange("p (q j d) -> p q j d", q=QUADS, j=4), ALU.add)


def weigh_values(core, name, parts_dram, qs, ks, v, oT):
    nc = core.nc
    NP, NU = len(PIECES), len(UNITS)
    MAX_BANKS = 3
    FREE = 2
    SLOTS = 2 * NU
    PIECE_SLOTS = 18
    PARTS_AT, TURN_AT, COPY_AT = 18, 19, 9
    V_PARTS = 4
    with Stage(core, f"{name}w") as st:
        block = st.opened
        v_now = st.sb("v_now", [P, NT, 4, 32])
        piece_max = st.sb("piece_max", [P, 4, NT, 2])
        low = st.sb("low", [P, 4 * NT])
        left = st.sb("left", [P, 4 * NT])
        max_parts = st.sb("max_parts", [P, 3, 4 * NT], BF16)
        max_rows = st.sb("max_rows", [3 * 4 * NT, P], BF16)
        weights = [st.sb(f"weights{n}", [P, 2, HALF]) for n in range(4)]
        ps_max = [st.psum(f"max{n}", [P, HALF]) for n in range(MAX_BANKS)]
        ps_scores = [st.psum(f"scores{n}", [P, 2, HALF]) for n in range(2)]
        ps_out = st.psum("out", [P, HALF])

        scored, peaked, combined = st.sem("scored"), st.sem("peaked"), st.sem("combined")
        parted, part_step, max_turned = st.sem("parted"), st.sem("part_step"), st.sem("max_turned")
        max_kept, max_in, stacked = st.sem("max_kept"), st.sem("max_in"), st.sem("stacked")
        rescored, exped, added = st.sem("rescored"), st.sem("exped"), st.sem("added")
        out_copied, v_in, filled = st.sem("out_copied"), st.sem("v_in"), st.sem("filled")

        max_stored = st.sem("max_stored")
        max_dram = nc.dram_tensor(f"{st.name}_max", (3 * 4 * NT, P), BF16).ap()

        def first_query(unit):
            kt, half = UNITS[unit]
            return max(kt * P - half * HALF, 0)

        def pieces_of(s):
            if s >= PIECE_SLOTS:
                return range(0)
            return range(s * NP // PIECE_SLOTS, (s + 1) * NP // PIECE_SLOTS)

        @block.sync
        def _(sp):
            def stack(i):
                stack_parts(sp, qs, ks, parts_dram, i, stacked)
                sp.wait_ge(stacked, STACKED * i)

            def store_max(i):
                sp.wait_ge(max_kept, i + 1)
                sp.dma_start(max_dram, max_rows[:]).then_inc(max_stored, 16)
                sp.wait_ge(max_stored, 16 * i + 16)
                sp.dma_start(qs[SPLIT:WITH_MAX, 4 * i:4 * i + 4, :],
                             max_dram.rearrange("(i h t) q -> i h (t q)", i=3, h=4)).then_inc(max_in, 16)
                sp.wait_ge(max_in, 16 * i + 16)

            for i in range(QUADS):
                if i + 1 < QUADS:
                    stack(i + 1)
                store_max(i)

        @block.gpsimd
        def _(pool):
            nc.gpsimd.memset(piece_max[:], 3.0e38).then_inc(filled, 1)
            st.clear_old(pool)
            pool.wait_ge(filled, 1)
            with pool.Fori(0, QUADS) as i:
                pool.wait_ge(added, i * NU + FREE)
                for n in range(V_PARTS):
                    part = slice(n * NT // V_PARTS, (n + 1) * NT // V_PARTS)
                    nc.gpsimd.tensor_copy(v_now[:, part], v[:, bass.ds(i, 1), part].rearrange(
                        "p a t j d -> p (a t) j d")).then_inc(v_in, 1)

        @block.tensor
        def _(pe):
            pe.sem_inc(added, FREE)

            def piece(i, n):
                j, t, c = PIECES[n]
                pe.wait_ge(peaked, i * NP + (n + 1))
                a, b = c * HALF, min((c + 1) * HALF, (t + 1) * P)
                masks = b == (t + 1) * P
                to = ps_max[n % MAX_BANKS]
                last = nc.tensor.matmul(to[:, 0:b - a],
                                        qs[0:SPLIT, bass.ds(4 * i + j, 1), t * P:(t + 1) * P].rearrange(
                                            "p a t -> p (a t)"),
                                        ks[0:SPLIT, bass.ds(4 * i + j, 1), a:b].rearrange("p a t -> p (a t)"),
                                        start=True, stop=not masks)
                if masks:
                    last = nc.tensor.matmul(to[:, b - a - P:b - a], core.ident_bf[:], core.causal[:],
                                            start=False, stop=True)
                last.then_inc(scored, 1)

            def turn_max(i):
                pe.wait_ge(parted, i + 1)
                nc.tensor.transpose(ps_max[0][:].bitcast(BF16)[0:3 * 4 * NT, 0:P],
                                    max_parts[:].rearrange("p i a -> p (i a)"), core.ident_bf[:]
                                    ).then_inc(max_turned, 1)

            def scores(i, s):
                kt, half = UNITS[s // 2]
                at = first_query(s // 2)
                if s == 0:
                    pe.wait_ge(max_in, i * 16 + 16)
                pe.wait_ge(exped, i * SLOTS + (s + 1))
                for e in range(2):
                    h = bass.ds(4 * i + s % 2 * 2 + e, 1)
                    to = ps_scores[s % 2]
                    masks = kt >= 4 * half
                    last = nc.tensor.matmul(to[:, e, at:],
                                            ks[:, h, kt * P:(kt + 1) * P].rearrange("p a t -> p (a t)"),
                                            qs[:, h, half * HALF + at:(half + 1) * HALF].rearrange(
                                                "p a t -> p (a t)"),
                                            start=True, stop=not masks)
                    if masks:
                        last = nc.tensor.matmul(to[:, e, at:at + P], core.ident_bf[:], core.causal_turned[:],
                                                start=False, stop=True)
                last.then_inc(rescored, 1)

            def add_values(i, n):
                kt, half = UNITS[n]
                at = first_query(n)
                pe.wait_ge(exped, i * SLOTS + (FREE + 2 * n + 2))
                pe.wait_ge(v_in, i * V_PARTS + (kt * V_PARTS // NT + 1))
                if kt == 0:
                    pe.wait_ge(out_copied, i * 2 + (half + 1))
                for j in range(4):
                    last = nc.tensor.matmul(ps_out[32 * j:32 * j + 32, at:], v_now[:, kt, j, :],
                                            weights[(2 * n + j // 2) % 4][:, j % 2, at:],
                                            start=(kt == 0), stop=(kt == 4 * half + 3))
                last.then_inc(added, 1)

            def quad(i, ahead):
                for s in range(SLOTS):
                    pieces = pieces_of(s) if ahead else ()
                    for n in pieces[0:1]:
                        if n == 0:
                            pe.wait_ge(max_kept, i + 1)
                            pe.wait_ge(stacked, i * STACKED + STACKED)
                        piece(i + 1, n)
                    if ahead and s == TURN_AT:
                        turn_max(i + 1)
                    scores(i, s)
                    for n in pieces[1:2]:
                        piece(i + 1, n)
                    if s % 2 and s > 1:
                        add_values(i, s // 2 - 1)
                    for n in pieces[2:]:
                        piece(i + 1, n)
                add_values(i, NU - 1)

            for n in range(NP):
                piece(0, n)
            turn_max(0)
            with pe.Fori(0, QUADS - 1) as i:
                quad(i, True)
            quad(QUADS - 1, False)

        @block.scalar
        def _(act):
            act.sem_inc(exped, FREE)
            act.sem_inc(out_copied, 1)

            def weigh(i, s):
                n = s // 2
                at = first_query(n)
                act.wait_ge(rescored, i * SLOTS + (s + 1))
                act.wait_ge(added, i * NU + (n + 1))
                nc.scalar.activation(weights[s % 4][:, :, at:], ps_scores[s % 2][:, :, at:], ACT.Exp,
                                     scale=HD ** -0.5).then_inc(exped, 1)

            def copy_out(i, half):
                act.wait_ge(added, i * NU + (FREE + (NU if half else 4)))
                nc.scalar.copy(oT[:, bass.ds(i, 1), half * HALF:(half + 1) * HALF].rearrange("p a t -> p (a t)"),
                               ps_out[:]).then_inc(out_copied, 1)

            def quad(i):
                for s in range(SLOTS):
                    weigh(i, s)
                    if s == COPY_AT:
                        copy_out(i, 0)
                copy_out(i, 1)

            with act.Fori(0, QUADS) as i:
                quad(i)

        @block.vector
        def _(dve):
            dve.sem_inc(peaked, MAX_BANKS)

            def find_max(i, n):
                j, t, c = PIECES[n]
                dve.wait_ge(scored, i * NP + (n + 1))
                width = min((t + 1) * P - c * HALF, HALF)
                nc.vector.tensor_reduce(piece_max[:, j, t, c:c + 1], ps_max[n % MAX_BANKS][:, 0:width], AX, ALU.max,
                                        negate=True).then_inc(peaked, 1)

            def part_max(i):
                dve.wait_ge(peaked, i * NP + (NP + MAX_BANKS))
                nc.vector.tensor_reduce(low[:], piece_max[:].rearrange("p j t c -> p (j t) c"), AX, ALU.min
                                        ).then_inc(part_step, 1)
                dve.wait_ge(part_step, 4 * i + 1)
                nc.vector.tensor_copy(max_parts[:, 0, :], low[:]).then_inc(part_step, 1)
                dve.wait_ge(part_step, 4 * i + 2)
                nc.vector.tensor_tensor(left[:], low[:], max_parts[:, 0, :], ALU.subtract).then_inc(part_step, 1)
                dve.wait_ge(part_step, 4 * i + 3)
                nc.vector.tensor_copy(max_parts[:, 1, :], left[:]).then_inc(part_step, 1)
                dve.wait_ge(part_step, 4 * i + 4)
                nc.vector.tensor_tensor(max_parts[:, 2, :], left[:], max_parts[:, 1, :], ALU.subtract
                                        ).then_inc(parted, 1)

            def keep_max(i, first):
                dve.wait_ge(max_turned, i + 1)
                if not first:
                    dve.wait_ge(max_stored, 16 * i)
                nc.vector.tensor_copy(max_rows[:], ps_max[0][:].bitcast(BF16)[0:3 * 4 * NT, 0:P]
                                      ).then_inc(max_kept, 1)

            def quad(i):
                for s in range(SLOTS):
                    for n in pieces_of(s):
                        find_max(i + 1, n)
                    if s == PARTS_AT:
                        part_max(i + 1)
                    if s == TURN_AT:
                        keep_max(i + 1, False)

            dve.wait_ge(filled, 1)
            for n in range(NP):
                find_max(0, n)
            part_max(0)
            keep_max(0, True)
            with dve.Fori(0, QUADS - 1) as i:
                quad(i)


def project_heads(core, name, oT, out_bias, into):
    nc, x = core.nc, core.x
    BANKS = 3
    lots = [(half, q) for half in range(2) for q in range(QUADS)]
    with Stage(core, f"{name}o") as st:
        block = st.opened
        wo = st.sb("wo", [P, QUADS, D])
        o_bias = st.sb("o_bias", [P, D])
        inverse = st.sb("inverse", [P, NT, QUADS, 4])
        wide = st.sb("wide", [P, NT, QUADS, P])
        ps_sums = st.psum("sums", [P, NT, QUADS, 4])
        ps_spread = [st.psum(f"spread{n}", [P, HALF]) for n in range(BANKS)]
        ps = [st.psum(f"y{n}", [P, HALF]) for n in range(4)]
        wo_in, ready, biased = st.sem("wo_in"), st.sem("ready"), st.sem("biased")
        turned, inverted, spread, divided = st.sem("turned"), st.sem("inverted"), st.sem("spread"), st.sem("divided")
        widened = [st.sem("widened_dve"), st.sem("widened_act")]

        def widen(copy, half):
            rows = slice(4 * half, 4 * half + 4)
            copy(wide[:, rows].rearrange("p t q (j r) -> p (t q j) r", j=4),
                 inverse[:, rows].rearrange("p t q j -> p (t q j)").unsqueeze(2).broadcast_to([P, 16 * 4, 32])
                 ).then_inc(widened[half], 1)

        @block.sync
        def _(sp):
            sp.dma_start(wo[:], core.dram[f"{name}_won"]).then_inc(wo_in, 16)
            if out_bias:
                sp.dma_start(o_bias[:], core.dram[out_bias].broadcast_to([P, D])).then_inc(wo_in, 16)

        @block.gpsimd
        def _(pool):
            st.clear_old(pool)
            if out_bias:
                pool.wait_ge(wo_in, 32)
                nc.gpsimd.tensor_tensor(x[:], x[:], o_bias[:].unsqueeze(1).broadcast_to([P, NT, D]), ALU.add
                                        ).then_inc(biased, 1)

        @block.tensor
        def _(pe):
            for t in range(NT):
                for q in range(QUADS):
                    last = nc.tensor.matmul(ps_sums[:, t, q, :], oT[:, q, t * P:(t + 1) * P],
                                            core.ident[:, HD::32], start=True, stop=True)
            last.then_inc(turned, 1)
            for n, (half, q) in enumerate(lots):
                if q == 0:
                    pe.wait_ge(widened[half], 1)
                if n >= BANKS:
                    pe.wait_ge(divided, n - BANKS + 1)
                for i in range(4):
                    last = nc.tensor.transpose(ps_spread[n % BANKS][:, i * P:(i + 1) * P],
                                               wide[:, 4 * half + i, q, :], core.ident[:])
                last.then_inc(spread, 1)
            pe.wait_ge(wo_in, 32 if out_bias else 16)
            for t in range(NT):
                pe.wait_ge(divided, QUADS * (t // 4 + 1))
                for q in range(QUADS):
                    last = nc.tensor.matmul(ps[t // 2][:, t % 2 * D:(t % 2 + 1) * D], oT[:, q, t * P:(t + 1) * P],
                                            wo[:, q, :], start=(q == 0), stop=(q == QUADS - 1))
                if t % 2:
                    last.then_inc(ready, 1)

        @block.scalar
        def _(act):
            act.wait_ge(inverted, 1)
            widen(nc.scalar.copy, 1)

        @block.vector
        def _(dve):
            dve.wait_ge(turned, 1)
            nc.vector.reciprocal(inverse[:], ps_sums[:]).then_inc(inverted, 1)
            dve.wait_ge(inverted, 1)
            widen(nc.vector.tensor_copy, 0)
            for n, (half, q) in enumerate(lots):
                dve.wait_ge(spread, n + 1)
                part = oT[:, q, half * HALF:(half + 1) * HALF]
                nc.vector.tensor_tensor(part, part, ps_spread[n % BANKS][:], ALU.mult).then_inc(divided, 1)
            if out_bias:
                dve.wait_ge(biased, 1)
            for n in range(4):
                dve.wait_ge(ready, n + 1)
                src = ps[n][:].rearrange("p (t d) -> p t d", t=2)
                if into is not None:
                    nc.vector.tensor_copy(into[:, 2 * n:2 * n + 2, :], src)
                else:
                    two = x[:, 2 * n:2 * n + 2, :]
                    nc.vector.tensor_tensor(two, two, src, ALU.add)


STEPS = "s0 s1 q0 s2 q1 o0 s3 k0 o1 s4 k1 o2 s5 o3 s6 m0 v0 s7 t0 v1 s8 s9 s10 b0 s11 b1 o4 o5 o6 o7".split()
MAKES = [s for s in STEPS if s[0] in "qkvmtb"]
QUARTER = P // 4


def capped_attention(core, name, heads, softcap):
    nc, x, hT = core.nc, core.x, core.hT
    scale = P ** -0.5 / softcap
    NU = len(UNITS)
    with ExitStack() as layer:
        rows = layer.enter_context(nc.sbuf_tensor(f"{name}_rows", [P, NT, heads * P], F32))
        wo = layer.enter_context(nc.sbuf_tensor(f"{name}_wo", [P, heads, D], F32))
        with Stage(core, name) as st:
            block = st.opened
            w = [st.sb(f"w{n}", [P, DC, 3 * P]) for n in range(2)]
            q, k = [st.sb(f"q{n}", [P, TOK]) for n in range(2)], [st.sb(f"k{n}", [P, TOK]) for n in range(2)]
            v = [st.sb(f"v{n}", [P, NT, P + 1]) for n in range(2)]
            squares = st.sb("squares", [P, 2, TOK])
            means = st.sb("means", [P, HALF])
            factors = st.sb("factors", [P, 2])
            turned, power = st.sb("turned", [P, 2 * NT]), st.sb("power", [P, 2 * NT])
            inverse = [st.sb(f"inverse{n}", [P, 2 * NT]) for n in range(2)]
            tanhs = [st.sb(f"tanh{n}", [P, HALF]) for n in range(3)]
            weights = [st.sb(f"weights{u}", [P, HALF]) for u in range(NU)]
            sum_inverse = st.sb("sum_inverse", [P, NT])
            keep = st.sb("keep", [P, P])
            turns, pair = st.sb("turns", [P, 4, heads]), st.sb("pair", [P, 2, heads])
            ps_make = [st.psum(f"make{n}", [P, HALF]) for n in range(2)]
            ps_scores = [st.psum(f"scores{n}", [P, HALF]) for n in range(3)]
            ps_out = [st.psum(f"out{n}", [P, HALF]) for n in range(2)]
            ps_sums = st.psum("sums", [P, HALF])

            w_in = [st.sem("w_in_even"), st.sem("w_in_odd")]
            wo_in, turns_in = st.sem("wo_in"), st.sem("turns_in")
            made, kept, filled = st.sem("made"), st.sem("kept"), st.sem("filled")
            squares_summed, meaned, inverted = st.sem("squares_summed"), st.sem("meaned"), st.sem("inverted")
            scored, capped, exped, masked = st.sem("scored"), st.sem("capped"), st.sem("exped"), st.sem("masked")
            summed, sum_inverted, scaled = st.sem("summed"), st.sem("sum_inverted"), st.sem("scaled")
            pair_step, squared = st.sem("pair_step"), st.sem("squared")
            means_turned, turned_kept = st.sem("means_turned"), st.sem("turned_kept")

            TWO, THREE, TILES = 2, 3, NT
            made_order = [s for s in MAKES if s[0] not in "mt"]
            NM = len(made_order)

            def span(unit):
                kt, half = UNITS[unit]
                return kt, half, max(kt * P - half * HALF, 0)

            @block.sync
            def _(sp):
                for h in range(heads):
                    if h >= 2:
                        sp.wait_ge(made, (h - 1) * NM - 2)
                    sp.dma_start(w[h % 2][:], core.dram[f"{name}_w"][h]).then_inc(w_in[h % 2], 16)
                    if h == 0:
                        sp.dma_start(turns[:], core.dram[f"{name}_turns"]).then_inc(turns_in, 16)
                sp.dma_start(wo[:], core.dram[f"{name}_wo"]).then_inc(wo_in, 16)
                sp.wait_ge(wo_in, 16)

            @block.gpsimd
            def _(pool):
                nc.gpsimd.memset(keep[:], 1.0).then_inc(filled, 1)
                nc.gpsimd.memset(power[:], -0.5).then_inc(filled, 1)
                pool.wait_ge(filled, 2)
                for n, factor in ((0, 1.0), (1, scale ** -2)):
                    part = slice(n * P // 2, (n + 1) * P // 2)
                    nc.gpsimd.memset(factors[part, 0:1], factor / P).then_inc(filled, 1)
                    nc.gpsimd.memset(factors[part, 1:2], factor * 1e-6).then_inc(filled, 1)
                    pool.wait_ge(filled, 4 + 2 * n)
                for n in range(2):
                    nc.gpsimd.memset(v[n][:, :, P:P + 1], 1.0).then_inc(filled, 1)
                pool.wait_ge(filled, 8)
                nc.gpsimd.affine_select(out=keep[:], in_=keep[:], compare_op=ALU.is_ge, fill=0.0, base=0,
                                        pattern=[[1, P]], channel_multiplier=-1).then_inc(filled, 1)
                st.clear_old(pool)
                pool.wait_ge(filled, 9)

                def invert(h, e):
                    pool.wait_ge(turned_kept, h + 1)
                    nc.gpsimd.tensor_tensor(inverse[e][:], turned[:], power[:], ALU.pow).then_inc(inverted, 1)

                def mask(h, t):
                    u = UNITS.index((t, t // 4))
                    pool.wait_ge(exped, h * NU + (u + 1 + THREE))
                    block_at = span(u)[2]
                    to = weights[u][:, block_at:block_at + P]
                    nc.gpsimd.tensor_tensor(to, to, keep[:], ALU.mult).then_inc(masked, 1)

                def square(h, e, step):
                    n, half = made_order.index(step), int(step[1])
                    part = slice(half * HALF, (half + 1) * HALF)
                    src = (q if step[0] == "q" else k)[e]
                    pool.wait_ge(kept, h * NM + (n + 1 + TWO))
                    nc.gpsimd.tensor_tensor(squares[:, "qk".index(step[0]), part], src[:, part], src[:, part],
                                            ALU.mult).then_inc(squared, 1)

                def head(h, e, more):
                    for step in STEPS:
                        if step[0] == "s":
                            kt, half = UNITS[int(step[1:])]
                            if kt >= 4 * half:
                                mask(h, kt)
                        elif more and step[0] in "qk":
                            square(h + 1, 1 - e, step)
                        elif more and step[0] == "t":
                            invert(h + 1, 1 - e)

                for step in MAKES[0:4]:
                    square(0, 0, step)
                invert(0, 0)
                with pool.Fori(0, heads // 2 - 1) as g:
                    head(2 * g, 0, True)
                    head(2 * g + 1, 1, True)
                head(heads - 2, 0, True)
                head(heads - 1, 1, False)

            @block.tensor
            def _(pe):
                pe.sem_inc(summed, TILES)

                def make(h, e, step):
                    kind, half = step[0], int(step[1])
                    if kind == "m":
                        pe.wait_ge(squared, h * 4 + 4)
                        for n in range(4):
                            last = nc.tensor.matmul(ps_sums[n * QUARTER:(n + 1) * QUARTER, :],
                                                    core.ones[:, 0:QUARTER],
                                                    squares[:, n // 2, n % 2 * HALF:(n % 2 + 1) * HALF],
                                                    start=True, stop=True)
                        last.then_inc(squares_summed, 1)
                        return
                    if kind == "t":
                        pe.wait_ge(meaned, h + 1)
                        for i in range(4):
                            last = nc.tensor.matmul(ps_sums[:, 4 * i:4 * i + 4], means[:, i * P:(i + 1) * P],
                                                    core.ident[:, ::QUARTER], start=True, stop=True)
                        last.then_inc(means_turned, 1)
                        return
                    n = made_order.index(step)
                    pe.wait_ge(kept, h * NM + (n - 2 + 1 + TWO))
                    to = ps_make[n % 2]
                    if step == "q0":
                        pe.wait_ge(w_in[e], h * 8 + (16 - 8 * e))
                    if kind == "b":
                        pe.wait_ge(inverted, h + 1)
                    for c in range(DC if kind in "qk" else 0):
                        at = "qk".index(kind) * P
                        last = nc.tensor.matmul(to[:], w[e][:, c, at:at + P], hT[:, c, half * HALF:(half + 1) * HALF],
                                                start=(c == 0), stop=(c == DC - 1))
                    for i in range(4 if kind in "vb" else 0):
                        t = 4 * half + i
                        part = to[:, i * P:(i + 1) * P]
                        if kind == "b":
                            last = nc.tensor.matmul(part, inverse[e][:, t:t + 1].broadcast_to([P, P]), core.ident[:],
                                                    start=True, stop=True)
                        for c in range(DC if kind == "v" else 0):
                            last = nc.tensor.matmul(part, hT[:, c, t * P:(t + 1) * P], w[e][:, c, 2 * P:],
                                                    start=(c == 0), stop=(c == DC - 1))
                    last.then_inc(made, 1)

                def score(h, e, u):
                    kt, half, at = span(u)
                    if u == 0:
                        pe.wait_ge(kept, h * NM + (NM + TWO))
                    pe.wait_ge(capped, h * NU + (u - 3 + 1 + THREE))
                    nc.tensor.matmul(ps_scores[u % 3][:, at:], k[e][:, kt * P:(kt + 1) * P],
                                     q[e][:, half * HALF + at:(half + 1) * HALF], start=True, stop=True
                                     ).then_inc(scored, 1)

                def output(h, e, t):
                    pe.wait_ge(masked, h * NT + (t + 1))
                    pe.wait_ge(scaled, h * NT + (t - 2 + 1 + TWO))
                    at = t % 4 * P
                    for kt in range(t + 1):
                        last = nc.tensor.matmul(ps_out[t % 2][:, 0:P + 1],
                                                weights[UNITS.index((kt, t // 4))][:, at:at + P], v[e][:, kt, :],
                                                start=(kt == 0), stop=(kt == t))
                    last.then_inc(summed, 1)

                def head(h, e, more):
                    for step in STEPS:
                        if step[0] == "s":
                            score(h, e, int(step[1:]))
                        elif step[0] == "o":
                            output(h, e, int(step[1:]))
                        elif more:
                            make(h + 1, 1 - e, step)

                pe.wait_ge(filled, 9)
                for step in MAKES:
                    make(0, 0, step)
                with pe.Fori(0, heads // 2 - 1) as g:
                    head(2 * g, 0, True)
                    head(2 * g + 1, 1, True)
                head(heads - 2, 0, True)
                head(heads - 1, 1, False)

            @block.scalar
            def _(act):
                for s in (capped, exped):
                    act.sem_inc(s, THREE)

                def cap(h, e, u):
                    kt, half, at = span(u)
                    act.wait_ge(scored, h * NU + (u + 1))
                    if u == 0:
                        act.wait_ge(inverted, h + 1)
                    act.wait_ge(exped, h * NU + (u - 3 + 1 + THREE))
                    nc.scalar.activation(tanhs[u % 3][:, at:], ps_scores[u % 3][:, at:], ACT.Tanh,
                                         scale=inverse[e][:, NT + kt:NT + kt + 1]).then_inc(capped, 1)

                def weigh(h, u):
                    kt, half, at = span(u)
                    act.wait_ge(capped, h * NU + (u + 1 + THREE))
                    act.wait_ge(summed, h * NT + (TILES - 4 if u < 4 else TILES))
                    nc.scalar.activation(weights[u][:, at:], tanhs[u % 3][:, at:], ACT.Exp, scale=softcap
                                         ).then_inc(exped, 1)

                def head(h, e):
                    for u in range(NU + 1):
                        if u < NU:
                            cap(h, e, u)
                        if u >= 1:
                            weigh(h, u - 1)

                with act.Fori(0, heads // 2) as g:
                    head(2 * g, 0)
                    head(2 * g + 1, 1)

            @block.vector
            def _(dve):
                for s in (kept, scaled):
                    dve.sem_inc(s, TWO)
                dve.wait_ge(turns_in, 16)
                pairs = linker(dve, pair_step)
                for n in range(2):
                    pairs(nc.vector.tensor_tensor(pair[:, n], turns[:, n], turns[:, n], ALU.mult))
                pairs(nc.vector.tensor_tensor(pair[:, 0], pair[:, 0], pair[:, 1], ALU.add))
                for n in range(2):
                    pairs(nc.vector.tensor_tensor(pair[:, 0], pair[:, 0], turns[:, 2 + n], ALU.mult))

                def keep_made(h, e, step):
                    kind, half = step[0], int(step[1])
                    if kind == "m":
                        dve.wait_ge(squares_summed, h + 1)
                        nc.vector.tensor_scalar(means[:], ps_sums[:], factors[:, 0:1], factors[:, 1:2],
                                                ALU.mult, ALU.add).then_inc(meaned, 1)
                        return
                    if kind == "t":
                        dve.wait_ge(means_turned, h + 1)
                        nc.vector.tensor_copy(turned[:].rearrange("p (n i) -> p n i", n=4),
                                              ps_sums[:, 0:2 * NT].rearrange("p (i n) -> p n i", n=4)
                                              ).then_inc(turned_kept, 1)
                        return
                    n = made_order.index(step)
                    src = ps_make[n % 2]
                    part = slice(half * HALF, (half + 1) * HALF)
                    dve.wait_ge(made, h * NM + (n + 1))
                    if kind == "q":
                        nc.vector.tensor_copy(q[e][:, part], src[:]).then_inc(kept, 1)
                    elif kind == "k":
                        nc.vector.tensor_copy(k[e][:, part], src[:]).then_inc(kept, 1)
                    elif kind == "v":
                        nc.vector.tensor_copy(v[e][:, 4 * half:4 * half + 4, 0:P],
                                              src[:].rearrange("p (t c) -> p t c", t=4)).then_inc(kept, 1)
                    else:
                        dve.wait_ge(kept, h * NM + (2 + TWO))
                        nc.vector.scalar_tensor_tensor(q[e][:, part], q[e][:, part], pair[:, 0, bass.ds(h, 1)], src[:],
                                                       ALU.mult, ALU.mult).then_inc(kept, 1)

                def scale_output(h, t):
                    dve.wait_ge(summed, h * NT + (t + 1 + TILES))
                    nc.vector.reciprocal(sum_inverse[:, t:t + 1], ps_out[t % 2][:, P:P + 1]).then_inc(sum_inverted, 1)
                    dve.wait_ge(sum_inverted, h * NT + (t + 1))
                    nc.vector.tensor_scalar(rows[:, t, bass.ds(h * P, P)], ps_out[t % 2][:, 0:P],
                                            sum_inverse[:, t:t + 1], None, ALU.mult).then_inc(scaled, 1)

                def head(h, e, more):
                    for step in STEPS:
                        if step[0] == "o":
                            scale_output(h, int(step[1:]))
                        elif step[0] != "s" and more:
                            keep_made(h + 1, 1 - e, step)

                for step in MAKES:
                    keep_made(0, 0, step)
                with dve.Fori(0, heads // 2 - 1) as g:
                    head(2 * g, 0, True)
                    head(2 * g + 1, 1, True)
                head(heads - 2, 0, True)
                head(heads - 1, 1, False)
        project_rows(core, name, rows, wo, heads)


def project_rows(core, name, rows, wo, chunks):
    nc, x = core.nc, core.x
    with Stage(core, f"{name}o") as st:
        block = st.opened
        turned = [st.sb(f"turned{n}", [P, HALF]) for n in range(3)]
        ps_turn = [st.psum(f"turn{n}", [P, HALF]) for n in range(3)]
        ps_y = [st.psum(f"y{n}", [P, HALF]) for n in range(2)]
        rows_turned, ready = st.sem("rows_turned"), st.sem("ready")
        kept = [st.sem("kept_dve"), st.sem("kept_act")]
        added = st.sem("added")
        lots = [(t, a) for t in range(NT) for a in range(0, chunks, 4)]
        NL = len(lots)

        def wait_kept(engine, n):
            engine.wait_ge(kept[n % 2], n // 2 + 1)

        @block.gpsimd
        def _(pool):
            st.clear_old(pool)

        @block.tensor
        def _(pe):
            for n in range(NL + 2):
                if n < NL:
                    t, a = lots[n]
                    if n >= 3:
                        wait_kept(pe, n - 3)
                    for c in range(4):
                        last = nc.tensor.transpose(ps_turn[n % 3][:, c * P:(c + 1) * P],
                                                   rows[:, t, (a + c) * P:(a + c + 1) * P], core.ident[:])
                    last.then_inc(rows_turned, 1)
                if n >= 2:
                    t, a = lots[n - 2]
                    wait_kept(pe, n - 2)
                    if a == 0 and t >= 2:
                        pe.wait_ge(added, t - 1)
                    for c in range(4):
                        last = nc.tensor.matmul(ps_y[t % 2][:, 0:D], turned[(n - 2) % 3][:, c * P:(c + 1) * P],
                                                wo[:, a + c, :], start=(a + c == 0), stop=(a + c == chunks - 1))
                    last.then_inc(ready, 1)

        def copy_lot(engine, copy, n):
            engine.wait_ge(rows_turned, n + 1)
            if n >= 3:
                engine.wait_ge(ready, n - 2)
            copy(turned[n % 3][:], ps_turn[n % 3][:]).then_inc(kept[n % 2], 1)

        @block.scalar
        def _(act):
            for n in range(1, NL, 2):
                copy_lot(act, nc.scalar.copy, n)

        @block.vector
        def _(dve):
            per = chunks // 4
            for n in range(0, NL, 2):
                copy_lot(dve, nc.vector.tensor_copy, n)
                t = n // per - 1
                if n % per == per - 2 and t >= 0:
                    dve.wait_ge(ready, (t + 1) * per)
                    nc.vector.tensor_tensor(x[:, t, :], x[:, t, :], ps_y[t % 2][:, 0:D], ALU.add).then_inc(added, 1)
            dve.wait_ge(ready, NL)
            nc.vector.tensor_tensor(x[:, NT - 1, :], x[:, NT - 1, :], ps_y[(NT - 1) % 2][:, 0:D], ALU.add)


ROW_ORDER = (0, 2, 4, 6, 7, 5, 3, 1)
MADE = ("q0", "q1", "k0", "k1", "v0", "v1")
MAKE_IN = {0: 0, 1: 1, 2: 2, 5: 3, 6: 4, 7: 5}


def wide_attention(core, name, heads, scale):
    nc, hT = core.nc, core.hT
    NM = len(MADE)
    seconds = [sum(1 for t in ROW_ORDER[:i] if t >= 4) for i in range(NT + 1)]
    NS = seconds[NT]
    NB = NT + NS
    with ExitStack() as layer:
        rows = layer.enter_context(nc.sbuf_tensor(f"{name}_rows", [P, NT, heads * P], F32))
        wo = layer.enter_context(nc.sbuf_tensor(f"{name}_wo", [P, heads, D], F32))
        with Stage(core, name) as st:
            block = st.opened
            w = [st.sb(f"w{n}", [P, DC, 3 * P]) for n in range(2)]
            q, k = [st.sb(f"q{n}", [P, TOK]) for n in range(2)], [st.sb(f"k{n}", [P, TOK]) for n in range(2)]
            v = [st.sb(f"v{n}", [P, NT, P]) for n in range(2)]
            probs = [st.sb(f"probs{n}", [P, TOK]) for n in range(2)]
            probsT = [st.sb(f"probsT{n}", [P, TOK]) for n in range(2)]
            negmax, row_sum, inverse = st.sb("negmax", [P, NT]), st.sb("row_sum", [P, NT]), st.sb("inverse", [P, NT])
            ps_scores = [st.psum(f"scores{n}", [P, TOK]) for n in range(2)]
            ps_turn = [st.psum(f"turn{n}", [P, HALF]) for n in range(2)]
            ps_out, ps_make = st.psum("out", [P, HALF]), st.psum("make", [P, HALF])

            w_in = [st.sem("w_in_even"), st.sem("w_in_odd")]
            wo_in, made, kept = st.sem("wo_in"), st.sem("made"), st.sem("kept")
            scored, peaked, maxed, exped = st.sem("scored"), st.sem("peaked"), st.sem("maxed"), st.sem("exped")
            turned, first_kept, second_kept = st.sem("turned"), st.sem("first_kept"), st.sem("second_kept")
            summed, inverted, scaled = st.sem("summed"), st.sem("inverted"), st.sem("scaled")

            ONE, TWO = 1, 2

            def width(i):
                return (ROW_ORDER[i] + 1) * P

            def banks(i):
                return i + 1 + seconds[i + 1] if i >= 0 else banks(i + NT) - NB

            def items_of(h, slot, lag, first):
                if slot >= lag:
                    return h, slot - lag
                return (None if first else h - 1), slot - lag + NT

            @block.sync
            def _(sp):
                for h in range(heads):
                    if h >= 2:
                        sp.wait_ge(made, (h - 1) * NM)
                    sp.dma_start(w[h % 2][:], core.dram[f"{name}_w"][h]).then_inc(w_in[h % 2], 16)
                sp.dma_start(wo[:], core.dram[f"{name}_wo"]).then_inc(wo_in, 16)
                sp.wait_ge(wo_in, 16)

            @block.gpsimd
            def _(pool):
                st.clear_old(pool)

            @block.tensor
            def _(pe):
                pe.sem_inc(summed, TWO)
                pe.sem_inc(turned, NB)

                def make(h, e, n):
                    kind, half = MADE[n][0], int(MADE[n][1])
                    if n == 0:
                        pe.wait_ge(w_in[e], h * 8 + (16 - 8 * e))
                    pe.wait_ge(kept, h * NM + (n + ONE))
                    for c in range(DC if kind in "qk" else 0):
                        at = "qk".index(kind) * P
                        last = nc.tensor.matmul(ps_make[:], w[e][:, c, at:at + P],
                                                hT[:, c, half * HALF:(half + 1) * HALF],
                                                start=(c == 0), stop=(c == DC - 1))
                    for i in range(4 if kind == "v" else 0):
                        t = 4 * half + i
                        for c in range(DC):
                            last = nc.tensor.matmul(ps_make[:, i * P:(i + 1) * P], hT[:, c, t * P:(t + 1) * P],
                                                    w[e][:, c, 2 * P:], start=(c == 0), stop=(c == DC - 1))
                    last.then_inc(made, 1)

                def score(h, e, i):
                    t = ROW_ORDER[i]
                    if i == 0:
                        pe.wait_ge(kept, h * NM + (4 + ONE))
                    pe.wait_ge(exped, h * NT + (i - 2 + 1 + TWO))
                    for a in range(0, width(i), HALF):
                        b = min(a + HALF, width(i))
                        nc.tensor.matmul(ps_scores[i % 2][:, a:b], q[e][:, t * P:(t + 1) * P], k[e][:, a:b],
                                         start=True, stop=b < width(i))
                    nc.tensor.matmul(ps_scores[i % 2][:, t * P:(t + 1) * P], core.ident_bf[:], core.causal[:],
                                     start=False, stop=True).then_inc(scored, 1)

                def turn(h, i):
                    pe.wait_ge(exped, h * NT + (i + 1 + TWO))
                    for c in range(width(i) // P):
                        if c == 0:
                            pe.wait_ge(first_kept, h * NT + (i + ONE))
                        if c == 4:
                            pe.wait_ge(second_kept, h * NS + (seconds[i] + ONE))
                        last = nc.tensor.transpose(ps_turn[c // 4][:, c % 4 * P:(c % 4 + 1) * P],
                                                   probs[i % 2][:, c * P:(c + 1) * P], core.ident[:])
                        if c == 3 and width(i) > HALF:
                            last.then_inc(turned, 1)
                    last.then_inc(turned, 1)

                def weigh(h, e, i):
                    if i == 0:
                        pe.wait_ge(kept, h * NM + (NM + ONE))
                    pe.wait_ge(first_kept, h * NT + (i + 1 + ONE))
                    if width(i) > HALF:
                        pe.wait_ge(second_kept, h * NS + (seconds[i + 1] + ONE))
                    pe.wait_ge(scaled, h * NT + (i + ONE))
                    for c in range(width(i) // P):
                        last = nc.tensor.matmul(ps_out[:, 0:P], probsT[i % 2][:, c * P:(c + 1) * P], v[e][:, c, :],
                                                start=(c == 0), stop=(c == width(i) // P - 1))
                    last.then_inc(summed, 1)

                def head(h, e, first, more):
                    for s in range(NT):
                        score(h, e, s)
                        if more and s in MAKE_IN:
                            make(h + 1, 1 - e, MAKE_IN[s])
                        to, i = items_of(h, s, 1, first)
                        if to is not None:
                            turn(to, i)
                        to, i = items_of(h, s, 2, first)
                        if to is not None:
                            weigh(to, e if s >= 2 else 1 - e, i)

                for n in range(NM):
                    make(0, 0, n)
                head(0, 0, True, True)
                with pe.Fori(0, heads // 2 - 1) as g:
                    head(2 * g + 1, 1, False, True)
                    head(2 * g + 2, 0, False, True)
                head(heads - 1, 1, False, False)
                turn(heads - 1, NT - 1)
                weigh(heads - 1, 1, NT - 2)
                weigh(heads - 1, 1, NT - 1)

            @block.scalar
            def _(act):
                act.sem_inc(exped, TWO)
                act.sem_inc(first_kept, ONE)
                act.sem_inc(kept, ONE)

                def keep_made(h, e, n):
                    kind, half = MADE[n][0], int(MADE[n][1])
                    act.wait_ge(made, h * NM + (n + 1))
                    if kind == "v":
                        to, src = v[e][:, 4 * half:4 * half + 4, :], ps_make[:].rearrange("p (t c) -> p t c", t=4)
                    else:
                        to, src = (q if kind == "q" else k)[e][:, half * HALF:(half + 1) * HALF], ps_make[:]
                    nc.scalar.copy(to, src).then_inc(kept, 1)

                def exp(h, i):
                    act.wait_ge(maxed, h * NT + (i + 1))
                    act.wait_ge(turned, h * NB + (banks(i - 2) + NB))
                    nc.scalar.activation(probs[i % 2][:, 0:width(i)], ps_scores[i % 2][:, 0:width(i)], ACT.Exp,
                                         bias=negmax[:, i:i + 1], scale=scale, accum_out=row_sum[:, i:i + 1]
                                         ).then_inc(exped, 1)

                def keep_first(h, i):
                    act.wait_ge(turned, h * NB + (banks(i) - (width(i) > HALF) + NB))
                    act.wait_ge(summed, h * NT + (i - 2 + 1 + TWO))
                    b = min(width(i), HALF)
                    nc.scalar.copy(probsT[i % 2][:, 0:b], ps_turn[0][:, 0:b]).then_inc(first_kept, 1)

                def head(h, e, first, more):
                    for s in range(NT):
                        exp(h, s)
                        if more and s in MAKE_IN:
                            keep_made(h + 1, 1 - e, MAKE_IN[s])
                        to, i = items_of(h, s, 1, first)
                        if to is not None:
                            keep_first(to, i)

                for n in range(NM):
                    keep_made(0, 0, n)
                head(0, 0, True, True)
                with act.Fori(0, heads // 2 - 1) as g:
                    head(2 * g + 1, 1, False, True)
                    head(2 * g + 2, 0, False, True)
                head(heads - 1, 1, False, False)
                keep_first(heads - 1, NT - 1)

            @block.vector
            def _(dve):
                dve.sem_inc(second_kept, ONE)
                dve.sem_inc(scaled, ONE)

                def find_max(h, i):
                    dve.wait_ge(scored, h * NT + (i + 1))
                    nc.vector.tensor_reduce(negmax[:, i:i + 1], ps_scores[i % 2][:, 0:width(i)], AX, ALU.max,
                                            negate=True).then_inc(peaked, 1)
                    dve.wait_ge(peaked, h * NT + (i + 1))
                    nc.vector.tensor_scalar(negmax[:, i:i + 1], negmax[:, i:i + 1], scale, None, ALU.mult
                                            ).then_inc(maxed, 1)

                def keep_second(h, i):
                    if width(i) > HALF:
                        dve.wait_ge(turned, h * NB + (banks(i) + NB))
                        dve.wait_ge(summed, h * NT + (i - 2 + 1 + TWO))
                        nc.vector.tensor_copy(probsT[i % 2][:, HALF:width(i)], ps_turn[1][:, 0:width(i) - HALF]
                                              ).then_inc(second_kept, 1)
                    dve.wait_ge(exped, h * NT + (i + 1 + TWO))
                    nc.vector.reciprocal(inverse[:, i:i + 1], row_sum[:, i:i + 1]).then_inc(inverted, 1)

                def scale_output(h, i):
                    dve.wait_ge(inverted, h * NT + (i + 1))
                    dve.wait_ge(summed, h * NT + (i + 1 + TWO))
                    nc.vector.tensor_scalar(rows[:, ROW_ORDER[i], bass.ds(h * P, P)], ps_out[:, 0:P],
                                            inverse[:, i:i + 1], None, ALU.mult).then_inc(scaled, 1)

                def head(h, first):
                    for s in range(NT):
                        find_max(h, s)
                        to, i = items_of(h, s, 1, first)
                        if to is not None:
                            keep_second(to, i)
                        to, i = items_of(h, s, 2, first)
                        if to is not None:
                            scale_output(to, i)

                head(0, True)
                with dve.Fori(0, heads // 2 - 1) as g:
                    head(2 * g + 1, False)
                    head(2 * g + 2, False)
                head(heads - 1, False)
                keep_second(heads - 1, NT - 1)
                scale_output(heads - 1, NT - 2)
                scale_output(heads - 1, NT - 1)
        project_rows(core, name, rows, wo, heads)


def gated_feed_forward(core, name, tiles, body, source=None, scaled=False, low_rank=None, combine=None,
                       down_scale=None):
    nc, x = core.nc, core.x
    hT = source if source is not None else core.hT
    UNITS = 2 * body
    TURNS = tiles // body
    FREE = 4
    wide = 3 * D + (P if low_rank is not None else 0) + (2 if scaled else 0)
    low0 = 3 * D
    scale0 = low0 + (P if low_rank is not None else 0)

    with Stage(core, name) as st:
        block = st.opened
        w = [st.sb(f"w{n}", [P, wide]) for n in range(2)]
        gate = [st.sb(f"gate{n}", [P, HALF]) for n in range(2)]
        inner = [st.sb(f"inner{n}", [P, HALF]) for n in range(2)]
        zeros = st.sb("zeros", [P, HALF], BF16)
        if combine is not None:
            weight = [st.sb(f"weight{n}", [P, TOK]) for n in range(2)]
        if down_scale:
            down_by = st.sb("down_by", [P, D])
        ps_gate = [st.psum(f"gate{n}", [P, HALF]) for n in range(2)]
        ps_up = [st.psum(f"up{n}", [P, HALF]) for n in range(2)]
        ps_out = [st.psum(f"out{n}", [P, HALF]) for n in range(4)]

        w_in = [st.sem(f"w_in{n}") for n in range(2)]
        weight_in = [st.sem(f"weight_in{n}") for n in range(2)]
        zeroed, consts_in, opened = st.sem("zeroed"), st.sem("consts_in"), st.sem("opened")
        gated_up, silued, weighted = st.sem("gated_up"), st.sem("silued"), st.sem("weighted")
        multiplied, lowered, finished = st.sem("multiplied"), st.sem("lowered"), st.sem("finished")

        @block.sync
        def _(sp):
            if down_scale:
                sp.dma_start(down_by[:], core.dram[down_scale].broadcast_to([P, D])).then_inc(consts_in, 16)
            with sp.Fori(0, TURNS) as k:
                for b in range(body):
                    sp.wait_ge(lowered, k * UNITS + (2 * b + 2))
                    sp.dma_start(w[b % 2][:], core.dram[f"{name}_w"][bass.ds(k * body + b, 1)].rearrange(
                        "a p n -> (a p) n")).then_inc(w_in[b % 2], 16)
                    if combine is not None:
                        row, left, at = b * P, P, 0
                        while left:
                            e, n = row // 96, min(left, 96 - row % 96)
                            src = combine[bass.ds(k * (body * P // 96) + e, 1)].broadcast_to([n, TOK])
                            sp.dma_start(weight[b % 2][at:at + n, :], src).then_inc(weight_in[b % 2], 16)
                            row, left, at = row + n, left - n, at + n

        @block.gpsimd
        def _(pool):
            nc.gpsimd.memset(zeros[:], 0.0).then_inc(zeroed, 1)
            st.clear_old(pool)
            if combine is not None:
                with pool.Fori(0, TURNS) as k:
                    for u in range(UNITS):
                        b, half = u // 2, u % 2
                        pool.wait_ge(silued, k * UNITS + (u + 1))
                        pool.wait_ge(weight_in[b % 2], k * (32 * body // 2) + 32 * (b // 2 + 1))
                        nc.gpsimd.tensor_tensor(gate[u % 2][:], gate[u % 2][:],
                                                weight[b % 2][:, half * HALF:(half + 1) * HALF], ALU.mult
                                                ).then_inc(weighted, 1)

        @block.tensor
        def _(pe):
            pe.sem_inc(lowered, FREE)
            pe.wait_ge(zeroed, 1)
            for n in range(4):
                nc.tensor.matmul(ps_out[n][:], zeros[:, 0:P], zeros[:], start=True, stop=False)

            def gate_and_up(k, u):
                b, half = u // 2, u % 2
                tokens = slice(half * HALF, (half + 1) * HALF)
                pe.wait_ge(w_in[b % 2], k * (16 * body // 2) + 16 * (b // 2 + 1))
                pe.wait_ge(multiplied, k * UNITS + (u + FREE - 1))
                for c in range(DC):
                    nc.tensor.matmul(ps_gate[u % 2][:], w[b % 2][:, c * P:(c + 1) * P], hT[:, c, tokens],
                                     start=(c == 0), stop=(c == DC - 1 and low_rank is None))
                if low_rank is not None:
                    nc.tensor.matmul(ps_gate[u % 2][:], w[b % 2][0:16, low0:low0 + P], low_rank[:, tokens],
                                     start=False, stop=True)
                for c in range(DC):
                    last = nc.tensor.matmul(ps_up[u % 2][:], w[b % 2][:, D + c * P:D + (c + 1) * P],
                                            hT[:, c, tokens], start=(c == 0), stop=(c == DC - 1))
                last.then_inc(gated_up, 1)

            def down(k, u):
                b, half = u // 2, u % 2
                pe.wait_ge(multiplied, k * UNITS + (u + FREE + 1))
                for i in range(4):
                    t = 4 * half + i
                    last = nc.tensor.matmul(ps_out[t // 2][:, t % 2 * D:(t % 2 + 1) * D],
                                            inner[u % 2][:, i * P:(i + 1) * P], w[b % 2][:, 2 * D:3 * D],
                                            start=False, stop=False, skip_group_check=True)
                last.then_inc(lowered, 1)

            with pe.Fori(0, TURNS) as k:
                for u in range(UNITS):
                    gate_and_up(k, u)
                    if u:
                        down(k, u - 1)
                down(k, UNITS - 1)
            for n in range(4):
                last = nc.tensor.matmul(ps_out[n][:], zeros[:, 0:P], zeros[:], start=False, stop=True)
            last.then_inc(finished, 1)

        @block.scalar
        def _(act):
            with act.Fori(0, TURNS) as k:
                for u in range(UNITS):
                    b = u // 2
                    act.wait_ge(gated_up, k * UNITS + (u + 1))
                    act.wait_ge(multiplied, k * UNITS + (u + FREE - 1))
                    by = w[b % 2][:, scale0:scale0 + 1] if scaled else 1.0
                    nc.scalar.activation(gate[u % 2][:], ps_gate[u % 2][:], ACT.Silu, scale=by
                                         ).then_inc(silued, 1)

        @block.vector
        def _(dve):
            dve.sem_inc(multiplied, FREE)
            with dve.Fori(0, TURNS) as k:
                for u in range(UNITS):
                    b = u // 2
                    dve.wait_ge(weighted if combine is not None else silued, k * UNITS + (u + 1))
                    dve.wait_ge(lowered, k * UNITS + (u + FREE - 1))
                    if scaled:
                        nc.vector.scalar_tensor_tensor(inner[u % 2][:], ps_up[u % 2][:],
                                                       w[b % 2][:, scale0 + 1:scale0 + 2], gate[u % 2][:],
                                                       ALU.mult, ALU.mult).then_inc(multiplied, 1)
                    else:
                        nc.vector.tensor_tensor(inner[u % 2][:], ps_up[u % 2][:], gate[u % 2][:], ALU.mult
                                                ).then_inc(multiplied, 1)
            dve.wait_ge(finished, 1)
            if down_scale:
                dve.wait_ge(consts_in, 16)
            for t in range(NT):
                src = ps_out[t // 2][:, t % 2 * D:(t % 2 + 1) * D]
                if down_scale:
                    buffer = inner[t % 2][:, 0:D]
                    nc.vector.tensor_tensor(buffer, src, down_by[:], ALU.mult).then_inc(consts_in, 1)
                    dve.wait_ge(consts_in, 16 + t + 1)
                    src = buffer
                nc.vector.tensor_tensor(x[:, t, :], x[:, t, :], src, ALU.add)


def feed_forward_0(core):
    with ExitStack() as layer:
        count = core.count

        def sb(name, shape):
            return layer.enter_context(core.nc.sbuf_tensor(f"ff{count}_{name}", shape, F32))

        h2T = sb("h2T", [P, DC, TOK])
        attended = sb("attended", [P, NT, D])
        modT = sb("modT", [16, TOK])
        loaded, loads = narrow_loads(core, layer, "L0f")
        normalise(core, [(core.hT, ["L0f_ln1"]), (h2T, ["L0f_ln2"])], second=("rms", 1e-6), keep=True,
                  loads=loads)
        narrow_attention(core, "L0f", loaded, into=attended)
        low_rank_factor(core, attended, h2T, modT)
        gated_feed_forward(core, "L0g", tiles=8, body=2, source=h2T, low_rank=modT)


def low_rank_factor(core, attended, h2T, modT):
    nc = core.nc
    with Stage(core, "factor") as st:
        block = st.opened
        a = st.sb("a", [P, DC, 16])
        attendedT = st.sb("attendedT", [P, DC, TOK])
        factor = st.sb("factor", [16, TOK])
        ps_turn = [st.psum(f"turn{n}", [P, HALF]) for n in range(4)]
        ps_factor = [st.psum(f"factor{n}", [16, HALF]) for n in range(2)]
        ps_low = [st.psum(f"low{n}", [16, HALF]) for n in range(2)]
        a_in, turned, kept = st.sem("a_in"), st.sem("turned"), st.sem("kept")
        factored, tanhed = st.sem("factored"), st.sem("tanhed")

        @block.sync
        def _(sp):
            sp.dma_start(a[:], core.dram["L0f_A"]).then_inc(a_in, 16)

        @block.gpsimd
        def _(pool):
            st.clear_old(pool)

        @block.tensor
        def _(pe):
            for half in range(2):
                for c in range(DC):
                    for i in range(4):
                        last = nc.tensor.transpose(ps_turn[2 * half + c][:, i * P:(i + 1) * P],
                                                   attended[:, 4 * half + i, c * P:(c + 1) * P], core.ident[:])
                    last.then_inc(turned, 1)
            pe.wait_ge(a_in, 16)
            for half in range(2):
                tokens = slice(half * HALF, (half + 1) * HALF)
                for c in range(DC):
                    nc.tensor.matmul(ps_low[half][:], a[:, c, :], h2T[:, c, tokens],
                                     start=(c == 0), stop=(c == DC - 1))
                for c in range(DC):
                    pe.wait_ge(kept, 2 * half + c + 1)
                    last = nc.tensor.matmul(ps_factor[half][:], a[:, c, :], attendedT[:, c, tokens],
                                            start=(c == 0), stop=(c == DC - 1))
                last.then_inc(factored, 1)

        @block.scalar
        def _(act):
            for half in range(2):
                act.wait_ge(factored, half + 1)
                nc.scalar.activation(factor[:, half * HALF:(half + 1) * HALF], ps_factor[half][:], ACT.Tanh
                                     ).then_inc(tanhed, 1)

        @block.vector
        def _(dve):
            for half in range(2):
                for c in range(DC):
                    dve.wait_ge(turned, 2 * half + c + 1)
                    nc.vector.tensor_copy(attendedT[:, c, half * HALF:(half + 1) * HALF],
                                          ps_turn[2 * half + c][:]).then_inc(kept, 1)
            for half in range(2):
                tokens = slice(half * HALF, (half + 1) * HALF)
                dve.wait_ge(tanhed, half + 1)
                nc.vector.scalar_tensor_tensor(modT[:, tokens], factor[:, tokens], 0.1, ps_low[half][:],
                                               ALU.mult, ALU.mult)


def ternary_feed_forward(core):
    normalise(core, [(core.hT, [])])
    gated_feed_forward(core, "L2f", tiles=6, body=2, scaled=True, down_scale="L2f_down_s")


EXPERTS, TOP = 32, 8


def experts(core):
    with ExitStack() as stack:
        loaded, loads = early(core, stack, "experts", [
            ([P, DC, EXPERTS], core.dram["L1f_router"]),
            ([P, EXPERTS], core.dram["expert_number"].broadcast_to([P, EXPERTS]))])
        normalise(core, [(core.hT, [])], loads=loads)
        combine = core.nc.dram_tensor(f"combine{core.count}", (EXPERTS, TOK), F32).ap()
        route(core, *loaded, combine)
    gated_feed_forward(core, "L1f", tiles=24, body=6, combine=combine)


def route(core, wr, number, combine):
    nc, hT = core.nc, core.hT
    with Stage(core, "route") as st:
        block = st.opened
        logits, p = st.sb("logits", [P, NT, EXPERTS]), st.sb("p", [P, NT, EXPERTS])
        peak, total, inverse = st.sb("peak", [P, NT]), st.sb("total", [P, NT]), st.sb("inverse", [P, NT])
        top, share = st.sb("top", [P, NT, TOP]), st.sb("share", [P, NT, TOP])
        index, index_f = st.sb("index", [P, NT, TOP], U32), st.sb("index_f", [P, NT, TOP])
        chosen = st.sb("chosen", [P, NT, EXPERTS, TOP])
        weights = st.sb("weights", [P, NT, EXPERTS])
        weightsT = st.sb("weightsT", [EXPERTS, TOK])
        ps_logits = st.psum("logits", [P, NT, EXPERTS])
        ps_turn = [st.psum(f"turn{n}", [EXPERTS, HALF]) for n in range(2)]
        step, projected, exped = st.sem("step"), st.sem("projected"), st.sem("exped")
        shifted, ready, turned = st.sem("shifted"), st.sem("ready"), st.sem("turned")
        copied, stored = st.sem("copied"), st.sem("stored")
        found = st.sem("found")

        def over_top(a):
            return a[:].unsqueeze(2).broadcast_to([P, NT, TOP])

        def over_experts(a):
            return a[:].unsqueeze(2).broadcast_to([P, NT, EXPERTS])

        @block.sync
        def _(sp):
            sp.wait_ge(copied, 2)
            sp.dma_start(combine, weightsT[:]).then_inc(stored, 16)
            sp.wait_ge(stored, 16)

        @block.gpsimd
        def _(pool):
            st.clear_old(pool)

        @block.tensor
        def _(pe):
            for t in range(NT):
                for c in range(DC):
                    last = nc.tensor.matmul(ps_logits[:, t, :], hT[:, c, t * P:(t + 1) * P], wr[:, c, :],
                                            start=(c == 0), stop=(c == DC - 1))
            last.then_inc(projected, 1)
            pe.wait_ge(ready, 1)
            for t in range(NT):
                last = nc.tensor.transpose(ps_turn[t // 4][:, t % 4 * P:(t % 4 + 1) * P], weights[:, t, :],
                                           core.ident[:])
                if t % 4 == 3:
                    last.then_inc(turned, 1)

        @block.scalar
        def _(act):
            act.wait_ge(shifted, 1)
            nc.scalar.activation(p[:], logits[:], ACT.Exp).then_inc(exped, 1)

        @block.vector
        def _(dve):
            link = linker(dve, step)
            dve.wait_ge(projected, 1)
            link(nc.vector.tensor_reduce(peak[:], ps_logits[:], AX, ALU.max))
            nc.vector.tensor_tensor(logits[:], ps_logits[:], over_experts(peak), ALU.subtract
                                    ).then_inc(shifted, 1)
            dve.wait_ge(exped, 1)
            link(nc.vector.tensor_reduce(total[:], p[:], AX, ALU.add))
            link(nc.vector.reciprocal(inverse[:], total[:]))
            link(nc.vector.tensor_tensor(p[:], p[:], over_experts(inverse), ALU.mult))
            for t in range(NT):
                nc.vector.max(top[:, t, :], p[:, t, :]).then_inc(found, 1)
            for t in range(NT):
                dve.wait_ge(found, t + 1)
                nc.vector.max_index(index[:, t, :], top[:, t, :], p[:, t, :]).then_inc(found, 1)
            dve.wait_ge(found, 2 * NT)
            link(nc.vector.tensor_copy(index_f[:], index[:]))
            link(nc.vector.tensor_reduce(total[:], top[:], AX, ALU.add))
            link(nc.vector.tensor_scalar(total[:], total[:], 1e-12, None, ALU.max))
            link(nc.vector.reciprocal(inverse[:], total[:]))
            link(nc.vector.tensor_tensor(share[:], top[:], over_top(inverse), ALU.mult))
            for k in range(1, TOP):
                link(nc.vector.tensor_tensor(share[:, :, k], share[:, :, k], share[:, :, k - 1], ALU.add))
            link(nc.vector.tensor_scalar(share[:], share[:], 0.8, None, ALU.is_lt))
            link(nc.vector.tensor_tensor(top[:, :, 1:], top[:, :, 1:], share[:, :, 0:TOP - 1], ALU.mult))
            link(nc.vector.tensor_reduce(total[:], top[:], AX, ALU.add))
            link(nc.vector.tensor_scalar(total[:], total[:], 1e-12, None, ALU.max))
            link(nc.vector.reciprocal(inverse[:], total[:]))
            link(nc.vector.tensor_tensor(top[:], top[:], over_top(inverse), ALU.mult))
            for t in range(NT):
                nc.vector.tensor_tensor(chosen[:, t], index_f[:, t].unsqueeze(1).broadcast_to([P, EXPERTS, TOP]),
                                        number[:].unsqueeze(2).broadcast_to([P, EXPERTS, TOP]), ALU.is_equal
                                        ).then_inc(found, 1)
            for t in range(NT):
                dve.wait_ge(found, 2 * NT + t + 1)
                nc.vector.tensor_tensor(chosen[:, t], chosen[:, t],
                                        top[:, t].unsqueeze(1).broadcast_to([P, EXPERTS, TOP]), ALU.mult
                                        ).then_inc(found, 1)
            dve.wait_ge(found, 4 * NT)
            nc.vector.tensor_reduce(weights[:], chosen[:], AX, ALU.add).then_inc(ready, 1)
            for n in range(2):
                dve.wait_ge(turned, n + 1)
                nc.vector.tensor_copy(weightsT[:, n * HALF:(n + 1) * HALF], ps_turn[n][:]).then_inc(copied, 1)


def decay_scan(core):
    nc, x, hT = core.nc, core.x, core.hT
    with ExitStack() as layer:
        (w, bias), loads = early(core, layer, "decay", [([P, DC, D], core.dram["L1b_w"]),
                                                        ([P, DC], core.dram["L1b_b"])])
        normalise(core, [(core.hT, [])], loads=loads)
        st = layer.enter_context(Stage(core, "decay"))
        block = st.opened
        lam, fed, s = st.sb("lam", [P, DC, TOK]), st.sb("fed", [P, DC, TOK]), st.sb("s", [P, DC, TOK])
        ps_lam = [st.psum(f"lam{n}", [P, HALF]) for n in range(4)]
        ps_rows = [st.psum(f"rows{n}", [P, HALF]) for n in range(4)]
        projected, decays, feeds = st.sem("projected"), st.sem("decays"), st.sem("feeds")
        scanned, turned = st.sem("scanned"), st.sem("turned")

        @block.gpsimd
        def _(pool):
            st.clear_old(pool)

        @block.tensor
        def _(pe):
            for e in range(DC):
                for half in range(2):
                    for c in range(DC):
                        last = nc.tensor.matmul(ps_lam[2 * e + half][:], w[:, c, e * P:(e + 1) * P],
                                                hT[:, c, half * HALF:(half + 1) * HALF],
                                                start=(c == 0), stop=(c == DC - 1))
                    last.then_inc(projected, 1)
            pe.wait_ge(scanned, 2)
            for t in range(NT):
                for c in range(DC):
                    last = nc.tensor.transpose(ps_rows[t // 2][:, t % 2 * D + c * P:t % 2 * D + (c + 1) * P],
                                               s[:, c, t * P:(t + 1) * P], core.ident[:])
                if t % 2:
                    last.then_inc(turned, 1)

        @block.scalar
        def _(act):
            for e in range(DC):
                for half in range(2):
                    act.wait_ge(projected, 2 * e + half + 1)
                    nc.scalar.activation(lam[:, e, half * HALF:(half + 1) * HALF], ps_lam[2 * e + half][:],
                                         ACT.Sigmoid, bias=bias[:, e:e + 1]).then_inc(decays, 1)

        @block.vector
        def _(dve):
            for e in range(DC):
                dve.wait_ge(decays, 2 * e + 2)
                nc.vector.scalar_tensor_tensor(fed[:, e, :], lam[:, e, :], 1.0, hT[:, e, :], ALU.subtract,
                                               ALU.mult).then_inc(feeds, 1)
                dve.wait_ge(feeds, e + 1)
                nc.vector.tensor_tensor_scan(s[:, e, :], lam[:, e, :], fed[:, e, :], 0.0, ALU.mult,
                                             ALU.subtract).then_inc(scanned, 1)
            for n in range(4):
                dve.wait_ge(turned, n + 1)
                two = x[:, 2 * n:2 * n + 2, :]
                nc.vector.tensor_tensor(two, two, ps_rows[n][:].rearrange("p (t d) -> p t d", t=2), ALU.add)


ROUTES, RANK = 6, 16


def low_rank_experts(core):
    nc, x, hT = core.nc, core.x, core.hT
    LOW = RANK * (1 + ROUTES)
    with ExitStack() as layer:
        loaded, loads = early(core, layer, "low", [
            ([P, DC, LOW + ROUTES], core.dram["L3f_w1"]), ([P, DC, D], core.dram["L3f_base"]),
            ([LOW + 1, D], core.dram["L3f_w2"]),
            ([P, ROUTES], core.dram["L3f_router_bias"].broadcast_to([P, ROUTES])),
            ([P, ROUTES], core.dram["expert_number"][:, 0:ROUTES].broadcast_to([P, ROUTES]))])
        w1, base, w2, router_bias, number = loaded
        normalise(core, [(core.hT, [])], loads=loads)
        st = layer.enter_context(Stage(core, "low"))
        block = st.opened
        zeros = st.sb("zeros", [P, HALF], BF16)
        p, shifted_logits = st.sb("p", [P, NT, 8]), st.sb("shifted_logits", [P, NT, ROUTES])
        peak, total, inverse = st.sb("peak", [P, NT]), st.sb("total", [P, NT]), st.sb("inverse", [P, NT])
        top, index, index_f = st.sb("top", [P, NT, 8]), st.sb("index", [P, NT, 8], U32), st.sb("index_f", [P, NT, 8])
        chosen, weights = st.sb("chosen", [P, NT, ROUTES, 2]), st.sb("weights", [P, NT, ROUTES])
        z, zT = st.sb("z", [P, NT, LOW + 1]), st.sb("zT", [LOW + 1, TOK])
        ps_z = st.psum("z", [P, NT, P])
        ps_turn = [st.psum(f"turn{n}", [LOW + 1, HALF]) for n in range(2)]
        ps_out = [st.psum(f"out{n}", [P, HALF]) for n in range(4)]
        step, projected, shifted, zeroed = st.sem("step"), st.sem("projected"), st.sem("shifted"), st.sem("zeroed")
        exped, found, weighted = st.sem("exped"), st.sem("found"), st.sem("weighted")
        turned, kept, out_ready, filled = st.sem("turned"), st.sem("kept"), st.sem("out_ready"), st.sem("filled")
        kept_act = st.sem("kept_act")

        def out_of(t):
            return ps_out[t // 2][:, t % 2 * D:(t % 2 + 1) * D]

        @block.gpsimd
        def _(pool):
            nc.gpsimd.memset(zeros[:], 0.0).then_inc(zeroed, 1)
            nc.gpsimd.memset(p[:], -1.0).then_inc(filled, 1)
            nc.gpsimd.memset(z[:], 1.0).then_inc(filled, 1)
            st.clear_old(pool)

        @block.tensor
        def _(pe):
            for t in range(NT):
                for c in range(DC):
                    last = nc.tensor.matmul(ps_z[:, t, 0:LOW + ROUTES], hT[:, c, t * P:(t + 1) * P], w1[:, c, :],
                                            start=(c == 0), stop=(c == DC - 1))
            last.then_inc(projected, 1)
            pe.wait_ge(zeroed, 1)
            for n in range(4):
                nc.tensor.matmul(ps_out[n][:], zeros[:, 0:P], zeros[:], start=True, stop=True)
            for t in range(NT):
                for c in range(DC):
                    nc.tensor.matmul(out_of(t), hT[:, c, t * P:(t + 1) * P], base[:, c, :],
                                     start=False, stop=False, skip_group_check=True)
            pe.wait_ge(weighted, 2)
            for t in range(NT):
                last = nc.tensor.transpose(ps_turn[t // 4][:, t % 4 * P:(t % 4 + 1) * P], z[:, t, :],
                                           core.ident[:])
                if t % 4 == 3:
                    last.then_inc(turned, 1)
            for t in range(NT):
                if t % 4 == 0:
                    pe.wait_ge(kept if t == 0 else kept_act, 1)
                last = nc.tensor.matmul(out_of(t), zT[:, t * P:(t + 1) * P], w2[:], start=False, stop=True,
                                        skip_group_check=True)
                if t % 2:
                    last.then_inc(out_ready, 1)

        @block.scalar
        def _(act):
            act.wait_ge(shifted, 1)
            act.wait_ge(filled, 1)
            nc.scalar.activation(p[:, :, 0:ROUTES], shifted_logits[:], ACT.Exp).then_inc(exped, 1)
            act.wait_ge(turned, 2)
            nc.scalar.copy(zT[:, HALF:], ps_turn[1][:]).then_inc(kept_act, 1)

        @block.vector
        def _(dve):
            link = linker(dve, step)

            def over_routes(a):
                return a[:].unsqueeze(2).broadcast_to([P, NT, ROUTES])

            dve.wait_ge(projected, 1)
            link(nc.vector.tensor_tensor(shifted_logits[:], ps_z[:, :, LOW:LOW + ROUTES],
                                         router_bias[:].unsqueeze(1).broadcast_to([P, NT, ROUTES]), ALU.add))
            link(nc.vector.tensor_reduce(peak[:], shifted_logits[:], AX, ALU.max))
            nc.vector.tensor_tensor(shifted_logits[:], shifted_logits[:], over_routes(peak), ALU.subtract
                                    ).then_inc(shifted, 1)
            dve.wait_ge(exped, 1)
            link(nc.vector.tensor_reduce(total[:], p[:, :, 0:ROUTES], AX, ALU.add))
            link(nc.vector.reciprocal(inverse[:], total[:]))
            link(nc.vector.tensor_tensor(p[:, :, 0:ROUTES], p[:, :, 0:ROUTES], over_routes(inverse), ALU.mult))
            for t in range(NT):
                nc.vector.max(top[:, t, :], p[:, t, :]).then_inc(found, 1)
            for t in range(NT):
                dve.wait_ge(found, t + 1)
                nc.vector.max_index(index[:, t, :], top[:, t, :], p[:, t, :]).then_inc(found, 1)
            dve.wait_ge(found, 2 * NT)
            link(nc.vector.tensor_copy(index_f[:], index[:]))
            for k in range(2):
                nc.vector.tensor_tensor(chosen[:, :, :, k],
                                        index_f[:, :, k].unsqueeze(2).broadcast_to([P, NT, ROUTES]),
                                        number[:].unsqueeze(1).broadcast_to([P, NT, ROUTES]), ALU.is_equal
                                        ).then_inc(found, 1)
            for k in range(2):
                dve.wait_ge(found, 2 * NT + k + 1)
                nc.vector.tensor_tensor(chosen[:, :, :, k], chosen[:, :, :, k],
                                        top[:, :, k].unsqueeze(2).broadcast_to([P, NT, ROUTES]), ALU.mult
                                        ).then_inc(found, 1)
            dve.wait_ge(found, 2 * NT + 4)
            link(nc.vector.tensor_tensor(weights[:], chosen[:, :, :, 0], chosen[:, :, :, 1], ALU.add))
            dve.wait_ge(filled, 2)
            nc.vector.tensor_copy(z[:, :, 0:RANK], ps_z[:, :, 0:RANK]).then_inc(weighted, 1)
            nc.vector.tensor_tensor(z[:, :, RANK:LOW].rearrange("p t (e r) -> p t e r", e=ROUTES),
                                    ps_z[:, :, RANK:LOW].rearrange("p t (e r) -> p t e r", e=ROUTES),
                                    weights[:].unsqueeze(3).broadcast_to([P, NT, ROUTES, RANK]), ALU.mult
                                    ).then_inc(weighted, 1)
            dve.wait_ge(turned, 1)
            nc.vector.tensor_copy(zT[:, 0:HALF], ps_turn[0][:]).then_inc(kept, 1)
            for n in range(4):
                dve.wait_ge(out_ready, n + 1)
                two = x[:, 2 * n:2 * n + 2, :]
                nc.vector.tensor_tensor(two, two, ps_out[n][:].rearrange("p (t d) -> p t d", t=2), ALU.add)


STATES = 16


def state_space(core):
    with ExitStack() as layer:
        count = core.count
        loaded, loads = early(core, layer, "steps", [
            ([P, DC, P + 2 * STATES], core.dram["L3b_wx"]), ([P, D], core.dram["L3b_wdt"]),
            ([P, DC], core.dram["L3b_bdt"])])
        normalise(core, [(core.hT, [])], loads=loads)
        nc = core.nc

        def sb(name, shape):
            return layer.enter_context(nc.sbuf_tensor(f"ss{count}_{name}", shape, F32))

        delta, fed = sb("delta", [P, DC, TOK]), sb("fed", [P, DC, TOK])
        bc = nc.dram_tensor(f"bc{count}", (2 * STATES, TOK), F32).ap()
        steps_and_feeds(core, *loaded, delta, fed, bc)
        scan_states(core, delta, fed, bc)


def steps_and_feeds(core, wx, wdt, bias, delta, fed, bc):
    nc, hT = core.nc, core.hT
    with Stage(core, "steps") as st:
        block = st.opened
        dtT, bcT = st.sb("dtT", [P, TOK]), st.sb("bcT", [2 * STATES, TOK])
        raw, size = st.sb("raw", [P, DC, TOK]), st.sb("size", [P, DC, TOK])
        small, one_more, log = st.sb("small", [P, DC, TOK]), st.sb("one_more", [P, DC, TOK]), st.sb("log", [P, DC, TOK])
        ps_dt = [st.psum(f"dt{n}", [P, HALF]) for n in range(2)]
        ps_bc = [st.psum(f"bc{n}", [2 * STATES, HALF]) for n in range(2)]
        ps_raw = [st.psum(f"raw{n}", [P, HALF]) for n in range(4)]
        projected, kept, bc_kept = st.sem("projected"), st.sem("kept"), st.sem("bc_kept")
        raw_ready, biased, sized = st.sem("raw_ready"), st.sem("biased"), st.sem("sized")
        small_ready, added, logged = st.sem("small_ready"), st.sem("added"), st.sem("logged")
        step, stored = st.sem("step"), st.sem("stored")

        @block.sync
        def _(sp):
            sp.wait_ge(bc_kept, 2)
            sp.dma_start(bc, bcT[:]).then_inc(stored, 16)
            sp.wait_ge(stored, 16)

        @block.gpsimd
        def _(pool):
            st.clear_old(pool)

        @block.tensor
        def _(pe):
            for half in range(2):
                tokens = slice(half * HALF, (half + 1) * HALF)
                for c in range(DC):
                    nc.tensor.matmul(ps_dt[half][:], wx[:, c, 0:P], hT[:, c, tokens],
                                     start=(c == 0), stop=(c == DC - 1))
                for c in range(DC):
                    last = nc.tensor.matmul(ps_bc[half][:], wx[:, c, P:], hT[:, c, tokens],
                                            start=(c == 0), stop=(c == DC - 1))
                last.then_inc(projected, 1)
            for half in range(2):
                pe.wait_ge(kept, half + 1)
                for e in range(DC):
                    nc.tensor.matmul(ps_raw[2 * half + e][:], wdt[:, e * P:(e + 1) * P],
                                     dtT[:, half * HALF:(half + 1) * HALF], start=True, stop=True
                                     ).then_inc(raw_ready, 1)

        @block.scalar
        def _(act):
            for half in range(2):
                tokens = slice(half * HALF, (half + 1) * HALF)
                act.wait_ge(projected, half + 1)
                nc.scalar.copy(dtT[:, tokens], ps_dt[half][:]).then_inc(kept, 1)
                nc.scalar.copy(bcT[:, tokens], ps_bc[half][:]).then_inc(bc_kept, 1)
            act.wait_ge(sized, 1)
            nc.scalar.activation(small[:], size[:], ACT.Exp, scale=-1.0).then_inc(small_ready, 1)
            act.wait_ge(added, 1)
            nc.scalar.activation(log[:], one_more[:], ACT.Ln).then_inc(logged, 1)

        @block.vector
        def _(dve):
            link = linker(dve, step)
            for half in range(2):
                for e in range(DC):
                    dve.wait_ge(raw_ready, 2 * half + e + 1)
                    nc.vector.tensor_scalar(raw[:, e, half * HALF:(half + 1) * HALF], ps_raw[2 * half + e][:],
                                            bias[:, e:e + 1], None, ALU.add).then_inc(biased, 1)
            dve.wait_ge(biased, 4)
            nc.vector.scalar_tensor_tensor(size[:], raw[:], -1.0, raw[:], ALU.mult, ALU.max).then_inc(sized, 1)
            dve.wait_ge(small_ready, 1)
            nc.vector.tensor_scalar(one_more[:], small[:], 1.0, None, ALU.add).then_inc(added, 1)
            dve.wait_ge(added, 1)
            link(nc.vector.scalar_tensor_tensor(size[:], one_more[:], 1.0, small[:], ALU.subtract, ALU.subtract))
            link(nc.vector.scalar_tensor_tensor(size[:], raw[:], 0.0, size[:], ALU.max, ALU.subtract))
            dve.wait_ge(logged, 1)
            link(nc.vector.tensor_tensor(delta[:], size[:], log[:], ALU.add))
            nc.vector.tensor_tensor(fed[:], delta[:], hT[:], ALU.mult)


def scan_states(core, delta, fed, bc):
    nc, x, hT = core.nc, core.x, core.hT
    PAIRS = STATES // 2
    FREE = 4
    with Stage(core, "scan") as st:
        block = st.opened
        a, skip = st.sb("a", [P, DC, STATES]), st.sb("skip", [P, DC])
        spread_b = [st.sb(f"spread_b{n}", [P, TOK]) for n in range(2)]
        spread_c = [st.sb(f"spread_c{n}", [P, TOK]) for n in range(2)]
        decay = [st.sb(f"decay{n}", [P, TOK]) for n in range(2)]
        feed = [st.sb(f"feed{n}", [P, TOK]) for n in range(2)]
        state = [st.sb(f"state{n}", [P, TOK]) for n in range(2)]
        seen = [st.sb(f"seen{n}", [P, TOK]) for n in range(2)]
        yT = st.sb("yT", [P, DC, TOK])
        ps_y = [st.psum(f"y{n}", [P, HALF]) for n in range(4)]
        ps_rows = [st.psum(f"rows{n}", [P, HALF]) for n in range(4)]
        zeros = st.sb("zeros", [P, HALF], BF16)
        a_in, b_in, c_in = st.sem("a_in"), [st.sem(f"b_in{n}") for n in range(2)], [st.sem(f"c_in{n}") for n in range(2)]
        decays, feeds, scans, seens = st.sem("decays"), st.sem("feeds"), st.sem("scans"), st.sem("seens")
        summed, zeroed, finished, y_ready, turned = (st.sem("summed"), st.sem("zeroed"), st.sem("finished"),
                                                     st.sem("y_ready"), st.sem("turned"))

        @block.sync
        def _(sp):
            sp.dma_start(a[:], core.dram["L3b_A"]).then_inc(a_in, 16)
            sp.dma_start(skip[:], core.dram["L3b_D"]).then_inc(a_in, 16)
            with sp.Fori(0, PAIRS) as k:
                for b in range(2):
                    sp.wait_ge(feeds, k * 4 + (2 * b + 2))
                    sp.dma_start(spread_b[b][:], bc[bass.ds(2 * k + b, 1)].broadcast_to([P, TOK])
                                 ).then_inc(b_in[b], 16)
                    sp.wait_ge(seens, k * 4 + (2 * b + 2))
                    sp.dma_start(spread_c[b][:], bc[bass.ds(2 * k + b + STATES, 1)].broadcast_to([P, TOK])
                                 ).then_inc(c_in[b], 16)

        @block.gpsimd
        def _(pool):
            pool.sem_inc(feeds, FREE)
            nc.gpsimd.memset(zeros[:], 0.0).then_inc(zeroed, 1)
            st.clear_old(pool)
            with pool.Fori(0, PAIRS) as k:
                for u in range(4):
                    b, c = u // 2, u % 2
                    pool.wait_ge(b_in[b], k * 16 + 16)
                    pool.wait_ge(scans, k * 4 + (u + FREE - 1))
                    nc.gpsimd.tensor_tensor(feed[c][:], fed[:, c, :], spread_b[b][:], ALU.mult
                                            ).then_inc(feeds, 1)

        @block.scalar
        def _(act):
            act.wait_ge(a_in, 32)
            with act.Fori(0, PAIRS) as k:
                for u in range(4):
                    b, c = u // 2, u % 2
                    act.wait_ge(scans, k * 4 + (u + FREE - 1))
                    nc.scalar.activation(decay[c][:], delta[:, c, :], ACT.Exp,
                                         scale=a[:, c, bass.ds(2 * k + b, 1)]).then_inc(decays, 1)

        @block.vector
        def _(dve):
            dve.sem_inc(scans, FREE)
            dve.sem_inc(seens, FREE)
            with dve.Fori(0, PAIRS) as k:
                for u in range(4):
                    b, c = u // 2, u % 2
                    dve.wait_ge(decays, k * 4 + (u + 1))
                    dve.wait_ge(feeds, k * 4 + (u + FREE + 1))
                    dve.wait_ge(seens, k * 4 + (u + FREE - 1))
                    nc.vector.tensor_tensor_scan(state[c][:], decay[c][:], feed[c][:], 0.0, ALU.mult, ALU.add
                                                 ).then_inc(scans, 1)
                    dve.wait_ge(scans, k * 4 + (u + FREE + 1))
                    dve.wait_ge(c_in[b], k * 16 + 16)
                    dve.wait_ge(summed, k * 4 + (u + FREE - 1))
                    nc.vector.tensor_tensor(seen[c][:], state[c][:], spread_c[b][:], ALU.mult
                                            ).then_inc(seens, 1)
            dve.wait_ge(finished, 1)
            dve.wait_ge(a_in, 32)
            for c in range(DC):
                for half in range(2):
                    tokens = slice(half * HALF, (half + 1) * HALF)
                    nc.vector.scalar_tensor_tensor(yT[:, c, tokens], hT[:, c, tokens], skip[:, c:c + 1],
                                                   ps_y[2 * c + half][:], ALU.mult, ALU.add
                                                   ).then_inc(y_ready, 1)
            for n in range(4):
                dve.wait_ge(turned, n + 1)
                two = x[:, 2 * n:2 * n + 2, :]
                nc.vector.tensor_tensor(two, two, ps_rows[n][:].rearrange("p (t d) -> p t d", t=2), ALU.add)

        @block.tensor
        def _(pe):
            pe.sem_inc(summed, FREE)
            pe.wait_ge(zeroed, 1)
            for n in range(4):
                nc.tensor.matmul(ps_y[n][:], zeros[:, 0:P], zeros[:], start=True, stop=False)
            with pe.Fori(0, PAIRS) as k:
                for u in range(4):
                    c = u % 2
                    pe.wait_ge(seens, k * 4 + (u + FREE + 1))
                    for half in range(2):
                        last = nc.tensor.matmul(ps_y[2 * c + half][:], core.ident[:],
                                                seen[c][:, half * HALF:(half + 1) * HALF],
                                                start=False, stop=False, skip_group_check=True)
                    last.then_inc(summed, 1)
            for n in range(4):
                last = nc.tensor.matmul(ps_y[n][:], zeros[:, 0:P], zeros[:], start=False, stop=True)
            last.then_inc(finished, 1)
            pe.wait_ge(y_ready, 4)
            for t in range(NT):
                for c in range(DC):
                    last = nc.tensor.transpose(ps_rows[t // 2][:, t % 2 * D + c * P:t % 2 * D + (c + 1) * P],
                                               yT[:, c, t * P:(t + 1) * P], core.ident[:])
                if t % 2:
                    last.then_inc(turned, 1)


CHUNK = 64
KEYS = 16


def linear_attention(core):
    nc = core.nc
    with ExitStack() as layer:
        def sb(name, shape):
            return layer.enter_context(nc.sbuf_tensor(f"la_{name}", shape, F32))

        h = sb("h", [P, NT, D])
        anchored_q, anchored_k = sb("anchored_q", [KEYS, TOK]), sb("anchored_k", [KEYS, TOK])
        decayed_q = sb("decayed_q", [KEYS, TOK])
        kept_k = sb("kept_k", [P, NT, KEYS])
        chunk_decay = sb("chunk_decay", [KEYS, 2 * NT])
        o = sb("o", [P, NT, D])
        loaded, loads = early(core, layer, "keys", [
            ([P, DC, 2 * KEYS], core.dram["L1a_wqk"]), ([P, 3, P], core.dram["chunk_sums"]),
            ([P, 2], core.dram["chunk_ends"])])
        normalise(core, [(core.hT, [])], rows=h, loads=loads)
        decayed_keys(core, *loaded, anchored_q, anchored_k, decayed_q, kept_k, chunk_decay)
        chunks(core, h, anchored_q, anchored_k, decayed_q, kept_k, chunk_decay, o)
        gate_and_project(core, o)


def decayed_keys(core, w, sums, ends, anchored_q, anchored_k, decayed_q, kept_k, chunk_decay):
    nc, hT = core.nc, core.hT
    with Stage(core, "keys") as st:
        block = st.opened
        q, k = st.sb("q", [P, NT, KEYS]), st.sb("k", [P, NT, KEYS])
        peak, total = st.sb("peak", [P, NT]), st.sb("total", [P, NT])
        g = st.sb("g", [P, NT, KEYS])
        turn_in = [st.sb(f"turn_in{n}", [P, NT, KEYS]) for n in range(3)]
        exps = [st.sb(f"exps{n}", [P, NT, KEYS]) for n in range(4)]
        ps_qk = st.psum("qk", [P, NT, 2 * KEYS])
        ps_sum = [st.psum(f"sum{n}", [P, NT, KEYS]) for n in range(3)]
        ps_end = st.psum("end", [KEYS, 2 * NT])
        ps_turn = [st.psum(f"turn{n}", [KEYS, HALF]) for n in range(3)]
        step, projected, shifted = st.sem("step"), st.sem("projected"), st.sem("shifted")
        exped, gates, summed, exps_ready = st.sem("exped"), st.sem("gates"), st.sem("summed"), st.sem("exps_ready")
        ready, turned, kept = st.sem("ready"), st.sem("turned"), st.sem("kept")
        act_step, e_ready = st.sem("act_step"), st.sem("e_ready")

        @block.gpsimd
        def _(pool):
            st.clear_old(pool)

        @block.tensor
        def _(pe):
            for t in range(NT):
                for c in range(DC):
                    last = nc.tensor.matmul(ps_qk[:, t, :], hT[:, c, t * P:(t + 1) * P], w[:, c, :],
                                            start=(c == 0), stop=(c == DC - 1))
            last.then_inc(projected, 1)
            pe.wait_ge(gates, 1)
            for n in range(3):
                nc.tensor.matmul(ps_sum[n][:], sums[:, n, :], g[:], start=True, stop=True)
            for t in range(NT):
                last = nc.tensor.matmul(ps_end[:, 2 * t:2 * t + 2], g[:, t, :], ends[:], start=True, stop=True)
            last.then_inc(summed, 1)
            for n in range(6):
                pe.wait_ge(ready, n // 2 + 1)
                if n >= 3:
                    pe.wait_ge(kept, n - 2)
                for i in range(4):
                    last = nc.tensor.transpose(ps_turn[n % 3][:, i * P:(i + 1) * P],
                                               turn_in[n // 2][:, n % 2 * 4 + i, :], core.ident[:])
                last.then_inc(turned, 1)

        @block.scalar
        def _(act):
            link = linker(act, act_step)
            act.wait_ge(projected, 1)
            link(nc.scalar.activation(k[:], ps_qk[:, :, KEYS:], ACT.Sigmoid))
            link(nc.scalar.activation(g[:], k[:], ACT.Exp))
            act.wait_ge(shifted, 1)
            nc.scalar.activation(q[:], q[:], ACT.Exp).then_inc(exped, 1)
            act.wait_ge(e_ready, 1)
            nc.scalar.activation(g[:], g[:], ACT.Ln).then_inc(gates, 1)
            act.wait_ge(summed, 1)
            nc.scalar.activation(exps[0][:], ps_sum[0][:], ACT.Exp, scale=-1.0).then_inc(exps_ready, 1)
            nc.scalar.activation(exps[1][:], ps_sum[0][:], ACT.Exp).then_inc(exps_ready, 1)
            nc.scalar.activation(exps[2][:], ps_sum[1][:], ACT.Exp, scale=-1.0).then_inc(exps_ready, 1)
            nc.scalar.activation(exps[3][:], ps_sum[2][:], ACT.Exp, scale=-1.0).then_inc(exps_ready, 1)
            nc.scalar.activation(chunk_decay[:], ps_end[:], ACT.Exp, scale=-1.0).then_inc(exps_ready, 1)

        @block.vector
        def _(dve):
            link = linker(dve, step)
            dve.wait_ge(act_step, 2)
            nc.vector.tensor_scalar(g[:], g[:], 1.0, None, ALU.add).then_inc(e_ready, 1)
            link(nc.vector.tensor_reduce(peak[:], ps_qk[:, :, 0:KEYS], AX, ALU.max))
            nc.vector.tensor_tensor(q[:], ps_qk[:, :, 0:KEYS], peak[:].unsqueeze(2).broadcast_to([P, NT, KEYS]),
                                    ALU.subtract).then_inc(shifted, 1)
            dve.wait_ge(exped, 1)
            link(nc.vector.tensor_reduce(total[:], q[:], AX, ALU.add))
            link(nc.vector.reciprocal(peak[:], total[:]))
            link(nc.vector.tensor_tensor(q[:], q[:], peak[:].unsqueeze(2).broadcast_to([P, NT, KEYS]), ALU.mult))
            for n, (a, out) in enumerate(((q, turn_in[0]), (k, turn_in[1]), (q, turn_in[2]), (k, kept_k))):
                dve.wait_ge(exps_ready, n + 1)
                nc.vector.tensor_tensor(out[:], a[:], exps[n][:], ALU.mult).then_inc(ready, 1)
            for n in range(6):
                to = (anchored_q, anchored_k, decayed_q)[n // 2]
                dve.wait_ge(turned, n + 1)
                nc.vector.tensor_copy(to[:, n % 2 * HALF:(n % 2 + 1) * HALF], ps_turn[n % 3][:]).then_inc(kept, 1)


def chunks(core, h, anchored_q, anchored_k, decayed_q, kept_k, chunk_decay, o):
    nc = core.nc
    NC = 2 * NT
    with Stage(core, "chunks") as st:
        block = st.opened
        mask = st.sb("mask", [P, CHUNK])
        scores = st.sb("scores", [P, NT, CHUNK])
        states = st.sb("states", [KEYS, NC, D])
        ps_scores = st.psum("scores", [P, NT, CHUNK])
        ps_state = [st.psum(f"state{n}", [KEYS, HALF]) for n in range(4)]
        ps_o = [st.psum(f"o{n}", [P, HALF]) for n in range(2)]
        in_, scored, masked, zeroed = st.sem("in"), st.sem("scored"), st.sem("masked"), st.sem("zeroed")
        added, state_ready, o_ready, o_kept = st.sem("added"), st.sem("state_ready"), st.sem("o_ready"), st.sem("o_kept")

        def place(c):
            return c // 2, slice(c % 2 * CHUNK, (c % 2 + 1) * CHUNK)

        def state_bank(c):
            return ps_state[c // 4 % 2 * 2 + c % 2][:, c // 2 % 2 * D:(c // 2 % 2 + 1) * D]

        @block.sync
        def _(sp):
            sp.dma_start(mask[:], core.dram["chunk_mask"]).then_inc(in_, 16)

        @block.gpsimd
        def _(pool):
            nc.gpsimd.memset(states[:, 0, :], 0.0).then_inc(zeroed, 1)
            st.clear_old(pool)

        @block.tensor
        def _(pe):
            for c in range(NC):
                t, at = place(c)
                tokens = slice(c * CHUNK, (c + 1) * CHUNK)
                last = nc.tensor.matmul(ps_scores[at, t, :], anchored_k[:, tokens], anchored_q[:, tokens],
                                        start=True, stop=True)
            last.then_inc(scored, 1)
            for c in range(NC):
                t, at = place(c)
                if c % 4 == 0 and c >= 8:
                    pe.wait_ge(state_ready, c - 4)
                nc.tensor.matmul(state_bank(c), kept_k[at, t, :], h[at, t, :], start=True, stop=True
                                 ).then_inc(added, 1)
            pe.wait_ge(masked, 1)
            pe.wait_ge(zeroed, 1)
            for c in range(NC):
                t, at = place(c)
                pe.wait_ge(state_ready, max(c, 1))
                if c % 4 == 0 and c >= 8:
                    pe.wait_ge(o_kept, c // 4 - 1)
                to = ps_o[t // 2 % 2][at, t % 2 * D:(t % 2 + 1) * D]
                nc.tensor.matmul(to, scores[at, t, :], h[at, t, :], start=True, stop=False)
                last = nc.tensor.matmul(to, decayed_q[:, c * CHUNK:(c + 1) * CHUNK], states[:, c, :],
                                        start=False, stop=True)
                if c % 4 == 3:
                    last.then_inc(o_ready, 1)

        @block.scalar
        def _(act):
            for n in range(4):
                act.wait_ge(o_ready, n + 1)
                nc.scalar.copy(o[:, 2 * n:2 * n + 2, :], ps_o[n % 2][:].rearrange("p (t d) -> p t d", t=2)
                               ).then_inc(o_kept, 1)

        @block.vector
        def _(dve):
            dve.wait_ge(scored, 1)
            dve.wait_ge(in_, 16)
            nc.vector.tensor_tensor(scores[:], ps_scores[:], mask[:].unsqueeze(1).broadcast_to([P, NT, CHUNK]),
                                    ALU.mult).then_inc(masked, 1)
            dve.wait_ge(zeroed, 1)
            for c in range(NC):
                if c == NC - 1:
                    break
                dve.wait_ge(added, c // 4 * 4 + 4)
                if c:
                    dve.wait_ge(state_ready, c)
                nc.vector.scalar_tensor_tensor(states[:, c + 1, :], states[:, c, :], chunk_decay[:, c:c + 1], state_bank(c),
                                               ALU.mult, ALU.add).then_inc(state_ready, 1)


def gate_and_project(core, o):
    nc, x, hT = core.nc, core.x, core.hT
    with Stage(core, "gate") as st:
        block = st.opened
        w = st.sb("w", [P, 3, DC, D])
        norm_w = st.sb("norm_w", [P, DC])
        oT, rT = st.sb("oT", [P, DC, TOK]), st.sb("rT", [P, DC, TOK])
        squares = st.sb("squares", [P, 2, D])
        square_sum, inverse = st.sb("square_sum", [P, NT]), st.sb("inverse", [P, NT])
        silu, r = st.sb("silu", [P, NT, D]), st.sb("r", [P, NT, D])
        ps_turn = [st.psum(f"turn{n}", [P, HALF]) for n in range(4)]
        ps_go = [st.psum(f"go{n}", [P, HALF]) for n in range(2)]
        ps_y = [st.psum(f"y{n}", [P, HALF]) for n in range(2)]
        in_, turned, kept, gone = st.sem("in"), st.sem("turned"), st.sem("kept"), st.sem("gone")
        squared, root, step, silued = st.sem("squared"), st.sem("root"), st.sem("step"), st.sem("silued")
        gated, r_turned, r_kept, y_ready = st.sem("gated"), st.sem("r_turned"), st.sem("r_kept"), st.sem("y_ready")
        y_added, mean_ready = st.sem("y_added"), st.sem("mean_ready")

        @block.sync
        def _(sp):
            sp.dma_start(w[:], core.dram["L1a_w"]).then_inc(in_, 16)
            sp.dma_start(norm_w[:], core.dram["L1a_norm"]).then_inc(in_, 16)

        @block.gpsimd
        def _(pool):
            st.clear_old(pool)

        @block.tensor
        def _(pe):
            for half in range(2):
                for c in range(DC):
                    for i in range(4):
                        last = nc.tensor.transpose(ps_turn[2 * half + c][:, i * P:(i + 1) * P],
                                                   o[:, 4 * half + i, c * P:(c + 1) * P], core.ident[:])
                    last.then_inc(turned, 1)
            pe.wait_ge(in_, 32)
            for t in range(NT):
                pe.wait_ge(kept, 2 if t < 4 else 4)
                if t % 2 == 0 and t >= 4:
                    pe.wait_ge(silued, t // 2 - 1)
                to = ps_go[t // 2 % 2][:, t % 2 * D:(t % 2 + 1) * D]
                for n, src in enumerate((oT, hT)):
                    for c in range(DC):
                        last = nc.tensor.matmul(to, src[:, c, t * P:(t + 1) * P], w[:, n, c, :],
                                                start=(n == 0 and c == 0), stop=(n == 1 and c == DC - 1))
                if t % 2:
                    last.then_inc(gone, 1)
            for half in range(2):
                for c in range(DC):
                    for i in range(4):
                        pe.wait_ge(gated, (4 * half + i) // 2 + 1)
                        last = nc.tensor.transpose(ps_turn[2 * half + c][:, i * P:(i + 1) * P],
                                                   r[:, 4 * half + i, c * P:(c + 1) * P], core.ident[:])
                    last.then_inc(r_turned, 1)
            for t in range(NT):
                pe.wait_ge(r_kept, 2 if t < 4 else 4)
                if t % 2 == 0 and t >= 4:
                    pe.wait_ge(y_added, t // 2 - 1)
                for c in range(DC):
                    last = nc.tensor.matmul(ps_y[t // 2 % 2][:, t % 2 * D:(t % 2 + 1) * D],
                                            rT[:, c, t * P:(t + 1) * P], w[:, 2, c, :],
                                            start=(c == 0), stop=(c == DC - 1))
                if t % 2:
                    last.then_inc(y_ready, 1)

        @block.scalar
        def _(act):
            for t in range(NT):
                if t >= 2:
                    act.wait_ge(squared, t - 1)
                nc.scalar.activation(squares[:, t % 2, :], o[:, t, :], ACT.Square,
                                     accum_out=square_sum[:, t:t + 1]).then_inc(squared, 1)
            act.wait_ge(mean_ready, 1)
            nc.scalar.activation(square_sum[:], square_sum[:], ACT.Sqrt).then_inc(root, 1)
            for n in range(4):
                act.wait_ge(gone, n + 1)
                nc.scalar.activation(silu[:, 2 * n:2 * n + 2, :], ps_go[n % 2][:].rearrange(
                    "p (t d) -> p t d", t=2), ACT.Silu).then_inc(silued, 1)

        @block.vector
        def _(dve):
            link = linker(dve, step)
            for n in range(4):
                dve.wait_ge(turned, n + 1)
                nc.vector.tensor_copy(oT[:, n % 2, n // 2 * HALF:(n // 2 + 1) * HALF], ps_turn[n][:]
                                      ).then_inc(kept, 1)
            dve.wait_ge(squared, NT)
            nc.vector.tensor_scalar(square_sum[:], square_sum[:], 1.0 / D, 1e-5, ALU.mult, ALU.add
                                    ).then_inc(mean_ready, 1)
            dve.wait_ge(root, 1)
            link(nc.vector.reciprocal(inverse[:], square_sum[:]))
            for t in range(NT):
                dve.wait_ge(silued, t // 2 + 1)
                last = nc.vector.scalar_tensor_tensor(r[:, t, :], o[:, t, :], inverse[:, t:t + 1], silu[:, t, :],
                                                      ALU.mult, ALU.mult)
                if t % 2:
                    last.then_inc(gated, 1)
            dve.wait_ge(in_, 32)
            for n in range(4):
                dve.wait_ge(r_turned, n + 1)
                c = n % 2
                nc.vector.tensor_scalar(rT[:, c, n // 2 * HALF:(n // 2 + 1) * HALF], ps_turn[n][:],
                                        norm_w[:, c:c + 1], None, ALU.mult).then_inc(r_kept, 1)
            for n in range(4):
                dve.wait_ge(y_ready, n + 1)
                two = x[:, 2 * n:2 * n + 2, :]
                nc.vector.tensor_tensor(two, two, ps_y[n % 2][:].rearrange("p (t d) -> p t d", t=2), ALU.add
                                        ).then_inc(y_added, 1)


def build(nc, dram, out, first, last):
    with ExitStack() as whole:
        core = Core(nc, dram, whole)
        load_input(core)
        layers = [
            attention_layer_0a, feed_forward_0, attention_layer_0b, feed_forward_0,
            linear_attention, experts, decay_scan, experts,
            attention_layer_2a, ternary_feed_forward, attention_layer_2b, ternary_feed_forward,
            attention_layer_3a, low_rank_experts, state_space, low_rank_experts,
        ]
        for layer in layers[first:last]:
            layer(core)
        store_output(core, out)


def attention_layer_0a(core):
    with ExitStack() as layer:
        loaded, loads = narrow_loads(core, layer, "L0a")
        normalise(core, [(core.hT, [])], loads=loads)
        narrow_attention(core, "L0a", loaded)


def attention_layer_0b(core):
    normalise(core, [(core.hT, ["L0b_norm", "L0b_split"])], second=("norm", 1e-8), keep=True)
    attention(core, "L0b", groups=2, heads=2, hd=64, scale=0.125)


def attention_layer_2a(core):
    normalise(core, [(core.hT, [])])
    wide_attention(core, "L2a", 16, 128 ** -0.5)


def attention_layer_2b(core):
    normalise(core, [(core.hT, [])])
    capped_attention(core, "L2b", 16, 50.0)


def attention_layer_3a(core):
    with ExitStack() as layer:
        loaded, loads = narrow_loads(core, layer, "L3a", bias=True)
        normalise(core, [(core.hT, [])], loads=loads)
        narrow_attention(core, "L3a", loaded, bias=True, out_bias="L3a_bo")



def rows_in_chunks(w):
    k, n = w.shape
    return np.ascontiguousarray(w.reshape(k // P, P, n).transpose(1, 0, 2))


def column_pairs(v):
    return np.ascontiguousarray(v.reshape(-1, P).T)


def spread_heads(w, group, heads, hd):
    to = np.zeros((w.shape[0], P), w.dtype)
    for j in range(heads):
        h = group * heads + j
        to[:, j * (P // heads):j * (P // heads) + hd] = w[:, h * hd:(h + 1) * hd]
    return to


def attention_weights(wq, wk, wv, groups, heads, hd, shared_kv):
    out = []
    for g in range(groups):
        q = spread_heads(wq, g, heads, hd)
        if shared_kv:
            k = np.concatenate([wk[:, g * hd:(g + 1) * hd]] * heads, 1)
            v = wv[:, g * hd:(g + 1) * hd]
        else:
            k = spread_heads(wk, g, heads, hd)
            v = wv[:, g * heads * hd:(g + 1) * heads * hd]
        out.append(rows_in_chunks(np.concatenate([q, k, v], 1)))
    return np.stack(out)


def spread_rows(w):
    to = np.zeros((P, QUADS, D), w.dtype)
    for h in range(HEADS):
        to[32 * (h % 4):32 * (h % 4) + HD, h // 4] = w[h * HD:(h + 1) * HD]
    return to


def gated_weights(gate, up, down, *more):
    tiles = -(-gate.shape[0] // P)
    parts = []
    for w in (gate, up, down):
        whole = np.zeros((tiles * P, D), w.dtype)
        whole[0:w.shape[0]] = w
        parts.append(whole.reshape(tiles, P, D))
    turned = [w.reshape(tiles, P, DC, P).transpose(0, 3, 2, 1).reshape(tiles, P, D) for w in parts[0:2]]
    return np.concatenate([*turned, parts[2], *more], 2)


def lay_out(a):
    o = {"x": a["L0_attn_a_x"][0]}
    o["L0a_wn"] = rows_in_chunks(np.concatenate([a["L0_attn_a_W" + n].T for n in "qkv"], 1))
    o["L0a_won"] = spread_rows(a["L0_attn_a_Wo"].T)
    o["L0b_w"] = attention_weights(a["L0_attn_b_Wq"].T, a["L0_attn_b_Wk"].T, a["L0_attn_b_Wv"].T, 2, 2, 64, True)
    o["L0b_wo"] = rows_in_chunks(a["L0_attn_b_Wo"].T)
    o["L0b_norm"] = column_pairs(a["L0_attn_b_norm_scale"])
    o["L0b_split"] = column_pairs(a["L0_attn_b_split_scale"])
    o["L2a_w"] = attention_weights(*(a["L2_attn_a_W_" + n].reshape(-1, D).T for n in "QKV"), 16, 1, 128, False)
    o["L2a_wo"] = rows_in_chunks(a["L2_attn_a_W_O"].transpose(0, 2, 1).reshape(-1, D))
    o["L2b_w"] = attention_weights(*(a["L2_attn_b_w" + n].T for n in "qkv"), 16, 1, 128, False)
    o["L2b_wo"] = rows_in_chunks(a["L2_attn_b_wo"].T)
    o["L2b_turns"] = np.stack([np.repeat(a["L2_attn_b_rope_cos"][0:16].T, 2, 0),
                               np.repeat(a["L2_attn_b_rope_sin"][0:16].T, 2, 0),
                               np.repeat(a["L2_attn_b_q_norm_w"][:, None], 16, 1),
                               np.repeat(a["L2_attn_b_k_norm_w"][:, None], 16, 1)], 1)
    o["L3a_wn"] = rows_in_chunks(np.concatenate(
        [a["L3_attn_a_W" + n].transpose(1, 0, 2).reshape(D, -1) for n in "qkv"], 1))
    o["L3a_won"] = spread_rows(a["L3_attn_a_Wo"])
    o["L3a_bn"] = np.stack([a["L3_attn_a_b" + n].reshape(2, P)[g] for g in range(2) for n in "qk"], 1)
    o["L3a_v_bias"] = a["L3_attn_a_bv"].reshape(1, -1)
    o["L3a_bo"] = a["L3_attn_a_bo"].reshape(1, -1)
    o["L0f_wn"] = rows_in_chunks(np.concatenate([a["L0_ffn_W" + n].T for n in "qkv"], 1))
    o["L0f_won"] = spread_rows(a["L0_ffn_Wo"].T)
    o["L0f_ln1"], o["L0f_ln2"] = column_pairs(a["L0_ffn_ln1_w"]), column_pairs(a["L0_ffn_ln2_w"])
    o["L0f_A"] = rows_in_chunks(a["L0_ffn_A"])
    low = np.zeros((8, P, P), np.float32)
    low[:, 0:16] = a["L0_ffn_B"].reshape(16, 8, P).transpose(1, 0, 2)
    o["L0g_w"] = gated_weights(a["L0_ffn_W_in_base"], a["L0_ffn_W_up_base"], a["L0_ffn_W_down"].T, low)
    scales = np.zeros((6 * P, 2), np.float32)
    scales[0:704, 0], scales[0:704, 1] = a["L2_ffn_gate_s"], a["L2_ffn_up_s"]
    o["L2f_w"] = gated_weights(a["L2_ffn_gate_w"], a["L2_ffn_up_w"], a["L2_ffn_down_w"].T,
                               scales.reshape(6, P, 2))
    o["L2f_down_s"] = a["L2_ffn_down_s"].reshape(1, D)
    gu = a["L1_ffn_gate_up_proj"]
    o["L1f_w"] = gated_weights(gu[:, 0:96].reshape(-1, D), gu[:, 96:].reshape(-1, D),
                               a["L1_ffn_down_proj"].transpose(0, 2, 1).reshape(-1, D))
    o["L1f_router"] = rows_in_chunks(a["L1_ffn_gate_weight"].T)
    o["expert_number"] = np.arange(EXPERTS, dtype=np.float32).reshape(1, -1)
    o["L1b_w"], o["L1b_b"] = rows_in_chunks(a["L1_attn_b_W"].T), column_pairs(a["L1_attn_b_b"])
    routed = a["L3_ffn_A_r"].transpose(1, 0, 2).reshape(D, -1)
    o["L3f_w1"] = rows_in_chunks(np.concatenate([a["L3_ffn_A_s"], routed, a["L3_ffn_W_router"]], 1))
    o["L3f_base"] = rows_in_chunks(a["L3_ffn_W_base"])
    o["L3f_w2"] = np.concatenate([a["L3_ffn_B_s"], a["L3_ffn_B_r"].reshape(-1, D),
                                  a["L3_ffn_b_base"].reshape(1, D)])
    o["L3f_router_bias"] = a["L3_ffn_b_router"].reshape(1, -1)
    o["L3b_wx"], o["L3b_wdt"] = rows_in_chunks(a["L3_attn_b_W_xproj"].T), a["L3_attn_b_W_dt"].T
    o["L3b_bdt"], o["L3b_D"] = column_pairs(a["L3_attn_b_b_dt"]), column_pairs(a["L3_attn_b_D"])
    o["L3b_A"] = rows_in_chunks(a["L3_attn_b_A"])
    o["L1a_wqk"] = rows_in_chunks(np.concatenate([a["L1_attn_a_Wq"], a["L1_attn_a_Wk"]]).T)
    o["L1a_w"] = np.stack([rows_in_chunks(a["L1_attn_a_W" + n].T) for n in ("og", "ig", "o")], 1)
    o["L1a_norm"] = column_pairs(a["L1_attn_a_g_norm_w"])
    frm, to = np.arange(P)[:, None], np.arange(P)[None, :]
    chunk = frm // CHUNK == to // CHUNK
    here, middle = chunk & (frm <= to), chunk & (frm % CHUNK < CHUNK // 2)
    o["chunk_sums"] = np.stack([here.astype(np.float32) - middle, here, chunk & (frm > to)], 1).astype(np.float32)
    o["chunk_ends"] = (np.arange(P)[:, None] // CHUNK == np.arange(2)[None, :]).astype(np.float32)
    o["chunk_mask"] = (frm % CHUNK <= np.arange(CHUNK)[None, :]).astype(np.float32)
    return {n: np.ascontiguousarray(v) for n, v in o.items()}


FIRST, LAST = 0, 16


def kernel(**inputs):
    import concourse.bacc as bacc
    from concourse.bass_utils import run_bass_kernel_spmd

    nc = bacc.Bacc("TRN2", target_bir_lowering=False, num_devices=1)
    arrays = lay_out({n: np.asarray(v) for n, v in inputs.items()})
    dram = {n: nc.dram_tensor(f"in_{n}", v.shape, mybir.dt.from_np(v.dtype), kind="ExternalInput").ap()
            for n, v in arrays.items()}
    out = nc.dram_tensor("out", (TOK, D), F32, kind="ExternalOutput").ap()
    build(nc, dram, out, FIRST, LAST)
    r = run_bass_kernel_spmd(nc, [{f"in_{n}": v for n, v in arrays.items()}], core_ids=[0])
    return r.results[0]["out"].reshape(1, TOK, D)
```
